# Optimizing a Trainium2 kernel written in Bass

```python
import numpy as np
import jax
import jax.numpy as jnp

def _softmax(x, axis=-1):
    return jax.nn.softmax(x, axis=axis)

def _gelu(x):
    return jax.nn.gelu(x, approximate=True)

def _silu(x):
    return jax.nn.silu(x)

def _sigmoid(x):
    return jax.nn.sigmoid(x)

def _layernorm(x, axis=-1, eps=1e-05):
    m = jnp.mean(x, axis=axis, keepdims=True)
    v = jnp.var(x, axis=axis, keepdims=True)
    return (x - m) / jnp.sqrt(v + eps)

def _scatter_add(tgt, idx, src, axis=0):
    return tgt.at[idx].add(src)

def _segment_sum(src, seg, n):
    return jax.ops.segment_sum(src, seg, n)
kernel_name = 'mk_decoder_postln_d2_seqx_r4_30f1e1'

def setup_inputs(seed: int=0):
    np.random.seed(seed)
    _w = jnp.asarray

    def _rec_inputs():
        import jax
        import jax.numpy as jnp
        _rk = jax.random.key(seed)
        x = 0.0003765 + 1 * jax.random.normal(jax.random.fold_in(_rk, 1), (8, 256, 512), jnp.float32)
        _lenS = 256 - jax.random.randint(jax.random.fold_in(_rk, 7), (8,), 0, max(1, 256 // 4) + 1, jnp.int32)
        _lenS2 = 256 - jax.random.randint(jax.random.fold_in(_rk, 8), (8,), 0, max(1, 256 // 4) + 1, jnp.int32)
        _ctx_2048P = jax.random.normal(jax.random.fold_in(_rk, 11), (8, 16, 512), jnp.float32)
        _ctx_2048c = jax.random.dirichlet(jax.random.fold_in(_rk, 511), 0.3 * jnp.ones((16,), jnp.float32), (8, 256))
        _ctx_2048t = jnp.einsum('bsk,bkd->bsd', _ctx_2048c, _ctx_2048P)
        _ctx_2048t = _ctx_2048t * jax.lax.rsqrt(jnp.mean(jnp.square(_ctx_2048t)) + 1e-12) * 0.953939
        ctx_2048 = -0.000292821 + 1.00034 * (_ctx_2048t + 0.3 * jax.random.normal(jax.random.fold_in(_rk, 611), (8, 256, 512), jnp.float32))
        return (x, ctx_2048)
    x, ctx_2048 = _rec_inputs()

    def _L0_attn_setup():
        import jax, jax.numpy as jnp
        import numpy as np
        key = jax.random.key(seed)
        ks = jax.random.split(key, 8)
        B, L, D = (4, 512, 512)
        H, Dh, S = (24, 64, 64)
        Di = H * Dh
        P = H * (1 + 2 * S)
        return {'hidden_states': jax.random.normal(ks[0], (B, L, D), jnp.float32), 'norm_w': jnp.ones((D,), jnp.float32), 'in_proj_w': jax.random.normal(ks[1], (2 * Di, D), jnp.float32) * 0.02, 'in_proj_b': jnp.zeros((2 * Di,), jnp.float32), 'conv_w': jax.random.normal(ks[2], (Di, 1, 4), jnp.float32) * 0.2, 'conv_b': jnp.zeros((Di,), jnp.float32), 'x_proj_w': jax.random.normal(ks[3], (P, Di), jnp.float32) * 0.02, 'x_proj_b': jnp.zeros((P,), jnp.float32), 'A_log': jnp.full((H,), np.log(0.5), jnp.float32), 'log2_alpha_base': jnp.full((H,), -1.0, jnp.float32), 'log2_beta': jnp.zeros((H,), jnp.float32), 'surprise_ema': jnp.ones((H,), jnp.float32), 'out_proj_w': jax.random.normal(ks[4], (D, Di), jnp.float32) * 0.02, 'out_proj_b': jnp.zeros((D,), jnp.float32), 'res_gate': jnp.full((1,), 1.0 / np.sqrt(2 * 24), jnp.float32)}
    _L0_attn_all = _L0_attn_setup()
    _L0_attn_in = {k: v for k, v in _L0_attn_all.items() if k in ('norm_w', 'in_proj_w', 'in_proj_b', 'conv_w', 'conv_b', 'x_proj_w', 'x_proj_b', 'A_log', 'log2_alpha_base', 'log2_beta', 'surprise_ema', 'out_proj_w', 'out_proj_b', 'res_gate')}
    del _L0_attn_all

    def _L0_xattn_setup():
        import jax, jax.numpy as jnp
        import numpy as np
        key = jax.random.key(seed)
        k1, k2, k3, k4, k5 = jax.random.split(key, 5)
        B, D_MODEL, L = (2, 256, 512)
        HEAD_DIM = 8
        H = D_MODEL // HEAD_DIM
        return {'k': jax.random.normal(k1, (B, D_MODEL, L), dtype=jnp.float32), 'v': jax.random.normal(k2, (B, D_MODEL, L), dtype=jnp.float32), 'q': jax.random.normal(k3, (B, D_MODEL, L), dtype=jnp.float32), 'ssm_kernel': jax.random.normal(k4, (H, L), dtype=jnp.float32), 'D': jax.random.normal(k5, (H,), dtype=jnp.float32), 'head_dim': HEAD_DIM}
    _L0_xattn_all = _L0_xattn_setup()
    _L0_xattn_in = {k: v for k, v in _L0_xattn_all.items() if k in ('ssm_kernel', 'D')}
    del _L0_xattn_all

    def _L0_ffn_setup():
        import jax, jax.numpy as jnp
        import numpy as np
        B, S, H = (2, 256, 512)
        E, K, F = (64, 8, 192)
        CAP = 128
        key = jax.random.key(seed)
        k1, k2, k3, k4, k5 = jax.random.split(key, 5)
        scale_h = 1.0 / np.sqrt(H)
        scale_f = 1.0 / np.sqrt(F)
        return {'hidden_states': jax.random.normal(k1, (B, S, H), jnp.float32), 'router_w': jax.random.normal(k2, (E, H), jnp.float32) * scale_h, 'w_gate': jax.random.normal(k3, (E, H, F), jnp.float32) * scale_h, 'w_up': jax.random.normal(k4, (E, H, F), jnp.float32) * scale_h, 'w_down': jax.random.normal(k5, (E, F, H), jnp.float32) * scale_f}
    _L0_ffn_all = _L0_ffn_setup()
    _L0_ffn_in = {k: v for k, v in _L0_ffn_all.items() if k in ('router_w', 'w_gate', 'w_up', 'w_down')}
    del _L0_ffn_all

    def _L1_attn_setup():
        import jax, jax.numpy as jnp
        import numpy as np
        B, L = (2, 256)
        D_MODEL, D_INNER, D_STATE, D_CONV, DT_RANK = (512, 1024, 16, 4, 128)
        key = jax.random.key(seed)
        ks = jax.random.split(key, 9)
        s = 0.02
        x = jax.random.normal(ks[0], (B, L, D_MODEL), jnp.float32)
        W_in = jax.random.normal(ks[1], (2 * D_INNER, D_MODEL), jnp.float32) * s
        conv_w = jax.random.normal(ks[2], (D_INNER, D_CONV), jnp.float32) * s
        conv_b = jax.random.normal(ks[3], (D_INNER,), jnp.float32) * s
        W_x = jax.random.normal(ks[4], (DT_RANK + 2 * D_STATE, D_INNER), jnp.float32) * s
        W_dt = jax.random.normal(ks[5], (D_INNER, DT_RANK), jnp.float32) * s
        b_dt = jax.random.normal(ks[6], (D_INNER,), jnp.float32) * s
        A_log = jnp.log(jnp.broadcast_to(jnp.arange(1, D_STATE + 1, dtype=jnp.float32), (D_INNER, D_STATE)))
        D = jnp.ones((D_INNER,), jnp.float32)
        W_out = jax.random.normal(ks[7], (D_MODEL, D_INNER), jnp.float32) * s
        return {'x': x, 'W_in': W_in, 'conv_w': conv_w, 'conv_b': conv_b, 'W_x': W_x, 'W_dt': W_dt, 'b_dt': b_dt, 'A_log': A_log, 'D': D, 'W_out': W_out}
    _L1_attn_all = _L1_attn_setup()
    _L1_attn_in = {k: v for k, v in _L1_attn_all.items() if k in ('W_in', 'conv_w', 'conv_b', 'W_x', 'W_dt', 'b_dt', 'A_log', 'D', 'W_out')}
    del _L1_attn_all

    def _L1_xattn_setup():
        import jax, jax.numpy as jnp
        import numpy as np
        EPS = 1e-06
        NUM_HEADS = 16

        def _feature_map(x):
            return jnp.where(x > 0, x + 1.0, jnp.exp(x))
        key = jax.random.key(seed)
        ks = jax.random.split(key, 7)
        B, L, S, D = (4, 1024, 1024, 512)
        sc = 1.0 / np.sqrt(D)
        return {'query': jax.random.normal(ks[0], (B, L, D), jnp.float32), 'kv': jax.random.normal(ks[1], (B, S, D), jnp.float32), 'Wq': jax.random.normal(ks[2], (D, D), jnp.float32) * sc, 'Wg': jax.random.normal(ks[3], (D, D), jnp.float32) * sc, 'bg': jnp.ones((D,), jnp.float32), 'Wkv': jax.random.normal(ks[4], (2 * D, D), jnp.float32) * sc, 'Wo': jax.random.normal(ks[5], (D, D), jnp.float32) * sc}
    _L1_xattn_all = _L1_xattn_setup()
    _L1_xattn_in = {k: v for k, v in _L1_xattn_all.items() if k in ('Wq', 'Wg', 'bg', 'Wkv', 'Wo')}
    del _L1_xattn_all

    def _L1_ffn_setup():
        import jax, jax.numpy as jnp
        import numpy as np
        B, T, D, E, H = (4, 512, 512, 4, 2048)
        TOPK = 2
        CAPACITY_FACTOR = 1
        key = jax.random.key(seed)
        k0, k1, k2, k3 = jax.random.split(key, 4)
        x = jax.random.normal(k0, (B, T, D), dtype=jnp.float32)
        Wg = jax.random.normal(k1, (D, E), dtype=jnp.float32) * 0.02
        bg = jnp.zeros((E,), dtype=jnp.float32)
        W1 = jax.random.normal(k2, (E, D, H), dtype=jnp.float32) * (1.0 / np.sqrt(D))
        W2 = jax.random.normal(k3, (E, H, D), dtype=jnp.float32) * (1.0 / np.sqrt(H))
        return {'x': x, 'Wg': Wg, 'bg': bg, 'W1': W1, 'W2': W2}
    _L1_ffn_all = _L1_ffn_setup()
    _L1_ffn_in = {k: v for k, v in _L1_ffn_all.items() if k in ('Wg', 'bg', 'W1', 'W2')}
    del _L1_ffn_all
    return {'x': x, 'ctx_2048': ctx_2048, 'L0_attn_norm_w': _L0_attn_in['norm_w'], 'L0_attn_in_proj_w': _L0_attn_in['in_proj_w'], 'L0_attn_in_proj_b': _L0_attn_in['in_proj_b'], 'L0_attn_conv_w': _L0_attn_in['conv_w'], 'L0_attn_conv_b': _L0_attn_in['conv_b'], 'L0_attn_x_proj_w': _L0_attn_in['x_proj_w'], 'L0_attn_x_proj_b': _L0_attn_in['x_proj_b'], 'L0_attn_A_log': _L0_attn_in['A_log'], 'L0_attn_log2_alpha_base': _L0_attn_in['log2_alpha_base'], 'L0_attn_log2_beta': _L0_attn_in['log2_beta'], 'L0_attn_surprise_ema': _L0_attn_in['surprise_ema'], 'L0_attn_out_proj_w': _L0_attn_in['out_proj_w'], 'L0_attn_out_proj_b': _L0_attn_in['out_proj_b'], 'L0_attn_res_gate': _L0_attn_in['res_gate'], 'L0_xattn_ssm_kernel': _L0_xattn_in['ssm_kernel'], 'L0_xattn_D': _L0_xattn_in['D'], 'L0_ffn_router_w': _L0_ffn_in['router_w'], 'L0_ffn_w_gate': _L0_ffn_in['w_gate'], 'L0_ffn_w_up': _L0_ffn_in['w_up'], 'L0_ffn_w_down': _L0_ffn_in['w_down'], 'L1_attn_W_in': _L1_attn_in['W_in'], 'L1_attn_conv_w': _L1_attn_in['conv_w'], 'L1_attn_conv_b': _L1_attn_in['conv_b'], 'L1_attn_W_x': _L1_attn_in['W_x'], 'L1_attn_W_dt': _L1_attn_in['W_dt'], 'L1_attn_b_dt': _L1_attn_in['b_dt'], 'L1_attn_A_log': _L1_attn_in['A_log'], 'L1_attn_D': _L1_attn_in['D'], 'L1_attn_W_out': _L1_attn_in['W_out'], 'L1_xattn_Wq': _L1_xattn_in['Wq'], 'L1_xattn_Wg': _L1_xattn_in['Wg'], 'L1_xattn_bg': _L1_xattn_in['bg'], 'L1_xattn_Wkv': _L1_xattn_in['Wkv'], 'L1_xattn_Wo': _L1_xattn_in['Wo'], 'L1_ffn_Wg': _L1_ffn_in['Wg'], 'L1_ffn_bg': _L1_ffn_in['bg'], 'L1_ffn_W1': _L1_ffn_in['W1'], 'L1_ffn_W2': _L1_ffn_in['W2']}

def reference(x, ctx_2048, L0_attn_norm_w, L0_attn_in_proj_w, L0_attn_in_proj_b, L0_attn_conv_w, L0_attn_conv_b, L0_attn_x_proj_w, L0_attn_x_proj_b, L0_attn_A_log, L0_attn_log2_alpha_base, L0_attn_log2_beta, L0_attn_surprise_ema, L0_attn_out_proj_w, L0_attn_out_proj_b, L0_attn_res_gate, L0_xattn_ssm_kernel, L0_xattn_D, L0_ffn_router_w, L0_ffn_w_gate, L0_ffn_w_up, L0_ffn_w_down, L1_attn_W_in, L1_attn_conv_w, L1_attn_conv_b, L1_attn_W_x, L1_attn_W_dt, L1_attn_b_dt, L1_attn_A_log, L1_attn_D, L1_attn_W_out, L1_xattn_Wq, L1_xattn_Wg, L1_xattn_bg, L1_xattn_Wkv, L1_xattn_Wo, L1_ffn_Wg, L1_ffn_bg, L1_ffn_W1, L1_ffn_W2):
    import jax
    import jax.numpy as jnp

    def _L0_attn_ref(hidden_states, norm_w, in_proj_w, in_proj_b, conv_w, conv_b, x_proj_w, x_proj_b, A_log, log2_alpha_base, log2_beta, surprise_ema, out_proj_w, out_proj_b, res_gate):
        import jax, jax.numpy as jnp
        import numpy as np
        Bsz, L, D = hidden_states.shape
        H = A_log.shape[0]
        S = (x_proj_b.shape[0] // H - 1) // 2
        Di = in_proj_w.shape[0] // 2
        Dh = Di // H
        eps = jnp.finfo(jnp.float32).eps
        x = hidden_states * jax.lax.rsqrt(jnp.mean(hidden_states ** 2, -1, keepdims=True) + eps) * norm_w
        xz = x @ in_proj_w.T + in_proj_b
        x, z = (xz[..., :Di], xz[..., Di:])
        xc = jax.lax.conv_general_dilated(x.transpose(0, 2, 1), conv_w, (1,), [(3, 0)], dimension_numbers=('NCH', 'OIH', 'NCH'), feature_group_count=Di)
        x = jax.nn.silu((xc + conv_b[None, :, None]).transpose(0, 2, 1))
        xp = (x @ x_proj_w.T + x_proj_b).reshape(Bsz, L, H, 1 + 2 * S)
        dt = xp[..., 0]
        Bs = xp[..., 1:1 + S]
        Cs = xp[..., 1 + S:]
        Bs = Bs / jnp.maximum(jnp.linalg.norm(Bs, axis=-1, keepdims=True), 1e-12)
        Cs = Cs / jnp.maximum(jnp.linalg.norm(Cs, axis=-1, keepdims=True), 1e-12)
        A = jnp.clip(A_log, -2.3, -0.01)[None, None, :] * jax.nn.softplus(dt)
        A_decay = jnp.exp(A)
        X = x.reshape(Bsz, L, H, Dh)
        alpha_base = 1.0 - 2.0 ** jnp.clip(log2_alpha_base, -3.32, -0.015)
        beta = 2.0 ** jnp.clip(log2_beta, -2.0, 2.0)

        def step(carry, xs):
            h, h_red = carry
            x_t, a_t, B_t, C_t = xs
            u_red = B_t * x_t.mean(-1)[..., None]
            diff = (1.0 - a_t)[..., None] * u_red
            pe = jnp.mean(diff ** 2, -1)
            ns = pe / (surprise_ema[None, :] + 1e-06)
            boost = jax.nn.relu(jnp.tanh(beta[None, :] * ns))
            alpha = jnp.clip(alpha_base[None, :] + (1.0 - alpha_base[None, :]) * boost, 0.01, 0.999)
            u_t = B_t[..., None] * x_t[:, :, None, :]
            h = alpha[..., None, None] * h + (1.0 - alpha)[..., None, None] * u_t
            h_red = h.mean(-1)
            y = jnp.einsum('bhs,bhsd->bhd', C_t, h)
            return ((h, h_red), y)
        h0 = jnp.zeros((Bsz, H, S, Dh), jnp.float32)
        hr0 = jnp.zeros((Bsz, H, S), jnp.float32)
        xs = (X.transpose(1, 0, 2, 3), A_decay.transpose(1, 0, 2), Bs.transpose(1, 0, 2, 3), Cs.transpose(1, 0, 2, 3))
        _, Yt = jax.lax.scan(step, (h0, hr0), xs)
        Y = Yt.transpose(1, 0, 2, 3).reshape(Bsz, L, Di)
        Y = Y * jax.nn.silu(z)
        out = Y @ out_proj_w.T + out_proj_b
        return hidden_states + res_gate * out

    def _L0_xattn_ref(k, v, q, ssm_kernel, D, head_dim):
        import jax, jax.numpy as jnp
        import numpy as np
        B, HD, L = k.shape
        H = HD // head_dim
        fft_size = 2 * L
        k_ = k.reshape(B, H, head_dim, L)
        v_ = v.reshape(B, H, head_dim, L)
        q_ = q.reshape(B, H, head_dim, L)
        kv = jnp.einsum('bhil,bhjl->bijhl', k_, v_)
        kv_f = jnp.fft.rfft(kv, n=fft_size)
        kernel_f = jnp.fft.rfft(ssm_kernel, n=fft_size)
        y = jnp.fft.irfft(kv_f * kernel_f, n=fft_size)[..., :L]
        out = y + kv * D[None, None, None, :, None]
        out = jnp.einsum('bijhl,bhil->bjhl', out, q_)
        out = jnp.transpose(out, (0, 2, 1, 3)).reshape(B, H * head_dim, L)
        return out.astype(k.dtype)

    def _L0_ffn_ref(hidden_states, router_w, w_gate, w_up, w_down):
        import jax, jax.numpy as jnp
        import numpy as np
        B, S, H = (2, 256, 512)
        E, K, F = (64, 8, 192)
        CAP = 128
        b, s, h = hidden_states.shape
        T = b * s
        xf = hidden_states.reshape(T, h)
        logits = xf @ router_w.T
        scores = jax.nn.softmax(logits.astype(jnp.float32), axis=-1)
        topk_w, topk_idx = jax.lax.top_k(scores, K)
        topk_w = topk_w / (topk_w.sum(axis=-1, keepdims=True) + 1e-20)
        slot_expert = topk_idx.reshape(-1)
        slot_token = jnp.repeat(jnp.arange(T), K)
        onehot = jax.nn.one_hot(slot_expert, E, dtype=jnp.int32)
        pos = (jnp.cumsum(onehot, axis=0) * onehot).sum(-1) - 1
        valid = pos < CAP
        dest = jnp.where(valid, slot_expert * CAP + pos, E * CAP)
        buf = jnp.zeros((E * CAP + 1, h), xf.dtype).at[dest].set(xf[slot_token])
        xb = buf[:E * CAP].reshape(E, CAP, h)
        gate = jnp.einsum('ech,ehf->ecf', xb, w_gate)
        up = jnp.einsum('ech,ehf->ecf', xb, w_up)
        hmid = jax.nn.silu(gate) * up
        yb = jnp.einsum('ecf,efh->ech', hmid, w_down).reshape(E * CAP, h)
        yb = jnp.concatenate([yb, jnp.zeros((1, h), yb.dtype)], axis=0)
        slot_out = yb[dest] * topk_w.reshape(-1)[:, None].astype(yb.dtype)
        out = jnp.zeros((T, h), yb.dtype).at[slot_token].add(slot_out)
        return out.reshape(b, s, h)

    def _L1_attn_ref(x, W_in, conv_w, conv_b, W_x, W_dt, b_dt, A_log, D, W_out):
        import jax, jax.numpy as jnp
        import numpy as np
        B, L = (2, 256)
        D_MODEL, D_INNER, D_STATE, D_CONV, DT_RANK = (512, 1024, 16, 4, 128)
        silu = jax.nn.silu
        b, l, _ = x.shape
        d_inner, d_conv = conv_w.shape
        dt_rank = W_dt.shape[1]
        d_state = A_log.shape[1]
        proj = x @ W_in.T
        xs, z = jnp.split(proj, 2, axis=-1)
        xp = jnp.pad(xs, ((0, 0), (d_conv - 1, 0), (0, 0)))
        conv = conv_b
        for k in range(d_conv):
            conv = conv + xp[:, k:k + l, :] * conv_w[:, k]
        u = silu(conv)
        x_dbl = u @ W_x.T
        dt_r = x_dbl[..., :dt_rank]
        Bm = x_dbl[..., dt_rank:dt_rank + d_state]
        Cm = x_dbl[..., dt_rank + d_state:]
        dt = jax.nn.softplus(dt_r @ W_dt.T + b_dt)
        A = -jnp.exp(A_log)
        dA = jnp.exp(dt[..., None] * A)
        dBu = dt[..., None] * Bm[:, :, None, :] * u[..., None]

        def step(h, inp):
            dA_t, dBu_t, C_t = inp
            h = dA_t * h + dBu_t
            y = jnp.einsum('bds,bs->bd', h, C_t)
            return (h, y)
        h0 = jnp.zeros((b, d_inner, d_state), x.dtype)
        _, ys = jax.lax.scan(step, h0, (jnp.moveaxis(dA, 1, 0), jnp.moveaxis(dBu, 1, 0), jnp.moveaxis(Cm, 1, 0)))
        y = jnp.moveaxis(ys, 0, 1) + u * D
        y = y * silu(z)
        return y @ W_out.T

    def _L1_xattn_ref(query, kv, Wq, Wg, bg, Wkv, Wo):
        import jax, jax.numpy as jnp
        import numpy as np
        EPS = 1e-06
        NUM_HEADS = 16

        def _feature_map(x):
            return jnp.where(x > 0, x + 1.0, jnp.exp(x))
        B, L, D = query.shape
        S = kv.shape[1]
        H = NUM_HEADS
        hd = D // H
        q = query @ Wq.T
        gate = jax.nn.sigmoid(query @ Wg.T + bg)
        kvp = kv @ Wkv.T
        k, v = jnp.split(kvp, 2, axis=-1)
        q = _feature_map(q.reshape(B, L, H, hd).transpose(0, 2, 1, 3))
        k = _feature_map(k.reshape(B, S, H, hd).transpose(0, 2, 1, 3))
        v = v.reshape(B, S, H, hd).transpose(0, 2, 1, 3)
        kv_summary = jnp.einsum('bhsd,bhse->bhde', k, v)
        k_sum = k.sum(axis=-2)
        z = 1.0 / (jnp.einsum('bhld,bhd->bhl', q, k_sum)[..., None] + EPS)
        attn = jnp.einsum('bhld,bhde->bhle', q, kv_summary) * z
        attn = attn.transpose(0, 2, 1, 3).reshape(B, L, D)
        out = attn * gate @ Wo.T
        return out

    def _L1_ffn_ref(x, Wg, bg, W1, W2):
        import jax, jax.numpy as jnp
        import numpy as np
        B, T, D, E, H = (4, 512, 512, 4, 2048)
        TOPK = 2
        CAPACITY_FACTOR = 1
        Bq, Tq, Dq = x.shape
        N = Bq * Tq
        capacity = int(N * CAPACITY_FACTOR / E)
        flat_x = x.reshape(N, Dq)
        logits = flat_x @ Wg + bg
        top_vals, top_idx = jax.lax.top_k(logits, TOPK)
        sparse = jnp.full_like(logits, -jnp.inf)
        sparse = sparse.at[jnp.arange(N)[:, None], top_idx].set(top_vals)
        probs = jax.nn.softmax(sparse, axis=-1)
        out = jnp.zeros_like(flat_x)
        for i in range(E):
            assigned = (top_idx == i).any(axis=-1)
            score = jnp.where(assigned, probs[:, i], -jnp.inf)
            sel_p, sel_idx = jax.lax.top_k(score, capacity)
            p = jnp.where(jnp.isfinite(sel_p), sel_p, 0.0)[:, None]
            tok = flat_x[sel_idx]
            h = jax.nn.gelu(tok @ W1[i], approximate=False)
            y = h @ W2[i] * p
            out = out.at[sel_idx].add(y)
        return out.reshape(Bq, Tq, Dq)
    x = _layernorm(x + _L0_attn_ref(x, L0_attn_norm_w, L0_attn_in_proj_w, L0_attn_in_proj_b, L0_attn_conv_w, L0_attn_conv_b, L0_attn_x_proj_w, L0_attn_x_proj_b, L0_attn_A_log, L0_attn_log2_alpha_base, L0_attn_log2_beta, L0_attn_surprise_ema, L0_attn_out_proj_w, L0_attn_out_proj_b, L0_attn_res_gate), axis=-1)
    x = _layernorm(x + _L0_xattn_ref(ctx_2048, ctx_2048, x, L0_xattn_ssm_kernel, L0_xattn_D, 8), axis=-1)
    x = _layernorm(x + _L0_ffn_ref(x, L0_ffn_router_w, L0_ffn_w_gate, L0_ffn_w_up, L0_ffn_w_down), axis=-1)
    x = _layernorm(x + _L1_attn_ref(x, L1_attn_W_in, L1_attn_conv_w, L1_attn_conv_b, L1_attn_W_x, L1_attn_W_dt, L1_attn_b_dt, L1_attn_A_log, L1_attn_D, L1_attn_W_out), axis=-1)
    x = _layernorm(x + _L1_xattn_ref(x, ctx_2048, L1_xattn_Wq, L1_xattn_Wg, L1_xattn_bg, L1_xattn_Wkv, L1_xattn_Wo), axis=-1)
    x = _layernorm(x + _L1_ffn_ref(x, L1_ffn_Wg, L1_ffn_bg, L1_ffn_W1, L1_ffn_W2), axis=-1)
    return x

_drawn_inputs = setup_inputs


def setup_inputs(seed=0):
    import zlib

    import numpy as np

    out = dict(_drawn_inputs(seed))
    spreads = {'L0_attn_norm_w': (1.0, 0.6),
     'L0_attn_in_proj_b': (0.0, 0.8),
     'L0_attn_conv_b': (0.0, 0.8),
     'L0_attn_x_proj_b': (0.0, 0.8),
     'L0_attn_A_log': (-0.6931471824645996, 0.6),
     'L0_attn_log2_alpha_base': (-1.0, 0.6),
     'L0_attn_log2_beta': (0.0, 0.8),
     'L0_attn_surprise_ema': (1.0, 0.6),
     'L0_attn_out_proj_b': (0.0, 0.1),
     'L1_attn_D': (1.0, 0.6),
     'L1_xattn_bg': (1.0, 0.2),
     'L1_ffn_bg': (0.0, 0.1)}
    factors = {'L0_attn_in_proj_w': 8.0,
     'L0_attn_conv_w': 8.0,
     'L0_attn_x_proj_w': 8.0,
     'L0_attn_out_proj_w': 8.0,
     'L1_attn_W_in': 5.832,
     'L1_attn_conv_w': 4.084,
     'L1_attn_conv_b': 5.372,
     'L1_attn_W_x': 8.0,
     'L1_attn_W_dt': 8.0,
     'L1_attn_b_dt': 8.0,
     'L1_attn_A_log': 8.0,
     'L1_attn_W_out': 5.61}
    for name, (base, spread) in spreads.items():
        noise = np.random.default_rng([zlib.crc32(name.encode()), seed]).standard_normal(out[name].shape)
        drawn = base * np.exp(spread * noise) if base else spread * noise
        out[name] = jnp.asarray(drawn.astype(out[name].dtype))
    for name, factor in factors.items():
        out[name] = (out[name] * factor).astype(out[name].dtype)
    return out
```

```python
from contextlib import ExitStack

import concourse.bass as bass
from concourse import mybir
from concourse.alu_op_type import AluOpType as ALU

ACT = mybir.ActivationFunctionType
AX = mybir.AxisListType
F32 = mybir.dt.float32
U32 = mybir.dt.uint32
P = 128
NB, L, D = 8, 256, 512
T = NB * L
KD = D // P
TILES = T // P
BANK = 512


class Space:

    def __init__(self, nc, name, phase):
        self.nc, self.name, self.phase, self.sems = nc, name, phase, []
        phase.callback(self.clear)

    def sb(self, name, shape, dt=F32):
        return self.phase.enter_context(self.nc.sbuf_tensor(f"{self.name}_{name}", shape, dt))

    def ps(self, name, shape=(P, BANK), dt=F32):
        return self.phase.enter_context(self.nc.psum_tensor(f"{self.name}_{name}", list(shape), dt))

    def sem(self, name):
        self.sems.append(self.nc.alloc_semaphore(name=f"{self.name}_{name}"))
        return self.sems[-1]

    def clear(self):
        self.nc.clear_and_free_semaphores(self.sems)
        self.nc.all_engine_barrier()


def alone(eng, tick):
    eng.sem_inc(tick, 1)


def linker(eng, sem, base=0):
    count = [0]

    def link(ins):
        count[0] += 1
        ins.then_inc(sem, 1)
        eng.wait_ge(sem, base + count[0])
    link.count = count
    return link


def ssm0_project(nc, x, ident, norm_w, w_in, b_in, conv_w, conv_b, u_feat, u_tok, z_tok, to_clear=()):
    DI = 1536
    F = DI // P
    EPS = 1.1920928955078125e-07
    LINKS_V, LINKS_A = 1 + 3 * F, 2
    with ExitStack() as phase:
        m = Space(nc, "a1", phase)
        w_sb = m.sb("w", [P, KD, 2 * DI])
        ident_sb = m.sb("ident", [P, P])
        nw_sb = m.sb("nw", [P, KD])
        bx_sb = m.sb("bx", [P, F])
        bz_sb = m.sb("bz", [P, DI])
        cw_sb = m.sb("cw", [P, F, 4])
        cb_sb = m.sb("cb", [P, F])
        eps_sb = m.sb("eps", [P, 1])
        x_sb = m.sb("x", [P, 2, D])
        sq_sb = m.sb("sq", [P, D])
        ss_sb = m.sb("ss", [P, 2])
        rt_sb = m.sb("rt", [P, 2])
        xn_sb = m.sb("xn", [P, 2, D])
        xnT_sb = m.sb("xnT", [P, KD, L])
        xpad = [m.sb(f"xpad{i}", [P, 3 + L]) for i in range(2)]
        acc = [m.sb(f"acc{i}", [P, L]) for i in range(2)]
        u_sb = m.sb("u", [P, F, L])
        ut_sb = m.sb("ut", [P, 2, DI])
        zb = [m.sb(f"zb{i}", [P, BANK]) for i in range(2)]
        z_sb = m.sb("z", [P, 2, DI])
        zeros = m.sb("zeros", [P, 4, D])
        pT = m.ps("pT", (P, 2, BANK))
        px = [m.ps(f"px{i}") for i in range(2)]
        pz = [m.ps(f"pz{i}") for i in range(2)]
        pu = [m.ps(f"pu{i}") for i in range(2)]
        s_const, s_wload, s_set, s_x = m.sem("const"), m.sem("wload"), m.sem("set"), m.sem("x")
        s_ss, s_root, s_xn, s_T, s_xnT = m.sem("ss"), m.sem("root"), m.sem("xn"), m.sem("T"), m.sem("xnT")
        s_px, s_xpad, s_conv, s_u = m.sem("px"), m.sem("xpad"), m.sem("conv"), m.sem("u")
        s_pz, s_zb, s_z = m.sem("pz"), m.sem("zb"), m.sem("z")
        s_pu, s_ut = m.sem("pu"), m.sem("ut")
        s_out, s_lv, s_la, s_zero, s_clear = m.sem("out"), m.sem("lv"), m.sem("la"), m.sem("zero"), m.sem("clear")
        tick_sp = m.sem("tick_sp")
        block = phase.enter_context(nc.Block())

        @block.sync
        def _(sp):
            for dst, src in ((ident_sb[:, :], ident), (nw_sb[:, :], norm_w.rearrange("(k p) -> p k", p=P)),
                             (bx_sb[:, :], b_in[0:DI].rearrange("(k p) -> p k", p=P)),
                             (bz_sb[:, :], b_in[DI:2 * DI].partition_broadcast(P)),
                             (cw_sb[:, :, :], conv_w.rearrange("(k p) c -> p k c", p=P)),
                             (cb_sb[:, :], conv_b.rearrange("(k p) -> p k", p=P))):
                sp.dma_start(dst, src, allow_slow_non_contiguous=True).then_inc(s_const, 16)
            sp.dma_start(w_sb[:, :, :], w_in.rearrange("(k p) n -> p k n", p=P)).then_inc(s_wload, 16)
            with sp.Fori(0, NB) as b:
                sp.wait_ge(s_xn, b * 2)
                sp.dma_start(x_sb[:, :, :], x[bass.ds(b * L, L), :].rearrange("(c p) n -> p c n", p=P)).then_inc(s_x, 16)
                sp.wait_ge(s_u, b * F + F)
                alone(sp, tick_sp)
                sp.dma_start(u_feat[:, :, bass.ds(b * L, L)].rearrange("k p t -> p k t"), u_sb[:, :, :]).then_inc(s_out, 16)
                sp.wait_ge(s_z, b * 6 + 6)
                sp.dma_start(z_tok[bass.ds(b * L, L), :].rearrange("(c p) n -> p c n", p=P), z_sb[:, :, :]).then_inc(s_out, 16)
                sp.wait_ge(s_ut, b * 6 + 6)
                sp.dma_start(u_tok[bass.ds(b * L, L), :].rearrange("(c p) n -> p c n", p=P), ut_sb[:, :, :]).then_inc(s_out, 16)
            sp.wait_ge(s_out, NB * 48)

        @block.gpsimd
        def _(pool):
            pool.memset(zeros[:, :, :], 0.0).then_inc(s_zero, 1)
            pool.wait_ge(s_zero, 1)
            stores = 0
            for rows in to_clear:
                n = rows.shape[0] // (4 * P)
                with pool.Fori(0, n) as r:
                    pool.dma_start(rows[bass.ds(r * 4 * P, 4 * P), :].rearrange("(p c) n -> p c n", p=P), zeros[:, :, :]).then_inc(s_clear, 16)
                stores += n
            if stores:
                pool.wait_ge(s_clear, stores * 16)

        @block.scalar
        def _(act):
            act.wait_ge(s_const, 96)
            act.wait_ge(s_set, 3)
            with act.Fori(0, NB) as b:
                link = linker(act, s_la, b * LINKS_A)
                act.wait_ge(s_x, b * 16 + 16)
                for c in range(2):
                    link(nc.scalar.activation(sq_sb[:, :], x_sb[:, c, :], ACT.Square, accum_out=ss_sb[:, c:c + 1]))
                nc.scalar.activation(rt_sb[:, :], ss_sb[:, :], ACT.Sqrt, bias=eps_sb[:, :], scale=1.0 / D).then_inc(s_root, 1)
                assert link.count[0] == LINKS_A
                act.wait_ge(s_T, b + 1)
                for k in range(KD):
                    nc.scalar.activation(xnT_sb[:, k, :], pT[:, k // 2, (k % 2) * L:(k % 2 + 1) * L], ACT.Copy,
                                         scale=nw_sb[:, k:k + 1]).then_inc(s_xnT, 1)
                act.wait_ge(s_out, b * 48)
                for f in range(F + 1):
                    if f < F:
                        act.wait_ge(s_px, b * F + f + 1)
                        if f >= 2:
                            act.wait_ge(s_conv, b * F + f - 1)
                        nc.scalar.activation(xpad[f % 2][:, 3:3 + L], px[f % 2][:, 0:L], ACT.Identity,
                                             bias=bx_sb[:, f:f + 1]).then_inc(s_xpad, 1)
                    if f >= 1:
                        g = f - 1
                        act.wait_ge(s_conv, b * F + g + 1)
                        nc.scalar.activation(u_sb[:, g, :], acc[g % 2][:, :], ACT.Silu, bias=cb_sb[:, g:g + 1]).then_inc(s_u, 1)
                for n in range(6):
                    act.wait_ge(s_zb, b * 6 + n + 1)
                    nc.scalar.activation(z_sb[:, n // 3, (n % 3) * BANK:(n % 3 + 1) * BANK], zb[n % 2][:, :], ACT.Silu).then_inc(s_z, 1)

        @block.vector
        def _(dve):
            for i in range(2):
                nc.vector.memset(xpad[i][:, 0:3], 0.0).then_inc(s_set, 1)
            nc.vector.memset(eps_sb[:, :], EPS).then_inc(s_set, 1)
            dve.wait_ge(s_set, 3)
            dve.wait_ge(s_const, 96)
            with dve.Fori(0, NB) as b:
                link = linker(dve, s_lv, b * LINKS_V)
                dve.wait_ge(s_root, b + 1)
                link(nc.vector.reciprocal(ss_sb[:, :], rt_sb[:, :]))
                dve.wait_ge(s_x, b * 16 + 16)
                dve.wait_ge(s_T, b)
                for c in range(2):
                    nc.vector.tensor_scalar(xn_sb[:, c, :], x_sb[:, c, :], ss_sb[:, c:c + 1], None, ALU.mult).then_inc(s_xn, 1)
                for f in range(F):
                    a, xp = acc[f % 2], xpad[f % 2]
                    dve.wait_ge(s_xpad, b * F + f + 1)
                    if f >= 2:
                        dve.wait_ge(s_u, b * F + f - 1)
                    else:
                        dve.wait_ge(s_u, b * F)
                    link(nc.vector.tensor_scalar(a[:, :], xp[:, 3:3 + L], cw_sb[:, f, 3:4], None, ALU.mult))
                    for j in (2, 1):
                        link(nc.vector.scalar_tensor_tensor(a[:, :], xp[:, j:j + L], cw_sb[:, f, j:j + 1], a[:, :], ALU.mult, ALU.add))
                    ins = nc.vector.scalar_tensor_tensor(a[:, :], xp[:, 0:L], cw_sb[:, f, 0:1], a[:, :], ALU.mult, ALU.add)
                    ins.then_inc(s_conv, 1)
                for n in range(6):
                    dve.wait_ge(s_pz, b * 6 + n + 1)
                    if n >= 2:
                        dve.wait_ge(s_z, b * 6 + n - 1)
                    nc.vector.tensor_tensor(zb[n % 2][:, :], pz[n % 2][:, :], bz_sb[:, (n % 3) * BANK:(n % 3 + 1) * BANK], ALU.add).then_inc(s_zb, 1)
                dve.wait_ge(s_out, b * 48)
                for n in range(6):
                    dve.wait_ge(s_pu, b * 6 + n + 1)
                    nc.vector.tensor_copy(ut_sb[:, n // 3, (n % 3) * BANK:(n % 3 + 1) * BANK], pu[n % 2][:, :]).then_inc(s_ut, 1)
                LV = link.count[0]
            assert LV == 1 + 3 * F, LV

        @block.tensor
        def _(pe):
            pe.wait_ge(s_const, 96)
            pe.wait_ge(s_wload, 16)
            with pe.Fori(0, NB) as b:
                pe.wait_ge(s_xn, b * 2 + 2)
                pe.wait_ge(s_xnT, b * KD)
                for k in range(KD):
                    for c in range(2):
                        at = (k % 2) * L + c * P
                        ins = nc.tensor.transpose(pT[:, k // 2, at:at + P], xn_sb[:, c, k * P:(k + 1) * P], ident_sb[:, :])
                ins.then_inc(s_T, 1)
                pe.wait_ge(s_xnT, b * KD + KD)
                for f in range(F):
                    pe.wait_ge(s_xpad, b * F + max(f - 1, 0))
                    for k in range(KD):
                        ins = nc.tensor.matmul(px[f % 2][:, 0:L], w_sb[:, k, f * P:(f + 1) * P], xnT_sb[:, k, :],
                                               start=(k == 0), stop=(k == KD - 1))
                    ins.then_inc(s_px, 1)
                for n in range(6):
                    pe.wait_ge(s_zb, b * 6 + max(n - 1, 0))
                    c, j = n // 3, n % 3
                    for k in range(KD):
                        ins = nc.tensor.matmul(pz[n % 2][:, :], xnT_sb[:, k, c * P:(c + 1) * P],
                                               w_sb[:, k, DI + j * BANK:DI + (j + 1) * BANK], start=(k == 0), stop=(k == KD - 1))
                    ins.then_inc(s_pz, 1)
                pe.wait_ge(s_u, b * F + F)
                for n in range(6):
                    pe.wait_ge(s_ut, b * 6 + max(n - 1, 0))
                    c, j = n // 3, n % 3
                    for q in range(4):
                        ins = nc.tensor.transpose(pu[n % 2][:, q * P:(q + 1) * P], u_sb[:, j * 4 + q, c * P:(c + 1) * P], ident_sb[:, :])
                    ins.then_inc(s_pu, 1)


def ssm0_scan(nc, u_feat, u_tok, y_tok, ident, w_bc, b_bc, w_dt, head_mean, head_pair, b_dt, a_log, l2_alpha, l2_beta, ema):
    H, S, F = 24, 64, 12
    PAIRS = H // 2
    LN2 = 0.6931471805599453
    with ExitStack() as phase:
        m = Space(nc, "a2", phase)
        uT = m.sb("uT", [P, F, T])
        w_sb = m.sb("w", [P, F, 2 * P])
        bias_sb = m.sb("bias", [P, 2])
        wdt_sb = m.sb("wdt", [P, F, 2 * H])
        pair_sb = m.sb("pair", [P, 2])
        idz = m.sb("idz", [P, 2 * P])
        BT, CT = m.sb("BT", [P, T]), m.sb("CT", [P, T])
        sq = [m.sb(f"sq{i}", [P, BANK]) for i in range(2)]
        ut_sb = m.sb("ut", [P, TILES, P])
        y_sb = m.sb("y", [P, TILES, P])
        hv = m.sb("hv", [P, 5, H])
        base_sb = m.sb("base", [P, H])
        rest_sb = m.sb("rest", [P, H])
        gain_sb = m.sb("gain", [P, H, TILES])
        t0, t1, t2 = (m.sb(f"t{i}", [P, H, TILES]) for i in range(3))
        base_w, rest_w = m.sb("basew", [P, H, TILES]), m.sb("restw", [P, H, TILES])
        nrm = m.sb("nrm", [P, 2, 2, TILES])
        inv = m.sb("inv", [P, 2, 2, TILES])
        al = m.sb("al", [P, 2, TILES])
        cB = m.sb("cB", [P, 2, TILES])
        q0 = m.sb("q0", [P, 2, TILES])
        M = [m.sb(f"M{i}", [P, 3 * P]) for i in range(2)]
        W = [m.sb(f"W{i}", [P, 3 * P]) for i in range(2)]
        one_sb = m.sb("one", [P, 1])
        pB = [m.ps(f"pB{i}") for i in range(2)]
        pn = m.ps("pn")
        pa = [m.ps(f"pa{i}") for i in range(2)]
        pG = [m.ps(f"pG{i}") for i in range(2)]
        py = [m.ps("py"), pn]
        s_const, s_u, s_w, s_ut = m.sem("const"), m.sem("u"), m.sem("w"), m.sem("ut")
        s_dt, s_hv, s_prep, s_lv, s_la = m.sem("dt"), m.sem("hv"), m.sem("prep"), m.sem("lv"), m.sem("la")
        s_pB, s_sq, s_pn, s_root, s_bt = m.sem("pB"), m.sem("sq"), m.sem("pn"), m.sem("root"), m.sem("bt")
        s_arg, s_tanh, s_al, s_pa, s_M, s_G, s_W, s_y, s_ye, s_out = (m.sem(n) for n in "arg tanh al pa M G W y ye out".split())
        s_va, s_av = m.sem("va"), m.sem("av")
        block = phase.enter_context(nc.Block())
        LV = 10
        NI = 16

        @block.sync
        def _(sp):
            sp.dma_start(uT[:, :, :], u_feat.rearrange("k p t -> p k t")).then_inc(s_u, 16)
            sp.dma_start(idz[:, 0:P], ident).then_inc(s_const, 16)
            sp.dma_start(pair_sb[:, :], head_pair).then_inc(s_const, 16)
            sp.dma_start(wdt_sb[:, :, 0:H], w_dt.rearrange("(k p) h -> p k h", p=P)).then_inc(s_const, 16)
            sp.dma_start(wdt_sb[:, :, H:2 * H], head_mean.rearrange("(k p) h -> p k h", p=P)).then_inc(s_const, 16)
            for n, v in enumerate((b_dt, a_log, l2_alpha, l2_beta, ema)):
                sp.dma_start(hv[:, n, :], v.partition_broadcast(P)).then_inc(s_const, 16)
            with sp.Fori(0, PAIRS) as p:
                sp.wait_ge(s_bt, p * 16)
                sp.dma_start(w_sb[:, :, :], w_bc[bass.ds(p, 1), :, :, :].rearrange("a p k n -> (a p) k n")).then_inc(s_w, 16)
                sp.dma_start(bias_sb[:, :], b_bc[bass.ds(p, 1), :, :].rearrange("a p n -> (a p) n")).then_inc(s_w, 16)
                sp.wait_ge(s_y, p * NI)
                sp.dma_start(ut_sb[:, :, :], u_tok[:, bass.ds(p * P, P)].rearrange("(c p) n -> p c n", p=P)).then_inc(s_ut, 16)
                sp.wait_ge(s_ye, p * NB + NB)
                sp.dma_start(y_tok[:, bass.ds(p * P, P)].rearrange("(c p) n -> p c n", p=P), y_sb[:, :, :]).then_inc(s_out, 16)
            sp.wait_ge(s_out, PAIRS * 16)

        @block.scalar
        def _(act):
            link = linker(act, s_la)
            dtv = t0[:, :, :]
            act.wait_ge(s_va, 1)
            link(nc.scalar.activation(t1[:, :, :], dtv, ACT.Abs))
            link(nc.scalar.activation(t1[:, :, :], t1[:, :, :], ACT.Exp, scale=-1.0))
            link(nc.scalar.activation(t1[:, :, :], t1[:, :, :], ACT.Ln, bias=one_sb[:, :], scale=1.0))
            nc.scalar.activation(t2[:, :, :], dtv, ACT.Relu).then_inc(s_av, 1)
            act.wait_ge(s_va, 2)
            nc.scalar.activation(t1[:, :, :], t1[:, :, :], ACT.Exp).then_inc(s_av, 1)
            act.wait_ge(s_hv, 1)
            link(nc.scalar.activation(hv[:, 2, :], hv[:, 2, :], ACT.Exp, scale=LN2))
            nc.scalar.activation(hv[:, 3, :], hv[:, 3, :], ACT.Exp, scale=LN2).then_inc(s_av, 1)
            with act.Fori(0, PAIRS) as p:
                act.wait_ge(s_w, p * 32 + 32)
                act.wait_ge(s_W, p * NI)
                act.wait_ge(s_G, p * NI)
                for n in range(8):
                    dst = (BT, CT)[n // 4]
                    act.wait_ge(s_pB, p * 8 + n + 1)
                    src, bias = pB[n % 2][:, :], bias_sb[:, n // 4:n // 4 + 1]
                    nc.scalar.activation(dst[:, (n % 4) * BANK:(n % 4 + 1) * BANK], src, ACT.Identity, bias=bias).then_inc(s_bt, 1)
                    act.wait_ge(s_pn, p * 8 + max(n - 1, 0))
                    nc.scalar.activation(sq[n % 2][:, :], src, ACT.Square, bias=bias).then_inc(s_bt, 1)
                act.wait_ge(s_pn, p * 8 + 8)
                nc.scalar.activation(nrm[:, :, :, :].rearrange("p a b c -> p (a b c)"), pn[:, 0:4 * TILES], ACT.Sqrt).then_inc(s_root, 1)
                act.wait_ge(s_arg, p + 1)
                nc.scalar.activation(q0[:, :, :], q0[:, :, :], ACT.Tanh).then_inc(s_tanh, 1)

        @block.vector
        def _(dve):
            link = linker(dve, s_lv)
            link(nc.vector.memset(idz[:, P:2 * P], 0.0))
            link(nc.vector.memset(one_sb[:, :], 1.0))
            dve.wait_ge(s_const, 16 * 9)
            dve.wait_ge(s_dt, 1)

            def wide(v):
                return v.unsqueeze(2).to_broadcast([P, H, TILES])
            link(nc.vector.tensor_tensor(t0[:, :, 0:8], pa[0][:, 0:8 * 2 * H].rearrange("p (c h) -> p h c", h=2 * H)[:, 0:H, :],
                                         hv[:, 0, :].unsqueeze(2).to_broadcast([P, H, 8]), ALU.add))
            ins = nc.vector.tensor_tensor(t0[:, :, 8:16], pa[1][:, 0:8 * 2 * H].rearrange("p (c h) -> p h c", h=2 * H)[:, 0:H, :],
                                          hv[:, 0, :].unsqueeze(2).to_broadcast([P, H, 8]), ALU.add)
            ins.then_inc(s_va, 1)
            for n, (lo, hi) in ((1, (-2.3, -0.01)), (2, (-3.32, -0.015)), (3, (-2.0, 2.0))):
                link(nc.vector.tensor_scalar(hv[:, n, :], hv[:, n, :], lo, hi, ALU.max, ALU.min))
            link(nc.vector.tensor_scalar(hv[:, 4, :], hv[:, 4, :], 1e-6, None, ALU.add))
            nc.vector.reciprocal(hv[:, 4, :], hv[:, 4, :]).then_inc(s_hv, 1)
            dve.wait_ge(s_av, 1)
            link(nc.vector.tensor_tensor(t1[:, :, :], t1[:, :, :], t2[:, :, :], ALU.add))
            nc.vector.tensor_tensor(t1[:, :, :], t1[:, :, :], wide(hv[:, 1, :]), ALU.mult).then_inc(s_va, 1)
            dve.wait_ge(s_av, 2)
            link(nc.vector.tensor_scalar(t1[:, :, :], t1[:, :, :], -1.0, 1.0, ALU.mult, ALU.add))
            for c in range(2):
                link(nc.vector.tensor_tensor(t2[:, :, 8 * c:8 * c + 8], t1[:, :, 8 * c:8 * c + 8],
                                             pa[c][:, 0:8 * 2 * H].rearrange("p (c h) -> p h c", h=2 * H)[:, H:2 * H, :], ALU.mult))
            nc.vector.tensor_tensor(t2[:, :, :], t2[:, :, :], t2[:, :, :], ALU.mult).then_inc(s_prep, 1)
            dve.wait_ge(s_prep, 1)
            dve.wait_ge(s_av, 3)
            dve.wait_ge(s_hv, 1)
            link(nc.vector.tensor_tensor(t2[:, :, :], t2[:, :, :], wide(hv[:, 4, :]), ALU.mult))
            link(nc.vector.tensor_scalar(hv[:, 3, :], hv[:, 3, :], 1.0 / S, None, ALU.mult))
            link(nc.vector.tensor_tensor(gain_sb[:, :, :], t2[:, :, :], wide(hv[:, 3, :]), ALU.mult))
            link(nc.vector.tensor_scalar(base_w[:, :, :], wide(hv[:, 2, :]), -1.0, 1.0, ALU.mult, ALU.add))
            link(nc.vector.tensor_scalar(rest_w[:, :, :], base_w[:, :, :], -1.0, 1.0, ALU.mult, ALU.add))
            done = link.count[0]
            with dve.Fori(0, PAIRS) as p:
                link = linker(dve, s_lv, p * LV + done)
                dve.wait_ge(s_root, p + 1)
                link(nc.vector.tensor_scalar(nrm[:, :, :, :], nrm[:, :, :, :], 1e-12, None, ALU.max))
                dve.wait_ge(s_ye, p * NB)
                link(nc.vector.reciprocal(inv[:, :, :, :], nrm[:, :, :, :]))
                rB = inv[:, 0, :, :]
                link(nc.vector.tensor_tensor(q0[:, :, :], pn[:, 0:2 * TILES].rearrange("p (h c) -> p h c", h=2), rB, ALU.mult))
                link(nc.vector.tensor_tensor(q0[:, :, :], q0[:, :, :], rB, ALU.mult))
                nc.vector.tensor_tensor(q0[:, :, :], q0[:, :, :], gain_sb[:, bass.ds(2 * p, 2), :], ALU.mult).then_inc(s_arg, 1)
                dve.wait_ge(s_tanh, p + 1)
                link(nc.vector.tensor_scalar(q0[:, :, :], q0[:, :, :], 0.0, None, ALU.max))
                link(nc.vector.tensor_tensor(q0[:, :, :], q0[:, :, :], rest_w[:, bass.ds(2 * p, 2), :], ALU.mult))
                link(nc.vector.tensor_tensor(q0[:, :, :], q0[:, :, :], base_w[:, bass.ds(2 * p, 2), :], ALU.add))
                dve.wait_ge(s_pa, p * NB)
                nc.vector.tensor_scalar(al[:, :, :], q0[:, :, :], 0.01, 0.999, ALU.max, ALU.min).then_inc(s_al, 1)
                dve.wait_ge(s_al, p + 1)
                link(nc.vector.tensor_scalar(cB[:, :, :], al[:, :, :], -1.0, 1.0, ALU.mult, ALU.add))
                link(nc.vector.tensor_tensor(cB[:, :, :], cB[:, :, :], rB, ALU.mult))
                link(nc.vector.tensor_scalar(cB[:, :, :], cB[:, :, :], 1.0, None, ALU.mult))
                assert link.count[0] == LV, link.count[0]
                for i in range(NI + 1):
                    if i < NI:
                        b, h = i // 2, i % 2
                        dve.wait_ge(s_pa, p * NB + b + 1)
                        nc.vector.tensor_tensor_scan(M[i % 2][:, 0:2 * P], pa[b % 2][:, h * L:(h + 1) * L], idz[:, :], 0.0, ALU.mult, ALU.add).then_inc(s_M, 1)
                        nc.vector.tensor_tensor_scan(M[i % 2][:, 2 * P:3 * P], pa[b % 2][:, h * L + P:(h + 1) * L], idz[:, 0:P], 0.0, ALU.mult, ALU.add).then_inc(s_M, 1)
                        dve.wait_ge(s_M, (p * NI + i) * 2 + 2)
                        dve.wait_ge(s_G, p * NI + i + 1)
                        if i >= 2:
                            dve.wait_ge(s_y, p * NI + i - 1)
                        for a, (lo, hi) in enumerate(((0, 2 * P), (2 * P, 3 * P))):
                            ins = nc.vector.scalar_tensor_tensor(W[i % 2][:, lo:hi], pG[i % 2][:, lo:hi], cB[:, h, 2 * b + a:2 * b + a + 1],
                                                                 M[i % 2][:, lo:hi], ALU.mult, ALU.mult)
                        ins.then_inc(s_W, 1)
                    if i >= 2 and i % 2 == 0:
                        b = i // 2 - 1
                        if b == 0:
                            dve.wait_ge(s_out, p * 16)
                        dve.wait_ge(s_y, p * NI + i)
                        pyb = py[b % 2][:, 0:L].rearrange("p (h c n) -> p h c n", h=2, c=2)
                        for h in range(2):
                            ins = nc.vector.tensor_tensor(y_sb[:, 2 * b:2 * b + 2, h * S:(h + 1) * S], pyb[:, h, :, :],
                                                          inv[:, 1, h, 2 * b:2 * b + 2].unsqueeze(2).to_broadcast([P, 2, S]), ALU.mult)
                        ins.then_inc(s_ye, 1)

        @block.tensor
        def _(pe):
            pe.wait_ge(s_const, 16 * 9)
            pe.wait_ge(s_u, 16)
            for c in range(TILES):
                for k in range(F):
                    ins = nc.tensor.matmul(pa[c // 8][:, (c % 8) * 2 * H:(c % 8 + 1) * 2 * H], uT[:, k, c * P:(c + 1) * P], wdt_sb[:, k, :],
                                           start=(k == 0), stop=(k == F - 1))
            ins.then_inc(s_dt, 1)
            pe.wait_ge(s_prep, 1)
            with pe.Fori(0, PAIRS) as p:
                pe.wait_ge(s_w, p * 32 + 32)

                def norms(n):
                    pe.wait_ge(s_bt, p * 16 + 2 * n + 2)
                    if n == 0:
                        pe.wait_ge(s_ye, p * NB)
                    for q in range(4):
                        c = (n % 4) * 4 + q
                        ins = nc.tensor.matmul(pn[:, (n // 4) * 2 * TILES:(n // 4 + 1) * 2 * TILES].rearrange("p (h c) -> p h c", h=2)[:, :, c],
                                               sq[n % 2][:, q * P:(q + 1) * P], pair_sb[:, :], start=True, stop=True)
                    ins.then_inc(s_pn, 1)
                for n in range(8):
                    pe.wait_ge(s_bt, p * 16 + 2 * max(n - 1, 0))
                    for k in range(F):
                        ins = nc.tensor.matmul(pB[n % 2][:, :], w_sb[:, k, (n // 4) * P:(n // 4 + 1) * P],
                                               uT[:, k, (n % 4) * BANK:(n % 4 + 1) * BANK], start=(k == 0), stop=(k == F - 1))
                    ins.then_inc(s_pB, 1)
                    if n >= 1:
                        norms(n - 1)
                norms(7)
                pe.wait_ge(s_al, p + 1)
                pe.wait_ge(s_ut, p * 16 + 16)

                def decays(b):
                    if b >= 2:
                        pe.wait_ge(s_M, (p * NI + 2 * (b - 1)) * 2)
                    for h in range(2):
                        for c in range(2):
                            ins = nc.tensor.matmul(pa[b % 2][:, h * L + c * P:h * L + (c + 1) * P],
                                                   al[:, h, 2 * b + c:2 * b + c + 1].to_broadcast([P, P]), idz[:, 0:P], start=True, stop=True)
                    ins.then_inc(s_pa, 1)
                pe.wait_ge(s_M, p * NI * 2)
                decays(0)
                decays(1)
                for i in range(NI + 1):
                    if i < NI:
                        b, h = i // 2, i % 2
                        at, r = b * L, slice(h * S, (h + 1) * S)
                        pe.wait_ge(s_W, p * NI + max(i - 1, 0))
                        nc.tensor.matmul(pG[i % 2][:, 0:L], BT[r, at:at + P], CT[r, at:at + L], start=True, stop=True)
                        nc.tensor.matmul(pG[i % 2][:, L:L + P], BT[r, at + P:at + L], CT[r, at + P:at + L], start=True, stop=True).then_inc(s_G, 1)
                    if i >= 1:
                        j = i - 1
                        b, h = j // 2, j % 2
                        pe.wait_ge(s_W, p * NI + j + 1)
                        if h == 0:
                            pe.wait_ge(s_ye, p * NB + max(b - 1, 0))
                        o, pyb = h * 2 * S, py[b % 2]
                        u0, u1 = ut_sb[:, 2 * b, h * S:(h + 1) * S], ut_sb[:, 2 * b + 1, h * S:(h + 1) * S]
                        nc.tensor.matmul(pyb[:, o:o + S], W[j % 2][:, 0:P], u0, start=True, stop=True)
                        nc.tensor.matmul(pyb[:, o + S:o + 2 * S], W[j % 2][:, P:2 * P], u0, start=True, stop=False)
                        nc.tensor.matmul(pyb[:, o + S:o + 2 * S], W[j % 2][:, 2 * P:3 * P], u1, start=False, stop=True).then_inc(s_y, 1)
                        if h == 1 and b + 2 < NB:
                            decays(b + 2)


LN_EPS = 1e-5


def ssm0_out(nc, x, y_tok, z_tok, w_out, b_out, gate, ident, x1, x1_feat):
    DI = 1536
    F = DI // P
    with ExitStack() as phase:
        m = Space(nc, "a3", phase)
        w_sb = m.sb("w", [P, F, D])
        ident_sb = m.sb("ident", [P, P])
        b_sb, g_sb, eps_sb = m.sb("b", [P, D]), m.sb("g", [P, 1]), m.sb("eps", [P, 1])
        x_sb = [m.sb(f"x{i}", [P, 2, D]) for i in range(2)]
        y_sb = [m.sb(f"y{i}", [P, 2, DI]) for i in range(2)]
        z_sb = [m.sb(f"z{i}", [P, 2, DI]) for i in range(2)]
        yT = m.sb("yT", [P, 2, F, P])
        v_sb = m.sb("v", [P, 2, D])
        st, mv, sd = m.sb("st", [P, 2, 6]), m.sb("mv", [P, 2, 2]), m.sb("sd", [P, 2])
        o_sb = m.sb("o", [P, 2, D])
        oT = m.sb("oT", [P, 2, KD, P])
        pT = [m.ps(f"pT{i}") for i in range(2)]
        po = [m.ps(f"po{i}") for i in range(2)]
        px = [m.ps(f"px{i}") for i in range(2)]
        s_const, s_set, s_out, s_lv = (m.sem(n) for n in "const set out lv".split())
        s_in = [m.sem(f"in{i}") for i in range(2)]
        s_yz, s_T, s_yT, s_o, s_var, s_sd, s_ln, s_xT, s_oT = (m.sem(n) for n in "yz T yT o var sd ln xT oT".split())
        tick_dve = m.sem("tick_dve")
        block = phase.enter_context(nc.Block())
        LV = 9

        def rows(a, b, n):
            return a[bass.ds(b * L, n), :].rearrange("(c p) n -> p c n", p=P)

        @block.sync
        def _(sp):
            for dst, src in ((ident_sb[:, :], ident), (b_sb[:, :], b_out.partition_broadcast(P)), (g_sb[:, :], gate.partition_broadcast(P)),
                             (w_sb[:, :, :], w_out.rearrange("(k p) n -> p k n", p=P))):
                sp.dma_start(dst, src).then_inc(s_const, 16)
            with sp.Fori(0, NB // 2) as r:
                for i in range(2):
                    b = 2 * r + i
                    sp.wait_ge(s_ln, r * 4)
                    for dst, src in ((x_sb, x), (y_sb, y_tok), (z_sb, z_tok)):
                        sp.dma_start(dst[i][:, :, :], rows(src, b, L)).then_inc(s_in[i], 16)
                for i in range(2):
                    b = 2 * r + i
                    sp.wait_ge(s_oT, b * 2 + 2)
                    sp.dma_start(rows(x1, b, L), o_sb[:, :, :]).then_inc(s_out, 16)
                    sp.dma_start(x1_feat[:, :, bass.ds(b * L, L)].rearrange("k p (c t) -> p c k t", c=2)[:, 0, :, :], oT[:, 0, :, :]).then_inc(s_out, 16)
                    sp.dma_start(x1_feat[:, :, bass.ds(b * L, L)].rearrange("k p (c t) -> p c k t", c=2)[:, 1, :, :], oT[:, 1, :, :]).then_inc(s_out, 16)
            sp.wait_ge(s_out, NB * 48)

        @block.scalar
        def _(act):
            act.wait_ge(s_set, 1)
            with act.Fori(0, NB) as b:
                for n in range(6):
                    act.wait_ge(s_T, b * 6 + n + 1)
                    if n == 0:
                        act.wait_ge(s_o, b * 2)
                    nc.scalar.copy(yT[:, n // 3, (n % 3) * 4:(n % 3) * 4 + 4, :].rearrange("p k t -> p (k t)"), pT[n % 2][:, :]).then_inc(s_yT, 1)
                act.wait_ge(s_var, b * 2 + 2)
                nc.scalar.activation(sd[:, :], mv[:, :, 1], ACT.Sqrt, bias=eps_sb[:, :], scale=1.0).then_inc(s_sd, 1)
                act.wait_ge(s_out, b * 48)
                for c in range(2):
                    act.wait_ge(s_xT, b * 2 + c + 1)
                    nc.scalar.copy(oT[:, c, :, :].rearrange("p k t -> p (k t)"), px[c][:, :]).then_inc(s_oT, 1)

        @block.vector
        def _(dve):
            nc.vector.memset(eps_sb[:, :], LN_EPS).then_inc(s_set, 1)
            dve.wait_ge(s_const, 64)
            with dve.Fori(0, NB // 2) as r:
                for i in range(2):
                    b = 2 * r + i
                    link = linker(dve, s_lv, b * LV)
                    dve.wait_ge(s_in[i], r * 48 + 48)
                    for c in range(2):
                        nc.vector.tensor_tensor(y_sb[i][:, c, :], y_sb[i][:, c, :], z_sb[i][:, c, :], ALU.mult).then_inc(s_yz, 1)
                    for c in range(2):
                        dve.wait_ge(s_o, b * 2 + c + 1)
                        v = v_sb[:, c, :]
                        link(nc.vector.tensor_tensor(v, po[c][:, :], b_sb[:, :], ALU.add))
                        link(nc.vector.scalar_tensor_tensor(v, v, g_sb[:, 0:1], x_sb[i][:, c, :], ALU.mult, ALU.add))
                        link(nc.vector.tensor_tensor(v, v, x_sb[i][:, c, :], ALU.add))
                        link(nc.vector.bn_stats(st[:, c, :], v))
                        alone(dve, tick_dve)
                        nc.vector.bn_aggr(mv[:, c, :], st[:, c, :]).then_inc(s_var, 1)
                    dve.wait_ge(s_sd, b + 1)
                    link(nc.vector.reciprocal(sd[:, :], sd[:, :]))
                    dve.wait_ge(s_out, b * 48)
                    for c in range(2):
                        nc.vector.tensor_scalar(o_sb[:, c, :], v_sb[:, c, :], mv[:, c, 0:1], sd[:, c:c + 1], ALU.subtract, ALU.mult).then_inc(s_ln, 1)
                    assert link.count[0] == LV

        @block.tensor
        def _(pe):
            pe.wait_ge(s_const, 64)
            with pe.Fori(0, NB // 2) as r:
                for i in range(2):
                    b = 2 * r + i
                    for n in range(6):
                        c, j = n // 3, n % 3
                        pe.wait_ge(s_yz, b * 2 + c + 1)
                        pe.wait_ge(s_yT, b * 6 + max(n - 1, 0))
                        for q in range(4):
                            ins = nc.tensor.transpose(pT[n % 2][:, q * P:(q + 1) * P], y_sb[i][:, c, (j * 4 + q) * P:(j * 4 + q + 1) * P], ident_sb[:, :])
                        ins.then_inc(s_T, 1)
                    for c in range(2):
                        pe.wait_ge(s_yT, b * 6 + 3 * c + 3)
                        pe.wait_ge(s_var, b * 2)
                        for k in range(F):
                            ins = nc.tensor.matmul(po[c][:, :], yT[:, c, k, :], w_sb[:, k, :], start=(k == 0), stop=(k == F - 1))
                        ins.then_inc(s_o, 1)
                    for c in range(2):
                        pe.wait_ge(s_ln, b * 2 + c + 1)
                        pe.wait_ge(s_oT, b * 2)
                        for k in range(KD):
                            ins = nc.tensor.transpose(px[c][:, k * P:(k + 1) * P], o_sb[:, c, k * P:(k + 1) * P], ident_sb[:, :])
                        ins.then_inc(s_xT, 1)


def long_conv(nc, x_feat, ctx_turned, taps, skip, exchange, r_feat):
    HEADS, R = 32, 8
    PAIRS = R * (R + 1) // 2
    OFF = [R * i - i * (i - 1) // 2 for i in range(R)]
    N = NB * PAIRS
    with ExitStack() as phase:
        m = Space(nc, "b1", phase)
        x_sb, c_sb = m.sb("x", [P, KD, T]), m.sb("c", [P, KD, T])
        x4 = x_sb[:, :, :].rearrange("p k (b t) -> p k b t", b=NB)
        c4 = c_sb[:, :, :].rearrange("p k (b t) -> p k b t", b=NB)
        exchange_sb, skip_sb = m.sb("exchange", [P, P]), m.sb("skip", [P, HEADS])
        toe = [m.sb(f"toe{i}", [P, D]) for i in range(2)]
        dg = [m.sb(f"dg{i}", [P, P]) for i in range(2)]
        kv = [m.sb(f"kv{i}", [P, KD, NB, PAIRS]) for i in range(2)]
        prod = [m.sb(f"prod{i}", [P, KD, NB, R, R]) for i in range(2)]
        red = [m.sb(f"red{i}", [P, KD, NB, R]) for i in range(2)]
        py = [m.ps(f"py{i}", (P, KD, BANK)) for i in range(2)]
        s_const, s_x, s_c, s_out, s_lv = (m.sem(n) for n in "const x c out lv".split())
        s_toe = [m.sem(f"toe{i}") for i in range(2)]
        s_kv, s_dg, s_y, s_prod, s_red, s_sum = (m.sem(n) for n in "kv dg y prod red sum".split())
        block = phase.enter_context(nc.Block())

        @block.sync
        def _(sp):
            sp.dma_start(exchange_sb[:, :], exchange).then_inc(s_const, 16)
            sp.dma_start(skip_sb[:, :], skip.partition_broadcast(P)).then_inc(s_const, 16)
            sp.dma_start(c_sb[:, :, :], ctx_turned.rearrange("k p t -> p k t")).then_inc(s_c, 16)
            sp.dma_start(x_sb[:, :, :], x_feat.rearrange("k p t -> p k t")).then_inc(s_x, 16)
            with sp.Fori(0, HEADS // 2) as g:
                for i in range(2):
                    row = taps[bass.ds(2 * g + i, 1), 0:D]
                    sp.wait_ge(s_y, 2 * g)
                    sp.dma_start(toe[i][:, :], bass.AP(row.tensor, row.offset, [[1, P], [1, D]])).then_inc(s_toe[i], 16)
            sp.wait_ge(s_sum, HEADS)
            sp.dma_start(r_feat.rearrange("k p t -> p k t"), x_sb[:, :, :]).then_inc(s_out, 16)
            sp.wait_ge(s_out, 16)

        @block.gpsimd
        def _(pool):
            pool.wait_ge(s_c, 16)

            def add_back(g, i):
                h = 2 * g + i
                pool.wait_ge(s_red, h + 1)
                at = x4[:, :, :, bass.ds(h * R, R)]
                pool.tensor_tensor(at, at, red[i][:, :, :, :], ALU.add).then_inc(s_sum, 1)
            with pool.Fori(0, HEADS // 2) as g:
                for i in range(2):
                    h = 2 * g + i
                    pool.wait_ge(s_y, 2 * g)
                    for r in range(R):
                        ins = pool.tensor_tensor(kv[i][:, :, :, OFF[r]:OFF[r] + R - r], c4[:, :, :, bass.ds(h * R + r, R - r)],
                                                 c4[:, :, :, bass.ds(h * R + r, 1)].to_broadcast([P, KD, NB, R - r]), ALU.mult)
                        ins.then_inc(s_kv, 1)
                for i in range(2):
                    add_back(g, i)

        @block.vector
        def _(dve):
            dve.wait_ge(s_const, 32)
            dve.wait_ge(s_x, 16)
            with dve.Fori(0, HEADS // 2) as g:
                for i in range(2):
                    h = 2 * g + i
                    link = linker(dve, s_lv, h * 1)
                    dve.wait_ge(s_toe[i], g * 16 + 16)
                    link(nc.vector.tensor_scalar(dg[i][:, :], exchange_sb[:, :], skip_sb[:, bass.ds(h, 1)], None, ALU.mult))
                    nc.vector.tensor_tensor(toe[i][:, 0:P], toe[i][:, 0:P], dg[i][:, :], ALU.add).then_inc(s_dg, 1)
                for i in range(2):
                    h = 2 * g + i
                    dve.wait_ge(s_y, h + 1)
                    dve.wait_ge(s_red, 2 * g)
                    for r in range(R):
                        n = R - r
                        src = py[i][:, :, 0:N].rearrange("p k (b n) -> p k b n", b=NB)
                        ins = nc.vector.tensor_tensor(prod[i][:, :, :, r:R, r], src[:, :, :, OFF[r]:OFF[r] + n],
                                                      x4[:, :, :, bass.ds(h * R + r, 1)].to_broadcast([P, KD, NB, n]), ALU.mult)
                        ins.then_inc(s_prod, 1)
                        if n > 1:
                            ins = nc.vector.tensor_tensor(prod[i][:, :, :, r, r + 1:R], src[:, :, :, OFF[r] + 1:OFF[r] + n],
                                                          x4[:, :, :, bass.ds(h * R + r + 1, n - 1)], ALU.mult)
                            ins.then_inc(s_prod, 1)
                    dve.wait_ge(s_prod, h * (2 * R - 1) + 2 * R - 1)
                    dve.wait_ge(s_sum, 2 * g)
                    nc.vector.tensor_reduce(red[i][:, :, :, :].rearrange("p k b r -> p (k b r)"),
                                            prod[i][:, :, :, :, :].rearrange("p k b o r -> p (k b o) r"), AX.X, ALU.add).then_inc(s_red, 1)

        @block.tensor
        def _(pe):
            with pe.Fori(0, HEADS // 2) as g:
                for i in range(2):
                    h = 2 * g + i
                    pe.wait_ge(s_dg, h + 1)
                    pe.wait_ge(s_kv, h * R + R)
                    pe.wait_ge(s_prod, 2 * g * (2 * R - 1))
                    for o in range(KD):
                        for k in range(o + 1):
                            ins = nc.tensor.matmul(py[i][:, o, 0:N], toe[i][:, (o - k) * P:(o - k + 1) * P],
                                                   kv[i][:, k, :, :].rearrange("p b n -> p (b n)"), start=(k == 0), stop=(k == o))
                    ins.then_inc(s_y, 1)


def norm_from_feat(nc, name, v_feat, ident, o_tok, o_feat):
    LN_EPS = 1e-5
    with ExitStack() as phase:
        m = Space(nc, name, phase)
        ident_sb, eps_sb = m.sb("ident", [P, P]), m.sb("eps", [P, 1])
        v_sb = [m.sb(f"v{i}", [P, KD, P]) for i in range(2)]
        st = [m.sb(f"st{i}", [P, 6]) for i in range(2)]
        mv = [m.sb(f"mv{i}", [P, 2]) for i in range(2)]
        sd = [m.sb(f"sd{i}", [P, 1]) for i in range(2)]
        o_sb = [m.sb(f"o{i}", [P, D]) for i in range(2)]
        oT = [m.sb(f"oT{i}", [P, KD, P]) for i in range(2)]
        pv = [m.ps(f"pv{i}") for i in range(2)]
        po = [m.ps(f"po{i}") for i in range(2)]
        s_const, s_set, s_lv = m.sem("const"), m.sem("set"), m.sem("lv")
        s_in = [m.sem(f"in{i}") for i in range(2)]
        s_out = [m.sem(f"out{i}") for i in range(2)]
        s_T, s_var, s_sd, s_ln, s_oT, s_oc = (m.sem(n) for n in "T var sd ln oT oc".split())
        tick_dve = m.sem("tick_dve")
        block = phase.enter_context(nc.Block())
        LV = 2

        @block.sync
        def _(sp):
            sp.dma_start(ident_sb[:, :], ident).then_inc(s_const, 16)
            with sp.Fori(0, TILES // 2) as r:
                for i in range(2):
                    t = 2 * r + i
                    sp.wait_ge(s_T, 2 * r)
                    sp.dma_start(v_sb[i][:, :, :], v_feat[:, :, bass.ds(t * P, P)].rearrange("k p t -> p k t")).then_inc(s_in[i], 16)
                for i in range(2):
                    t = 2 * r + i
                    sp.wait_ge(s_oc, t + 1)
                    sp.dma_start(o_tok[bass.ds(t * P, P), :], o_sb[i][:, :]).then_inc(s_out[i], 16)
                    sp.dma_start(o_feat[:, :, bass.ds(t * P, P)].rearrange("k p t -> p k t"), oT[i][:, :, :]).then_inc(s_out[i], 16)
            for i in range(2):
                sp.wait_ge(s_out[i], TILES // 2 * 32)

        @block.scalar
        def _(act):
            act.wait_ge(s_set, 1)
            with act.Fori(0, TILES // 2) as r:
                for i in range(2):
                    act.wait_ge(s_var, 2 * r + i + 1)
                    nc.scalar.activation(sd[i][:, :], mv[i][:, 1:2], ACT.Sqrt, bias=eps_sb[:, :], scale=1.0).then_inc(s_sd, 1)
                for i in range(2):
                    act.wait_ge(s_oT, 2 * r + i + 1)
                    act.wait_ge(s_out[i], r * 32)
                    nc.scalar.copy(oT[i][:, :, :].rearrange("p k t -> p (k t)"), po[i][:, :]).then_inc(s_oc, 1)

        @block.vector
        def _(dve):
            nc.vector.memset(eps_sb[:, :], LN_EPS).then_inc(s_set, 1)
            with dve.Fori(0, TILES // 2) as r:
                for i in range(2):
                    link = linker(dve, s_lv, (2 * r + i) * LV)
                    dve.wait_ge(s_T, 2 * r + i + 1)
                    link(nc.vector.bn_stats(st[i][:, :], pv[i][:, :]))
                    alone(dve, tick_dve)
                    nc.vector.bn_aggr(mv[i][:, :], st[i][:, :]).then_inc(s_var, 1)
                    dve.wait_ge(s_sd, 2 * r + i + 1)
                    link(nc.vector.reciprocal(sd[i][:, :], sd[i][:, :]))
                    dve.wait_ge(s_out[i], r * 32)
                    nc.vector.tensor_scalar(o_sb[i][:, :], pv[i][:, :], mv[i][:, 0:1], sd[i][:, :], ALU.subtract, ALU.mult).then_inc(s_ln, 1)

        @block.tensor
        def _(pe):
            pe.wait_ge(s_const, 16)
            with pe.Fori(0, TILES // 2) as r:
                for i in range(2):
                    pe.wait_ge(s_in[i], r * 16 + 16)
                    pe.wait_ge(s_ln, 2 * r)
                    for k in range(KD):
                        ins = nc.tensor.transpose(pv[i][:, k * P:(k + 1) * P], v_sb[i][:, k, :], ident_sb[:, :])
                    ins.then_inc(s_T, 1)
                for i in range(2):
                    pe.wait_ge(s_ln, 2 * r + i + 1)
                    pe.wait_ge(s_oc, 2 * r)
                    for k in range(KD):
                        ins = nc.tensor.transpose(po[i][:, k * P:(k + 1) * P], o_sb[i][:, k * P:(k + 1) * P], ident_sb[:, :])
                    ins.then_inc(s_oT, 1)


E_, K_, CAP, FF = 64, 8, 128, 192
SLOTS = E_ * CAP
FAR = 1 << 20


def moe0_route(nc, x_tok, x_feat, router, ident, before, ramp, x_slots, places, weights):
    with ExitStack() as phase:
        m = Space(nc, "c1", phase)
        rw = m.sb("rw", [P, KD, E_])
        before_sb = m.sb("before", [P, P])
        ones = m.sb("ones", [P, P])
        ramp_sb = m.sb("ramp", [P, E_])
        xf = [m.sb(f"xf{i}", [P, KD, P]) for i in range(2)]
        xt = [m.sb(f"xt{i}", [P, D]) for i in range(2)]
        mx, se, wn = m.sb("mx", [P, 1]), m.sb("se", [P, 1]), m.sb("wn", [P, 1])
        ex = m.sb("ex", [P, E_])
        top = m.sb("top", [P, K_])
        idx = m.sb("idx", [P, K_], U32)
        idf = m.sb("idf", [P, K_])
        hot = m.sb("hot", [P, K_, E_])
        tmp = m.sb("tmp", [P, K_, E_])
        A = m.sb("A", [P, E_])
        S = m.sb("S", [P, E_])
        pk, ok, pf = m.sb("pk", [P, K_]), m.sb("ok", [P, K_]), m.sb("pf", [P, K_])
        wk = [m.sb(f"wk{i}", [P, K_]) for i in range(2)]
        pl = [m.sb(f"pl{i}", [P, K_], U32) for i in range(2)]
        pL, pP = m.ps("pL"), m.ps("pP")
        s_const, s_set, s_lv = m.sem("const"), m.sem("set"), m.sem("lv")
        s_in = [m.sem(f"in{i}") for i in range(2)]
        s_log, s_neg, s_exp, s_A, s_pos, s_pl, s_used = (m.sem(n) for n in "log neg exp A pos pl used".split())
        s_out = [m.sem(f"out{i}") for i in range(2)]
        s_sc = [m.sem(f"sc{i}") for i in range(2)]
        tick_dve, tick_pool = m.sem("tick_dve"), m.sem("tick_pool")
        block = phase.enter_context(nc.Block())
        LV = 17

        @block.sync
        def _(sp):
            for dst, src in ((rw[:, :, :], router.rearrange("(k p) e -> p k e", p=P)), (before_sb[:, :], before), (ramp_sb[:, :], ramp.partition_broadcast(P))):
                sp.dma_start(dst, src).then_inc(s_const, 16)
            with sp.Fori(0, TILES // 2) as r:
                for i in range(2):
                    t = 2 * r + i
                    sp.wait_ge(s_log, 2 * r)
                    sp.wait_ge(s_sc[i], r * K_ * 16)
                    sp.dma_start(xf[i][:, :, :], x_feat[:, :, bass.ds(t * P, P)].rearrange("k p t -> p k t")).then_inc(s_in[i], 16)
                    sp.dma_start(xt[i][:, :], x_tok[bass.ds(t * P, P), :]).then_inc(s_in[i], 16)
                for i in range(2):
                    t = 2 * r + i
                    sp.wait_ge(s_pl, t + 1)
                    sp.dma_start(places[bass.ds(t * P, P), :], pl[i][:, :]).then_inc(s_out[i], 16)
                    sp.dma_start(weights[bass.ds(t * P, P), :], wk[i][:, :]).then_inc(s_out[i], 16)
            for i in range(2):
                sp.wait_ge(s_out[i], TILES // 2 * 32)

        @block.gpsimd
        def _(pool):
            with pool.Fori(0, TILES // 2) as r:
                for i in range(2):
                    t = 2 * r + i
                    pool.wait_ge(s_in[i], r * 32 + 32)
                    pool.wait_ge(s_pl, t + 1)
                    alone(pool, tick_pool)
                    for k in range(K_):
                        pool.indirect_dma_start(x_slots, bass.IndirectOffsetOnAxis(ap=pl[i][:, k:k + 1], axis=0), xt[i][:, :], None,
                                                bounds_check=SLOTS - 1, oob_is_err=False).then_inc(s_sc[i], 16)
            for i in range(2):
                pool.wait_ge(s_sc[i], TILES // 2 * K_ * 16)

        @block.scalar
        def _(act):
            with act.Fori(0, TILES) as t:
                act.wait_ge(s_neg, t + 1)
                nc.scalar.activation(ex[:, :], pL[:, 0:E_], ACT.Exp, bias=mx[:, :], scale=1.0, accum_out=se[:, :]).then_inc(s_exp, 1)

        @block.vector
        def _(dve):
            nc.vector.memset(ones[:, :], 1.0).then_inc(s_set, 1)
            nc.vector.memset(S[:, :], 0.0).then_inc(s_set, 1)
            dve.wait_ge(s_set, 2)
            dve.wait_ge(s_const, 48)
            with dve.Fori(0, TILES // 2) as r:
                for i in range(2):
                    t = 2 * r + i
                    link = linker(dve, s_lv, t * LV)
                    dve.wait_ge(s_log, t + 1)
                    link(nc.vector.tensor_reduce(mx[:, :], pL[:, 0:E_], AX.X, ALU.max))
                    nc.vector.tensor_scalar(mx[:, :], mx[:, :], -1.0, None, ALU.mult).then_inc(s_neg, 1)
                    dve.wait_ge(s_exp, t + 1)
                    link(nc.vector.reciprocal(se[:, :], se[:, :]))
                    link(nc.vector.tensor_scalar(ex[:, :], ex[:, :], se[:, :], None, ALU.mult))
                    alone(dve, tick_dve)
                    link(nc.vector.max(top[:, :], ex[:, :]))
                    alone(dve, tick_dve)
                    link(nc.vector.max_index(idx[:, :], top[:, :], ex[:, :]))
                    link(nc.vector.tensor_copy(idf[:, :], idx[:, :]))
                    link(nc.vector.tensor_tensor(hot[:, :, :], ramp_sb[:, :].unsqueeze(1).to_broadcast([P, K_, E_]),
                                                 idf[:, :].unsqueeze(2).to_broadcast([P, K_, E_]), ALU.is_equal))
                    dve.wait_ge(s_pos, t)
                    nc.vector.tensor_reduce(A[:, :], hot[:, :, :].rearrange("p k e -> p e k"), AX.X, ALU.add).then_inc(s_A, 1)
                    link(nc.vector.tensor_reduce(wn[:, :], top[:, :], AX.X, ALU.add))
                    link(nc.vector.tensor_scalar(wn[:, :], wn[:, :], 1e-20, None, ALU.add))
                    link(nc.vector.reciprocal(wn[:, :], wn[:, :]))
                    dve.wait_ge(s_pos, t + 1)
                    link(nc.vector.tensor_tensor(S[:, :], S[:, :], A[:, :], ALU.add))
                    link(nc.vector.tensor_tensor(tmp[:, :, :], hot[:, :, :], pP[:, 0:E_].unsqueeze(1).to_broadcast([P, K_, E_]), ALU.mult))
                    link(nc.vector.tensor_reduce(pk[:, :], tmp[:, :, :], AX.X, ALU.add))
                    link(nc.vector.tensor_scalar(ok[:, :], pk[:, :], float(CAP), None, ALU.is_lt))
                    link(nc.vector.scalar_tensor_tensor(pf[:, :], idf[:, :], float(CAP), pk[:, :], ALU.mult, ALU.add))
                    link(nc.vector.tensor_scalar(pk[:, :], ok[:, :], -float(FAR), float(FAR), ALU.mult, ALU.add))
                    dve.wait_ge(s_sc[i], r * K_ * 16)
                    dve.wait_ge(s_out[i], r * 32)
                    link(nc.vector.scalar_tensor_tensor(wk[i][:, :], top[:, :], wn[:, :], ok[:, :], ALU.mult, ALU.mult))
                    nc.vector.tensor_tensor(pl[i][:, :], pf[:, :], pk[:, :], ALU.add).then_inc(s_pl, 1)
                    assert link.count[0] == LV, link.count[0]

        @block.tensor
        def _(pe):
            pe.wait_ge(s_const, 48)
            pe.wait_ge(s_set, 2)
            with pe.Fori(0, TILES // 2) as r:
                for i in range(2):
                    t = 2 * r + i
                    pe.wait_ge(s_in[i], r * 32 + 32)
                    pe.wait_ge(s_exp, t)
                    for k in range(KD):
                        ins = nc.tensor.matmul(pL[:, 0:E_], xf[i][:, k, :], rw[:, k, :], start=(k == 0), stop=(k == KD - 1))
                    ins.then_inc(s_log, 1)
                    pe.wait_ge(s_A, t + 1)
                    pe.wait_ge(s_pl, t)
                    nc.tensor.matmul(pP[:, 0:E_], before_sb[:, :], A[:, :], start=True, stop=False)
                    nc.tensor.matmul(pP[:, 0:E_], ones[:, :], S[:, :], start=False, stop=True).then_inc(s_pos, 1)


def moe0_experts(nc, x_slots, w_gu, w_down, ident, y_slots):
    U, BUF = 8, 4
    F2 = FF - P
    with ExitStack() as phase:
        m = Space(nc, "c2", phase)
        ident_sb = m.sb("ident", [P, P])
        gu = [m.sb(f"gu{i}", [P, KD, 2 * FF]) for i in range(BUF)]
        wd = [m.sb(f"wd{i}", [P, 2, D]) for i in range(BUF)]
        xb = [m.sb(f"xb{i}", [P, D]) for i in range(BUF)]
        xT = [m.sb(f"xT{i}", [P, D]) for i in range(2)]
        g_sb = [m.sb(f"g{i}", [P, FF]) for i in range(2)]
        h_sb = [m.sb(f"h{i}", [P, FF]) for i in range(2)]
        hT = [m.sb(f"hT{i}", [P, 2, P]) for i in range(2)]
        y_sb = [m.sb(f"y{i}", [P, D]) for i in range(2)]
        pT = [m.ps(f"pT{i}") for i in range(2)]
        pG = [m.ps(f"pG{i}") for i in range(2)]
        pH = [m.ps(f"pH{i}") for i in range(2)]
        pY = [m.ps(f"pY{i}") for i in range(2)]
        s_const = m.sem("const")
        s_in = [m.sem(f"in{i}") for i in range(BUF)]
        s_T, s_xT, s_G, s_g, s_h, s_H, s_hT, s_Y, s_y = (m.sem(n) for n in "T xT G g h H hT Y y".split())
        s_out = [m.sem(f"out{i}") for i in range(2)]
        block = phase.enter_context(nc.Block())

        @block.sync
        def _(sp):
            sp.dma_start(ident_sb[:, :], ident).then_inc(s_const, 16)
            with sp.Fori(0, E_ // U) as r:
                for j in range(U):
                    e, q = r * U + j, j % BUF
                    sp.wait_ge(s_Y, e + 1)
                    sp.dma_start(gu[q][:, :, :], w_gu[bass.ds(e, 1), :, :, :].rearrange("e p k n -> (e p) k n")).then_inc(s_in[q], 16)
                    sp.dma_start(wd[q][:, 0, :], w_down[bass.ds(e, 1), 0:P, :].rearrange("e p n -> (e p) n")).then_inc(s_in[q], 16)
                    sp.dma_start(wd[q][0:F2, 1, :], w_down[bass.ds(e, 1), P:FF, :].rearrange("e p n -> (e p) n")).then_inc(s_in[q], 16)
                    sp.dma_start(xb[q][:, :], x_slots[bass.ds(e * CAP, CAP), :]).then_inc(s_in[q], 16)

        @block.gpsimd
        def _(pool):
            with pool.Fori(0, E_ // U) as r:
                for j in range(U):
                    e, q = r * U + j, j % 2
                    pool.wait_ge(s_y, e + 1)
                    pool.dma_start(y_slots[bass.ds(e * CAP, CAP), :], y_sb[q][:, :]).then_inc(s_out[q], 16)
            for q in range(2):
                pool.wait_ge(s_out[q], E_ // 2 * 16)

        def later(e, n, j):
            return e - n if j >= n else e - j

        @block.scalar
        def _(act):
            with act.Fori(0, E_ // U) as r:
                for s in range(U + 2):
                    if s < U:
                        e = r * U + s
                        act.wait_ge(s_T, e + 1)
                        act.wait_ge(s_G, later(e, 1, s))
                        nc.scalar.copy(xT[s % 2][:, :], pT[s % 2][:, :]).then_inc(s_xT, 1)
                    if 1 <= s <= U:
                        j = s - 1
                        e = r * U + j
                        act.wait_ge(s_G, e + 1)
                        act.wait_ge(s_h, later(e, 1, j))
                        nc.scalar.activation(g_sb[j % 2][:, :], pG[j % 2][:, 0:FF], ACT.Silu).then_inc(s_g, 1)

        @block.vector
        def _(dve):
            with dve.Fori(0, E_ // U) as r:
                for s in range(U + 2):
                    if s < U:
                        e = r * U + s
                        dve.wait_ge(s_g, e + 1)
                        dve.wait_ge(s_H, later(e, 1, s))
                        nc.vector.tensor_tensor(h_sb[s % 2][:, :], g_sb[s % 2][:, :], pG[s % 2][:, FF:2 * FF], ALU.mult).then_inc(s_h, 1)
                    if 1 <= s <= U:
                        j = s - 1
                        e = r * U + j
                        dve.wait_ge(s_H, e + 1)
                        dve.wait_ge(s_Y, BUF + later(e, 1, j))
                        nc.vector.tensor_copy(hT[j % 2][:, 0, :], pH[j % 2][:, 0:P]).then_inc(s_hT, 1)
                        nc.vector.tensor_copy(hT[j % 2][0:F2, 1, :], pH[j % 2][0:F2, P:2 * P]).then_inc(s_hT, 1)
                    if s >= 2:
                        j = s - 2
                        e = r * U + j
                        dve.wait_ge(s_Y, BUF + e + 1)
                        dve.wait_ge(s_out[j % 2], (r * (U // 2) + j // 2) * 16)
                        nc.vector.tensor_copy(y_sb[j % 2][:, :], pY[j % 2][:, :]).then_inc(s_y, 1)

        @block.tensor
        def _(pe):
            nc.tensor.sem_inc(s_Y, BUF)
            pe.wait_ge(s_const, 16)
            with pe.Fori(0, E_ // U) as r:
                for s in range(U + 3):
                    if s < U:
                        e, q = r * U + s, s % BUF
                        pe.wait_ge(s_in[q], (r * (U // BUF) + s // BUF + 1) * 64)
                        pe.wait_ge(s_xT, later(e, 1, s))
                        for k in range(KD):
                            ins = nc.tensor.transpose(pT[s % 2][:, k * P:(k + 1) * P], xb[q][:, k * P:(k + 1) * P], ident_sb[:, :])
                        ins.then_inc(s_T, 1)
                    if 1 <= s <= U:
                        j = s - 1
                        e = r * U + j
                        pe.wait_ge(s_xT, e + 1)
                        pe.wait_ge(s_h, later(e, 1, j))
                        for k in range(KD):
                            ins = nc.tensor.matmul(pG[j % 2][:, 0:2 * FF], xT[j % 2][:, k * P:(k + 1) * P], gu[j % BUF][:, k, :], start=(k == 0), stop=(k == KD - 1))
                        ins.then_inc(s_G, 1)
                    if 2 <= s <= U + 1:
                        j = s - 2
                        e = r * U + j
                        pe.wait_ge(s_h, e + 1)
                        pe.wait_ge(s_hT, 2 * later(e, 1, j))
                        nc.tensor.transpose(pH[j % 2][:, 0:P], h_sb[j % 2][:, 0:P], ident_sb[:, :])
                        nc.tensor.transpose(pH[j % 2][0:F2, P:2 * P], h_sb[j % 2][:, P:FF], ident_sb[:, :]).then_inc(s_H, 1)
                    if s >= 3:
                        j = s - 3
                        e = r * U + j
                        pe.wait_ge(s_hT, 2 * e + 2)
                        pe.wait_ge(s_y, later(e, 1, j))
                        nc.tensor.matmul(pY[j % 2][:, :], hT[j % 2][:, 0, :], wd[j % BUF][:, 0, :], start=True, stop=False)
                        nc.tensor.matmul(pY[j % 2][:, :], hT[j % 2][0:F2, 1, :], wd[j % BUF][0:F2, 1, :], start=False, stop=True).then_inc(s_Y, 1)


def gather_mix_norm(nc, name, K, y_slots, slots, x_tok, places, weights, ident, o_tok, o_feat):
    LN_EPS = 1e-5
    with ExitStack() as phase:
        m = Space(nc, name, phase)
        ident_sb, eps_sb = m.sb("ident", [P, P]), m.sb("eps", [P, 1])
        x_sb = [m.sb(f"x{i}", [P, D]) for i in range(2)]
        pl = [m.sb(f"pl{i}", [P, K], U32) for i in range(2)]
        wk = [m.sb(f"wk{i}", [P, K]) for i in range(2)]
        g = [m.sb(f"g{i}", [P, K, D]) for i in range(2)]
        st, mv, sd = m.sb("st", [P, 6]), m.sb("mv", [P, 2]), m.sb("sd", [P, 1])
        o_sb = [m.sb(f"o{i}", [P, D]) for i in range(2)]
        oT = [m.sb(f"oT{i}", [P, KD, P]) for i in range(2)]
        po = [m.ps(f"po{i}") for i in range(2)]
        s_const, s_set, s_lv = m.sem("const"), m.sem("set"), m.sem("lv")
        s_in = [m.sem(f"in{i}") for i in range(2)]
        s_g = [m.sem(f"g{i}") for i in range(2)]
        s_out = [m.sem(f"out{i}") for i in range(2)]
        s_var, s_sd, s_ln, s_oT, s_oc = (m.sem(n) for n in "var sd ln oT oc".split())
        tick_dve, tick_pool, tick_sp = m.sem("tick_dve"), m.sem("tick_pool"), m.sem("tick_sp")
        block = phase.enter_context(nc.Block())
        LV = K + 2

        @block.sync
        def _(sp):
            sp.dma_start(ident_sb[:, :], ident).then_inc(s_const, 16)
            with sp.Fori(0, TILES // 2) as r:
                for i in range(2):
                    t = 2 * r + i
                    sp.wait_ge(s_ln, 2 * r)
                    for dst, src in ((x_sb, x_tok), (pl, places), (wk, weights)):
                        sp.dma_start(dst[i][:, :], src[bass.ds(t * P, P), :]).then_inc(s_in[i], 16)
                for i in range(2):
                    t = 2 * r + i
                    sp.wait_ge(s_ln, t + 1)
                    sp.dma_start(o_tok[bass.ds(t * P, P), :], o_sb[i][:, :]).then_inc(s_out[i], 16)
                    if o_feat is not None:
                        sp.wait_ge(s_oc, t + 1)
                        alone(sp, tick_sp)
                        sp.dma_start(o_feat[:, :, bass.ds(t * P, P)].rearrange("k p t -> p k t"), oT[i][:, :, :]).then_inc(s_out[i], 16)
            for i in range(2):
                sp.wait_ge(s_out[i], TILES // 2 * (16 if o_feat is None else 32))
        stores = 16 if o_feat is None else 32

        @block.gpsimd
        def _(pool):
            pool.wait_ge(s_set, 3)
            with pool.Fori(0, TILES // 2) as r:
                for i in range(2):
                    pool.wait_ge(s_in[i], r * 48 + 48)
                    pool.wait_ge(s_ln, 2 * r)
                    alone(pool, tick_pool)
                    for k in range(K):
                        pool.indirect_dma_start(g[i][:, k, :], None, y_slots, bass.IndirectOffsetOnAxis(ap=pl[i][:, k:k + 1], axis=0),
                                                bounds_check=slots - 1, oob_is_err=False).then_inc(s_g[i], 16)

        @block.scalar
        def _(act):
            act.wait_ge(s_set, 1)
            with act.Fori(0, TILES // 2) as r:
                for i in range(2):
                    act.wait_ge(s_var, 2 * r + i + 1)
                    nc.scalar.activation(sd[:, :], mv[:, 1:2], ACT.Sqrt, bias=eps_sb[:, :], scale=1.0).then_inc(s_sd, 1)
                    if o_feat is not None:
                        act.wait_ge(s_oT, 2 * r + i + 1)
                        act.wait_ge(s_out[i], r * stores)
                        nc.scalar.copy(oT[i][:, :, :].rearrange("p k t -> p (k t)"), po[i][:, :]).then_inc(s_oc, 1)

        @block.vector
        def _(dve):
            nc.vector.memset(eps_sb[:, :], LN_EPS).then_inc(s_set, 1)
            for i in range(2):
                nc.vector.memset(g[i][:, :, :], 0.0).then_inc(s_set, 1)
            dve.wait_ge(s_set, 3)
            with dve.Fori(0, TILES // 2) as r:
                for i in range(2):
                    t = 2 * r + i
                    link = linker(dve, s_lv, t * LV)
                    dve.wait_ge(s_in[i], r * 48 + 48)
                    dve.wait_ge(s_g[i], (r + 1) * K * 16)
                    x = x_sb[i][:, :]
                    for k in range(K):
                        link(nc.vector.scalar_tensor_tensor(x, g[i][:, k, :], wk[i][:, k:k + 1], x, ALU.mult, ALU.add))
                    link(nc.vector.bn_stats(st[:, :], x))
                    alone(dve, tick_dve)
                    nc.vector.bn_aggr(mv[:, :], st[:, :]).then_inc(s_var, 1)
                    dve.wait_ge(s_sd, t + 1)
                    link(nc.vector.reciprocal(sd[:, :], sd[:, :]))
                    dve.wait_ge(s_out[i], r * stores)
                    nc.vector.tensor_scalar(o_sb[i][:, :], x, mv[:, 0:1], sd[:, :], ALU.subtract, ALU.mult).then_inc(s_ln, 1)

        if o_feat is not None:
            @block.tensor
            def _(pe):
                pe.wait_ge(s_const, 16)
                with pe.Fori(0, TILES // 2) as r:
                    for i in range(2):
                        pe.wait_ge(s_ln, 2 * r + i + 1)
                        pe.wait_ge(s_oc, 2 * r)
                        for k in range(KD):
                            ins = nc.tensor.transpose(po[i][:, k * P:(k + 1) * P], o_sb[i][:, k * P:(k + 1) * P], ident_sb[:, :])
                        ins.then_inc(s_oT, 1)


DI1, N1 = 1024, 16
F1 = DI1 // P


def ssm1_project(nc, x_feat, w_in, conv_w, conv_b, w_x, w_dt, b_dt, u_feat, z_feat, dt_feat, bc_feat):
    with ExitStack() as phase:
        m = Space(nc, "d1", phase)
        w_sb = m.sb("w", [P, KD, 2 * DI1])
        wx_sb = m.sb("wx", [P, F1, P + 2 * N1])
        wdt_sb = m.sb("wdt", [P, DI1])
        cw_sb, cb_sb, bdt_sb = m.sb("cw", [P, F1, 4]), m.sb("cb", [P, F1]), m.sb("bdt", [P, F1])
        one_sb = m.sb("one", [P, 1])
        xT = [m.sb(f"xT{i}", [P, KD, L]) for i in range(2)]
        xpad = [m.sb(f"xpad{i}", [P, 3 + L]) for i in range(2)]
        acc = [m.sb(f"acc{i}", [P, L]) for i in range(2)]
        u_sb, z_sb, dt_sb = m.sb("u", [P, F1, L]), m.sb("z", [P, F1, L]), m.sb("dt", [P, F1, L])
        v_sb, r_sb = m.sb("v", [P, F1, L]), m.sb("r", [P, F1, L])
        dr_sb, bc_sb = m.sb("dr", [P, L]), m.sb("bc", [2 * N1, L])
        px = [m.ps(f"px{i}") for i in range(2)]
        pz = [m.ps(f"pz{i}") for i in range(2)]
        pd = [m.ps(f"pd{i}") for i in range(2)]
        pr, pb = m.ps("pr"), m.ps("pb")
        s_const, s_set, s_lv = m.sem("const"), m.sem("set"), m.sem("lv")
        s_x = [m.sem(f"x{i}") for i in range(2)]
        s_px, s_xpad, s_conv, s_u, s_pz, s_z, s_pr, s_dr, s_pb, s_bc, s_pd, s_v, s_r, s_la, s_dt, s_out = (
            m.sem(n) for n in "px xpad conv u pz z pr dr pb bc pd v r la dt out".split())
        block = phase.enter_context(nc.Block())
        CONSTS = 6

        @block.sync
        def _(sp):
            for dst, src in ((cw_sb[:, :, :], conv_w.rearrange("(k p) c -> p k c", p=P)), (cb_sb[:, :], conv_b.rearrange("(k p) -> p k", p=P)),
                             (bdt_sb[:, :], b_dt.rearrange("(k p) -> p k", p=P)), (w_sb[:, :, :], w_in.rearrange("(k p) n -> p k n", p=P)),
                             (wx_sb[:, :, :], w_x.rearrange("(k p) n -> p k n", p=P)), (wdt_sb[:, :], w_dt)):
                sp.dma_start(dst, src, allow_slow_non_contiguous=True).then_inc(s_const, 16)
            with sp.Fori(0, NB // 2) as r:
                for i in range(2):
                    b = 2 * r + i
                    sp.wait_ge(s_pz, 2 * r * F1)
                    sp.dma_start(xT[i][:, :, :], x_feat[:, :, bass.ds(b * L, L)].rearrange("k p t -> p k t")).then_inc(s_x[i], 16)
                for i in range(2):
                    b = 2 * r + i
                    for s, src, dst, n in ((s_u, u_sb, u_feat, F1), (s_z, z_sb, z_feat, F1), (s_dt, dt_sb, dt_feat, 1)):
                        sp.wait_ge(s, b * n + n)
                        sp.dma_start(dst[:, :, bass.ds(b * L, L)].rearrange("k p t -> p k t"), src[:, :, :]).then_inc(s_out, 16)
                    sp.wait_ge(s_bc, b + 1)
                    sp.dma_start(bc_feat[:, bass.ds(b * L, L)], bc_sb[:, :]).then_inc(s_out, 16)
            sp.wait_ge(s_out, NB * 64)

        @block.scalar
        def _(act):
            act.wait_ge(s_const, 16 * CONSTS)
            act.wait_ge(s_set, 3)
            with act.Fori(0, NB) as b:
                act.wait_ge(s_out, b * 64)
                for f in range(F1 + 1):
                    if f < F1:
                        act.wait_ge(s_px, b * F1 + f + 1)
                        act.wait_ge(s_conv, b * F1 + max(f - 1, 0))
                        nc.scalar.copy(xpad[f % 2][:, 3:3 + L], px[f % 2][:, 0:L]).then_inc(s_xpad, 1)
                    if f >= 1:
                        g = f - 1
                        act.wait_ge(s_conv, b * F1 + g + 1)
                        nc.scalar.activation(u_sb[:, g, :], acc[g % 2][:, :], ACT.Silu, bias=cb_sb[:, g:g + 1]).then_inc(s_u, 1)
                for f in range(F1):
                    act.wait_ge(s_pz, b * F1 + f + 1)
                    nc.scalar.activation(z_sb[:, f, :], pz[f % 2][:, 0:L], ACT.Silu).then_inc(s_z, 1)
                act.wait_ge(s_dt, b)
                for f in range(F1):
                    act.wait_ge(s_pd, b * F1 + f + 1)
                    nc.scalar.activation(v_sb[:, f, :], pd[f % 2][:, 0:L], ACT.Abs, bias=bdt_sb[:, f:f + 1], scale=1.0).then_inc(s_v, 1)
                    nc.scalar.activation(r_sb[:, f, :], pd[f % 2][:, 0:L], ACT.Relu, bias=bdt_sb[:, f:f + 1], scale=1.0).then_inc(s_v, 1)
                act.wait_ge(s_v, (b + 1) * 2 * F1)
                link = linker(act, s_la, b)
                link(nc.scalar.activation(v_sb[:, :, :], v_sb[:, :, :], ACT.Exp, scale=-1.0))
                nc.scalar.activation(v_sb[:, :, :], v_sb[:, :, :], ACT.Ln, bias=one_sb[:, :], scale=1.0).then_inc(s_r, 1)

        @block.vector
        def _(dve):
            for i in range(2):
                nc.vector.memset(xpad[i][:, 0:3], 0.0).then_inc(s_set, 1)
            nc.vector.memset(one_sb[:, :], 1.0).then_inc(s_set, 1)
            dve.wait_ge(s_set, 3)
            dve.wait_ge(s_const, 16 * CONSTS)
            with dve.Fori(0, NB) as b:
                link = linker(dve, s_lv, b * 3 * F1)
                for f in range(F1):
                    a, xp = acc[f % 2], xpad[f % 2]
                    dve.wait_ge(s_xpad, b * F1 + f + 1)
                    dve.wait_ge(s_u, b * F1 + max(f - 1, 0))
                    link(nc.vector.tensor_scalar(a[:, :], xp[:, 3:3 + L], cw_sb[:, f, 3:4], None, ALU.mult))
                    for j in (2, 1):
                        link(nc.vector.scalar_tensor_tensor(a[:, :], xp[:, j:j + L], cw_sb[:, f, j:j + 1], a[:, :], ALU.mult, ALU.add))
                    nc.vector.scalar_tensor_tensor(a[:, :], xp[:, 0:L], cw_sb[:, f, 0:1], a[:, :], ALU.mult, ALU.add).then_inc(s_conv, 1)
                dve.wait_ge(s_pr, b + 1)
                nc.vector.tensor_copy(dr_sb[:, :], pr[:, 0:L]).then_inc(s_dr, 1)
                dve.wait_ge(s_pb, b + 1)
                dve.wait_ge(s_out, b * 64)
                nc.vector.tensor_copy(bc_sb[:, :], pb[0:2 * N1, 0:L]).then_inc(s_bc, 1)
                dve.wait_ge(s_r, b + 1)
                nc.vector.tensor_tensor(dt_sb[:, :, :], v_sb[:, :, :], r_sb[:, :, :], ALU.add).then_inc(s_dt, 1)

        @block.tensor
        def _(pe):
            pe.wait_ge(s_const, 16 * CONSTS)
            with pe.Fori(0, NB // 2) as r:
                for i in range(2):
                    b = 2 * r + i
                    pe.wait_ge(s_x[i], r * 16 + 16)
                    for f in range(F1):
                        pe.wait_ge(s_xpad, b * F1 + max(f - 1, 0))
                        for k in range(KD):
                            ins = nc.tensor.matmul(px[f % 2][:, 0:L], w_sb[:, k, f * P:(f + 1) * P], xT[i][:, k, :], start=(k == 0), stop=(k == KD - 1))
                        ins.then_inc(s_px, 1)
                    for f in range(F1):
                        pe.wait_ge(s_z, b * F1 + max(f - 1, 0))
                        for k in range(KD):
                            ins = nc.tensor.matmul(pz[f % 2][:, 0:L], w_sb[:, k, DI1 + f * P:DI1 + (f + 1) * P], xT[i][:, k, :], start=(k == 0), stop=(k == KD - 1))
                        ins.then_inc(s_pz, 1)
                    pe.wait_ge(s_u, b * F1 + F1)
                    pe.wait_ge(s_dr, b)
                    for k in range(F1):
                        ins = nc.tensor.matmul(pr[:, 0:L], wx_sb[:, k, 0:P], u_sb[:, k, :], start=(k == 0), stop=(k == F1 - 1))
                    ins.then_inc(s_pr, 1)
                    pe.wait_ge(s_bc, b)
                    for k in range(F1):
                        ins = nc.tensor.matmul(pb[0:2 * N1, 0:L], wx_sb[:, k, P:P + 2 * N1], u_sb[:, k, :], start=(k == 0), stop=(k == F1 - 1))
                    ins.then_inc(s_pb, 1)
                    pe.wait_ge(s_dr, b + 1)
                    for f in range(F1):
                        pe.wait_ge(s_v, (b * F1 + max(f - 1, 0)) * 2)
                        nc.tensor.matmul(pd[f % 2][:, 0:L], wdt_sb[:, f * P:(f + 1) * P], dr_sb[:, :], start=True, stop=True).then_inc(s_pd, 1)


def ssm1_scan(nc, x_tok, u_feat, z_feat, dt_feat, bc_feat, a_log, skip, w_out, ident, o_tok, o_feat):
    LN_EPS = 1e-5
    G = 4
    Q = N1 // G
    C = F1 * Q
    RB, RH = 4, 4
    with ExitStack() as phase:
        m = Space(nc, "d2", phase)
        ident_sb, eps_sb, zero_sb = m.sb("ident", [P, P]), m.sb("eps", [P, 1]), m.sb("zero", [P, G])
        A_sb, D_sb = m.sb("A", [P, F1, N1]), m.sb("D", [P, F1])
        wo_sb = m.sb("wo", [P, F1, D])
        B_sb = [m.sb(f"B{i}", [P, N1, L]) for i in range(2)]
        C_sb = [m.sb(f"C{i}", [P, N1, L]) for i in range(2)]
        u_sb = [m.sb(f"u{i}", [P, F1, L]) for i in range(2)]
        z_sb = m.sb("z", [P, F1, L])
        dt_sb = [m.sb(f"dt{i}", [P, F1, L]) for i in range(2)]
        dtu = [m.sb(f"dtu{i}", [P, L]) for i in range(2)]
        dBu = [m.sb(f"dBu{i}", [P, G, L]) for i in range(RB)]
        hC = [m.sb(f"hC{i}", [P, G, L]) for i in range(RH)]
        t_sb = [m.sb(f"t{i}", [P, L]) for i in range(2)]
        yz = m.sb("yz", [P, F1, L])
        x_sb = m.sb("x", [P, 2, D])
        st, mv, sd = m.sb("st", [P, 2, 6]), m.sb("mv", [P, 2, 2]), m.sb("sd", [P, 2])
        oT = m.sb("oT", [P, 2, KD, P])
        ph = [m.ps(f"ph{i}", (P, G, L)) for i in range(2)]
        py = [m.ps(f"py{i}") for i in range(2)]
        po = [m.ps(f"po{i}") for i in range(2)]
        s_const, s_set, s_lv, s_A = m.sem("const"), m.sem("set"), m.sem("lv"), m.sem("A")
        s_B = [m.sem(f"ldB{i}") for i in range(2)]
        s_dt = [m.sem(f"lddt{i}") for i in range(2)]
        s_C, s_z, s_x, s_out = (m.sem("ld" + n) for n in "C z x out".split())
        s_dtu, s_dA, s_dBu, s_scan, s_hC, s_py, s_sum, s_yz, s_o, s_var, s_sd, s_ln, s_T, s_oc = (
            m.sem(n) for n in "dtu dA dBu scan hC py sum yz o var sd ln T oc".split())
        tick_dve, tick_sp = m.sem("tick_dve"), m.sem("tick_sp")
        block = phase.enter_context(nc.Block())
        CONSTS = 4

        def feat(a, b):
            return a[:, :, bass.ds(b * L, L)].rearrange("k p t -> p k t")

        def later(b, done, per, back):
            return b * per + max(done - back, 0)

        @block.sync
        def _(sp):
            for dst, src in ((ident_sb[:, :], ident), (A_sb[:, :, :], a_log.rearrange("(k p) n -> p k n", p=P)),
                             (D_sb[:, :], skip.rearrange("(k p) -> p k", p=P)), (wo_sb[:, :, :], w_out.rearrange("(k p) n -> p k n", p=P))):
                sp.dma_start(dst, src, allow_slow_non_contiguous=True).then_inc(s_const, 16)
            def inputs(b, i):
                sp.dma_start(dt_sb[i][:, :, :], feat(dt_feat, b)).then_inc(s_dt[i], 16)
                sp.dma_start(u_sb[i][:, :, :], feat(u_feat, b)).then_inc(s_dt[i], 16)
                sp.dma_start(B_sb[i][:, :, :], bc_feat[0:N1, bass.ds(b * L, L)].partition_broadcast(P)).then_inc(s_B[i], 16)
                sp.dma_start(C_sb[i][:, :, :], bc_feat[N1:2 * N1, bass.ds(b * L, L)].partition_broadcast(P)).then_inc(s_B[i], 16)

            def batch(b):
                sp.wait_ge(s_yz, b * F1)
                alone(sp, tick_sp)
                sp.dma_start(z_sb[:, :, :], feat(z_feat, b)).then_inc(s_z, 16)
                sp.wait_ge(s_T, b * 2)
                alone(sp, tick_sp)
                sp.wait_ge(s_out, b * 48)
                alone(sp, tick_sp)
                sp.dma_start(x_sb[:, :, :], x_tok[bass.ds(b * L, L), :].rearrange("(c p) n -> p c n", p=P)).then_inc(s_x, 16)
                sp.wait_ge(s_oc, b * 2 + 2)
                alone(sp, tick_sp)
                sp.dma_start(o_tok[bass.ds(b * L, L), :].rearrange("(c p) n -> p c n", p=P), x_sb[:, :, :]).then_inc(s_out, 16)
                for c in range(2):
                    sp.dma_start(o_feat[:, :, bass.ds(b * L + c * P, P)].rearrange("k p t -> p k t"), oT[:, c, :, :]).then_inc(s_out, 16)
            for i in range(2):
                inputs(i, i)
            with sp.Fori(0, NB // 2 - 1) as r:
                for i in range(2):
                    b = 2 * r + i
                    batch(b)
                    sp.wait_ge(s_dA, b * C + C)
                    alone(sp, tick_sp)
                    sp.wait_ge(s_yz, b * F1 + F1)
                    alone(sp, tick_sp)
                    inputs(b + 2, i)
            for i in range(2):
                batch(NB - 2 + i)
            sp.wait_ge(s_out, NB * 48)

        @block.gpsimd
        def _(pool):
            with pool.Fori(0, NB // 2) as r:
                for i in range(2):
                    b = 2 * r + i
                    pool.wait_ge(s_B[i], r * 32 + 32)
                    for c in range(C):
                        f, q = c // Q, c % Q
                        pool.wait_ge(s_dtu, b * F1 + f + 1)
                        pool.wait_ge(s_scan, later(b, c, C, RB - 1))
                        pool.tensor_tensor(dBu[c % RB][:, :, :], B_sb[i][:, q * G:(q + 1) * G, :],
                                           dtu[f % 2][:, :].unsqueeze(1).to_broadcast([P, G, L]), ALU.mult).then_inc(s_dBu, 1)

        @block.scalar
        def _(act):
            act.wait_ge(s_const, 16 * CONSTS)
            act.wait_ge(s_set, 2)
            nc.scalar.activation(A_sb[:, :, :], A_sb[:, :, :], ACT.Exp).then_inc(s_A, 1)
            act.wait_ge(s_A, 2)
            with act.Fori(0, NB // 2) as r:
                for i in range(2):
                    b = 2 * r + i
                    act.wait_ge(s_dt[i], r * 32 + 32)
                    for c in range(C):
                        f, q = c // Q, c % Q
                        act.wait_ge(s_hC, later(b, c, C, 1))
                        nc.scalar.copy(ph[c % 2][:, :, 0:1], zero_sb[:, :].unsqueeze(2))
                        for n in range(G):
                            ins = nc.scalar.activation(ph[c % 2][:, n, 1:L], dt_sb[i][:, f, 1:L], ACT.Exp, scale=A_sb[:, f, q * G + n:q * G + n + 1])
                        ins.then_inc(s_dA, 1)
                    act.wait_ge(s_var, b * 2 + 2)
                    nc.scalar.activation(sd[:, :], mv[:, :, 1], ACT.Sqrt, bias=eps_sb[:, :], scale=1.0).then_inc(s_sd, 1)
                    act.wait_ge(s_out, b * 48)
                    for c in range(2):
                        act.wait_ge(s_T, b * 2 + c + 1)
                        nc.scalar.copy(oT[:, c, :, :].rearrange("p k t -> p (k t)"), py[c][:, :]).then_inc(s_oc, 1)

        @block.vector
        def _(dve):
            nc.vector.memset(eps_sb[:, :], LN_EPS).then_inc(s_set, 1)
            nc.vector.memset(zero_sb[:, :], 0.0).then_inc(s_set, 1)
            dve.wait_ge(s_set, 2)
            dve.wait_ge(s_A, 1)
            nc.vector.tensor_scalar(A_sb[:, :, :], A_sb[:, :, :], -1.0, None, ALU.mult).then_inc(s_A, 1)
            LV = 5
            with dve.Fori(0, NB // 2) as r:
                for i in range(2):
                    b = 2 * r + i
                    link = linker(dve, s_lv, b * LV)
                    dve.wait_ge(s_dt[i], r * 32 + 32)
                    dve.wait_ge(s_B[i], r * 32 + 32)

                    def step_sizes(f):
                        dve.wait_ge(s_dBu, later(b, f * Q, C, Q))
                        nc.vector.tensor_tensor(dtu[f % 2][:, :], dt_sb[i][:, f, :], u_sb[i][:, f, :], ALU.mult).then_inc(s_dtu, 1)

                    def channel_out(g):
                        dve.wait_ge(s_py, b * C + (g + 1) * Q)
                        dve.wait_ge(s_yz, later(b, g, F1, 1))
                        nc.vector.scalar_tensor_tensor(t_sb[g % 2][:, :], u_sb[i][:, g, :], D_sb[:, g:g + 1], py[g % 2][:, 0:L], ALU.mult, ALU.add).then_inc(s_sum, 1)
                        dve.wait_ge(s_sum, b * F1 + g + 1)
                        dve.wait_ge(s_o, b * 2)
                        nc.vector.tensor_tensor(yz[:, g, :], t_sb[g % 2][:, :], z_sb[:, g, :], ALU.mult).then_inc(s_yz, 1)
                    step_sizes(0)
                    for c in range(C):
                        f, q = c // Q, c % Q
                        if q == 0 and f + 1 < F1:
                            step_sizes(f + 1)
                        dve.wait_ge(s_dA, b * C + c + 1)
                        dve.wait_ge(s_dBu, b * C + c + 1)
                        h = ph[c % 2][:, :, :].rearrange("p n t -> p (n t)")
                        nc.vector.tensor_tensor_scan(h, h, dBu[c % RB][:, :, :].rearrange("p n t -> p (n t)"), 0.0, ALU.mult, ALU.add).then_inc(s_scan, 1)
                        dve.wait_ge(s_scan, b * C + c + 1)
                        dve.wait_ge(s_py, later(b, c, C, RH - 1))
                        nc.vector.tensor_tensor(hC[c % RH][:, :, :], ph[c % 2][:, :, :], C_sb[i][:, q * G:(q + 1) * G, :], ALU.mult).then_inc(s_hC, 1)
                        if q == 1 and f >= 1:
                            if f == 1:
                                dve.wait_ge(s_z, b * 16 + 16)
                            channel_out(f - 1)
                    channel_out(F1 - 1)
                    dve.wait_ge(s_x, b * 16 + 16)
                    for c in range(2):
                        dve.wait_ge(s_o, b * 2 + c + 1)
                        link(nc.vector.tensor_tensor(x_sb[:, c, :], x_sb[:, c, :], po[c][:, :], ALU.add))
                        link(nc.vector.bn_stats(st[:, c, :], x_sb[:, c, :]))
                        alone(dve, tick_dve)
                        nc.vector.bn_aggr(mv[:, c, :], st[:, c, :]).then_inc(s_var, 1)
                    dve.wait_ge(s_sd, b + 1)
                    link(nc.vector.reciprocal(sd[:, :], sd[:, :]))
                    for c in range(2):
                        nc.vector.tensor_scalar(x_sb[:, c, :], x_sb[:, c, :], mv[:, c, 0:1], sd[:, c:c + 1], ALU.subtract, ALU.mult).then_inc(s_ln, 1)
                    assert link.count[0] == LV

        @block.tensor
        def _(pe):
            pe.wait_ge(s_const, 16 * CONSTS)
            with pe.Fori(0, NB) as b:

                def project(g):
                    pe.wait_ge(s_yz, b * F1 + g + 1)
                    if g == 0:
                        pe.wait_ge(s_var, b * 2)
                    for c in range(2):
                        ins = nc.tensor.matmul(po[c][:, :], yz[:, g, c * P:(c + 1) * P], wo_sb[:, g, :], start=(g == 0), stop=(g == F1 - 1))
                        if g == F1 - 1:
                            ins.then_inc(s_o, 1)
                for c in range(C):
                    f, q = c // Q, c % Q
                    pe.wait_ge(s_hC, b * C + c + 1)
                    if q == 0:
                        pe.wait_ge(s_sum, later(b, f, F1, 1))
                        pe.wait_ge(s_oc, b * 2)
                    for n in range(G):
                        ins = nc.tensor.matmul(py[f % 2][:, 0:L], ident_sb[:, :], hC[c % RH][:, n, :], start=(q == 0 and n == 0), stop=(q == Q - 1 and n == G - 1))
                    ins.then_inc(s_py, 1)
                    if q == 2 and f >= 2:
                        project(f - 2)
                project(F1 - 2)
                project(F1 - 1)
                for c in range(2):
                    pe.wait_ge(s_ln, b * 2 + c + 1)
                    for k in range(KD):
                        ins = nc.tensor.transpose(py[c][:, k * P:(k + 1) * P], x_sb[:, c, k * P:(k + 1) * P], ident_sb[:, :])
                    ins.then_inc(s_T, 1)


def linear_attention(nc, x_tok, x_feat, ctx_feat, w_q, w_g, b_g, w_kv, w_o, ident, heads_mask, o_tok, o_feat):
    LN_EPS, EPS = 1e-5, 1e-6
    with ExitStack() as phase:
        m = Space(nc, "e1", phase)
        ident_sb, eps_sb, mask_sb, ones = m.sb("ident", [P, P]), m.sb("eps", [P, 1]), m.sb("mask", [P, P]), m.sb("ones", [P, P])
        wq, wg, wo = m.sb("wq", [P, KD, D]), m.sb("wg", [P, KD, D]), m.sb("wo", [P, KD, D])
        wkv = m.sb("wkv", [P, KD, 2 * D])
        bg_sb = m.sb("bg", [P, KD])
        xf = [m.sb(f"xf{i}", [P, KD, L]) for i in range(2)]
        cf = [m.sb(f"cf{i}", [P, KD, L]) for i in range(2)]
        xt = [m.sb(f"xt{i}", [P, 2, D]) for i in range(2)]
        k_sb, v_sb = m.sb("k", [P, 2, D]), m.sb("v", [P, 2, D])
        kneg = [m.sb(f"kneg{i}", [P, D]) for i in range(2)]
        q_sb, g_sb = m.sb("q", [P, KD, L]), m.sb("g", [P, KD, L])
        qneg = [m.sb(f"qneg{i}", [P, L]) for i in range(2)]
        kv_sb, ks_sb = m.sb("kv", [P, KD, P]), m.sb("ks", [P, KD, P])
        den = m.sb("den", [P, KD, L])
        ag = m.sb("ag", [P, KD, L])
        st, mv, sd = m.sb("st", [P, 2, 6]), m.sb("mv", [P, 2, 2]), m.sb("sd", [P, 2])
        o_sb, oT = m.sb("o", [P, 2, D]), m.sb("oT", [P, 2, KD, P])
        pa = [m.ps(f"pa{i}") for i in range(2)]
        pb = [m.ps(f"pb{i}") for i in range(2)]
        ps = [m.ps(f"ps{i}") for i in range(2)]
        po = [m.ps(f"po{i}") for i in range(2)]
        s_const, s_set, s_lv, s_out = m.sem("const"), m.sem("set"), m.sem("lv"), m.sem("out")
        s_in = [m.sem(f"in{i}") for i in range(2)]
        s_pk, s_kn, s_k, s_pv, s_v, s_pq, s_qn, s_q, s_pg, s_g, s_ps, s_kv, s_pa, s_ag, s_o, s_var, s_sd, s_ln, s_T, s_oc, s_ke, s_qe = (
            m.sem(n) for n in "pk kn k pv v pq qn q pg g ps kv pa ag o var sd ln T oc ke qe".split())
        tick_dve = m.sem("tick_dve")
        block = phase.enter_context(nc.Block())
        CONSTS = 7

        @block.sync
        def _(sp):
            for dst, src in ((ident_sb[:, :], ident), (mask_sb[:, :], heads_mask), (bg_sb[:, :], b_g.rearrange("(k p) -> p k", p=P)),
                             (wkv[:, :, :], w_kv.rearrange("(k p) n -> p k n", p=P)), (wq[:, :, :], w_q.rearrange("(k p) n -> p k n", p=P)),
                             (wg[:, :, :], w_g.rearrange("(k p) n -> p k n", p=P)), (wo[:, :, :], w_o.rearrange("(k p) n -> p k n", p=P))):
                sp.dma_start(dst, src, allow_slow_non_contiguous=True).then_inc(s_const, 16)
            with sp.Fori(0, NB // 2) as r:
                for i in range(2):
                    b = 2 * r + i
                    sp.wait_ge(s_ln, 4 * r)
                    sp.dma_start(cf[i][:, :, :], ctx_feat[:, :, bass.ds(b * L, L)].rearrange("k p t -> p k t")).then_inc(s_in[i], 16)
                    sp.dma_start(xf[i][:, :, :], x_feat[:, :, bass.ds(b * L, L)].rearrange("k p t -> p k t")).then_inc(s_in[i], 16)
                    sp.dma_start(xt[i][:, :, :], x_tok[bass.ds(b * L, L), :].rearrange("(c p) n -> p c n", p=P)).then_inc(s_in[i], 16)
                for i in range(2):
                    b = 2 * r + i
                    sp.wait_ge(s_oc, b * 2 + 2)
                    sp.dma_start(o_tok[bass.ds(b * L, L), :].rearrange("(c p) n -> p c n", p=P), o_sb[:, :, :]).then_inc(s_out, 16)
                    for c in range(2):
                        sp.dma_start(o_feat[:, :, bass.ds(b * L + c * P, P)].rearrange("k p t -> p k t"), oT[:, c, :, :]).then_inc(s_out, 16)
            sp.wait_ge(s_out, NB * 48)

        @block.scalar
        def _(act):
            act.wait_ge(s_const, 16 * CONSTS)
            act.wait_ge(s_set, 3)
            with act.Fori(0, NB) as b:
                for c in range(2):
                    act.wait_ge(s_kn, b * 2 + c + 1)
                    nc.scalar.activation(kneg[c][:, :], kneg[c][:, :], ACT.Exp).then_inc(s_ke, 1)
                for c in range(2):
                    act.wait_ge(s_pv, b * 2 + c + 1)
                    nc.scalar.copy(v_sb[:, c, :], pa[c][:, :]).then_inc(s_v, 1)
                for k in range(KD):
                    act.wait_ge(s_pg, b * KD + k + 1)
                    act.wait_ge(s_ag, b * KD)
                    nc.scalar.activation(g_sb[:, k, :], pb[k % 2][:, 0:L], ACT.Exp, bias=bg_sb[:, k:k + 1], scale=-1.0).then_inc(s_g, 1)
                    act.wait_ge(s_qn, b * KD + k + 1)
                    nc.scalar.activation(qneg[k % 2][:, :], qneg[k % 2][:, :], ACT.Exp).then_inc(s_qe, 1)
                act.wait_ge(s_var, b * 2 + 2)
                nc.scalar.activation(sd[:, :], mv[:, :, 1], ACT.Sqrt, bias=eps_sb[:, :], scale=1.0).then_inc(s_sd, 1)
                act.wait_ge(s_out, b * 48)
                for c in range(2):
                    act.wait_ge(s_T, b * 2 + c + 1)
                    nc.scalar.copy(oT[:, c, :, :].rearrange("p k t -> p (k t)"), ps[c][:, :]).then_inc(s_oc, 1)

        @block.vector
        def _(dve):
            nc.vector.memset(eps_sb[:, :], LN_EPS).then_inc(s_set, 1)
            nc.vector.memset(ones[:, :], 1.0).then_inc(s_set, 1)
            dve.wait_ge(s_set, 2)
            dve.wait_ge(s_const, 16 * CONSTS)
            nc.vector.tensor_scalar(bg_sb[:, :], bg_sb[:, :], -1.0, None, ALU.mult).then_inc(s_set, 1)
            LV = 3 * KD + 5
            with dve.Fori(0, NB // 2) as r:
                for i in range(2):
                    b = 2 * r + i
                    link = linker(dve, s_lv, b * LV)
                    for c in range(2):
                        dve.wait_ge(s_pk, b * 2 + c + 1)
                        nc.vector.tensor_scalar(kneg[c][:, :], pa[c][:, :], 0.0, None, ALU.min).then_inc(s_kn, 1)
                    for c in range(2):
                        dve.wait_ge(s_ke, b * 2 + c + 1)
                        nc.vector.scalar_tensor_tensor(k_sb[:, c, :], pa[c][:, :], 0.0, kneg[c][:, :], ALU.max, ALU.add).then_inc(s_k, 1)
                    for k in range(KD + 1):
                        if k < KD:
                            dve.wait_ge(s_pq, b * KD + k + 1)
                            dve.wait_ge(s_q, b * KD + max(k - 1, 0))
                            nc.vector.tensor_scalar(qneg[k % 2][:, :], pa[k % 2][:, 0:L], 0.0, None, ALU.min).then_inc(s_qn, 1)
                        if k >= 1:
                            j = k - 1
                            dve.wait_ge(s_qe, b * KD + j + 1)
                            nc.vector.scalar_tensor_tensor(q_sb[:, j, :], pa[j % 2][:, 0:L], 0.0, qneg[j % 2][:, :], ALU.max, ALU.add).then_inc(s_q, 1)
                    dve.wait_ge(s_ps, b + 1)
                    for j in range(KD):
                        nc.vector.tensor_tensor(kv_sb[:, j, :], ps[0][:, j * P:(j + 1) * P], mask_sb[:, :], ALU.mult).then_inc(s_kv, 1)
                        nc.vector.tensor_tensor(ks_sb[:, j, :], ps[1][:, j * P:(j + 1) * P], mask_sb[:, :], ALU.mult).then_inc(s_kv, 1)
                    for j in range(KD):
                        dve.wait_ge(s_pa, b * KD + j + 1)
                        n = pb[j % 2]
                        link(nc.vector.tensor_scalar(den[:, j, :], n[:, L:2 * L], EPS, None, ALU.add))
                        dve.wait_ge(s_g, b * KD + j + 1)
                        link(nc.vector.scalar_tensor_tensor(den[:, j, :], g_sb[:, j, :], 1.0, den[:, j, :], ALU.add, ALU.mult))
                        link(nc.vector.reciprocal(den[:, j, :], den[:, j, :]))
                        nc.vector.tensor_tensor(ag[:, j, :], n[:, 0:L], den[:, j, :], ALU.mult).then_inc(s_ag, 1)
                    dve.wait_ge(s_in[i], r * 48 + 48)
                    for c in range(2):
                        x = xt[i][:, c, :]
                        dve.wait_ge(s_o, b * 2 + c + 1)
                        link(nc.vector.tensor_tensor(x, x, po[c][:, :], ALU.add))
                        link(nc.vector.bn_stats(st[:, c, :], x))
                        alone(dve, tick_dve)
                        nc.vector.bn_aggr(mv[:, c, :], st[:, c, :]).then_inc(s_var, 1)
                    dve.wait_ge(s_sd, b + 1)
                    link(nc.vector.reciprocal(sd[:, :], sd[:, :]))
                    dve.wait_ge(s_out, b * 48)
                    for c in range(2):
                        nc.vector.tensor_scalar(o_sb[:, c, :], xt[i][:, c, :], mv[:, c, 0:1], sd[:, c:c + 1], ALU.subtract, ALU.mult).then_inc(s_ln, 1)
                    assert link.count[0] == LV

        @block.tensor
        def _(pe):
            pe.wait_ge(s_const, 16 * CONSTS)
            pe.wait_ge(s_set, 2)
            with pe.Fori(0, NB // 2) as r:
                for i in range(2):
                    b = 2 * r + i
                    pe.wait_ge(s_in[i], r * 48 + 48)
                    pe.wait_ge(s_q, b * KD)
                    for c in range(2):
                        for k in range(KD):
                            ins = nc.tensor.matmul(pa[c][:, :], cf[i][:, k, c * P:(c + 1) * P], wkv[:, k, 0:D], start=(k == 0), stop=(k == KD - 1))
                        ins.then_inc(s_pk, 1)
                    pe.wait_ge(s_ag, b * KD)
                    for c in range(2):
                        pe.wait_ge(s_k, b * 2 + c + 1)
                        for k in range(KD):
                            ins = nc.tensor.matmul(pa[c][:, :], cf[i][:, k, c * P:(c + 1) * P], wkv[:, k, D:2 * D], start=(k == 0), stop=(k == KD - 1))
                        ins.then_inc(s_pv, 1)
                    for j in range(KD):
                        pe.wait_ge(s_g, b * KD + max(j - 1, 0))
                        for k in range(KD):
                            ins = nc.tensor.matmul(pb[j % 2][:, 0:L], wg[:, k, j * P:(j + 1) * P], xf[i][:, k, :], start=(k == 0), stop=(k == KD - 1))
                        ins.then_inc(s_pg, 1)
                        if j < 2:
                            pe.wait_ge(s_v, b * 2 + j + 1)
                        else:
                            pe.wait_ge(s_q, b * KD + j - 1)
                        for k in range(KD):
                            ins = nc.tensor.matmul(pa[j % 2][:, 0:L], wq[:, k, j * P:(j + 1) * P], xf[i][:, k, :], start=(k == 0), stop=(k == KD - 1))
                        ins.then_inc(s_pq, 1)
                    pe.wait_ge(s_oc, b * 2)
                    for j in range(KD):
                        g = slice(j * P, (j + 1) * P)
                        for c in range(2):
                            nc.tensor.matmul(ps[0][:, g], k_sb[:, c, g], v_sb[:, c, g], start=(c == 0), stop=(c == 1))
                        for c in range(2):
                            ins = nc.tensor.matmul(ps[1][:, g], k_sb[:, c, g], ones[:, :], start=(c == 0), stop=(c == 1))
                    ins.then_inc(s_ps, 1)
                    pe.wait_ge(s_kv, (b + 1) * 2 * KD)
                    pe.wait_ge(s_q, b * KD + KD)
                    pe.wait_ge(s_g, b * KD + KD)
                    for j in range(KD):
                        pe.wait_ge(s_ag, b * KD + max(j - 1, 0))
                        nc.tensor.matmul(pb[j % 2][:, 0:L], kv_sb[:, j, :], q_sb[:, j, :], start=True, stop=True)
                        nc.tensor.matmul(pb[j % 2][:, L:2 * L], ks_sb[:, j, :], q_sb[:, j, :], start=True, stop=True).then_inc(s_pa, 1)
                    pe.wait_ge(s_ag, b * KD + KD)
                    pe.wait_ge(s_var, 2 * b)
                    for c in range(2):
                        for k in range(KD):
                            ins = nc.tensor.matmul(po[c][:, :], ag[:, k, c * P:(c + 1) * P], wo[:, k, :], start=(k == 0), stop=(k == KD - 1))
                        ins.then_inc(s_o, 1)
                    for c in range(2):
                        pe.wait_ge(s_ln, b * 2 + c + 1)
                        for k in range(KD):
                            ins = nc.tensor.transpose(ps[c][:, k * P:(k + 1) * P], o_sb[:, c, k * P:(k + 1) * P], ident_sb[:, :])
                        ins.then_inc(s_T, 1)


EX, TOP, SEL, HID = 4, 2, 512, 2048
FAR = 1 << 20


def moe1_route(nc, x_tok, x_feat, w_router, b_router, ident, before, ramp, scores, x_rows, places, weights):
    with ExitStack() as phase:
        m = Space(nc, "f1", phase)
        ident_sb, before_sb, ramp_sb = m.sb("ident", [P, P]), m.sb("before", [P, P]), m.sb("ramp", [P, EX])
        xf, xt = m.sb("xf", [P, KD, T]), m.sb("xt", [P, TILES, D])
        rw, rb = m.sb("rw", [P, KD, EX]), m.sb("rb", [P, EX])
        lg = m.sb("lg", [P, TILES, 8])
        top, idx, idf = m.sb("top", [P, TILES, 8]), m.sb("idx", [P, TILES, 8], U32), m.sb("idf", [P, TILES, TOP])
        pr = m.sb("pr", [P, TILES, TOP])
        e_sb, d_sb = m.sb("e", [P, TILES]), m.sb("d", [P, TILES])
        hot = m.sb("hot", [P, TILES, TOP, EX])
        wt = m.sb("wt", [P, TILES, TOP, EX])
        sc = m.sb("sc", [P, EX, TILES])
        scT = m.sb("scT", [EX * TILES, P])
        every = m.sb("every", [P, EX, T])
        cmp_ = [m.sb(f"cmp{i}", [P, T]) for i in range(2)]
        cnt = m.sb("cnt", [P, EX, TILES, 3])
        rank = m.sb("rank", [P, EX, TILES])
        rk, ok, far = m.sb("rk", [P, TILES, TOP]), m.sb("ok", [P, TILES, TOP]), m.sb("far", [P, TILES, TOP])
        pl = m.sb("pl", [P, TILES, TOP], U32)
        wk = m.sb("wk", [P, TILES, TOP])
        pL, pS = m.ps("pL"), m.ps("pS")
        s_const, s_x, s_xt, s_set, s_lv, s_log, s_d, s_e, s_sc, s_T, s_scT, s_scd, s_every, s_pl, s_scat, s_out, s_cmp = (
            m.sem(n) for n in "const x xt set lv log d e sc T scT scd every pl scat out cmp".split())
        block = phase.enter_context(nc.Block())

        @block.sync
        def _(sp):
            for dst, src in ((ident_sb[:, :], ident), (before_sb[:, :], before), (ramp_sb[:, :], ramp[0:EX].partition_broadcast(P)),
                             (rw[:, :, :], w_router.rearrange("(k p) e -> p k e", p=P)), (rb[:, :], b_router.partition_broadcast(P))):
                sp.dma_start(dst, src).then_inc(s_const, 16)
            sp.dma_start(xf[:, :, :], x_feat.rearrange("k p t -> p k t")).then_inc(s_x, 16)
            sp.dma_start(xt[:, :, :], x_tok.rearrange("(c p) n -> p c n", p=P)).then_inc(s_xt, 16)
            sp.wait_ge(s_scT, 1)
            sp.dma_start(scores.rearrange("e (c p) -> (e c) p", p=P), scT[:, :]).then_inc(s_scd, 16)
            sp.wait_ge(s_scd, 16)
            sp.dma_start(every[:, :, :], scores.partition_broadcast(P)).then_inc(s_every, 16)
            sp.wait_ge(s_pl, 2)
            sp.dma_start(places.rearrange("(c p) k -> p c k", p=P), pl[:, :, :], allow_slow_non_contiguous=True).then_inc(s_out, 16)
            sp.dma_start(weights.rearrange("(c p) k -> p c k", p=P), wk[:, :, :], allow_slow_non_contiguous=True).then_inc(s_out, 16)
            sp.wait_ge(s_out, 32)

        @block.gpsimd
        def _(pool):
            pool.wait_ge(s_xt, 16)
            pool.wait_ge(s_pl, 2)
            for c in range(TILES):
                for k in range(TOP):
                    pool.indirect_dma_start(x_rows, bass.IndirectOffsetOnAxis(ap=pl[:, c, k:k + 1], axis=0), xt[:, c, :], None,
                                            bounds_check=EX * SEL - 1, oob_is_err=False).then_inc(s_scat, 16)
            pool.wait_ge(s_scat, TILES * TOP * 16)

        @block.scalar
        def _(act):
            act.wait_ge(s_d, 1)
            nc.scalar.activation(e_sb[:, :], d_sb[:, :], ACT.Exp).then_inc(s_e, 1)

        @block.vector
        def _(dve):
            link = linker(dve, s_lv)
            link(nc.vector.memset(lg[:, :, :], -3.0e38))
            dve.wait_ge(s_const, 80)
            dve.wait_ge(s_log, 1)
            link(nc.vector.tensor_tensor(lg[:, :, 0:EX], pL[:, 0:TILES * EX].rearrange("p (c e) -> p c e", e=EX),
                                         rb[:, :].unsqueeze(1).to_broadcast([P, TILES, EX]), ALU.add))
            for c in range(TILES):
                ins = nc.vector.max(top[:, c, :], lg[:, c, :])
            link(ins)
            for c in range(TILES):
                ins = nc.vector.max_index(idx[:, c, :], top[:, c, :], lg[:, c, :])
            link(ins)
            nc.vector.tensor_tensor(d_sb[:, :], top[:, :, 1], top[:, :, 0], ALU.subtract).then_inc(s_d, 1)
            link(nc.vector.tensor_copy(idf[:, :, :], idx[:, :, 0:TOP]))
            link(nc.vector.tensor_tensor(hot[:, :, :, :].rearrange("p c k e -> p (c k) e"), ramp_sb[:, :].unsqueeze(1).to_broadcast([P, TILES * TOP, EX]),
                                         idf[:, :, :].rearrange("p c k -> p (c k)").unsqueeze(2).to_broadcast([P, TILES * TOP, EX]), ALU.is_equal))
            dve.wait_ge(s_e, 1)
            link(nc.vector.tensor_scalar(pr[:, :, 0], e_sb[:, :], 1.0, None, ALU.add))
            link(nc.vector.reciprocal(pr[:, :, 0], pr[:, :, 0]))
            link(nc.vector.tensor_tensor(pr[:, :, 1], pr[:, :, 0], e_sb[:, :], ALU.mult))
            link(nc.vector.tensor_tensor(wt[:, :, :, :].rearrange("p c k e -> p (c k) e"), hot[:, :, :, :].rearrange("p c k e -> p (c k) e"),
                                         pr[:, :, :].rearrange("p c k -> p (c k)").unsqueeze(2).to_broadcast([P, TILES * TOP, EX]), ALU.mult))
            link(nc.vector.tensor_tensor(sc[:, :, :], hot[:, :, 0, :].rearrange("p c e -> p e c"), hot[:, :, 1, :].rearrange("p c e -> p e c"), ALU.add))
            link(nc.vector.tensor_scalar(sc[:, :, :], sc[:, :, :], -1.0, None, ALU.add))
            link(nc.vector.tensor_tensor(sc[:, :, :], sc[:, :, :], wt[:, :, 0, :].rearrange("p c e -> p e c"), ALU.add))
            nc.vector.tensor_tensor(sc[:, :, :], sc[:, :, :], wt[:, :, 1, :].rearrange("p c e -> p e c"), ALU.add).then_inc(s_sc, 1)
            dve.wait_ge(s_sc, 1)
            dve.wait_ge(s_T, 1)
            nc.vector.tensor_copy(scT[:, :], pS[0:EX * TILES, 0:P]).then_inc(s_scT, 1)
            link(nc.vector.memset(cnt[:, :, :, :], 0.0))
            dve.wait_ge(s_every, 16)
            n = 0
            for e in range(EX):
                for c in range(TILES):
                    own = sc[:, e, c:c + 1]
                    at = slice(c * P, (c + 1) * P)
                    buf = cmp_[n % 2]
                    n += 1
                    if c:
                        nc.vector.tensor_scalar(buf[:, 0:c * P], every[:, e, 0:c * P], own, None, ALU.is_ge, ALU.add,
                                                accum_out=cnt[:, e, c, 0:1]).then_inc(s_cmp, 1)
                    nc.vector.tensor_scalar(buf[:, c * P:T], every[:, e, c * P:T], own, None, ALU.is_gt, ALU.add,
                                            accum_out=cnt[:, e, c, 1:2]).then_inc(s_cmp, 1)
                    done = n * 2 - (e + 1)
                    dve.wait_ge(s_cmp, done + (n - 1))
                    nc.vector.scalar_tensor_tensor(buf[:, at], every[:, e, at], own, before_sb[:, :], ALU.is_equal, ALU.mult,
                                                   accum_out=cnt[:, e, c, 2:3]).then_inc(s_cmp, 1)
            dve.wait_ge(s_cmp, EX * (3 * TILES - 1))
            link(nc.vector.tensor_reduce(rank[:, :, :].rearrange("p e c -> p (e c)"), cnt[:, :, :, :].rearrange("p e c n -> p (e c) n"), AX.X, ALU.add))
            for k in range(TOP):
                link(nc.vector.tensor_tensor(wt[:, :, k, :], hot[:, :, k, :], rank[:, :, :].rearrange("p e c -> p c e"), ALU.mult))
            link(nc.vector.tensor_reduce(rk[:, :, :].rearrange("p c k -> p (c k)"), wt[:, :, :, :].rearrange("p c k e -> p (c k) e"), AX.X, ALU.add))
            link(nc.vector.tensor_scalar(ok[:, :, :], rk[:, :, :], float(SEL), None, ALU.is_lt))
            link(nc.vector.tensor_scalar(far[:, :, :], ok[:, :, :], -float(FAR), float(FAR), ALU.mult, ALU.add))
            link(nc.vector.scalar_tensor_tensor(rk[:, :, :], idf[:, :, :], float(SEL), rk[:, :, :], ALU.mult, ALU.add))
            nc.vector.tensor_tensor(pl[:, :, :], rk[:, :, :], far[:, :, :], ALU.add).then_inc(s_pl, 1)
            nc.vector.tensor_tensor(wk[:, :, :], pr[:, :, :], ok[:, :, :], ALU.mult).then_inc(s_pl, 1)

        @block.tensor
        def _(pe):
            pe.wait_ge(s_const, 80)
            pe.wait_ge(s_x, 16)
            for c in range(TILES):
                for k in range(KD):
                    ins = nc.tensor.matmul(pL[:, c * EX:(c + 1) * EX], xf[:, k, c * P:(c + 1) * P], rw[:, k, :], start=(k == 0), stop=(k == KD - 1))
            ins.then_inc(s_log, 1)
            pe.wait_ge(s_sc, 1)
            nc.tensor.transpose(pS[0:EX * TILES, 0:P], sc[:, :, :].rearrange("p e c -> p (e c)"), ident_sb[:, :]).then_inc(s_T, 1)


def moe1_experts(nc, x_rows, w1, w2, ident, y_rows):
    HB, RT = HID // P, SEL // P
    with ExitStack() as phase:
        m = Space(nc, "f2", phase)
        ident_sb = m.sb("ident", [P, P])
        w1_sb, w2_sb = m.sb("w1", [P, KD, HID]), m.sb("w2", [P, HB, D])
        x_sb = m.sb("x", [P, RT, D])
        xT = m.sb("xT", [P, KD, SEL])
        hT = m.sb("hT", [P, HB, SEL])
        y_sb = m.sb("y", [P, RT, D])
        pT = [m.ps(f"pT{i}") for i in range(2)]
        ph = [m.ps(f"ph{i}") for i in range(3)]
        py = [m.ps(f"py{i}") for i in range(2)]
        s_const, s_w1, s_w2, s_x, s_T, s_xT, s_h, s_g, s_y, s_ye, s_out = (m.sem(n) for n in "const w1 w2 x T xT h g y ye out".split())
        block = phase.enter_context(nc.Block())

        @block.sync
        def _(sp):
            sp.dma_start(ident_sb[:, :], ident).then_inc(s_const, 16)
            with sp.Fori(0, EX) as e:
                sp.wait_ge(s_T, e * KD)
                sp.dma_start(x_sb[:, :, :], x_rows[bass.ds(e * SEL, SEL), :].rearrange("(c p) n -> p c n", p=P)).then_inc(s_x, 16)
                sp.wait_ge(s_h, e * HB)
                sp.dma_start(w1_sb[:, :, :], w1[bass.ds(e, 1), :, :].rearrange("e (k p) n -> p (e k) n", p=P)).then_inc(s_w1, 16)
                sp.wait_ge(s_y, e * RT)
                sp.dma_start(w2_sb[:, :, :], w2[bass.ds(e, 1), :, :].rearrange("e (k p) n -> p (e k) n", p=P)).then_inc(s_w2, 16)
                sp.wait_ge(s_ye, e * RT + RT)
                sp.dma_start(y_rows[bass.ds(e * SEL, SEL), :].rearrange("(c p) n -> p c n", p=P), y_sb[:, :, :]).then_inc(s_out, 16)
            sp.wait_ge(s_out, EX * 16)

        @block.scalar
        def _(act):
            with act.Fori(0, EX) as e:
                act.wait_ge(s_y, e * RT)
                for n in range(HB):
                    act.wait_ge(s_h, e * HB + n + 1)
                    nc.scalar.activation(hT[:, n, :], ph[n % 3][:, :], ACT.Gelu).then_inc(s_g, 1)

        @block.vector
        def _(dve):
            with dve.Fori(0, EX) as e:
                dve.wait_ge(s_h, e * HB)
                for c in range(RT):
                    dve.wait_ge(s_T, e * RT + c + 1)
                    nc.vector.tensor_copy(xT[:, :, c * P:(c + 1) * P], pT[c % 2][:, :].rearrange("p (k t) -> p k t", k=KD)).then_inc(s_xT, 1)
                dve.wait_ge(s_out, e * 16)
                for c in range(RT):
                    dve.wait_ge(s_y, e * RT + c + 1)
                    nc.vector.tensor_copy(y_sb[:, c, :], py[c % 2][:, :]).then_inc(s_ye, 1)

        @block.tensor
        def _(pe):
            pe.wait_ge(s_const, 16)
            with pe.Fori(0, EX) as e:
                pe.wait_ge(s_x, e * 16 + 16)
                for c in range(RT):
                    pe.wait_ge(s_xT, e * RT + max(c - 1, 0))
                    for k in range(KD):
                        ins = nc.tensor.transpose(pT[c % 2][:, k * P:(k + 1) * P], x_sb[:, c, k * P:(k + 1) * P], ident_sb[:, :])
                    ins.then_inc(s_T, 1)
                pe.wait_ge(s_xT, e * RT + RT)
                pe.wait_ge(s_w1, e * 16 + 16)
                for n in range(HB):
                    pe.wait_ge(s_g, e * HB + max(n - 2, 0))
                    for k in range(KD):
                        ins = nc.tensor.matmul(ph[n % 3][:, :], w1_sb[:, k, n * P:(n + 1) * P], xT[:, k, :], start=(k == 0), stop=(k == KD - 1))
                    ins.then_inc(s_h, 1)
                pe.wait_ge(s_w2, e * 16 + 16)
                pe.wait_ge(s_g, e * HB + HB)
                for c in range(RT):
                    pe.wait_ge(s_ye, e * RT + max(c - 1, 0))
                    for n in range(HB):
                        ins = nc.tensor.matmul(py[c % 2][:, :], hT[:, n, c * P:(c + 1) * P], w2_sb[:, n, :], start=(n == 0), stop=(n == HB - 1))
                    ins.then_inc(s_y, 1)


def decoder(nc, a, out):
    def scratch(name, *shape, dt=F32):
        return nc.dram_tensor(name, list(shape), dt).ap()

    def both(name):
        return scratch(name + "_tok", T, D), scratch(name + "_feat", KD, P, T)

    u_feat, u_tok, z_tok, y_tok = scratch("u0_feat", 12, P, T), scratch("u0_tok", T, 1536), scratch("z0_tok", T, 1536), scratch("y0_tok", T, 1536)
    slots, slots_y = scratch("slots", SLOTS, D), scratch("slots_y", SLOTS, D)
    rows, rows_y = scratch("rows", EX * SEL, D), scratch("rows_y", EX * SEL, D)
    x1_tok, x1_feat = both("x1")
    ssm0_project(nc, a["x"], a["ident"], a["norm_w"], a["w_in0"], a["b_in0"], a["conv_w0"], a["conv_b0"], u_feat, u_tok, z_tok, (slots, rows))
    ssm0_scan(nc, u_feat, u_tok, y_tok, a["ident"], a["w_bc"], a["b_bc"], a["w_dt0"], a["head_mean"], a["head_pair"], a["b_dt0"],
              a["a_log0"], a["l2_alpha"], a["l2_beta"], a["ema"])
    ssm0_out(nc, a["x"], y_tok, z_tok, a["w_out0"], a["b_out0"], a["gate"], a["ident"], x1_tok, x1_feat)

    r_feat = scratch("r_feat", KD, P, T)
    x2_tok, x2_feat = both("x2")
    long_conv(nc, x1_feat, a["ctx_turned"], a["taps"], a["skip0"], a["exchange"], r_feat)
    norm_from_feat(nc, "b2", r_feat, a["ident"], x2_tok, x2_feat)

    places0, weights0 = scratch("places0", T, K_, dt=U32), scratch("weights0", T, K_)
    x3_tok, x3_feat = both("x3")
    moe0_route(nc, x2_tok, x2_feat, a["router0"], a["ident"], a["upper"], a["ramp"], slots, places0, weights0)
    moe0_experts(nc, slots, a["w_gu"], a["w_down"], a["ident"], slots_y)
    gather_mix_norm(nc, "c3", K_, slots_y, SLOTS, x2_tok, places0, weights0, a["ident"], x3_tok, x3_feat)

    u1, z1, dt1, bc1 = scratch("u1", F1, P, T), scratch("z1", F1, P, T), scratch("dt1", F1, P, T), scratch("bc1", 2 * N1, T)
    x4_tok, x4_feat = both("x4")
    ssm1_project(nc, x3_feat, a["w_in1"], a["conv_w1"], a["conv_b1"], a["w_x1"], a["w_dt1"], a["b_dt1"], u1, z1, dt1, bc1)
    ssm1_scan(nc, x3_tok, u1, z1, dt1, bc1, a["a_log1"], a["skip1"], a["w_out1"], a["ident"], x4_tok, x4_feat)

    x5_tok, x5_feat = both("x5")
    linear_attention(nc, x4_tok, x4_feat, a["ctx_feat"], a["w_q"], a["w_g"], a["b_g"], a["w_kv"], a["w_o"], a["ident"], a["heads_mask"], x5_tok, x5_feat)

    scores, places1, weights1 = scratch("scores", EX, T), scratch("places1", T, TOP, dt=U32), scratch("weights1", T, TOP)
    moe1_route(nc, x5_tok, x5_feat, a["router1"], a["b_router1"], a["ident"], a["lower"], a["ramp"], scores, rows, places1, weights1)
    moe1_experts(nc, rows, a["w1"], a["w2"], a["ident"], rows_y)
    gather_mix_norm(nc, "f3", TOP, rows_y, EX * SEL, x5_tok, places1, weights1, a["ident"], out, None)


def laid_out(i):
    import numpy as np
    H0, S0, DI0 = 24, 64, 1536
    by_feature = lambda v: v.reshape(T, D).T.reshape(KD, P, T)
    xp_w, xp_b = i["L0_attn_x_proj_w"].reshape(H0, 1 + 2 * S0, DI0), i["L0_attn_x_proj_b"].reshape(H0, 1 + 2 * S0)
    pairs = lambda w: w.reshape(H0 // 2, P, DI0 // P, P).transpose(0, 3, 2, 1)
    taps = np.zeros((32, P - 1 + D), np.float32)
    taps[:, P - 1:] = i["L0_xattn_ssm_kernel"]
    head_mean = np.zeros((DI0, H0), np.float32)
    for h in range(H0):
        head_mean[h * S0:(h + 1) * S0, h] = 1 / S0
    head_pair = np.zeros((P, 2), np.float32)
    head_pair[:S0, 0] = head_pair[S0:, 1] = 1
    heads_mask = np.zeros((P, P), np.float32)
    for h in range(4):
        heads_mask[h * 32:(h + 1) * 32, h * 32:(h + 1) * 32] = 1
    ident = np.eye(P, dtype=np.float32)
    upper = np.triu(np.ones((P, P), np.float32), 1)
    L0, L1 = (lambda n: i["L0_" + n]), (lambda n: i["L1_" + n])
    return {
        "ident": ident, "exchange": ident[::-1], "upper": upper, "lower": upper.T, "ramp": np.arange(E_, dtype=np.float32),
        "head_mean": head_mean, "head_pair": head_pair, "heads_mask": heads_mask,
        "x": i["x"].reshape(T, D), "ctx_feat": by_feature(i["ctx_2048"]), "ctx_turned": by_feature(i["ctx_2048"])[:, ::-1],
        "norm_w": L0("attn_norm_w"), "w_in0": L0("attn_in_proj_w").T, "b_in0": L0("attn_in_proj_b"),
        "conv_w0": L0("attn_conv_w").reshape(DI0, 4), "conv_b0": L0("attn_conv_b"),
        "w_bc": np.concatenate([pairs(xp_w[:, 1:1 + S0]), pairs(xp_w[:, 1 + S0:])], -1),
        "b_bc": np.stack([xp_b[:, 1:1 + S0].reshape(H0 // 2, P), xp_b[:, 1 + S0:].reshape(H0 // 2, P)], -1),
        "w_dt0": xp_w[:, 0].T, "b_dt0": xp_b[:, 0], "a_log0": L0("attn_A_log"), "l2_alpha": L0("attn_log2_alpha_base"),
        "l2_beta": L0("attn_log2_beta"), "ema": L0("attn_surprise_ema"), "w_out0": L0("attn_out_proj_w").T, "b_out0": L0("attn_out_proj_b"),
        "gate": L0("attn_res_gate"), "taps": taps, "skip0": L0("xattn_D"), "router0": L0("ffn_router_w").T,
        "w_gu": np.concatenate([L0("ffn_w_gate"), L0("ffn_w_up")], -1).reshape(E_, KD, P, 2 * FF).transpose(0, 2, 1, 3), "w_down": L0("ffn_w_down"),
        "w_in1": L1("attn_W_in").T, "conv_w1": L1("attn_conv_w"), "conv_b1": L1("attn_conv_b"), "w_x1": L1("attn_W_x").T, "w_dt1": L1("attn_W_dt").T,
        "b_dt1": L1("attn_b_dt"), "a_log1": L1("attn_A_log"), "skip1": L1("attn_D"), "w_out1": L1("attn_W_out").T,
        "w_q": L1("xattn_Wq").T, "w_g": L1("xattn_Wg").T, "b_g": L1("xattn_bg"), "w_kv": L1("xattn_Wkv").T, "w_o": L1("xattn_Wo").T,
        "router1": L1("ffn_Wg"), "b_router1": L1("ffn_bg"), "w1": L1("ffn_W1"), "w2": L1("ffn_W2"),
    }


def kernel(**inputs):
    import numpy as np
    import concourse.bacc as bacc
    from concourse.bass_utils import run_bass_kernel_spmd

    nc = bacc.Bacc("TRN2", target_bir_lowering=False, num_devices=1)
    arrays = {n: np.ascontiguousarray(v) for n, v in laid_out({n: np.asarray(v) for n, v in inputs.items()}).items()}
    aps = {n: nc.dram_tensor(n, v.shape, mybir.dt.from_np(v.dtype), kind="ExternalInput").ap() for n, v in arrays.items()}
    out = nc.dram_tensor("out", (T, D), F32, kind="ExternalOutput").ap()
    decoder(nc, aps, out)
    result = run_bass_kernel_spmd(nc, [arrays], core_ids=[0])
    return result.results[0]["out"].reshape(NB, L, D)
```

```python
from contextlib import ExitStack

import concourse.bass as bass
from concourse import mybir
from concourse.alu_op_type import AluOpType as ALU

ACT = mybir.ActivationFunctionType
AX = mybir.AxisListType
F32 = mybir.dt.float32
U32 = mybir.dt.uint32
P = 128
NB, L, D = 8, 256, 512
T = NB * L
KD = D // P
TILES = T // P
BANK = 512


class Space:

    def __init__(self, nc, name, phase):
        self.nc, self.name, self.phase, self.sems = nc, name, phase, []
        phase.callback(self.clear)

    def sb(self, name, shape, dt=F32):
        return self.phase.enter_context(self.nc.sbuf_tensor(f"{self.name}_{name}", shape, dt))

    def ps(self, name, shape=(P, BANK), dt=F32):
        return self.phase.enter_context(self.nc.psum_tensor(f"{self.name}_{name}", list(shape), dt))

    def sem(self, name):
        self.sems.append(self.nc.alloc_semaphore(name=f"{self.name}_{name}"))
        return self.sems[-1]

    def clear(self):
        self.nc.clear_and_free_semaphores(self.sems)
        self.nc.all_engine_barrier()


def alone(eng, tick):
    eng.sem_inc(tick, 1)


def linker(eng, sem, base=0):
    count = [0]

    def link(ins):
        count[0] += 1
        ins.then_inc(sem, 1)
        eng.wait_ge(sem, base + count[0])
    link.count = count
    return link


def ssm0_project(nc, x, ident, norm_w, w_in, b_in, conv_w, conv_b, u_feat, u_tok, z_tok, to_clear=()):
    DI = 1536
    F = DI // P
    EPS = 1.1920928955078125e-07
    LINKS_V, LINKS_A = 1 + 3 * F, 2
    with ExitStack() as phase:
        m = Space(nc, "a1", phase)
        w_sb = m.sb("w", [P, KD, 2 * DI])
        ident_sb = m.sb("ident", [P, P])
        nw_sb = m.sb("nw", [P, KD])
        bx_sb = m.sb("bx", [P, F])
        bz_sb = m.sb("bz", [P, DI])
        cw_sb = m.sb("cw", [P, F, 4])
        cb_sb = m.sb("cb", [P, F])
        eps_sb = m.sb("eps", [P, 1])
        x_sb = m.sb("x", [P, 2, D])
        sq_sb = m.sb("sq", [P, D])
        ss_sb = m.sb("ss", [P, 2])
        rt_sb = m.sb("rt", [P, 2])
        xn_sb = m.sb("xn", [P, 2, D])
        xnT_sb = m.sb("xnT", [P, KD, L])
        xpad = [m.sb(f"xpad{i}", [P, 3 + L]) for i in range(2)]
        acc = [m.sb(f"acc{i}", [P, L]) for i in range(2)]
        u_sb = m.sb("u", [P, F, L])
        ut_sb = m.sb("ut", [P, 2, DI])
        zb = [m.sb(f"zb{i}", [P, BANK]) for i in range(2)]
        z_sb = m.sb("z", [P, 2, DI])
        zeros = m.sb("zeros", [P, 4, D])
        pT = m.ps("pT", (P, 2, BANK))
        px = [m.ps(f"px{i}") for i in range(2)]
        pz = [m.ps(f"pz{i}") for i in range(2)]
        pu = [m.ps(f"pu{i}") for i in range(2)]
        s_const, s_wload, s_set, s_x = m.sem("const"), m.sem("wload"), m.sem("set"), m.sem("x")
        s_ss, s_root, s_xn, s_T, s_xnT = m.sem("ss"), m.sem("root"), m.sem("xn"), m.sem("T"), m.sem("xnT")
        s_px, s_xpad, s_conv, s_u = m.sem("px"), m.sem("xpad"), m.sem("conv"), m.sem("u")
        s_pz, s_zb, s_z = m.sem("pz"), m.sem("zb"), m.sem("z")
        s_pu, s_ut = m.sem("pu"), m.sem("ut")
        s_out, s_lv, s_la, s_zero, s_clear = m.sem("out"), m.sem("lv"), m.sem("la"), m.sem("zero"), m.sem("clear")
        tick_sp = m.sem("tick_sp")
        block = phase.enter_context(nc.Block())

        @block.sync
        def _(sp):
            for dst, src in ((ident_sb[:, :], ident), (nw_sb[:, :], norm_w.rearrange("(k p) -> p k", p=P)),
                             (bx_sb[:, :], b_in[0:DI].rearrange("(k p) -> p k", p=P)),
                             (bz_sb[:, :], b_in[DI:2 * DI].partition_broadcast(P)),
                             (cw_sb[:, :, :], conv_w.rearrange("(k p) c -> p k c", p=P)),
                             (cb_sb[:, :], conv_b.rearrange("(k p) -> p k", p=P))):
                sp.dma_start(dst, src, allow_slow_non_contiguous=True).then_inc(s_const, 16)
            sp.dma_start(w_sb[:, :, :], w_in.rearrange("(k p) n -> p k n", p=P)).then_inc(s_wload, 16)
            with sp.Fori(0, NB) as b:
                sp.wait_ge(s_xn, b * 2)
                sp.dma_start(x_sb[:, :, :], x[bass.ds(b * L, L), :].rearrange("(c p) n -> p c n", p=P)).then_inc(s_x, 16)
                sp.wait_ge(s_u, b * F + F)
                alone(sp, tick_sp)
                sp.dma_start(u_feat[:, :, bass.ds(b * L, L)].rearrange("k p t -> p k t"), u_sb[:, :, :]).then_inc(s_out, 16)
                sp.wait_ge(s_z, b * 6 + 6)
                sp.dma_start(z_tok[bass.ds(b * L, L), :].rearrange("(c p) n -> p c n", p=P), z_sb[:, :, :]).then_inc(s_out, 16)
                sp.wait_ge(s_ut, b * 6 + 6)
                sp.dma_start(u_tok[bass.ds(b * L, L), :].rearrange("(c p) n -> p c n", p=P), ut_sb[:, :, :]).then_inc(s_out, 16)
            sp.wait_ge(s_out, NB * 48)

        @block.gpsimd
        def _(pool):
            pool.memset(zeros[:, :, :], 0.0).then_inc(s_zero, 1)
            pool.wait_ge(s_zero, 1)
            stores = 0
            for rows in to_clear:
                n = rows.shape[0] // (4 * P)
                with pool.Fori(0, n) as r:
                    pool.dma_start(rows[bass.ds(r * 4 * P, 4 * P), :].rearrange("(p c) n -> p c n", p=P), zeros[:, :, :]).then_inc(s_clear, 16)
                stores += n
            if stores:
                pool.wait_ge(s_clear, stores * 16)

        @block.scalar
        def _(act):
            act.wait_ge(s_const, 96)
            act.wait_ge(s_set, 3)
            with act.Fori(0, NB) as b:
                link = linker(act, s_la, b * LINKS_A)
                act.wait_ge(s_x, b * 16 + 16)
                for c in range(2):
                    link(nc.scalar.activation(sq_sb[:, :], x_sb[:, c, :], ACT.Square, accum_out=ss_sb[:, c:c + 1]))
                nc.scalar.activation(rt_sb[:, :], ss_sb[:, :], ACT.Sqrt, bias=eps_sb[:, :], scale=1.0 / D).then_inc(s_root, 1)
                assert link.count[0] == LINKS_A
                act.wait_ge(s_T, b + 1)
                for k in range(KD):
                    nc.scalar.activation(xnT_sb[:, k, :], pT[:, k // 2, (k % 2) * L:(k % 2 + 1) * L], ACT.Copy,
                                         scale=nw_sb[:, k:k + 1]).then_inc(s_xnT, 1)
                act.wait_ge(s_out, b * 48)
                for f in range(F + 1):
                    if f < F:
                        act.wait_ge(s_px, b * F + f + 1)
                        if f >= 2:
                            act.wait_ge(s_conv, b * F + f - 1)
                        nc.scalar.activation(xpad[f % 2][:, 3:3 + L], px[f % 2][:, 0:L], ACT.Identity,
                                             bias=bx_sb[:, f:f + 1]).then_inc(s_xpad, 1)
                    if f >= 1:
                        g = f - 1
                        act.wait_ge(s_conv, b * F + g + 1)
                        nc.scalar.activation(u_sb[:, g, :], acc[g % 2][:, :], ACT.Silu, bias=cb_sb[:, g:g + 1]).then_inc(s_u, 1)
                for n in range(6):
                    act.wait_ge(s_zb, b * 6 + n + 1)
                    nc.scalar.activation(z_sb[:, n // 3, (n % 3) * BANK:(n % 3 + 1) * BANK], zb[n % 2][:, :], ACT.Silu).then_inc(s_z, 1)

        @block.vector
        def _(dve):
            for i in range(2):
                nc.vector.memset(xpad[i][:, 0:3], 0.0).then_inc(s_set, 1)
            nc.vector.memset(eps_sb[:, :], EPS).then_inc(s_set, 1)
            dve.wait_ge(s_set, 3)
            dve.wait_ge(s_const, 96)
            with dve.Fori(0, NB) as b:
                link = linker(dve, s_lv, b * LINKS_V)
                dve.wait_ge(s_root, b + 1)
                link(nc.vector.reciprocal(ss_sb[:, :], rt_sb[:, :]))
                dve.wait_ge(s_x, b * 16 + 16)
                dve.wait_ge(s_T, b)
                for c in range(2):
                    nc.vector.tensor_scalar(xn_sb[:, c, :], x_sb[:, c, :], ss_sb[:, c:c + 1], None, ALU.mult).then_inc(s_xn, 1)
                for f in range(F):
                    a, xp = acc[f % 2], xpad[f % 2]
                    dve.wait_ge(s_xpad, b * F + f + 1)
                    if f >= 2:
                        dve.wait_ge(s_u, b * F + f - 1)
                    else:
                        dve.wait_ge(s_u, b * F)
                    link(nc.vector.tensor_scalar(a[:, :], xp[:, 3:3 + L], cw_sb[:, f, 3:4], None, ALU.mult))
                    for j in (2, 1):
                        link(nc.vector.scalar_tensor_tensor(a[:, :], xp[:, j:j + L], cw_sb[:, f, j:j + 1], a[:, :], ALU.mult, ALU.add))
                    ins = nc.vector.scalar_tensor_tensor(a[:, :], xp[:, 0:L], cw_sb[:, f, 0:1], a[:, :], ALU.mult, ALU.add)
                    ins.then_inc(s_conv, 1)
                for n in range(6):
                    dve.wait_ge(s_pz, b * 6 + n + 1)
                    if n >= 2:
                        dve.wait_ge(s_z, b * 6 + n - 1)
                    nc.vector.tensor_tensor(zb[n % 2][:, :], pz[n % 2][:, :], bz_sb[:, (n % 3) * BANK:(n % 3 + 1) * BANK], ALU.add).then_inc(s_zb, 1)
                dve.wait_ge(s_out, b * 48)
                for n in range(6):
                    dve.wait_ge(s_pu, b * 6 + n + 1)
                    nc.vector.tensor_copy(ut_sb[:, n // 3, (n % 3) * BANK:(n % 3 + 1) * BANK], pu[n % 2][:, :]).then_inc(s_ut, 1)
                LV = link.count[0]
            assert LV == 1 + 3 * F, LV

        @block.tensor
        def _(pe):
            pe.wait_ge(s_const, 96)
            pe.wait_ge(s_wload, 16)
            with pe.Fori(0, NB) as b:
                pe.wait_ge(s_xn, b * 2 + 2)
                pe.wait_ge(s_xnT, b * KD)
                for k in range(KD):
                    for c in range(2):
                        at = (k % 2) * L + c * P
                        ins = nc.tensor.transpose(pT[:, k // 2, at:at + P], xn_sb[:, c, k * P:(k + 1) * P], ident_sb[:, :])
                ins.then_inc(s_T, 1)
                pe.wait_ge(s_xnT, b * KD + KD)
                for f in range(F):
                    pe.wait_ge(s_xpad, b * F + max(f - 1, 0))
                    for k in range(KD):
                        ins = nc.tensor.matmul(px[f % 2][:, 0:L], w_sb[:, k, f * P:(f + 1) * P], xnT_sb[:, k, :],
                                               start=(k == 0), stop=(k == KD - 1))
                    ins.then_inc(s_px, 1)
                for n in range(6):
                    pe.wait_ge(s_zb, b * 6 + max(n - 1, 0))
                    c, j = n // 3, n % 3
                    for k in range(KD):
                        ins = nc.tensor.matmul(pz[n % 2][:, :], xnT_sb[:, k, c * P:(c + 1) * P],
                                               w_sb[:, k, DI + j * BANK:DI + (j + 1) * BANK], start=(k == 0), stop=(k == KD - 1))
                    ins.then_inc(s_pz, 1)
                pe.wait_ge(s_u, b * F + F)
                for n in range(6):
                    pe.wait_ge(s_ut, b * 6 + max(n - 1, 0))
                    c, j = n // 3, n % 3
                    for q in range(4):
                        ins = nc.tensor.transpose(pu[n % 2][:, q * P:(q + 1) * P], u_sb[:, j * 4 + q, c * P:(c + 1) * P], ident_sb[:, :])
                    ins.then_inc(s_pu, 1)


F32R = mybir.dt.float32r


def ssm0_scan(nc, u_feat, u_tok, y_tok, ident, w_bc, b_bc, w_dt, head_mean, head_pair, b_dt, a_log, l2_alpha, l2_beta, ema):
    H, S, F = 24, 64, 12
    PAIRS = H // 2
    LN2 = 0.6931471805599453
    HALVES = 2
    TH = T // HALVES
    NBH = NB // HALVES
    TT = TH // P
    NI = 2 * NBH
    BLK = TH // BANK
    NQ = 2 * BLK
    KC = 2
    UCH = BLK * F // KC
    UNITS = HALVES * PAIRS
    with ExitStack() as phase:
        m = Space(nc, "a2", phase)
        u_raw = [m.sb(f"uraw{i}", [P, KC, BANK]) for i in range(2)]
        u_hi, u_lo = (m.sb("u" + n, [P, F, TH], F32R) for n in ("hi", "lo"))
        w_raw = m.sb("wraw", [P, F, 2 * P])
        w_hi, w_lo = (m.sb("w" + n, [P, F, 2 * P], F32R) for n in ("hi", "lo"))
        bias_sb = [m.sb(f"bias{i}", [P, 2]) for i in range(2)]
        wdt_raw = m.sb("wdtraw", [P, F, 2 * H])
        wdt_hi, wdt_lo = (m.sb("wdt" + n, [P, F, 2 * H], F32R) for n in ("hi", "lo"))
        pair_sb = m.sb("pair", [P, 2])
        idz = m.sb("idz", [P, 2 * P])
        BT, CT = ([m.sb(f"{n}{i}", [P, TH]) for i in range(2)] for n in ("BT", "CT"))
        sq = [m.sb(f"sq{i}", [P, BANK]) for i in range(2)]
        ut_sb = [m.sb(f"ut{i}", [P, TT, P]) for i in range(2)]
        y_sb = m.sb("y", [P, TT, P])
        hv = m.sb("hv", [P, 5, H])
        gain_sb = m.sb("gain", [P, H, TT])
        t0, t1, t2 = (m.sb(f"t{i}", [P, H, TT]) for i in range(3))
        base_w, rest_w = m.sb("basew", [P, H, TT]), m.sb("restw", [P, H, TT])
        nrm, inv = m.sb("nrm", [P, 2, 2, TT]), m.sb("inv", [P, 2, 2, TT])
        al, cB, q0 = (m.sb(n, [P, 2, TT]) for n in ("al", "cB", "q0"))
        M = [m.sb(f"M{i}", [P, 3 * P]) for i in range(2)]
        W = [m.sb(f"W{i}", [P, 3 * P]) for i in range(2)]
        one_sb = m.sb("one", [P, 1])
        pB = [m.ps(f"pB{i}") for i in range(2)]
        pn, py = m.ps("pn"), m.ps("py")
        pa = [m.ps(f"pa{i}") for i in range(2)]
        pG = [m.ps(f"pG{i}") for i in range(2)]
        s_const, s_w, s_ut, s_out = (m.sem(n) for n in "const w ut out".split())
        s_u = [m.sem(f"ld{n}") for n in ("u0", "u1")]
        s_uh, s_ul, s_wh, s_wl, s_dth, s_dtl = (m.sem(n) for n in "uh ul wh wl dth dtl".split())
        s_dt, s_hv, s_ab, s_lv, s_la, s_va, s_av, s_set = (m.sem(n) for n in "dt hv ab lv la va av set".split())
        s_pB, s_bt, s_pn, s_root, s_arg, s_tanh, s_al = (m.sem(n) for n in "pB bt pn root arg tanh al".split())
        s_pa, s_M, s_G, s_W, s_y, s_ye = (m.sem(n) for n in "pa M G W y ye".split())
        tick_sp = m.sem("tick_sp")
        block = phase.enter_context(nc.Block())
        CONSTS = 9
        LV = 9
        LV_HALF, LV_ONCE = 8, 5
        LA_HALF = 3
        B_COLS, C_COLS = slice(0, P), slice(P, 2 * P)

        def schedule(eng, half_start, step):
            for half in range(HALVES):
                first = half * PAIRS
                step(half, first - 1 if half else None, first, first=True)
                half_start(half)
                with eng.Fori(0, (PAIRS - 2) // 2) as r:
                    for i in range(2):
                        step(half, first + 2 * r + i, first + 2 * r + i + 1, parity=(i + 1) % 2)
                step(half, first + PAIRS - 2, first + PAIRS - 1)
            step(half, UNITS - 1, None)

        def parities(nxt, cur, parity):
            if parity is None:
                parity = nxt % 2 if nxt is not None else (cur + 1) % 2
            return parity, 1 - parity

        @block.sync
        def _(sp):
            sp.dma_start(idz[:, 0:P], ident).then_inc(s_const, 16)
            sp.dma_start(pair_sb[:, :], head_pair).then_inc(s_const, 16)
            sp.dma_start(wdt_raw[:, :, 0:H], w_dt.rearrange("(k p) h -> p k h", p=P)).then_inc(s_const, 16)
            sp.dma_start(wdt_raw[:, :, H:2 * H], head_mean.rearrange("(k p) h -> p k h", p=P)).then_inc(s_const, 16)
            for n, v in enumerate((b_dt, a_log, l2_alpha, l2_beta, ema)):
                sp.dma_start(hv[:, n, :], v.partition_broadcast(P)).then_inc(s_const, 16)

            def weights(pair, nxt, parity):
                sp.dma_start(w_raw[:, :, :], w_bc[bass.ds(pair, 1), :, :, :].rearrange("a p k n -> (a p) k n")).then_inc(s_w, 16)
                sp.dma_start(bias_sb[parity][:, :], b_bc[bass.ds(pair, 1), :, :].rearrange("a p n -> (a p) n")).then_inc(s_w, 16)

            def step(half, cur, nxt, parity=None, first=False):
                into, at = parities(nxt, cur, parity)
                pair = None if nxt is None else nxt - half * PAIRS
                if nxt is not None:
                    if first and half == 0:
                        weights(0, nxt, into)
                    if cur is not None:
                        sp.wait_ge(s_y, cur * NI)
                        alone(sp, tick_sp)
                    sp.dma_start(ut_sb[into][:, :, :], u_tok[half * TH:(half + 1) * TH, bass.ds(pair * P, P)]
                                 .rearrange("(c p) n -> p c n", p=P)).then_inc(s_ut, 16)
                    sp.wait_ge(s_wl, nxt * 2 + 2)
                    alone(sp, tick_sp)
                    sp.wait_ge(s_bt, nxt * 2 * NQ)
                    if parity is not None or nxt < UNITS - 1:
                        alone(sp, tick_sp)
                        last = parity is None and not first
                        weights(0 if last else pair + 1, nxt + 1, 1 - into)
                if cur is not None:
                    before = half - 1 if first else half
                    sp.wait_ge(s_ye, cur * NBH + NBH)
                    alone(sp, tick_sp)
                    sp.dma_start(y_tok[before * TH:(before + 1) * TH, bass.ds((cur - before * PAIRS) * P, P)]
                                 .rearrange("(c p) n -> p c n", p=P), y_sb[:, :, :]).then_inc(s_out, 16)
            schedule(sp, lambda half: None, step)
            sp.wait_ge(s_out, UNITS * 16)

        @block.gpsimd
        def _(pool):
            for half in range(HALVES):
                for c in range(UCH):
                    j = half * UCH + c
                    n, k = c // (F // KC), c % (F // KC) * KC
                    if j >= 2:
                        pool.wait_ge(s_ul, j - 1)
                    pool.dma_start(u_raw[j % 2][:, :, :], u_feat[k:k + KC, :, half * TH + n * BANK:half * TH + (n + 1) * BANK]
                                   .rearrange("k p t -> p k t")).then_inc(s_u[j % 2], 16)

        def split_u(eng, half, split, chunks):
            for c in chunks:
                n, k = c // (F // KC), c % (F // KC) * KC
                if half and c % (F // KC) == 0:
                    eng.wait_ge(s_pB, (half * PAIRS - 1) * NQ + BLK + n + 1)
                split(half * UCH + c, slice(k, k + KC), slice(n * BANK, (n + 1) * BANK))

        @block.scalar
        def _(act):
            act.wait_ge(s_const, 16 * CONSTS)
            nc.scalar.copy(wdt_hi[:, :, :], wdt_raw[:, :, :]).then_inc(s_dth, 1)

            def split(j, ks, ts):
                act.wait_ge(s_u[j % 2], 16 * (j // 2 + 1))
                nc.scalar.copy(u_hi[:, ks, ts], u_raw[j % 2][:, :, :]).then_inc(s_uh, 1)

            def weights_hi(nxt, cols):
                act.wait_ge(s_w, nxt * 32 + 32)
                nc.scalar.copy(w_hi[:, :, cols], w_raw[:, :, cols]).then_inc(s_wh, 1)

            def half_start(half):
                link = linker(act, s_la, half * LA_HALF)
                act.wait_ge(s_va, 2 * half + 1)
                link(nc.scalar.activation(t1[:, :, :], t0[:, :, :], ACT.Abs))
                link(nc.scalar.activation(t1[:, :, :], t1[:, :, :], ACT.Exp, scale=-1.0))
                link(nc.scalar.activation(t1[:, :, :], t1[:, :, :], ACT.Ln, bias=one_sb[:, :], scale=1.0))
                nc.scalar.activation(t2[:, :, :], t0[:, :, :], ACT.Relu).then_inc(s_av, 1)
                act.wait_ge(s_va, 2 * half + 2)
                nc.scalar.activation(t1[:, :, :], t1[:, :, :], ACT.Exp).then_inc(s_av, 1)
                if half == 0:
                    act.wait_ge(s_hv, 1)
                    for n in (2, 3):
                        nc.scalar.activation(hv[:, n, :], hv[:, n, :], ACT.Exp, scale=LN2).then_inc(s_ab, 1)

            def step(half, cur, nxt, parity=None, first=False):
                into, at = parities(nxt, cur, parity)
                if cur is not None:
                    act.wait_ge(s_pn, cur * NQ + NQ)
                    nc.scalar.activation(nrm[:, :, :, :].rearrange("p a b c -> p (a b c)"), pn[:, 0:4 * TT], ACT.Sqrt).then_inc(s_root, 1)
                    act.wait_ge(s_arg, cur + 1)
                    nc.scalar.activation(q0[:, :, :], q0[:, :, :], ACT.Tanh).then_inc(s_tanh, 1)
                if nxt is None:
                    return
                if first and half == 0:
                    weights_hi(nxt, B_COLS)
                if cur is not None:
                    act.wait_ge(s_pB, nxt * NQ)
                weights_hi(nxt, C_COLS)
                if first:
                    split_u(act, half, split, range(UCH))
                if cur is not None:
                    act.wait_ge(s_G, cur * NI)
                for n in range(NQ):
                    dst = (BT, CT)[n // BLK][into]
                    act.wait_ge(s_pB, nxt * NQ + n + 1)
                    src, bias = pB[n % 2][:, :], bias_sb[into][:, n // BLK:n // BLK + 1]
                    nc.scalar.activation(dst[:, (n % BLK) * BANK:(n % BLK + 1) * BANK], src, ACT.Identity, bias=bias).then_inc(s_bt, 1)
                    if cur is not None or n >= 1:
                        act.wait_ge(s_pn, nxt * NQ + n - 1)
                    nc.scalar.activation(sq[n % 2][:, :], src, ACT.Square, bias=bias).then_inc(s_bt, 1)
                    if n == BLK - 1 and (parity is not None or nxt < UNITS - 1):
                        weights_hi(nxt + 1, B_COLS)
            schedule(act, half_start, step)

        @block.vector
        def _(dve):
            nc.vector.memset(idz[:, P:2 * P], 0.0).then_inc(s_set, 1)
            nc.vector.memset(one_sb[:, :], 1.0).then_inc(s_set, 1)
            dve.wait_ge(s_dth, 1)
            nc.vector.tensor_tensor(wdt_lo[:, :, :], wdt_raw[:, :, :], wdt_hi[:, :, :].bitcast(F32), ALU.subtract).then_inc(s_dtl, 1)

            def split(j, ks, ts):
                dve.wait_ge(s_uh, j + 1)
                nc.vector.tensor_tensor(u_lo[:, ks, ts], u_raw[j % 2][:, :, :], u_hi[:, ks, ts].bitcast(F32), ALU.subtract).then_inc(s_ul, 1)

            def weights_lo(count, cols):
                dve.wait_ge(s_wh, count)
                nc.vector.tensor_tensor(w_lo[:, :, cols], w_raw[:, :, cols], w_hi[:, :, cols].bitcast(F32), ALU.subtract).then_inc(s_wl, 1)

            def wide(v, n=TT):
                return v.unsqueeze(2).to_broadcast([P, H, n])

            def half_start(half):
                link = linker(dve, s_lv, half * (LV_ONCE + LV_HALF + PAIRS * LV))
                if half == 0:
                    for n, (lo, hi) in ((1, (-2.3, -0.01)), (2, (-3.32, -0.015)), (3, (-2.0, 2.0))):
                        link(nc.vector.tensor_scalar(hv[:, n, :], hv[:, n, :], lo, hi, ALU.max, ALU.min))
                    link(nc.vector.tensor_scalar(hv[:, 4, :], hv[:, 4, :], 1e-6, None, ALU.add))
                    nc.vector.reciprocal(hv[:, 4, :], hv[:, 4, :]).then_inc(s_hv, 1)
                dve.wait_ge(s_dt, half + 1)
                pd = pa[0][:, 0:TT * 2 * H].rearrange("p (c h) -> p h c", h=2 * H)
                nc.vector.tensor_tensor(t0[:, :, :], pd[:, 0:H, :], wide(hv[:, 0, :]), ALU.add).then_inc(s_va, 1)
                dve.wait_ge(s_av, 2 * half + 1)
                link(nc.vector.tensor_tensor(t1[:, :, :], t1[:, :, :], t2[:, :, :], ALU.add))
                nc.vector.tensor_tensor(t1[:, :, :], t1[:, :, :], wide(hv[:, 1, :]), ALU.mult).then_inc(s_va, 1)
                dve.wait_ge(s_av, 2 * half + 2)
                link(nc.vector.tensor_scalar(t1[:, :, :], t1[:, :, :], -1.0, 1.0, ALU.mult, ALU.add))
                link(nc.vector.tensor_tensor(t2[:, :, :], t1[:, :, :], pd[:, H:2 * H, :], ALU.mult))
                dve.wait_ge(s_ab, 2)
                if half == 0:
                    link(nc.vector.tensor_scalar(hv[:, 3, :], hv[:, 3, :], 1.0 / S, None, ALU.mult))
                link(nc.vector.tensor_tensor(t2[:, :, :], t2[:, :, :], t2[:, :, :], ALU.mult))
                link(nc.vector.tensor_tensor(t2[:, :, :], t2[:, :, :], wide(hv[:, 4, :]), ALU.mult))
                link(nc.vector.tensor_tensor(gain_sb[:, :, :], t2[:, :, :], wide(hv[:, 3, :]), ALU.mult))
                link(nc.vector.tensor_scalar(base_w[:, :, :], wide(hv[:, 2, :]), -1.0, 1.0, ALU.mult, ALU.add))
                link(nc.vector.tensor_scalar(rest_w[:, :, :], base_w[:, :, :], -1.0, 1.0, ALU.mult, ALU.add))
                assert link.count[0] == LV_HALF + (0 if half else LV_ONCE), link.count[0]

            def step(half, cur, nxt, parity=None, first=False):
                into, at = parities(nxt, cur, parity)
                if cur is None:
                    weights_lo(1, B_COLS)
                    weights_lo(2, C_COLS)
                    split_u(dve, half, split, range(UCH))
                    weights_lo(3, B_COLS)
                    return
                of = half - 1 if first else half
                pair = cur - of * PAIRS
                link = linker(dve, s_lv, LV_ONCE + LV_HALF * (of + 1) + cur * LV)
                dve.wait_ge(s_root, cur + 1)
                link(nc.vector.tensor_scalar(nrm[:, :, :, :], nrm[:, :, :, :], 1e-12, None, ALU.max))
                dve.wait_ge(s_ye, cur * NBH)
                link(nc.vector.reciprocal(inv[:, :, :, :], nrm[:, :, :, :]))
                rB = inv[:, 0, :, :]
                link(nc.vector.tensor_tensor(q0[:, :, :], pn[:, 0:2 * TT].rearrange("p (h c) -> p h c", h=2), rB, ALU.mult))
                link(nc.vector.tensor_tensor(q0[:, :, :], q0[:, :, :], rB, ALU.mult))
                nc.vector.tensor_tensor(q0[:, :, :], q0[:, :, :], gain_sb[:, bass.ds(2 * pair, 2), :], ALU.mult).then_inc(s_arg, 1)
                dve.wait_ge(s_tanh, cur + 1)
                link(nc.vector.tensor_scalar(q0[:, :, :], q0[:, :, :], 0.0, None, ALU.max))
                link(nc.vector.tensor_tensor(q0[:, :, :], q0[:, :, :], rest_w[:, bass.ds(2 * pair, 2), :], ALU.mult))
                link(nc.vector.tensor_tensor(q0[:, :, :], q0[:, :, :], base_w[:, bass.ds(2 * pair, 2), :], ALU.add))
                dve.wait_ge(s_pa, cur * NBH)
                nc.vector.tensor_scalar(al[:, :, :], q0[:, :, :], 0.01, 0.999, ALU.max, ALU.min).then_inc(s_al, 1)
                dve.wait_ge(s_al, cur + 1)
                link(nc.vector.tensor_scalar(cB[:, :, :], al[:, :, :], -1.0, 1.0, ALU.mult, ALU.add))
                link(nc.vector.tensor_tensor(cB[:, :, :], cB[:, :, :], rB, ALU.mult))
                assert link.count[0] == LV, link.count[0]
                if nxt is not None:
                    weights_lo(nxt * 2 + 2, C_COLS)
                for i in range(NI + 1):
                    if i < NI:
                        b, h = i // 2, i % 2
                        dve.wait_ge(s_pa, cur * NBH + b + 1)
                        nc.vector.tensor_tensor_scan(M[i % 2][:, 0:2 * P], pa[b % 2][:, h * L:(h + 1) * L], idz[:, :], 0.0, ALU.mult, ALU.add).then_inc(s_M, 1)
                        nc.vector.tensor_tensor_scan(M[i % 2][:, 2 * P:3 * P], pa[b % 2][:, h * L + P:(h + 1) * L], idz[:, 0:P], 0.0, ALU.mult, ALU.add).then_inc(s_M, 1)
                        dve.wait_ge(s_M, (cur * NI + i) * 2 + 2)
                        dve.wait_ge(s_G, cur * NI + i + 1)
                        dve.wait_ge(s_y, cur * NI + max(i - 1, 0))
                        for a, (lo, hi) in enumerate(((0, 2 * P), (2 * P, 3 * P))):
                            ins = nc.vector.scalar_tensor_tensor(W[i % 2][:, lo:hi], pG[i % 2][:, lo:hi], cB[:, h, 2 * b + a:2 * b + a + 1],
                                                                 M[i % 2][:, lo:hi], ALU.mult, ALU.mult)
                        ins.then_inc(s_W, 1)
                        if first:
                            split_u(dve, half, split, range(UCH * i // NI, UCH * (i + 1) // NI))
                    if i >= 2 and i % 2 == 0:
                        b = i // 2 - 1
                        if b == 0:
                            dve.wait_ge(s_out, cur * 16)
                        dve.wait_ge(s_y, cur * NI + i)
                        pyb = py[:, 0:L].rearrange("p (h c n) -> p h c n", h=2, c=2)
                        for h in range(2):
                            ins = nc.vector.tensor_tensor(y_sb[:, 2 * b:2 * b + 2, h * S:(h + 1) * S], pyb[:, h, :, :],
                                                          inv[:, 1, h, 2 * b:2 * b + 2].unsqueeze(2).to_broadcast([P, 2, S]), ALU.mult)
                        ins.then_inc(s_ye, 1)
                    if i == NI // 2 and nxt is not None and not first and (parity is not None or nxt < UNITS - 1):
                        weights_lo(nxt * 2 + 3, B_COLS)
                if first:
                    weights_lo(nxt * 2 + 3, B_COLS)
            schedule(dve, half_start, step)

        @block.tensor
        def _(pe):
            pe.wait_ge(s_set, 2)
            pe.wait_ge(s_const, 16 * CONSTS)

            def parts(out, w, u, cols, k, ts):
                for n, (a, b) in enumerate(((w[0], u[0]), (w[0], u[1]), (w[1], u[0]))):
                    ins = nc.tensor.matmul(out, a[:, k, cols], b[:, k, ts], start=(k == 0 and n == 0), stop=(k == F - 1 and n == 2))
                return ins

            def norms(unit, n):
                pe.wait_ge(s_bt, unit * 2 * NQ + 2 * n + 2)
                for q in range(4):
                    c = (n % BLK) * 4 + q
                    at = (n // BLK) * 2 * TT
                    ins = nc.tensor.matmul(pn[:, at:at + 2 * TT].rearrange("p (h c) -> p h c", h=2)[:, :, c],
                                           sq[n % 2][:, q * P:(q + 1) * P], pair_sb[:, :], start=True, stop=True)
                ins.then_inc(s_pn, 1)

            def half_start(half):
                pe.wait_ge(s_dtl, 1)
                pe.wait_ge(s_M, half * PAIRS * NI * 2)
                for c in range(TT):
                    for k in range(F):
                        ts = slice(c * P, (c + 1) * P)
                        for n, (a, b) in enumerate(((u_hi, wdt_hi), (u_hi, wdt_lo), (u_lo, wdt_hi))):
                            ins = nc.tensor.matmul(pa[0][:, c * 2 * H:(c + 1) * 2 * H], a[:, k, ts], b[:, k, :],
                                                   start=(k == 0 and n == 0), stop=(k == F - 1 and n == 2))
                ins.then_inc(s_dt, 1)

            def step(half, cur, nxt, parity=None, first=False):
                into, at = parities(nxt, cur, parity)

                def decays(b):
                    pe.wait_ge(s_M, (cur * NI + 2 * max(b - 1, 0)) * 2)
                    for h in range(2):
                        for c in range(2):
                            ins = nc.tensor.matmul(pa[b % 2][:, h * L + c * P:h * L + (c + 1) * P],
                                                   al[:, h, 2 * b + c:2 * b + c + 1].to_broadcast([P, P]), idz[:, 0:P], start=True, stop=True)
                    ins.then_inc(s_pa, 1)

                def scores(i):
                    t, r = i // 2 * L, slice(i % 2 * S, (i % 2 + 1) * S)
                    B, C = BT[at], CT[at]
                    pe.wait_ge(s_W, cur * NI + max(i - 1, 0))
                    nc.tensor.matmul(pG[i % 2][:, 0:L], B[r, t:t + P], C[r, t:t + L], start=True, stop=True)
                    nc.tensor.matmul(pG[i % 2][:, L:L + P], B[r, t + P:t + L], C[r, t + P:t + L], start=True, stop=True).then_inc(s_G, 1)

                def output(i):
                    b, h = i // 2, i % 2
                    pe.wait_ge(s_W, cur * NI + i + 1)
                    if h == 0:
                        pe.wait_ge(s_ye, cur * NBH + b)
                    o = h * 2 * S
                    u0, u1 = ut_sb[at][:, 2 * b, h * S:(h + 1) * S], ut_sb[at][:, 2 * b + 1, h * S:(h + 1) * S]
                    nc.tensor.matmul(py[:, o:o + S], W[i % 2][:, 0:P], u0, start=True, stop=True)
                    nc.tensor.matmul(py[:, o + S:o + 2 * S], W[i % 2][:, P:2 * P], u0, start=True, stop=False)
                    nc.tensor.matmul(py[:, o + S:o + 2 * S], W[i % 2][:, 2 * P:3 * P], u1, start=False, stop=True).then_inc(s_y, 1)

                def project(j):
                    n, k = j // F, j % F
                    if k == 0:
                        if cur is not None or n >= 2:
                            pe.wait_ge(s_bt, nxt * 2 * NQ + 2 * (n - 1))
                        if n % BLK == 0:
                            pe.wait_ge(s_wl, nxt * 2 + n // BLK + 1)
                    if first and n < BLK and k % KC == 0:
                        pe.wait_ge(s_ul, half * UCH + n * (F // KC) + k // KC + 1)
                    cols = (B_COLS, C_COLS)[n // BLK]
                    ins = parts(pB[n % 2][:, :], (w_hi, w_lo), (u_hi, u_lo), cols, k, slice((n % BLK) * BANK, (n % BLK + 1) * BANK))
                    if k == F - 1:
                        ins.then_inc(s_pB, 1)
                    if k == 3 and n >= 1:
                        if n == 1 and cur is not None:
                            pe.wait_ge(s_arg, nxt)
                        norms(nxt, n - 1)
                if cur is not None:
                    norms(cur, NQ - 1)
                if cur is None:
                    for j in range(NQ * F):
                        project(j)
                    return
                slots = [[] for _ in range(NI + 1)]
                if nxt is not None and not first:
                    for j in range(F + 2):
                        project(j)
                    for j in range(F + 2, NQ * F):
                        slots[(j - F - 2) * (NI + 1) // (NQ * F - F - 2)].append(j)
                pe.wait_ge(s_al, cur + 1)
                pe.wait_ge(s_ut, cur * 16 + 16)
                decays(0)
                decays(1)
                scores(0)
                for i in range(NI + 1):
                    for j in slots[i]:
                        project(j)
                    if i < NI:
                        if i + 1 < NI:
                            scores(i + 1)
                        output(i)
                        if i % 2 == 1 and i // 2 + 2 < NBH:
                            decays(i // 2 + 2)
                if first:
                    for j in range(NQ * F):
                        project(j)
            schedule(pe, half_start, step)


LN_EPS = 1e-5


def ssm0_out(nc, x, y_tok, z_tok, w_out, b_out, gate, ident, x1, x1_feat):
    DI = 1536
    F = DI // P
    with ExitStack() as phase:
        m = Space(nc, "a3", phase)
        w_sb = m.sb("w", [P, F, D])
        ident_sb = m.sb("ident", [P, P])
        b_sb, g_sb, eps_sb = m.sb("b", [P, D]), m.sb("g", [P, 1]), m.sb("eps", [P, 1])
        x_sb = [m.sb(f"x{i}", [P, 2, D]) for i in range(2)]
        y_sb = [m.sb(f"y{i}", [P, 2, DI]) for i in range(2)]
        z_sb = [m.sb(f"z{i}", [P, 2, DI]) for i in range(2)]
        yT = m.sb("yT", [P, 2, F, P])
        v_sb = m.sb("v", [P, 2, D])
        st, mv, sd = m.sb("st", [P, 2, 6]), m.sb("mv", [P, 2, 2]), m.sb("sd", [P, 2])
        o_sb = m.sb("o", [P, 2, D])
        oT = m.sb("oT", [P, 2, KD, P])
        pT = [m.ps(f"pT{i}") for i in range(2)]
        po = [m.ps(f"po{i}") for i in range(2)]
        px = [m.ps(f"px{i}") for i in range(2)]
        s_const, s_set, s_out, s_lv = (m.sem(n) for n in "const set out lv".split())
        s_in = [m.sem(f"in{i}") for i in range(2)]
        s_yz, s_T, s_yT, s_o, s_var, s_sd, s_ln, s_xT, s_oT = (m.sem(n) for n in "yz T yT o var sd ln xT oT".split())
        tick_dve = m.sem("tick_dve")
        block = phase.enter_context(nc.Block())
        LV = 9

        def rows(a, b, n):
            return a[bass.ds(b * L, n), :].rearrange("(c p) n -> p c n", p=P)

        @block.sync
        def _(sp):
            for dst, src in ((ident_sb[:, :], ident), (b_sb[:, :], b_out.partition_broadcast(P)), (g_sb[:, :], gate.partition_broadcast(P)),
                             (w_sb[:, :, :], w_out.rearrange("(k p) n -> p k n", p=P))):
                sp.dma_start(dst, src).then_inc(s_const, 16)
            with sp.Fori(0, NB // 2) as r:
                for i in range(2):
                    b = 2 * r + i
                    sp.wait_ge(s_ln, r * 4)
                    for dst, src in ((x_sb, x), (y_sb, y_tok), (z_sb, z_tok)):
                        sp.dma_start(dst[i][:, :, :], rows(src, b, L)).then_inc(s_in[i], 16)
                for i in range(2):
                    b = 2 * r + i
                    sp.wait_ge(s_oT, b * 2 + 2)
                    sp.dma_start(rows(x1, b, L), o_sb[:, :, :]).then_inc(s_out, 16)
                    sp.dma_start(x1_feat[:, :, bass.ds(b * L, L)].rearrange("k p (c t) -> p c k t", c=2)[:, 0, :, :], oT[:, 0, :, :]).then_inc(s_out, 16)
                    sp.dma_start(x1_feat[:, :, bass.ds(b * L, L)].rearrange("k p (c t) -> p c k t", c=2)[:, 1, :, :], oT[:, 1, :, :]).then_inc(s_out, 16)
            sp.wait_ge(s_out, NB * 48)

        @block.scalar
        def _(act):
            act.wait_ge(s_set, 1)
            with act.Fori(0, NB) as b:
                for n in range(6):
                    act.wait_ge(s_T, b * 6 + n + 1)
                    if n == 0:
                        act.wait_ge(s_o, b * 2)
                    nc.scalar.copy(yT[:, n // 3, (n % 3) * 4:(n % 3) * 4 + 4, :].rearrange("p k t -> p (k t)"), pT[n % 2][:, :]).then_inc(s_yT, 1)
                act.wait_ge(s_var, b * 2 + 2)
                nc.scalar.activation(sd[:, :], mv[:, :, 1], ACT.Sqrt, bias=eps_sb[:, :], scale=1.0).then_inc(s_sd, 1)
                act.wait_ge(s_out, b * 48)
                for c in range(2):
                    act.wait_ge(s_xT, b * 2 + c + 1)
                    nc.scalar.copy(oT[:, c, :, :].rearrange("p k t -> p (k t)"), px[c][:, :]).then_inc(s_oT, 1)

        @block.vector
        def _(dve):
            nc.vector.memset(eps_sb[:, :], LN_EPS).then_inc(s_set, 1)
            dve.wait_ge(s_const, 64)
            with dve.Fori(0, NB // 2) as r:
                for i in range(2):
                    b = 2 * r + i
                    link = linker(dve, s_lv, b * LV)
                    dve.wait_ge(s_in[i], r * 48 + 48)
                    for c in range(2):
                        nc.vector.tensor_tensor(y_sb[i][:, c, :], y_sb[i][:, c, :], z_sb[i][:, c, :], ALU.mult).then_inc(s_yz, 1)
                    for c in range(2):
                        dve.wait_ge(s_o, b * 2 + c + 1)
                        v = v_sb[:, c, :]
                        link(nc.vector.tensor_tensor(v, po[c][:, :], b_sb[:, :], ALU.add))
                        link(nc.vector.scalar_tensor_tensor(v, v, g_sb[:, 0:1], x_sb[i][:, c, :], ALU.mult, ALU.add))
                        link(nc.vector.tensor_tensor(v, v, x_sb[i][:, c, :], ALU.add))
                        link(nc.vector.bn_stats(st[:, c, :], v))
                        alone(dve, tick_dve)
                        nc.vector.bn_aggr(mv[:, c, :], st[:, c, :]).then_inc(s_var, 1)
                    dve.wait_ge(s_sd, b + 1)
                    link(nc.vector.reciprocal(sd[:, :], sd[:, :]))
                    dve.wait_ge(s_out, b * 48)
                    for c in range(2):
                        nc.vector.tensor_scalar(o_sb[:, c, :], v_sb[:, c, :], mv[:, c, 0:1], sd[:, c:c + 1], ALU.subtract, ALU.mult).then_inc(s_ln, 1)
                    assert link.count[0] == LV

        @block.tensor
        def _(pe):
            pe.wait_ge(s_const, 64)
            with pe.Fori(0, NB // 2) as r:
                for i in range(2):
                    b = 2 * r + i
                    for n in range(6):
                        c, j = n // 3, n % 3
                        pe.wait_ge(s_yz, b * 2 + c + 1)
                        pe.wait_ge(s_yT, b * 6 + max(n - 1, 0))
                        for q in range(4):
                            ins = nc.tensor.transpose(pT[n % 2][:, q * P:(q + 1) * P], y_sb[i][:, c, (j * 4 + q) * P:(j * 4 + q + 1) * P], ident_sb[:, :])
                        ins.then_inc(s_T, 1)
                    for c in range(2):
                        pe.wait_ge(s_yT, b * 6 + 3 * c + 3)
                        pe.wait_ge(s_var, b * 2)
                        for k in range(F):
                            ins = nc.tensor.matmul(po[c][:, :], yT[:, c, k, :], w_sb[:, k, :], start=(k == 0), stop=(k == F - 1))
                        ins.then_inc(s_o, 1)
                    for c in range(2):
                        pe.wait_ge(s_ln, b * 2 + c + 1)
                        pe.wait_ge(s_oT, b * 2)
                        for k in range(KD):
                            ins = nc.tensor.transpose(px[c][:, k * P:(k + 1) * P], o_sb[:, c, k * P:(k + 1) * P], ident_sb[:, :])
                        ins.then_inc(s_xT, 1)


def long_conv(nc, x_feat, ctx_turned, taps, skip, exchange, r_feat):
    HEADS, R = 32, 8
    PAIRS = R * (R + 1) // 2
    OFF = [R * i - i * (i - 1) // 2 for i in range(R)]
    N = NB * PAIRS
    with ExitStack() as phase:
        m = Space(nc, "b1", phase)
        x_sb, c_sb = m.sb("x", [P, KD, T]), m.sb("c", [P, KD, T])
        x4 = x_sb[:, :, :].rearrange("p k (b t) -> p k b t", b=NB)
        c4 = c_sb[:, :, :].rearrange("p k (b t) -> p k b t", b=NB)
        exchange_sb, skip_sb = m.sb("exchange", [P, P]), m.sb("skip", [P, HEADS])
        toe = [m.sb(f"toe{i}", [P, D]) for i in range(2)]
        dg = [m.sb(f"dg{i}", [P, P]) for i in range(2)]
        kv = [m.sb(f"kv{i}", [P, KD, NB, PAIRS]) for i in range(2)]
        prod = [m.sb(f"prod{i}", [P, KD, NB, R, R]) for i in range(2)]
        red = [m.sb(f"red{i}", [P, KD, NB, R]) for i in range(2)]
        py = [m.ps(f"py{i}", (P, KD, BANK)) for i in range(2)]
        s_const, s_x, s_c, s_out, s_lv = (m.sem(n) for n in "const x c out lv".split())
        s_toe = [m.sem(f"toe{i}") for i in range(2)]
        s_kv, s_dg, s_y, s_prod, s_red, s_sum = (m.sem(n) for n in "kv dg y prod red sum".split())
        block = phase.enter_context(nc.Block())

        @block.sync
        def _(sp):
            sp.dma_start(exchange_sb[:, :], exchange).then_inc(s_const, 16)
            sp.dma_start(skip_sb[:, :], skip.partition_broadcast(P)).then_inc(s_const, 16)
            sp.dma_start(c_sb[:, :, :], ctx_turned.rearrange("k p t -> p k t")).then_inc(s_c, 16)
            sp.dma_start(x_sb[:, :, :], x_feat.rearrange("k p t -> p k t")).then_inc(s_x, 16)
            with sp.Fori(0, HEADS // 2) as g:
                for i in range(2):
                    row = taps[bass.ds(2 * g + i, 1), 0:D]
                    sp.wait_ge(s_y, 2 * g)
                    sp.dma_start(toe[i][:, :], bass.AP(row.tensor, row.offset, [[1, P], [1, D]])).then_inc(s_toe[i], 16)
            sp.wait_ge(s_sum, HEADS)
            sp.dma_start(r_feat.rearrange("k p t -> p k t"), x_sb[:, :, :]).then_inc(s_out, 16)
            sp.wait_ge(s_out, 16)

        @block.gpsimd
        def _(pool):
            pool.wait_ge(s_c, 16)

            def add_back(g, i):
                h = 2 * g + i
                pool.wait_ge(s_red, h + 1)
                at = x4[:, :, :, bass.ds(h * R, R)]
                pool.tensor_tensor(at, at, red[i][:, :, :, :], ALU.add).then_inc(s_sum, 1)
            with pool.Fori(0, HEADS // 2) as g:
                for i in range(2):
                    h = 2 * g + i
                    pool.wait_ge(s_y, 2 * g)
                    for r in range(R):
                        ins = pool.tensor_tensor(kv[i][:, :, :, OFF[r]:OFF[r] + R - r], c4[:, :, :, bass.ds(h * R + r, R - r)],
                                                 c4[:, :, :, bass.ds(h * R + r, 1)].to_broadcast([P, KD, NB, R - r]), ALU.mult)
                        ins.then_inc(s_kv, 1)
                for i in range(2):
                    add_back(g, i)

        @block.vector
        def _(dve):
            dve.wait_ge(s_const, 32)
            dve.wait_ge(s_x, 16)
            with dve.Fori(0, HEADS // 2) as g:
                for i in range(2):
                    h = 2 * g + i
                    link = linker(dve, s_lv, h * 1)
                    dve.wait_ge(s_toe[i], g * 16 + 16)
                    link(nc.vector.tensor_scalar(dg[i][:, :], exchange_sb[:, :], skip_sb[:, bass.ds(h, 1)], None, ALU.mult))
                    nc.vector.tensor_tensor(toe[i][:, 0:P], toe[i][:, 0:P], dg[i][:, :], ALU.add).then_inc(s_dg, 1)
                for i in range(2):
                    h = 2 * g + i
                    dve.wait_ge(s_y, h + 1)
                    dve.wait_ge(s_red, 2 * g)
                    for r in range(R):
                        n = R - r
                        src = py[i][:, :, 0:N].rearrange("p k (b n) -> p k b n", b=NB)
                        ins = nc.vector.tensor_tensor(prod[i][:, :, :, r:R, r], src[:, :, :, OFF[r]:OFF[r] + n],
                                                      x4[:, :, :, bass.ds(h * R + r, 1)].to_broadcast([P, KD, NB, n]), ALU.mult)
                        ins.then_inc(s_prod, 1)
                        if n > 1:
                            ins = nc.vector.tensor_tensor(prod[i][:, :, :, r, r + 1:R], src[:, :, :, OFF[r] + 1:OFF[r] + n],
                                                          x4[:, :, :, bass.ds(h * R + r + 1, n - 1)], ALU.mult)
                            ins.then_inc(s_prod, 1)
                    dve.wait_ge(s_prod, h * (2 * R - 1) + 2 * R - 1)
                    dve.wait_ge(s_sum, 2 * g)
                    nc.vector.tensor_reduce(red[i][:, :, :, :].rearrange("p k b r -> p (k b r)"),
                                            prod[i][:, :, :, :, :].rearrange("p k b o r -> p (k b o) r"), AX.X, ALU.add).then_inc(s_red, 1)

        @block.tensor
        def _(pe):
            with pe.Fori(0, HEADS // 2) as g:
                for i in range(2):
                    h = 2 * g + i
                    pe.wait_ge(s_dg, h + 1)
                    pe.wait_ge(s_kv, h * R + R)
                    pe.wait_ge(s_prod, 2 * g * (2 * R - 1))
                    for o in range(KD):
                        for k in range(o + 1):
                            ins = nc.tensor.matmul(py[i][:, o, 0:N], toe[i][:, (o - k) * P:(o - k + 1) * P],
                                                   kv[i][:, k, :, :].rearrange("p b n -> p (b n)"), start=(k == 0), stop=(k == o))
                    ins.then_inc(s_y, 1)


def norm_from_feat(nc, name, v_feat, ident, o_tok, o_feat):
    LN_EPS = 1e-5
    with ExitStack() as phase:
        m = Space(nc, name, phase)
        ident_sb, eps_sb = m.sb("ident", [P, P]), m.sb("eps", [P, 1])
        v_sb = [m.sb(f"v{i}", [P, KD, P]) for i in range(2)]
        st = [m.sb(f"st{i}", [P, 6]) for i in range(2)]
        mv = [m.sb(f"mv{i}", [P, 2]) for i in range(2)]
        sd = [m.sb(f"sd{i}", [P, 1]) for i in range(2)]
        o_sb = [m.sb(f"o{i}", [P, D]) for i in range(2)]
        oT = [m.sb(f"oT{i}", [P, KD, P]) for i in range(2)]
        pv = [m.ps(f"pv{i}") for i in range(2)]
        po = [m.ps(f"po{i}") for i in range(2)]
        s_const, s_set, s_lv = m.sem("const"), m.sem("set"), m.sem("lv")
        s_in = [m.sem(f"in{i}") for i in range(2)]
        s_out = [m.sem(f"out{i}") for i in range(2)]
        s_T, s_var, s_sd, s_ln, s_oT, s_oc = (m.sem(n) for n in "T var sd ln oT oc".split())
        tick_dve = m.sem("tick_dve")
        block = phase.enter_context(nc.Block())
        LV = 2

        @block.sync
        def _(sp):
            sp.dma_start(ident_sb[:, :], ident).then_inc(s_const, 16)
            with sp.Fori(0, TILES // 2) as r:
                for i in range(2):
                    t = 2 * r + i
                    sp.wait_ge(s_T, 2 * r)
                    sp.dma_start(v_sb[i][:, :, :], v_feat[:, :, bass.ds(t * P, P)].rearrange("k p t -> p k t")).then_inc(s_in[i], 16)
                for i in range(2):
                    t = 2 * r + i
                    sp.wait_ge(s_oc, t + 1)
                    sp.dma_start(o_tok[bass.ds(t * P, P), :], o_sb[i][:, :]).then_inc(s_out[i], 16)
                    sp.dma_start(o_feat[:, :, bass.ds(t * P, P)].rearrange("k p t -> p k t"), oT[i][:, :, :]).then_inc(s_out[i], 16)
            for i in range(2):
                sp.wait_ge(s_out[i], TILES // 2 * 32)

        @block.scalar
        def _(act):
            act.wait_ge(s_set, 1)
            with act.Fori(0, TILES // 2) as r:
                for i in range(2):
                    act.wait_ge(s_var, 2 * r + i + 1)
                    nc.scalar.activation(sd[i][:, :], mv[i][:, 1:2], ACT.Sqrt, bias=eps_sb[:, :], scale=1.0).then_inc(s_sd, 1)
                for i in range(2):
                    act.wait_ge(s_oT, 2 * r + i + 1)
                    act.wait_ge(s_out[i], r * 32)
                    nc.scalar.copy(oT[i][:, :, :].rearrange("p k t -> p (k t)"), po[i][:, :]).then_inc(s_oc, 1)

        @block.vector
        def _(dve):
            nc.vector.memset(eps_sb[:, :], LN_EPS).then_inc(s_set, 1)
            with dve.Fori(0, TILES // 2) as r:
                for i in range(2):
                    link = linker(dve, s_lv, (2 * r + i) * LV)
                    dve.wait_ge(s_T, 2 * r + i + 1)
                    link(nc.vector.bn_stats(st[i][:, :], pv[i][:, :]))
                    alone(dve, tick_dve)
                    nc.vector.bn_aggr(mv[i][:, :], st[i][:, :]).then_inc(s_var, 1)
                    dve.wait_ge(s_sd, 2 * r + i + 1)
                    link(nc.vector.reciprocal(sd[i][:, :], sd[i][:, :]))
                    dve.wait_ge(s_out[i], r * 32)
                    nc.vector.tensor_scalar(o_sb[i][:, :], pv[i][:, :], mv[i][:, 0:1], sd[i][:, :], ALU.subtract, ALU.mult).then_inc(s_ln, 1)

        @block.tensor
        def _(pe):
            pe.wait_ge(s_const, 16)
            with pe.Fori(0, TILES // 2) as r:
                for i in range(2):
                    pe.wait_ge(s_in[i], r * 16 + 16)
                    pe.wait_ge(s_ln, 2 * r)
                    for k in range(KD):
                        ins = nc.tensor.transpose(pv[i][:, k * P:(k + 1) * P], v_sb[i][:, k, :], ident_sb[:, :])
                    ins.then_inc(s_T, 1)
                for i in range(2):
                    pe.wait_ge(s_ln, 2 * r + i + 1)
                    pe.wait_ge(s_oc, 2 * r)
                    for k in range(KD):
                        ins = nc.tensor.transpose(po[i][:, k * P:(k + 1) * P], o_sb[i][:, k * P:(k + 1) * P], ident_sb[:, :])
                    ins.then_inc(s_oT, 1)


E_, K_, CAP, FF = 64, 8, 128, 192
SLOTS = E_ * CAP
FAR = 1 << 20


def moe0_route(nc, x_tok, x_feat, router, ident, before, ramp, x_slots, places, weights):
    with ExitStack() as phase:
        m = Space(nc, "c1", phase)
        rw = m.sb("rw", [P, KD, E_])
        before_sb = m.sb("before", [P, P])
        ones = m.sb("ones", [P, P])
        ramp_sb = m.sb("ramp", [P, E_])
        xf = [m.sb(f"xf{i}", [P, KD, P]) for i in range(2)]
        xt = [m.sb(f"xt{i}", [P, D]) for i in range(2)]
        mx, se, wn = m.sb("mx", [P, 1]), m.sb("se", [P, 1]), m.sb("wn", [P, 1])
        ex = m.sb("ex", [P, E_])
        top = m.sb("top", [P, K_])
        idx = m.sb("idx", [P, K_], U32)
        idf = m.sb("idf", [P, K_])
        hot = m.sb("hot", [P, K_, E_])
        tmp = m.sb("tmp", [P, K_, E_])
        A = m.sb("A", [P, E_])
        S = m.sb("S", [P, E_])
        pk, ok, pf = m.sb("pk", [P, K_]), m.sb("ok", [P, K_]), m.sb("pf", [P, K_])
        wk = [m.sb(f"wk{i}", [P, K_]) for i in range(2)]
        pl = [m.sb(f"pl{i}", [P, K_], U32) for i in range(2)]
        pL, pP = m.ps("pL"), m.ps("pP")
        s_const, s_set, s_lv = m.sem("const"), m.sem("set"), m.sem("lv")
        s_in = [m.sem(f"in{i}") for i in range(2)]
        s_log, s_neg, s_exp, s_A, s_pos, s_pl, s_used = (m.sem(n) for n in "log neg exp A pos pl used".split())
        s_out = [m.sem(f"out{i}") for i in range(2)]
        s_sc = [m.sem(f"sc{i}") for i in range(2)]
        tick_dve, tick_pool = m.sem("tick_dve"), m.sem("tick_pool")
        block = phase.enter_context(nc.Block())
        LV = 17

        @block.sync
        def _(sp):
            for dst, src in ((rw[:, :, :], router.rearrange("(k p) e -> p k e", p=P)), (before_sb[:, :], before), (ramp_sb[:, :], ramp.partition_broadcast(P))):
                sp.dma_start(dst, src).then_inc(s_const, 16)
            with sp.Fori(0, TILES // 2) as r:
                for i in range(2):
                    t = 2 * r + i
                    sp.wait_ge(s_log, 2 * r)
                    sp.wait_ge(s_sc[i], r * K_ * 16)
                    sp.dma_start(xf[i][:, :, :], x_feat[:, :, bass.ds(t * P, P)].rearrange("k p t -> p k t")).then_inc(s_in[i], 16)
                    sp.dma_start(xt[i][:, :], x_tok[bass.ds(t * P, P), :]).then_inc(s_in[i], 16)
                for i in range(2):
                    t = 2 * r + i
                    sp.wait_ge(s_pl, t + 1)
                    sp.dma_start(places[bass.ds(t * P, P), :], pl[i][:, :]).then_inc(s_out[i], 16)
                    sp.dma_start(weights[bass.ds(t * P, P), :], wk[i][:, :]).then_inc(s_out[i], 16)
            for i in range(2):
                sp.wait_ge(s_out[i], TILES // 2 * 32)

        @block.gpsimd
        def _(pool):
            with pool.Fori(0, TILES // 2) as r:
                for i in range(2):
                    t = 2 * r + i
                    pool.wait_ge(s_in[i], r * 32 + 32)
                    pool.wait_ge(s_pl, t + 1)
                    alone(pool, tick_pool)
                    for k in range(K_):
                        pool.indirect_dma_start(x_slots, bass.IndirectOffsetOnAxis(ap=pl[i][:, k:k + 1], axis=0), xt[i][:, :], None,
                                                bounds_check=SLOTS - 1, oob_is_err=False).then_inc(s_sc[i], 16)
            for i in range(2):
                pool.wait_ge(s_sc[i], TILES // 2 * K_ * 16)

        @block.scalar
        def _(act):
            with act.Fori(0, TILES) as t:
                act.wait_ge(s_neg, t + 1)
                nc.scalar.activation(ex[:, :], pL[:, 0:E_], ACT.Exp, bias=mx[:, :], scale=1.0, accum_out=se[:, :]).then_inc(s_exp, 1)

        @block.vector
        def _(dve):
            nc.vector.memset(ones[:, :], 1.0).then_inc(s_set, 1)
            nc.vector.memset(S[:, :], 0.0).then_inc(s_set, 1)
            dve.wait_ge(s_set, 2)
            dve.wait_ge(s_const, 48)
            with dve.Fori(0, TILES // 2) as r:
                for i in range(2):
                    t = 2 * r + i
                    link = linker(dve, s_lv, t * LV)
                    dve.wait_ge(s_log, t + 1)
                    link(nc.vector.tensor_reduce(mx[:, :], pL[:, 0:E_], AX.X, ALU.max))
                    nc.vector.tensor_scalar(mx[:, :], mx[:, :], -1.0, None, ALU.mult).then_inc(s_neg, 1)
                    dve.wait_ge(s_exp, t + 1)
                    link(nc.vector.reciprocal(se[:, :], se[:, :]))
                    link(nc.vector.tensor_scalar(ex[:, :], ex[:, :], se[:, :], None, ALU.mult))
                    alone(dve, tick_dve)
                    link(nc.vector.max(top[:, :], ex[:, :]))
                    alone(dve, tick_dve)
                    link(nc.vector.max_index(idx[:, :], top[:, :], ex[:, :]))
                    link(nc.vector.tensor_copy(idf[:, :], idx[:, :]))
                    link(nc.vector.tensor_tensor(hot[:, :, :], ramp_sb[:, :].unsqueeze(1).to_broadcast([P, K_, E_]),
                                                 idf[:, :].unsqueeze(2).to_broadcast([P, K_, E_]), ALU.is_equal))
                    dve.wait_ge(s_pos, t)
                    nc.vector.tensor_reduce(A[:, :], hot[:, :, :].rearrange("p k e -> p e k"), AX.X, ALU.add).then_inc(s_A, 1)
                    link(nc.vector.tensor_reduce(wn[:, :], top[:, :], AX.X, ALU.add))
                    link(nc.vector.tensor_scalar(wn[:, :], wn[:, :], 1e-20, None, ALU.add))
                    link(nc.vector.reciprocal(wn[:, :], wn[:, :]))
                    dve.wait_ge(s_pos, t + 1)
                    link(nc.vector.tensor_tensor(S[:, :], S[:, :], A[:, :], ALU.add))
                    link(nc.vector.tensor_tensor(tmp[:, :, :], hot[:, :, :], pP[:, 0:E_].unsqueeze(1).to_broadcast([P, K_, E_]), ALU.mult))
                    link(nc.vector.tensor_reduce(pk[:, :], tmp[:, :, :], AX.X, ALU.add))
                    link(nc.vector.tensor_scalar(ok[:, :], pk[:, :], float(CAP), None, ALU.is_lt))
                    link(nc.vector.scalar_tensor_tensor(pf[:, :], idf[:, :], float(CAP), pk[:, :], ALU.mult, ALU.add))
                    link(nc.vector.tensor_scalar(pk[:, :], ok[:, :], -float(FAR), float(FAR), ALU.mult, ALU.add))
                    dve.wait_ge(s_sc[i], r * K_ * 16)
                    dve.wait_ge(s_out[i], r * 32)
                    link(nc.vector.scalar_tensor_tensor(wk[i][:, :], top[:, :], wn[:, :], ok[:, :], ALU.mult, ALU.mult))
                    nc.vector.tensor_tensor(pl[i][:, :], pf[:, :], pk[:, :], ALU.add).then_inc(s_pl, 1)
                    assert link.count[0] == LV, link.count[0]

        @block.tensor
        def _(pe):
            pe.wait_ge(s_const, 48)
            pe.wait_ge(s_set, 2)
            with pe.Fori(0, TILES // 2) as r:
                for i in range(2):
                    t = 2 * r + i
                    pe.wait_ge(s_in[i], r * 32 + 32)
                    pe.wait_ge(s_exp, t)
                    for k in range(KD):
                        ins = nc.tensor.matmul(pL[:, 0:E_], xf[i][:, k, :], rw[:, k, :], start=(k == 0), stop=(k == KD - 1))
                    ins.then_inc(s_log, 1)
                    pe.wait_ge(s_A, t + 1)
                    pe.wait_ge(s_pl, t)
                    nc.tensor.matmul(pP[:, 0:E_], before_sb[:, :], A[:, :], start=True, stop=False)
                    nc.tensor.matmul(pP[:, 0:E_], ones[:, :], S[:, :], start=False, stop=True).then_inc(s_pos, 1)


def moe0_experts(nc, x_slots, w_gu, w_down, ident, y_slots):
    U, BUF = 8, 4
    F2 = FF - P
    with ExitStack() as phase:
        m = Space(nc, "c2", phase)
        ident_sb = m.sb("ident", [P, P])
        gu = [m.sb(f"gu{i}", [P, KD, 2 * FF]) for i in range(BUF)]
        wd = [m.sb(f"wd{i}", [P, 2, D]) for i in range(BUF)]
        xb = [m.sb(f"xb{i}", [P, D]) for i in range(BUF)]
        xT = [m.sb(f"xT{i}", [P, D]) for i in range(2)]
        g_sb = [m.sb(f"g{i}", [P, FF]) for i in range(2)]
        h_sb = [m.sb(f"h{i}", [P, FF]) for i in range(2)]
        hT = [m.sb(f"hT{i}", [P, 2, P]) for i in range(2)]
        y_sb = [m.sb(f"y{i}", [P, D]) for i in range(2)]
        pT = [m.ps(f"pT{i}") for i in range(2)]
        pG = [m.ps(f"pG{i}") for i in range(2)]
        pH = [m.ps(f"pH{i}") for i in range(2)]
        pY = [m.ps(f"pY{i}") for i in range(2)]
        s_const = m.sem("const")
        s_in = [m.sem(f"in{i}") for i in range(BUF)]
        s_T, s_xT, s_G, s_g, s_h, s_H, s_hT, s_Y, s_y = (m.sem(n) for n in "T xT G g h H hT Y y".split())
        s_out = [m.sem(f"out{i}") for i in range(2)]
        block = phase.enter_context(nc.Block())

        @block.sync
        def _(sp):
            sp.dma_start(ident_sb[:, :], ident).then_inc(s_const, 16)
            with sp.Fori(0, E_ // U) as r:
                for j in range(U):
                    e, q = r * U + j, j % BUF
                    sp.wait_ge(s_Y, e + 1)
                    sp.dma_start(gu[q][:, :, :], w_gu[bass.ds(e, 1), :, :, :].rearrange("e p k n -> (e p) k n")).then_inc(s_in[q], 16)
                    sp.dma_start(wd[q][:, 0, :], w_down[bass.ds(e, 1), 0:P, :].rearrange("e p n -> (e p) n")).then_inc(s_in[q], 16)
                    sp.dma_start(wd[q][0:F2, 1, :], w_down[bass.ds(e, 1), P:FF, :].rearrange("e p n -> (e p) n")).then_inc(s_in[q], 16)
                    sp.dma_start(xb[q][:, :], x_slots[bass.ds(e * CAP, CAP), :]).then_inc(s_in[q], 16)

        @block.gpsimd
        def _(pool):
            with pool.Fori(0, E_ // U) as r:
                for j in range(U):
                    e, q = r * U + j, j % 2
                    pool.wait_ge(s_y, e + 1)
                    pool.dma_start(y_slots[bass.ds(e * CAP, CAP), :], y_sb[q][:, :]).then_inc(s_out[q], 16)
            for q in range(2):
                pool.wait_ge(s_out[q], E_ // 2 * 16)

        def later(e, n, j):
            return e - n if j >= n else e - j

        @block.scalar
        def _(act):
            with act.Fori(0, E_ // U) as r:
                for s in range(U + 2):
                    if s < U:
                        e = r * U + s
                        act.wait_ge(s_T, e + 1)
                        act.wait_ge(s_G, later(e, 1, s))
                        nc.scalar.copy(xT[s % 2][:, :], pT[s % 2][:, :]).then_inc(s_xT, 1)
                    if 1 <= s <= U:
                        j = s - 1
                        e = r * U + j
                        act.wait_ge(s_G, e + 1)
                        act.wait_ge(s_h, later(e, 1, j))
                        nc.scalar.activation(g_sb[j % 2][:, :], pG[j % 2][:, 0:FF], ACT.Silu).then_inc(s_g, 1)

        @block.vector
        def _(dve):
            with dve.Fori(0, E_ // U) as r:
                for s in range(U + 2):
                    if s < U:
                        e = r * U + s
                        dve.wait_ge(s_g, e + 1)
                        dve.wait_ge(s_H, later(e, 1, s))
                        nc.vector.tensor_tensor(h_sb[s % 2][:, :], g_sb[s % 2][:, :], pG[s % 2][:, FF:2 * FF], ALU.mult).then_inc(s_h, 1)
                    if 1 <= s <= U:
                        j = s - 1
                        e = r * U + j
                        dve.wait_ge(s_H, e + 1)
                        dve.wait_ge(s_Y, BUF + later(e, 1, j))
                        nc.vector.tensor_copy(hT[j % 2][:, 0, :], pH[j % 2][:, 0:P]).then_inc(s_hT, 1)
                        nc.vector.tensor_copy(hT[j % 2][0:F2, 1, :], pH[j % 2][0:F2, P:2 * P]).then_inc(s_hT, 1)
                    if s >= 2:
                        j = s - 2
                        e = r * U + j
                        dve.wait_ge(s_Y, BUF + e + 1)
                        dve.wait_ge(s_out[j % 2], (r * (U // 2) + j // 2) * 16)
                        nc.vector.tensor_copy(y_sb[j % 2][:, :], pY[j % 2][:, :]).then_inc(s_y, 1)

        @block.tensor
        def _(pe):
            nc.tensor.sem_inc(s_Y, BUF)
            pe.wait_ge(s_const, 16)
            with pe.Fori(0, E_ // U) as r:
                for s in range(U + 3):
                    if s < U:
                        e, q = r * U + s, s % BUF
                        pe.wait_ge(s_in[q], (r * (U // BUF) + s // BUF + 1) * 64)
                        pe.wait_ge(s_xT, later(e, 1, s))
                        for k in range(KD):
                            ins = nc.tensor.transpose(pT[s % 2][:, k * P:(k + 1) * P], xb[q][:, k * P:(k + 1) * P], ident_sb[:, :])
                        ins.then_inc(s_T, 1)
                    if 1 <= s <= U:
                        j = s - 1
                        e = r * U + j
                        pe.wait_ge(s_xT, e + 1)
                        pe.wait_ge(s_h, later(e, 1, j))
                        for k in range(KD):
                            ins = nc.tensor.matmul(pG[j % 2][:, 0:2 * FF], xT[j % 2][:, k * P:(k + 1) * P], gu[j % BUF][:, k, :], start=(k == 0), stop=(k == KD - 1))
                        ins.then_inc(s_G, 1)
                    if 2 <= s <= U + 1:
                        j = s - 2
                        e = r * U + j
                        pe.wait_ge(s_h, e + 1)
                        pe.wait_ge(s_hT, 2 * later(e, 1, j))
                        nc.tensor.transpose(pH[j % 2][:, 0:P], h_sb[j % 2][:, 0:P], ident_sb[:, :])
                        nc.tensor.transpose(pH[j % 2][0:F2, P:2 * P], h_sb[j % 2][:, P:FF], ident_sb[:, :]).then_inc(s_H, 1)
                    if s >= 3:
                        j = s - 3
                        e = r * U + j
                        pe.wait_ge(s_hT, 2 * e + 2)
                        pe.wait_ge(s_y, later(e, 1, j))
                        nc.tensor.matmul(pY[j % 2][:, :], hT[j % 2][:, 0, :], wd[j % BUF][:, 0, :], start=True, stop=False)
                        nc.tensor.matmul(pY[j % 2][:, :], hT[j % 2][0:F2, 1, :], wd[j % BUF][0:F2, 1, :], start=False, stop=True).then_inc(s_Y, 1)


def gather_mix_norm(nc, name, K, y_slots, slots, x_tok, places, weights, ident, o_tok, o_feat):
    LN_EPS = 1e-5
    with ExitStack() as phase:
        m = Space(nc, name, phase)
        ident_sb, eps_sb = m.sb("ident", [P, P]), m.sb("eps", [P, 1])
        x_sb = [m.sb(f"x{i}", [P, D]) for i in range(2)]
        pl = [m.sb(f"pl{i}", [P, K], U32) for i in range(2)]
        wk = [m.sb(f"wk{i}", [P, K]) for i in range(2)]
        g = [m.sb(f"g{i}", [P, K, D]) for i in range(2)]
        st, mv, sd = m.sb("st", [P, 6]), m.sb("mv", [P, 2]), m.sb("sd", [P, 1])
        o_sb = [m.sb(f"o{i}", [P, D]) for i in range(2)]
        oT = [m.sb(f"oT{i}", [P, KD, P]) for i in range(2)]
        po = [m.ps(f"po{i}") for i in range(2)]
        s_const, s_set, s_lv = m.sem("const"), m.sem("set"), m.sem("lv")
        s_in = [m.sem(f"in{i}") for i in range(2)]
        s_g = [m.sem(f"g{i}") for i in range(2)]
        s_out = [m.sem(f"out{i}") for i in range(2)]
        s_var, s_sd, s_ln, s_oT, s_oc = (m.sem(n) for n in "var sd ln oT oc".split())
        tick_dve, tick_pool, tick_sp = m.sem("tick_dve"), m.sem("tick_pool"), m.sem("tick_sp")
        block = phase.enter_context(nc.Block())
        LV = K + 2

        @block.sync
        def _(sp):
            sp.dma_start(ident_sb[:, :], ident).then_inc(s_const, 16)
            with sp.Fori(0, TILES // 2) as r:
                for i in range(2):
                    t = 2 * r + i
                    sp.wait_ge(s_ln, 2 * r)
                    for dst, src in ((x_sb, x_tok), (pl, places), (wk, weights)):
                        sp.dma_start(dst[i][:, :], src[bass.ds(t * P, P), :]).then_inc(s_in[i], 16)
                for i in range(2):
                    t = 2 * r + i
                    sp.wait_ge(s_ln, t + 1)
                    sp.dma_start(o_tok[bass.ds(t * P, P), :], o_sb[i][:, :]).then_inc(s_out[i], 16)
                    if o_feat is not None:
                        sp.wait_ge(s_oc, t + 1)
                        alone(sp, tick_sp)
                        sp.dma_start(o_feat[:, :, bass.ds(t * P, P)].rearrange("k p t -> p k t"), oT[i][:, :, :]).then_inc(s_out[i], 16)
            for i in range(2):
                sp.wait_ge(s_out[i], TILES // 2 * (16 if o_feat is None else 32))
        stores = 16 if o_feat is None else 32

        @block.gpsimd
        def _(pool):
            pool.wait_ge(s_set, 3)
            with pool.Fori(0, TILES // 2) as r:
                for i in range(2):
                    pool.wait_ge(s_in[i], r * 48 + 48)
                    pool.wait_ge(s_ln, 2 * r)
                    alone(pool, tick_pool)
                    for k in range(K):
                        pool.indirect_dma_start(g[i][:, k, :], None, y_slots, bass.IndirectOffsetOnAxis(ap=pl[i][:, k:k + 1], axis=0),
                                                bounds_check=slots - 1, oob_is_err=False).then_inc(s_g[i], 16)

        @block.scalar
        def _(act):
            act.wait_ge(s_set, 1)
            with act.Fori(0, TILES // 2) as r:
                for i in range(2):
                    act.wait_ge(s_var, 2 * r + i + 1)
                    nc.scalar.activation(sd[:, :], mv[:, 1:2], ACT.Sqrt, bias=eps_sb[:, :], scale=1.0).then_inc(s_sd, 1)
                    if o_feat is not None:
                        act.wait_ge(s_oT, 2 * r + i + 1)
                        act.wait_ge(s_out[i], r * stores)
                        nc.scalar.copy(oT[i][:, :, :].rearrange("p k t -> p (k t)"), po[i][:, :]).then_inc(s_oc, 1)

        @block.vector
        def _(dve):
            nc.vector.memset(eps_sb[:, :], LN_EPS).then_inc(s_set, 1)
            for i in range(2):
                nc.vector.memset(g[i][:, :, :], 0.0).then_inc(s_set, 1)
            dve.wait_ge(s_set, 3)
            with dve.Fori(0, TILES // 2) as r:
                for i in range(2):
                    t = 2 * r + i
                    link = linker(dve, s_lv, t * LV)
                    dve.wait_ge(s_in[i], r * 48 + 48)
                    dve.wait_ge(s_g[i], (r + 1) * K * 16)
                    x = x_sb[i][:, :]
                    for k in range(K):
                        link(nc.vector.scalar_tensor_tensor(x, g[i][:, k, :], wk[i][:, k:k + 1], x, ALU.mult, ALU.add))
                    link(nc.vector.bn_stats(st[:, :], x))
                    alone(dve, tick_dve)
                    nc.vector.bn_aggr(mv[:, :], st[:, :]).then_inc(s_var, 1)
                    dve.wait_ge(s_sd, t + 1)
                    link(nc.vector.reciprocal(sd[:, :], sd[:, :]))
                    dve.wait_ge(s_out[i], r * stores)
                    nc.vector.tensor_scalar(o_sb[i][:, :], x, mv[:, 0:1], sd[:, :], ALU.subtract, ALU.mult).then_inc(s_ln, 1)

        if o_feat is not None:
            @block.tensor
            def _(pe):
                pe.wait_ge(s_const, 16)
                with pe.Fori(0, TILES // 2) as r:
                    for i in range(2):
                        pe.wait_ge(s_ln, 2 * r + i + 1)
                        pe.wait_ge(s_oc, 2 * r)
                        for k in range(KD):
                            ins = nc.tensor.transpose(po[i][:, k * P:(k + 1) * P], o_sb[i][:, k * P:(k + 1) * P], ident_sb[:, :])
                        ins.then_inc(s_oT, 1)


DI1, N1 = 1024, 16
F1 = DI1 // P


def ssm1_project(nc, x_feat, w_in, conv_w, conv_b, w_x, w_dt, b_dt, u_feat, z_feat, dt_feat, bc_feat):
    with ExitStack() as phase:
        m = Space(nc, "d1", phase)
        w_sb = m.sb("w", [P, KD, 2 * DI1])
        wx_sb = m.sb("wx", [P, F1, P + 2 * N1])
        wdt_sb = m.sb("wdt", [P, DI1])
        cw_sb, cb_sb, bdt_sb = m.sb("cw", [P, F1, 4]), m.sb("cb", [P, F1]), m.sb("bdt", [P, F1])
        one_sb = m.sb("one", [P, 1])
        xT = [m.sb(f"xT{i}", [P, KD, L]) for i in range(2)]
        xpad = [m.sb(f"xpad{i}", [P, 3 + L]) for i in range(2)]
        acc = [m.sb(f"acc{i}", [P, L]) for i in range(2)]
        u_sb, z_sb, dt_sb = m.sb("u", [P, F1, L]), m.sb("z", [P, F1, L]), m.sb("dt", [P, F1, L])
        v_sb, r_sb = m.sb("v", [P, F1, L]), m.sb("r", [P, F1, L])
        dr_sb, bc_sb = m.sb("dr", [P, L]), m.sb("bc", [2 * N1, L])
        px = [m.ps(f"px{i}") for i in range(2)]
        pz = [m.ps(f"pz{i}") for i in range(2)]
        pd = [m.ps(f"pd{i}") for i in range(2)]
        pr, pb = m.ps("pr"), m.ps("pb")
        s_const, s_set, s_lv = m.sem("const"), m.sem("set"), m.sem("lv")
        s_x = [m.sem(f"x{i}") for i in range(2)]
        s_px, s_xpad, s_conv, s_u, s_pz, s_z, s_pr, s_dr, s_pb, s_bc, s_pd, s_v, s_r, s_la, s_dt, s_out = (
            m.sem(n) for n in "px xpad conv u pz z pr dr pb bc pd v r la dt out".split())
        block = phase.enter_context(nc.Block())
        CONSTS = 6

        @block.sync
        def _(sp):
            for dst, src in ((cw_sb[:, :, :], conv_w.rearrange("(k p) c -> p k c", p=P)), (cb_sb[:, :], conv_b.rearrange("(k p) -> p k", p=P)),
                             (bdt_sb[:, :], b_dt.rearrange("(k p) -> p k", p=P)), (w_sb[:, :, :], w_in.rearrange("(k p) n -> p k n", p=P)),
                             (wx_sb[:, :, :], w_x.rearrange("(k p) n -> p k n", p=P)), (wdt_sb[:, :], w_dt)):
                sp.dma_start(dst, src, allow_slow_non_contiguous=True).then_inc(s_const, 16)
            with sp.Fori(0, NB // 2) as r:
                for i in range(2):
                    b = 2 * r + i
                    sp.wait_ge(s_pz, 2 * r * F1)
                    sp.dma_start(xT[i][:, :, :], x_feat[:, :, bass.ds(b * L, L)].rearrange("k p t -> p k t")).then_inc(s_x[i], 16)
                for i in range(2):
                    b = 2 * r + i
                    for s, src, dst, n in ((s_u, u_sb, u_feat, F1), (s_z, z_sb, z_feat, F1), (s_dt, dt_sb, dt_feat, 1)):
                        sp.wait_ge(s, b * n + n)
                        sp.dma_start(dst[:, :, bass.ds(b * L, L)].rearrange("k p t -> p k t"), src[:, :, :]).then_inc(s_out, 16)
                    sp.wait_ge(s_bc, b + 1)
                    sp.dma_start(bc_feat[:, bass.ds(b * L, L)], bc_sb[:, :]).then_inc(s_out, 16)
            sp.wait_ge(s_out, NB * 64)

        @block.scalar
        def _(act):
            act.wait_ge(s_const, 16 * CONSTS)
            act.wait_ge(s_set, 3)
            with act.Fori(0, NB) as b:
                act.wait_ge(s_out, b * 64)
                for f in range(F1 + 1):
                    if f < F1:
                        act.wait_ge(s_px, b * F1 + f + 1)
                        act.wait_ge(s_conv, b * F1 + max(f - 1, 0))
                        nc.scalar.copy(xpad[f % 2][:, 3:3 + L], px[f % 2][:, 0:L]).then_inc(s_xpad, 1)
                    if f >= 1:
                        g = f - 1
                        act.wait_ge(s_conv, b * F1 + g + 1)
                        nc.scalar.activation(u_sb[:, g, :], acc[g % 2][:, :], ACT.Silu, bias=cb_sb[:, g:g + 1]).then_inc(s_u, 1)
                for f in range(F1):
                    act.wait_ge(s_pz, b * F1 + f + 1)
                    nc.scalar.activation(z_sb[:, f, :], pz[f % 2][:, 0:L], ACT.Silu).then_inc(s_z, 1)
                act.wait_ge(s_dt, b)
                for f in range(F1):
                    act.wait_ge(s_pd, b * F1 + f + 1)
                    nc.scalar.activation(v_sb[:, f, :], pd[f % 2][:, 0:L], ACT.Abs, bias=bdt_sb[:, f:f + 1], scale=1.0).then_inc(s_v, 1)
                    nc.scalar.activation(r_sb[:, f, :], pd[f % 2][:, 0:L], ACT.Relu, bias=bdt_sb[:, f:f + 1], scale=1.0).then_inc(s_v, 1)
                act.wait_ge(s_v, (b + 1) * 2 * F1)
                link = linker(act, s_la, b)
                link(nc.scalar.activation(v_sb[:, :, :], v_sb[:, :, :], ACT.Exp, scale=-1.0))
                nc.scalar.activation(v_sb[:, :, :], v_sb[:, :, :], ACT.Ln, bias=one_sb[:, :], scale=1.0).then_inc(s_r, 1)

        @block.vector
        def _(dve):
            for i in range(2):
                nc.vector.memset(xpad[i][:, 0:3], 0.0).then_inc(s_set, 1)
            nc.vector.memset(one_sb[:, :], 1.0).then_inc(s_set, 1)
            dve.wait_ge(s_set, 3)
            dve.wait_ge(s_const, 16 * CONSTS)
            with dve.Fori(0, NB) as b:
                link = linker(dve, s_lv, b * 3 * F1)
                for f in range(F1):
                    a, xp = acc[f % 2], xpad[f % 2]
                    dve.wait_ge(s_xpad, b * F1 + f + 1)
                    dve.wait_ge(s_u, b * F1 + max(f - 1, 0))
                    link(nc.vector.tensor_scalar(a[:, :], xp[:, 3:3 + L], cw_sb[:, f, 3:4], None, ALU.mult))
                    for j in (2, 1):
                        link(nc.vector.scalar_tensor_tensor(a[:, :], xp[:, j:j + L], cw_sb[:, f, j:j + 1], a[:, :], ALU.mult, ALU.add))
                    nc.vector.scalar_tensor_tensor(a[:, :], xp[:, 0:L], cw_sb[:, f, 0:1], a[:, :], ALU.mult, ALU.add).then_inc(s_conv, 1)
                dve.wait_ge(s_pr, b + 1)
                nc.vector.tensor_copy(dr_sb[:, :], pr[:, 0:L]).then_inc(s_dr, 1)
                dve.wait_ge(s_pb, b + 1)
                dve.wait_ge(s_out, b * 64)
                nc.vector.tensor_copy(bc_sb[:, :], pb[0:2 * N1, 0:L]).then_inc(s_bc, 1)
                dve.wait_ge(s_r, b + 1)
                nc.vector.tensor_tensor(dt_sb[:, :, :], v_sb[:, :, :], r_sb[:, :, :], ALU.add).then_inc(s_dt, 1)

        @block.tensor
        def _(pe):
            pe.wait_ge(s_const, 16 * CONSTS)
            with pe.Fori(0, NB // 2) as r:
                for i in range(2):
                    b = 2 * r + i
                    pe.wait_ge(s_x[i], r * 16 + 16)
                    for f in range(F1):
                        pe.wait_ge(s_xpad, b * F1 + max(f - 1, 0))
                        for k in range(KD):
                            ins = nc.tensor.matmul(px[f % 2][:, 0:L], w_sb[:, k, f * P:(f + 1) * P], xT[i][:, k, :], start=(k == 0), stop=(k == KD - 1))
                        ins.then_inc(s_px, 1)
                    for f in range(F1):
                        pe.wait_ge(s_z, b * F1 + max(f - 1, 0))
                        for k in range(KD):
                            ins = nc.tensor.matmul(pz[f % 2][:, 0:L], w_sb[:, k, DI1 + f * P:DI1 + (f + 1) * P], xT[i][:, k, :], start=(k == 0), stop=(k == KD - 1))
                        ins.then_inc(s_pz, 1)
                    pe.wait_ge(s_u, b * F1 + F1)
                    pe.wait_ge(s_dr, b)
                    for k in range(F1):
                        ins = nc.tensor.matmul(pr[:, 0:L], wx_sb[:, k, 0:P], u_sb[:, k, :], start=(k == 0), stop=(k == F1 - 1))
                    ins.then_inc(s_pr, 1)
                    pe.wait_ge(s_bc, b)
                    for k in range(F1):
                        ins = nc.tensor.matmul(pb[0:2 * N1, 0:L], wx_sb[:, k, P:P + 2 * N1], u_sb[:, k, :], start=(k == 0), stop=(k == F1 - 1))
                    ins.then_inc(s_pb, 1)
                    pe.wait_ge(s_dr, b + 1)
                    for f in range(F1):
                        pe.wait_ge(s_v, (b * F1 + max(f - 1, 0)) * 2)
                        nc.tensor.matmul(pd[f % 2][:, 0:L], wdt_sb[:, f * P:(f + 1) * P], dr_sb[:, :], start=True, stop=True).then_inc(s_pd, 1)


def ssm1_scan(nc, x_tok, u_feat, z_feat, dt_feat, bc_feat, a_log, skip, w_out, ident, o_tok, o_feat):
    LN_EPS = 1e-5
    G = 4
    Q = N1 // G
    C = F1 * Q
    RB, RH = 4, 4
    with ExitStack() as phase:
        m = Space(nc, "d2", phase)
        ident_sb, eps_sb, zero_sb = m.sb("ident", [P, P]), m.sb("eps", [P, 1]), m.sb("zero", [P, G])
        A_sb, D_sb = m.sb("A", [P, F1, N1]), m.sb("D", [P, F1])
        wo_sb = m.sb("wo", [P, F1, D])
        B_sb = [m.sb(f"B{i}", [P, N1, L]) for i in range(2)]
        C_sb = [m.sb(f"C{i}", [P, N1, L]) for i in range(2)]
        u_sb = [m.sb(f"u{i}", [P, F1, L]) for i in range(2)]
        z_sb = m.sb("z", [P, F1, L])
        dt_sb = [m.sb(f"dt{i}", [P, F1, L]) for i in range(2)]
        dtu = [m.sb(f"dtu{i}", [P, L]) for i in range(2)]
        dBu = [m.sb(f"dBu{i}", [P, G, L]) for i in range(RB)]
        hC = [m.sb(f"hC{i}", [P, G, L]) for i in range(RH)]
        t_sb = [m.sb(f"t{i}", [P, L]) for i in range(2)]
        yz = m.sb("yz", [P, F1, L])
        x_sb = m.sb("x", [P, 2, D])
        st, mv, sd = m.sb("st", [P, 2, 6]), m.sb("mv", [P, 2, 2]), m.sb("sd", [P, 2])
        oT = m.sb("oT", [P, 2, KD, P])
        ph = [m.ps(f"ph{i}", (P, G, L)) for i in range(2)]
        py = [m.ps(f"py{i}") for i in range(2)]
        po = [m.ps(f"po{i}") for i in range(2)]
        s_const, s_set, s_lv, s_A = m.sem("const"), m.sem("set"), m.sem("lv"), m.sem("A")
        s_B = [m.sem(f"ldB{i}") for i in range(2)]
        s_dt = [m.sem(f"lddt{i}") for i in range(2)]
        s_C, s_z, s_x, s_out = (m.sem("ld" + n) for n in "C z x out".split())
        s_dtu, s_dA, s_dBu, s_scan, s_hC, s_py, s_sum, s_yz, s_o, s_var, s_sd, s_ln, s_T, s_oc = (
            m.sem(n) for n in "dtu dA dBu scan hC py sum yz o var sd ln T oc".split())
        tick_dve, tick_sp = m.sem("tick_dve"), m.sem("tick_sp")
        block = phase.enter_context(nc.Block())
        CONSTS = 4

        def feat(a, b):
            return a[:, :, bass.ds(b * L, L)].rearrange("k p t -> p k t")

        def later(b, done, per, back):
            return b * per + max(done - back, 0)

        @block.sync
        def _(sp):
            for dst, src in ((ident_sb[:, :], ident), (A_sb[:, :, :], a_log.rearrange("(k p) n -> p k n", p=P)),
                             (D_sb[:, :], skip.rearrange("(k p) -> p k", p=P)), (wo_sb[:, :, :], w_out.rearrange("(k p) n -> p k n", p=P))):
                sp.dma_start(dst, src, allow_slow_non_contiguous=True).then_inc(s_const, 16)
            def inputs(b, i):
                sp.dma_start(dt_sb[i][:, :, :], feat(dt_feat, b)).then_inc(s_dt[i], 16)
                sp.dma_start(u_sb[i][:, :, :], feat(u_feat, b)).then_inc(s_dt[i], 16)
                sp.dma_start(B_sb[i][:, :, :], bc_feat[0:N1, bass.ds(b * L, L)].partition_broadcast(P)).then_inc(s_B[i], 16)
                sp.dma_start(C_sb[i][:, :, :], bc_feat[N1:2 * N1, bass.ds(b * L, L)].partition_broadcast(P)).then_inc(s_B[i], 16)

            def batch(b):
                sp.wait_ge(s_yz, b * F1)
                alone(sp, tick_sp)
                sp.dma_start(z_sb[:, :, :], feat(z_feat, b)).then_inc(s_z, 16)
                sp.wait_ge(s_T, b * 2)
                alone(sp, tick_sp)
                sp.wait_ge(s_out, b * 48)
                alone(sp, tick_sp)
                sp.dma_start(x_sb[:, :, :], x_tok[bass.ds(b * L, L), :].rearrange("(c p) n -> p c n", p=P)).then_inc(s_x, 16)
                sp.wait_ge(s_oc, b * 2 + 2)
                alone(sp, tick_sp)
                sp.dma_start(o_tok[bass.ds(b * L, L), :].rearrange("(c p) n -> p c n", p=P), x_sb[:, :, :]).then_inc(s_out, 16)
                for c in range(2):
                    sp.dma_start(o_feat[:, :, bass.ds(b * L + c * P, P)].rearrange("k p t -> p k t"), oT[:, c, :, :]).then_inc(s_out, 16)
            for i in range(2):
                inputs(i, i)
            with sp.Fori(0, NB // 2 - 1) as r:
                for i in range(2):
                    b = 2 * r + i
                    batch(b)
                    sp.wait_ge(s_dA, b * C + C)
                    alone(sp, tick_sp)
                    sp.wait_ge(s_yz, b * F1 + F1)
                    alone(sp, tick_sp)
                    inputs(b + 2, i)
            for i in range(2):
                batch(NB - 2 + i)
            sp.wait_ge(s_out, NB * 48)

        @block.gpsimd
        def _(pool):
            with pool.Fori(0, NB // 2) as r:
                for i in range(2):
                    b = 2 * r + i
                    pool.wait_ge(s_B[i], r * 32 + 32)
                    for c in range(C):
                        f, q = c // Q, c % Q
                        pool.wait_ge(s_dtu, b * F1 + f + 1)
                        pool.wait_ge(s_scan, later(b, c, C, RB - 1))
                        pool.tensor_tensor(dBu[c % RB][:, :, :], B_sb[i][:, q * G:(q + 1) * G, :],
                                           dtu[f % 2][:, :].unsqueeze(1).to_broadcast([P, G, L]), ALU.mult).then_inc(s_dBu, 1)

        @block.scalar
        def _(act):
            act.wait_ge(s_const, 16 * CONSTS)
            act.wait_ge(s_set, 2)
            nc.scalar.activation(A_sb[:, :, :], A_sb[:, :, :], ACT.Exp).then_inc(s_A, 1)
            act.wait_ge(s_A, 2)
            with act.Fori(0, NB // 2) as r:
                for i in range(2):
                    b = 2 * r + i
                    act.wait_ge(s_dt[i], r * 32 + 32)
                    for c in range(C):
                        f, q = c // Q, c % Q
                        act.wait_ge(s_hC, later(b, c, C, 1))
                        nc.scalar.copy(ph[c % 2][:, :, 0:1], zero_sb[:, :].unsqueeze(2))
                        for n in range(G):
                            ins = nc.scalar.activation(ph[c % 2][:, n, 1:L], dt_sb[i][:, f, 1:L], ACT.Exp, scale=A_sb[:, f, q * G + n:q * G + n + 1])
                        ins.then_inc(s_dA, 1)
                    act.wait_ge(s_var, b * 2 + 2)
                    nc.scalar.activation(sd[:, :], mv[:, :, 1], ACT.Sqrt, bias=eps_sb[:, :], scale=1.0).then_inc(s_sd, 1)
                    act.wait_ge(s_out, b * 48)
                    for c in range(2):
                        act.wait_ge(s_T, b * 2 + c + 1)
                        nc.scalar.copy(oT[:, c, :, :].rearrange("p k t -> p (k t)"), py[c][:, :]).then_inc(s_oc, 1)

        @block.vector
        def _(dve):
            nc.vector.memset(eps_sb[:, :], LN_EPS).then_inc(s_set, 1)
            nc.vector.memset(zero_sb[:, :], 0.0).then_inc(s_set, 1)
            dve.wait_ge(s_set, 2)
            dve.wait_ge(s_A, 1)
            nc.vector.tensor_scalar(A_sb[:, :, :], A_sb[:, :, :], -1.0, None, ALU.mult).then_inc(s_A, 1)
            LV = 5
            with dve.Fori(0, NB // 2) as r:
                for i in range(2):
                    b = 2 * r + i
                    link = linker(dve, s_lv, b * LV)
                    dve.wait_ge(s_dt[i], r * 32 + 32)
                    dve.wait_ge(s_B[i], r * 32 + 32)

                    def step_sizes(f):
                        dve.wait_ge(s_dBu, later(b, f * Q, C, Q))
                        nc.vector.tensor_tensor(dtu[f % 2][:, :], dt_sb[i][:, f, :], u_sb[i][:, f, :], ALU.mult).then_inc(s_dtu, 1)

                    def channel_out(g):
                        dve.wait_ge(s_py, b * C + (g + 1) * Q)
                        dve.wait_ge(s_yz, later(b, g, F1, 1))
                        nc.vector.scalar_tensor_tensor(t_sb[g % 2][:, :], u_sb[i][:, g, :], D_sb[:, g:g + 1], py[g % 2][:, 0:L], ALU.mult, ALU.add).then_inc(s_sum, 1)
                        dve.wait_ge(s_sum, b * F1 + g + 1)
                        dve.wait_ge(s_o, b * 2)
                        nc.vector.tensor_tensor(yz[:, g, :], t_sb[g % 2][:, :], z_sb[:, g, :], ALU.mult).then_inc(s_yz, 1)
                    step_sizes(0)
                    for c in range(C):
                        f, q = c // Q, c % Q
                        if q == 0 and f + 1 < F1:
                            step_sizes(f + 1)
                        dve.wait_ge(s_dA, b * C + c + 1)
                        dve.wait_ge(s_dBu, b * C + c + 1)
                        h = ph[c % 2][:, :, :].rearrange("p n t -> p (n t)")
                        nc.vector.tensor_tensor_scan(h, h, dBu[c % RB][:, :, :].rearrange("p n t -> p (n t)"), 0.0, ALU.mult, ALU.add).then_inc(s_scan, 1)
                        dve.wait_ge(s_scan, b * C + c + 1)
                        dve.wait_ge(s_py, later(b, c, C, RH - 1))
                        nc.vector.tensor_tensor(hC[c % RH][:, :, :], ph[c % 2][:, :, :], C_sb[i][:, q * G:(q + 1) * G, :], ALU.mult).then_inc(s_hC, 1)
                        if q == 1 and f >= 1:
                            if f == 1:
                                dve.wait_ge(s_z, b * 16 + 16)
                            channel_out(f - 1)
                    channel_out(F1 - 1)
                    dve.wait_ge(s_x, b * 16 + 16)
                    for c in range(2):
                        dve.wait_ge(s_o, b * 2 + c + 1)
                        link(nc.vector.tensor_tensor(x_sb[:, c, :], x_sb[:, c, :], po[c][:, :], ALU.add))
                        link(nc.vector.bn_stats(st[:, c, :], x_sb[:, c, :]))
                        alone(dve, tick_dve)
                        nc.vector.bn_aggr(mv[:, c, :], st[:, c, :]).then_inc(s_var, 1)
                    dve.wait_ge(s_sd, b + 1)
                    link(nc.vector.reciprocal(sd[:, :], sd[:, :]))
                    for c in range(2):
                        nc.vector.tensor_scalar(x_sb[:, c, :], x_sb[:, c, :], mv[:, c, 0:1], sd[:, c:c + 1], ALU.subtract, ALU.mult).then_inc(s_ln, 1)
                    assert link.count[0] == LV

        @block.tensor
        def _(pe):
            pe.wait_ge(s_const, 16 * CONSTS)
            with pe.Fori(0, NB) as b:

                def project(g):
                    pe.wait_ge(s_yz, b * F1 + g + 1)
                    if g == 0:
                        pe.wait_ge(s_var, b * 2)
                    for c in range(2):
                        ins = nc.tensor.matmul(po[c][:, :], yz[:, g, c * P:(c + 1) * P], wo_sb[:, g, :], start=(g == 0), stop=(g == F1 - 1))
                        if g == F1 - 1:
                            ins.then_inc(s_o, 1)
                for c in range(C):
                    f, q = c // Q, c % Q
                    pe.wait_ge(s_hC, b * C + c + 1)
                    if q == 0:
                        pe.wait_ge(s_sum, later(b, f, F1, 1))
                        pe.wait_ge(s_oc, b * 2)
                    for n in range(G):
                        ins = nc.tensor.matmul(py[f % 2][:, 0:L], ident_sb[:, :], hC[c % RH][:, n, :], start=(q == 0 and n == 0), stop=(q == Q - 1 and n == G - 1))
                    ins.then_inc(s_py, 1)
                    if q == 2 and f >= 2:
                        project(f - 2)
                project(F1 - 2)
                project(F1 - 1)
                for c in range(2):
                    pe.wait_ge(s_ln, b * 2 + c + 1)
                    for k in range(KD):
                        ins = nc.tensor.transpose(py[c][:, k * P:(k + 1) * P], x_sb[:, c, k * P:(k + 1) * P], ident_sb[:, :])
                    ins.then_inc(s_T, 1)


def linear_attention(nc, x_tok, x_feat, ctx_feat, w_q, w_g, b_g, w_kv, w_o, ident, heads_mask, o_tok, o_feat):
    LN_EPS, EPS = 1e-5, 1e-6
    with ExitStack() as phase:
        m = Space(nc, "e1", phase)
        ident_sb, eps_sb, mask_sb, ones = m.sb("ident", [P, P]), m.sb("eps", [P, 1]), m.sb("mask", [P, P]), m.sb("ones", [P, P])
        wq, wg, wo = m.sb("wq", [P, KD, D]), m.sb("wg", [P, KD, D]), m.sb("wo", [P, KD, D])
        wkv = m.sb("wkv", [P, KD, 2 * D])
        bg_sb = m.sb("bg", [P, KD])
        xf = [m.sb(f"xf{i}", [P, KD, L]) for i in range(2)]
        cf = [m.sb(f"cf{i}", [P, KD, L]) for i in range(2)]
        xt = [m.sb(f"xt{i}", [P, 2, D]) for i in range(2)]
        k_sb, v_sb = m.sb("k", [P, 2, D]), m.sb("v", [P, 2, D])
        kneg = [m.sb(f"kneg{i}", [P, D]) for i in range(2)]
        q_sb, g_sb = m.sb("q", [P, KD, L]), m.sb("g", [P, KD, L])
        qneg = [m.sb(f"qneg{i}", [P, L]) for i in range(2)]
        kv_sb, ks_sb = m.sb("kv", [P, KD, P]), m.sb("ks", [P, KD, P])
        den = m.sb("den", [P, KD, L])
        ag = m.sb("ag", [P, KD, L])
        st, mv, sd = m.sb("st", [P, 2, 6]), m.sb("mv", [P, 2, 2]), m.sb("sd", [P, 2])
        o_sb, oT = m.sb("o", [P, 2, D]), m.sb("oT", [P, 2, KD, P])
        pa = [m.ps(f"pa{i}") for i in range(2)]
        pb = [m.ps(f"pb{i}") for i in range(2)]
        ps = [m.ps(f"ps{i}") for i in range(2)]
        po = [m.ps(f"po{i}") for i in range(2)]
        s_const, s_set, s_lv, s_out = m.sem("const"), m.sem("set"), m.sem("lv"), m.sem("out")
        s_in = [m.sem(f"in{i}") for i in range(2)]
        s_pk, s_kn, s_k, s_pv, s_v, s_pq, s_qn, s_q, s_pg, s_g, s_ps, s_kv, s_pa, s_ag, s_o, s_var, s_sd, s_ln, s_T, s_oc, s_ke, s_qe = (
            m.sem(n) for n in "pk kn k pv v pq qn q pg g ps kv pa ag o var sd ln T oc ke qe".split())
        tick_dve = m.sem("tick_dve")
        block = phase.enter_context(nc.Block())
        CONSTS = 7

        @block.sync
        def _(sp):
            for dst, src in ((ident_sb[:, :], ident), (mask_sb[:, :], heads_mask), (bg_sb[:, :], b_g.rearrange("(k p) -> p k", p=P)),
                             (wkv[:, :, :], w_kv.rearrange("(k p) n -> p k n", p=P)), (wq[:, :, :], w_q.rearrange("(k p) n -> p k n", p=P)),
                             (wg[:, :, :], w_g.rearrange("(k p) n -> p k n", p=P)), (wo[:, :, :], w_o.rearrange("(k p) n -> p k n", p=P))):
                sp.dma_start(dst, src, allow_slow_non_contiguous=True).then_inc(s_const, 16)
            with sp.Fori(0, NB // 2) as r:
                for i in range(2):
                    b = 2 * r + i
                    sp.wait_ge(s_ln, 4 * r)
                    sp.dma_start(cf[i][:, :, :], ctx_feat[:, :, bass.ds(b * L, L)].rearrange("k p t -> p k t")).then_inc(s_in[i], 16)
                    sp.dma_start(xf[i][:, :, :], x_feat[:, :, bass.ds(b * L, L)].rearrange("k p t -> p k t")).then_inc(s_in[i], 16)
                    sp.dma_start(xt[i][:, :, :], x_tok[bass.ds(b * L, L), :].rearrange("(c p) n -> p c n", p=P)).then_inc(s_in[i], 16)
                for i in range(2):
                    b = 2 * r + i
                    sp.wait_ge(s_oc, b * 2 + 2)
                    sp.dma_start(o_tok[bass.ds(b * L, L), :].rearrange("(c p) n -> p c n", p=P), o_sb[:, :, :]).then_inc(s_out, 16)
                    for c in range(2):
                        sp.dma_start(o_feat[:, :, bass.ds(b * L + c * P, P)].rearrange("k p t -> p k t"), oT[:, c, :, :]).then_inc(s_out, 16)
            sp.wait_ge(s_out, NB * 48)

        @block.scalar
        def _(act):
            act.wait_ge(s_const, 16 * CONSTS)
            act.wait_ge(s_set, 3)
            with act.Fori(0, NB) as b:
                for c in range(2):
                    act.wait_ge(s_kn, b * 2 + c + 1)
                    nc.scalar.activation(kneg[c][:, :], kneg[c][:, :], ACT.Exp).then_inc(s_ke, 1)
                for c in range(2):
                    act.wait_ge(s_pv, b * 2 + c + 1)
                    nc.scalar.copy(v_sb[:, c, :], pa[c][:, :]).then_inc(s_v, 1)
                for k in range(KD):
                    act.wait_ge(s_pg, b * KD + k + 1)
                    act.wait_ge(s_ag, b * KD)
                    nc.scalar.activation(g_sb[:, k, :], pb[k % 2][:, 0:L], ACT.Exp, bias=bg_sb[:, k:k + 1], scale=-1.0).then_inc(s_g, 1)
                    act.wait_ge(s_qn, b * KD + k + 1)
                    nc.scalar.activation(qneg[k % 2][:, :], qneg[k % 2][:, :], ACT.Exp).then_inc(s_qe, 1)
                act.wait_ge(s_var, b * 2 + 2)
                nc.scalar.activation(sd[:, :], mv[:, :, 1], ACT.Sqrt, bias=eps_sb[:, :], scale=1.0).then_inc(s_sd, 1)
                act.wait_ge(s_out, b * 48)
                for c in range(2):
                    act.wait_ge(s_T, b * 2 + c + 1)
                    nc.scalar.copy(oT[:, c, :, :].rearrange("p k t -> p (k t)"), ps[c][:, :]).then_inc(s_oc, 1)

        @block.vector
        def _(dve):
            nc.vector.memset(eps_sb[:, :], LN_EPS).then_inc(s_set, 1)
            nc.vector.memset(ones[:, :], 1.0).then_inc(s_set, 1)
            dve.wait_ge(s_set, 2)
            dve.wait_ge(s_const, 16 * CONSTS)
            nc.vector.tensor_scalar(bg_sb[:, :], bg_sb[:, :], -1.0, None, ALU.mult).then_inc(s_set, 1)
            LV = 3 * KD + 5
            with dve.Fori(0, NB // 2) as r:
                for i in range(2):
                    b = 2 * r + i
                    link = linker(dve, s_lv, b * LV)
                    for c in range(2):
                        dve.wait_ge(s_pk, b * 2 + c + 1)
                        nc.vector.tensor_scalar(kneg[c][:, :], pa[c][:, :], 0.0, None, ALU.min).then_inc(s_kn, 1)
                    for c in range(2):
                        dve.wait_ge(s_ke, b * 2 + c + 1)
                        nc.vector.scalar_tensor_tensor(k_sb[:, c, :], pa[c][:, :], 0.0, kneg[c][:, :], ALU.max, ALU.add).then_inc(s_k, 1)
                    for k in range(KD + 1):
                        if k < KD:
                            dve.wait_ge(s_pq, b * KD + k + 1)
                            dve.wait_ge(s_q, b * KD + max(k - 1, 0))
                            nc.vector.tensor_scalar(qneg[k % 2][:, :], pa[k % 2][:, 0:L], 0.0, None, ALU.min).then_inc(s_qn, 1)
                        if k >= 1:
                            j = k - 1
                            dve.wait_ge(s_qe, b * KD + j + 1)
                            nc.vector.scalar_tensor_tensor(q_sb[:, j, :], pa[j % 2][:, 0:L], 0.0, qneg[j % 2][:, :], ALU.max, ALU.add).then_inc(s_q, 1)
                    dve.wait_ge(s_ps, b + 1)
                    for j in range(KD):
                        nc.vector.tensor_tensor(kv_sb[:, j, :], ps[0][:, j * P:(j + 1) * P], mask_sb[:, :], ALU.mult).then_inc(s_kv, 1)
                        nc.vector.tensor_tensor(ks_sb[:, j, :], ps[1][:, j * P:(j + 1) * P], mask_sb[:, :], ALU.mult).then_inc(s_kv, 1)
                    for j in range(KD):
                        dve.wait_ge(s_pa, b * KD + j + 1)
                        n = pb[j % 2]
                        link(nc.vector.tensor_scalar(den[:, j, :], n[:, L:2 * L], EPS, None, ALU.add))
                        dve.wait_ge(s_g, b * KD + j + 1)
                        link(nc.vector.scalar_tensor_tensor(den[:, j, :], g_sb[:, j, :], 1.0, den[:, j, :], ALU.add, ALU.mult))
                        link(nc.vector.reciprocal(den[:, j, :], den[:, j, :]))
                        nc.vector.tensor_tensor(ag[:, j, :], n[:, 0:L], den[:, j, :], ALU.mult).then_inc(s_ag, 1)
                    dve.wait_ge(s_in[i], r * 48 + 48)
                    for c in range(2):
                        x = xt[i][:, c, :]
                        dve.wait_ge(s_o, b * 2 + c + 1)
                        link(nc.vector.tensor_tensor(x, x, po[c][:, :], ALU.add))
                        link(nc.vector.bn_stats(st[:, c, :], x))
                        alone(dve, tick_dve)
                        nc.vector.bn_aggr(mv[:, c, :], st[:, c, :]).then_inc(s_var, 1)
                    dve.wait_ge(s_sd, b + 1)
                    link(nc.vector.reciprocal(sd[:, :], sd[:, :]))
                    dve.wait_ge(s_out, b * 48)
                    for c in range(2):
                        nc.vector.tensor_scalar(o_sb[:, c, :], xt[i][:, c, :], mv[:, c, 0:1], sd[:, c:c + 1], ALU.subtract, ALU.mult).then_inc(s_ln, 1)
                    assert link.count[0] == LV

        @block.tensor
        def _(pe):
            pe.wait_ge(s_const, 16 * CONSTS)
            pe.wait_ge(s_set, 2)
            with pe.Fori(0, NB // 2) as r:
                for i in range(2):
                    b = 2 * r + i
                    pe.wait_ge(s_in[i], r * 48 + 48)
                    pe.wait_ge(s_q, b * KD)
                    for c in range(2):
                        for k in range(KD):
                            ins = nc.tensor.matmul(pa[c][:, :], cf[i][:, k, c * P:(c + 1) * P], wkv[:, k, 0:D], start=(k == 0), stop=(k == KD - 1))
                        ins.then_inc(s_pk, 1)
                    pe.wait_ge(s_ag, b * KD)
                    for c in range(2):
                        pe.wait_ge(s_k, b * 2 + c + 1)
                        for k in range(KD):
                            ins = nc.tensor.matmul(pa[c][:, :], cf[i][:, k, c * P:(c + 1) * P], wkv[:, k, D:2 * D], start=(k == 0), stop=(k == KD - 1))
                        ins.then_inc(s_pv, 1)
                    for j in range(KD):
                        pe.wait_ge(s_g, b * KD + max(j - 1, 0))
                        for k in range(KD):
                            ins = nc.tensor.matmul(pb[j % 2][:, 0:L], wg[:, k, j * P:(j + 1) * P], xf[i][:, k, :], start=(k == 0), stop=(k == KD - 1))
                        ins.then_inc(s_pg, 1)
                        if j < 2:
                            pe.wait_ge(s_v, b * 2 + j + 1)
                        else:
                            pe.wait_ge(s_q, b * KD + j - 1)
                        for k in range(KD):
                            ins = nc.tensor.matmul(pa[j % 2][:, 0:L], wq[:, k, j * P:(j + 1) * P], xf[i][:, k, :], start=(k == 0), stop=(k == KD - 1))
                        ins.then_inc(s_pq, 1)
                    pe.wait_ge(s_oc, b * 2)
                    for j in range(KD):
                        g = slice(j * P, (j + 1) * P)
                        for c in range(2):
                            nc.tensor.matmul(ps[0][:, g], k_sb[:, c, g], v_sb[:, c, g], start=(c == 0), stop=(c == 1))
                        for c in range(2):
                            ins = nc.tensor.matmul(ps[1][:, g], k_sb[:, c, g], ones[:, :], start=(c == 0), stop=(c == 1))
                    ins.then_inc(s_ps, 1)
                    pe.wait_ge(s_kv, (b + 1) * 2 * KD)
                    pe.wait_ge(s_q, b * KD + KD)
                    pe.wait_ge(s_g, b * KD + KD)
                    for j in range(KD):
                        pe.wait_ge(s_ag, b * KD + max(j - 1, 0))
                        nc.tensor.matmul(pb[j % 2][:, 0:L], kv_sb[:, j, :], q_sb[:, j, :], start=True, stop=True)
                        nc.tensor.matmul(pb[j % 2][:, L:2 * L], ks_sb[:, j, :], q_sb[:, j, :], start=True, stop=True).then_inc(s_pa, 1)
                    pe.wait_ge(s_ag, b * KD + KD)
                    pe.wait_ge(s_var, 2 * b)
                    for c in range(2):
                        for k in range(KD):
                            ins = nc.tensor.matmul(po[c][:, :], ag[:, k, c * P:(c + 1) * P], wo[:, k, :], start=(k == 0), stop=(k == KD - 1))
                        ins.then_inc(s_o, 1)
                    for c in range(2):
                        pe.wait_ge(s_ln, b * 2 + c + 1)
                        for k in range(KD):
                            ins = nc.tensor.transpose(ps[c][:, k * P:(k + 1) * P], o_sb[:, c, k * P:(k + 1) * P], ident_sb[:, :])
                        ins.then_inc(s_T, 1)


EX, TOP, SEL, HID = 4, 2, 512, 2048
FAR = 1 << 20


def moe1_route(nc, x_tok, x_feat, w_router, b_router, ident, before, ramp, scores, x_rows, places, weights):
    with ExitStack() as phase:
        m = Space(nc, "f1", phase)
        ident_sb, before_sb, ramp_sb = m.sb("ident", [P, P]), m.sb("before", [P, P]), m.sb("ramp", [P, EX])
        xf, xt = m.sb("xf", [P, KD, T]), m.sb("xt", [P, TILES, D])
        rw, rb = m.sb("rw", [P, KD, EX]), m.sb("rb", [P, EX])
        lg = m.sb("lg", [P, TILES, 8])
        top, idx, idf = m.sb("top", [P, TILES, 8]), m.sb("idx", [P, TILES, 8], U32), m.sb("idf", [P, TILES, TOP])
        pr = m.sb("pr", [P, TILES, TOP])
        e_sb, d_sb = m.sb("e", [P, TILES]), m.sb("d", [P, TILES])
        hot = m.sb("hot", [P, TILES, TOP, EX])
        wt = m.sb("wt", [P, TILES, TOP, EX])
        sc = m.sb("sc", [P, EX, TILES])
        scT = m.sb("scT", [EX * TILES, P])
        every = m.sb("every", [P, EX, T])
        cmp_ = [m.sb(f"cmp{i}", [P, T]) for i in range(2)]
        cnt = m.sb("cnt", [P, EX, TILES, 3])
        rank = m.sb("rank", [P, EX, TILES])
        rk, ok, far = m.sb("rk", [P, TILES, TOP]), m.sb("ok", [P, TILES, TOP]), m.sb("far", [P, TILES, TOP])
        pl = m.sb("pl", [P, TILES, TOP], U32)
        wk = m.sb("wk", [P, TILES, TOP])
        pL, pS = m.ps("pL"), m.ps("pS")
        s_const, s_x, s_xt, s_set, s_lv, s_log, s_d, s_e, s_sc, s_T, s_scT, s_scd, s_every, s_pl, s_scat, s_out, s_cmp = (
            m.sem(n) for n in "const x xt set lv log d e sc T scT scd every pl scat out cmp".split())
        block = phase.enter_context(nc.Block())

        @block.sync
        def _(sp):
            for dst, src in ((ident_sb[:, :], ident), (before_sb[:, :], before), (ramp_sb[:, :], ramp[0:EX].partition_broadcast(P)),
                             (rw[:, :, :], w_router.rearrange("(k p) e -> p k e", p=P)), (rb[:, :], b_router.partition_broadcast(P))):
                sp.dma_start(dst, src).then_inc(s_const, 16)
            sp.dma_start(xf[:, :, :], x_feat.rearrange("k p t -> p k t")).then_inc(s_x, 16)
            sp.dma_start(xt[:, :, :], x_tok.rearrange("(c p) n -> p c n", p=P)).then_inc(s_xt, 16)
            sp.wait_ge(s_scT, 1)
            sp.dma_start(scores.rearrange("e (c p) -> (e c) p", p=P), scT[:, :]).then_inc(s_scd, 16)
            sp.wait_ge(s_scd, 16)
            sp.dma_start(every[:, :, :], scores.partition_broadcast(P)).then_inc(s_every, 16)
            sp.wait_ge(s_pl, 2)
            sp.dma_start(places.rearrange("(c p) k -> p c k", p=P), pl[:, :, :], allow_slow_non_contiguous=True).then_inc(s_out, 16)
            sp.dma_start(weights.rearrange("(c p) k -> p c k", p=P), wk[:, :, :], allow_slow_non_contiguous=True).then_inc(s_out, 16)
            sp.wait_ge(s_out, 32)

        @block.gpsimd
        def _(pool):
            pool.wait_ge(s_xt, 16)
            pool.wait_ge(s_pl, 2)
            for c in range(TILES):
                for k in range(TOP):
                    pool.indirect_dma_start(x_rows, bass.IndirectOffsetOnAxis(ap=pl[:, c, k:k + 1], axis=0), xt[:, c, :], None,
                                            bounds_check=EX * SEL - 1, oob_is_err=False).then_inc(s_scat, 16)
            pool.wait_ge(s_scat, TILES * TOP * 16)

        @block.scalar
        def _(act):
            act.wait_ge(s_d, 1)
            nc.scalar.activation(e_sb[:, :], d_sb[:, :], ACT.Exp).then_inc(s_e, 1)

        @block.vector
        def _(dve):
            link = linker(dve, s_lv)
            link(nc.vector.memset(lg[:, :, :], -3.0e38))
            dve.wait_ge(s_const, 80)
            dve.wait_ge(s_log, 1)
            link(nc.vector.tensor_tensor(lg[:, :, 0:EX], pL[:, 0:TILES * EX].rearrange("p (c e) -> p c e", e=EX),
                                         rb[:, :].unsqueeze(1).to_broadcast([P, TILES, EX]), ALU.add))
            for c in range(TILES):
                ins = nc.vector.max(top[:, c, :], lg[:, c, :])
            link(ins)
            for c in range(TILES):
                ins = nc.vector.max_index(idx[:, c, :], top[:, c, :], lg[:, c, :])
            link(ins)
            nc.vector.tensor_tensor(d_sb[:, :], top[:, :, 1], top[:, :, 0], ALU.subtract).then_inc(s_d, 1)
            link(nc.vector.tensor_copy(idf[:, :, :], idx[:, :, 0:TOP]))
            link(nc.vector.tensor_tensor(hot[:, :, :, :].rearrange("p c k e -> p (c k) e"), ramp_sb[:, :].unsqueeze(1).to_broadcast([P, TILES * TOP, EX]),
                                         idf[:, :, :].rearrange("p c k -> p (c k)").unsqueeze(2).to_broadcast([P, TILES * TOP, EX]), ALU.is_equal))
            dve.wait_ge(s_e, 1)
            link(nc.vector.tensor_scalar(pr[:, :, 0], e_sb[:, :], 1.0, None, ALU.add))
            link(nc.vector.reciprocal(pr[:, :, 0], pr[:, :, 0]))
            link(nc.vector.tensor_tensor(pr[:, :, 1], pr[:, :, 0], e_sb[:, :], ALU.mult))
            link(nc.vector.tensor_tensor(wt[:, :, :, :].rearrange("p c k e -> p (c k) e"), hot[:, :, :, :].rearrange("p c k e -> p (c k) e"),
                                         pr[:, :, :].rearrange("p c k -> p (c k)").unsqueeze(2).to_broadcast([P, TILES * TOP, EX]), ALU.mult))
            link(nc.vector.tensor_tensor(sc[:, :, :], hot[:, :, 0, :].rearrange("p c e -> p e c"), hot[:, :, 1, :].rearrange("p c e -> p e c"), ALU.add))
            link(nc.vector.tensor_scalar(sc[:, :, :], sc[:, :, :], -1.0, None, ALU.add))
            link(nc.vector.tensor_tensor(sc[:, :, :], sc[:, :, :], wt[:, :, 0, :].rearrange("p c e -> p e c"), ALU.add))
            nc.vector.tensor_tensor(sc[:, :, :], sc[:, :, :], wt[:, :, 1, :].rearrange("p c e -> p e c"), ALU.add).then_inc(s_sc, 1)
            dve.wait_ge(s_sc, 1)
            dve.wait_ge(s_T, 1)
            nc.vector.tensor_copy(scT[:, :], pS[0:EX * TILES, 0:P]).then_inc(s_scT, 1)
            link(nc.vector.memset(cnt[:, :, :, :], 0.0))
            dve.wait_ge(s_every, 16)
            n = 0
            for e in range(EX):
                for c in range(TILES):
                    own = sc[:, e, c:c + 1]
                    at = slice(c * P, (c + 1) * P)
                    buf = cmp_[n % 2]
                    n += 1
                    if c:
                        nc.vector.tensor_scalar(buf[:, 0:c * P], every[:, e, 0:c * P], own, None, ALU.is_ge, ALU.add,
                                                accum_out=cnt[:, e, c, 0:1]).then_inc(s_cmp, 1)
                    nc.vector.tensor_scalar(buf[:, c * P:T], every[:, e, c * P:T], own, None, ALU.is_gt, ALU.add,
                                            accum_out=cnt[:, e, c, 1:2]).then_inc(s_cmp, 1)
                    done = n * 2 - (e + 1)
                    dve.wait_ge(s_cmp, done + (n - 1))
                    nc.vector.scalar_tensor_tensor(buf[:, at], every[:, e, at], own, before_sb[:, :], ALU.is_equal, ALU.mult,
                                                   accum_out=cnt[:, e, c, 2:3]).then_inc(s_cmp, 1)
            dve.wait_ge(s_cmp, EX * (3 * TILES - 1))
            link(nc.vector.tensor_reduce(rank[:, :, :].rearrange("p e c -> p (e c)"), cnt[:, :, :, :].rearrange("p e c n -> p (e c) n"), AX.X, ALU.add))
            for k in range(TOP):
                link(nc.vector.tensor_tensor(wt[:, :, k, :], hot[:, :, k, :], rank[:, :, :].rearrange("p e c -> p c e"), ALU.mult))
            link(nc.vector.tensor_reduce(rk[:, :, :].rearrange("p c k -> p (c k)"), wt[:, :, :, :].rearrange("p c k e -> p (c k) e"), AX.X, ALU.add))
            link(nc.vector.tensor_scalar(ok[:, :, :], rk[:, :, :], float(SEL), None, ALU.is_lt))
            link(nc.vector.tensor_scalar(far[:, :, :], ok[:, :, :], -float(FAR), float(FAR), ALU.mult, ALU.add))
            link(nc.vector.scalar_tensor_tensor(rk[:, :, :], idf[:, :, :], float(SEL), rk[:, :, :], ALU.mult, ALU.add))
            nc.vector.tensor_tensor(pl[:, :, :], rk[:, :, :], far[:, :, :], ALU.add).then_inc(s_pl, 1)
            nc.vector.tensor_tensor(wk[:, :, :], pr[:, :, :], ok[:, :, :], ALU.mult).then_inc(s_pl, 1)

        @block.tensor
        def _(pe):
            pe.wait_ge(s_const, 80)
            pe.wait_ge(s_x, 16)
            for c in range(TILES):
                for k in range(KD):
                    ins = nc.tensor.matmul(pL[:, c * EX:(c + 1) * EX], xf[:, k, c * P:(c + 1) * P], rw[:, k, :], start=(k == 0), stop=(k == KD - 1))
            ins.then_inc(s_log, 1)
            pe.wait_ge(s_sc, 1)
            nc.tensor.transpose(pS[0:EX * TILES, 0:P], sc[:, :, :].rearrange("p e c -> p (e c)"), ident_sb[:, :]).then_inc(s_T, 1)


def moe1_experts(nc, x_rows, w1, w2, ident, y_rows):
    HB, RT = HID // P, SEL // P
    with ExitStack() as phase:
        m = Space(nc, "f2", phase)
        ident_sb = m.sb("ident", [P, P])
        w1_sb, w2_sb = m.sb("w1", [P, KD, HID]), m.sb("w2", [P, HB, D])
        x_sb = m.sb("x", [P, RT, D])
        xT = m.sb("xT", [P, KD, SEL])
        hT = m.sb("hT", [P, HB, SEL])
        y_sb = m.sb("y", [P, RT, D])
        pT = [m.ps(f"pT{i}") for i in range(2)]
        ph = [m.ps(f"ph{i}") for i in range(3)]
        py = [m.ps(f"py{i}") for i in range(2)]
        s_const, s_w1, s_w2, s_x, s_T, s_xT, s_h, s_g, s_y, s_ye, s_out = (m.sem(n) for n in "const w1 w2 x T xT h g y ye out".split())
        block = phase.enter_context(nc.Block())

        @block.sync
        def _(sp):
            sp.dma_start(ident_sb[:, :], ident).then_inc(s_const, 16)
            with sp.Fori(0, EX) as e:
                sp.wait_ge(s_T, e * KD)
                sp.dma_start(x_sb[:, :, :], x_rows[bass.ds(e * SEL, SEL), :].rearrange("(c p) n -> p c n", p=P)).then_inc(s_x, 16)
                sp.wait_ge(s_h, e * HB)
                sp.dma_start(w1_sb[:, :, :], w1[bass.ds(e, 1), :, :].rearrange("e (k p) n -> p (e k) n", p=P)).then_inc(s_w1, 16)
                sp.wait_ge(s_y, e * RT)
                sp.dma_start(w2_sb[:, :, :], w2[bass.ds(e, 1), :, :].rearrange("e (k p) n -> p (e k) n", p=P)).then_inc(s_w2, 16)
                sp.wait_ge(s_ye, e * RT + RT)
                sp.dma_start(y_rows[bass.ds(e * SEL, SEL), :].rearrange("(c p) n -> p c n", p=P), y_sb[:, :, :]).then_inc(s_out, 16)
            sp.wait_ge(s_out, EX * 16)

        @block.scalar
        def _(act):
            with act.Fori(0, EX) as e:
                act.wait_ge(s_y, e * RT)
                for n in range(HB):
                    act.wait_ge(s_h, e * HB + n + 1)
                    nc.scalar.activation(hT[:, n, :], ph[n % 3][:, :], ACT.Gelu).then_inc(s_g, 1)

        @block.vector
        def _(dve):
            with dve.Fori(0, EX) as e:
                dve.wait_ge(s_h, e * HB)
                for c in range(RT):
                    dve.wait_ge(s_T, e * RT + c + 1)
                    nc.vector.tensor_copy(xT[:, :, c * P:(c + 1) * P], pT[c % 2][:, :].rearrange("p (k t) -> p k t", k=KD)).then_inc(s_xT, 1)
                dve.wait_ge(s_out, e * 16)
                for c in range(RT):
                    dve.wait_ge(s_y, e * RT + c + 1)
                    nc.vector.tensor_copy(y_sb[:, c, :], py[c % 2][:, :]).then_inc(s_ye, 1)

        @block.tensor
        def _(pe):
            pe.wait_ge(s_const, 16)
            with pe.Fori(0, EX) as e:
                pe.wait_ge(s_x, e * 16 + 16)
                for c in range(RT):
                    pe.wait_ge(s_xT, e * RT + max(c - 1, 0))
                    for k in range(KD):
                        ins = nc.tensor.transpose(pT[c % 2][:, k * P:(k + 1) * P], x_sb[:, c, k * P:(k + 1) * P], ident_sb[:, :])
                    ins.then_inc(s_T, 1)
                pe.wait_ge(s_xT, e * RT + RT)
                pe.wait_ge(s_w1, e * 16 + 16)
                for n in range(HB):
                    pe.wait_ge(s_g, e * HB + max(n - 2, 0))
                    for k in range(KD):
                        ins = nc.tensor.matmul(ph[n % 3][:, :], w1_sb[:, k, n * P:(n + 1) * P], xT[:, k, :], start=(k == 0), stop=(k == KD - 1))
                    ins.then_inc(s_h, 1)
                pe.wait_ge(s_w2, e * 16 + 16)
                pe.wait_ge(s_g, e * HB + HB)
                for c in range(RT):
                    pe.wait_ge(s_ye, e * RT + max(c - 1, 0))
                    for n in range(HB):
                        ins = nc.tensor.matmul(py[c % 2][:, :], hT[:, n, c * P:(c + 1) * P], w2_sb[:, n, :], start=(n == 0), stop=(n == HB - 1))
                    ins.then_inc(s_y, 1)


def decoder(nc, a, out):
    def scratch(name, *shape, dt=F32):
        return nc.dram_tensor(name, list(shape), dt).ap()

    def both(name):
        return scratch(name + "_tok", T, D), scratch(name + "_feat", KD, P, T)

    u_feat, u_tok, z_tok, y_tok = scratch("u0_feat", 12, P, T), scratch("u0_tok", T, 1536), scratch("z0_tok", T, 1536), scratch("y0_tok", T, 1536)
    slots, slots_y = scratch("slots", SLOTS, D), scratch("slots_y", SLOTS, D)
    rows, rows_y = scratch("rows", EX * SEL, D), scratch("rows_y", EX * SEL, D)
    x1_tok, x1_feat = both("x1")
    ssm0_project(nc, a["x"], a["ident"], a["norm_w"], a["w_in0"], a["b_in0"], a["conv_w0"], a["conv_b0"], u_feat, u_tok, z_tok, (slots, rows))
    ssm0_scan(nc, u_feat, u_tok, y_tok, a["ident"], a["w_bc"], a["b_bc"], a["w_dt0"], a["head_mean"], a["head_pair"], a["b_dt0"],
              a["a_log0"], a["l2_alpha"], a["l2_beta"], a["ema"])
    ssm0_out(nc, a["x"], y_tok, z_tok, a["w_out0"], a["b_out0"], a["gate"], a["ident"], x1_tok, x1_feat)

    r_feat = scratch("r_feat", KD, P, T)
    x2_tok, x2_feat = both("x2")
    long_conv(nc, x1_feat, a["ctx_turned"], a["taps"], a["skip0"], a["exchange"], r_feat)
    norm_from_feat(nc, "b2", r_feat, a["ident"], x2_tok, x2_feat)

    places0, weights0 = scratch("places0", T, K_, dt=U32), scratch("weights0", T, K_)
    x3_tok, x3_feat = both("x3")
    moe0_route(nc, x2_tok, x2_feat, a["router0"], a["ident"], a["upper"], a["ramp"], slots, places0, weights0)
    moe0_experts(nc, slots, a["w_gu"], a["w_down"], a["ident"], slots_y)
    gather_mix_norm(nc, "c3", K_, slots_y, SLOTS, x2_tok, places0, weights0, a["ident"], x3_tok, x3_feat)

    u1, z1, dt1, bc1 = scratch("u1", F1, P, T), scratch("z1", F1, P, T), scratch("dt1", F1, P, T), scratch("bc1", 2 * N1, T)
    x4_tok, x4_feat = both("x4")
    ssm1_project(nc, x3_feat, a["w_in1"], a["conv_w1"], a["conv_b1"], a["w_x1"], a["w_dt1"], a["b_dt1"], u1, z1, dt1, bc1)
    ssm1_scan(nc, x3_tok, u1, z1, dt1, bc1, a["a_log1"], a["skip1"], a["w_out1"], a["ident"], x4_tok, x4_feat)

    x5_tok, x5_feat = both("x5")
    linear_attention(nc, x4_tok, x4_feat, a["ctx_feat"], a["w_q"], a["w_g"], a["b_g"], a["w_kv"], a["w_o"], a["ident"], a["heads_mask"], x5_tok, x5_feat)

    scores, places1, weights1 = scratch("scores", EX, T), scratch("places1", T, TOP, dt=U32), scratch("weights1", T, TOP)
    moe1_route(nc, x5_tok, x5_feat, a["router1"], a["b_router1"], a["ident"], a["lower"], a["ramp"], scores, rows, places1, weights1)
    moe1_experts(nc, rows, a["w1"], a["w2"], a["ident"], rows_y)
    gather_mix_norm(nc, "f3", TOP, rows_y, EX * SEL, x5_tok, places1, weights1, a["ident"], out, None)


def laid_out(i):
    import numpy as np
    H0, S0, DI0 = 24, 64, 1536
    by_feature = lambda v: v.reshape(T, D).T.reshape(KD, P, T)
    xp_w, xp_b = i["L0_attn_x_proj_w"].reshape(H0, 1 + 2 * S0, DI0), i["L0_attn_x_proj_b"].reshape(H0, 1 + 2 * S0)
    pairs = lambda w: w.reshape(H0 // 2, P, DI0 // P, P).transpose(0, 3, 2, 1)
    taps = np.zeros((32, P - 1 + D), np.float32)
    taps[:, P - 1:] = i["L0_xattn_ssm_kernel"]
    head_mean = np.zeros((DI0, H0), np.float32)
    for h in range(H0):
        head_mean[h * S0:(h + 1) * S0, h] = 1 / S0
    head_pair = np.zeros((P, 2), np.float32)
    head_pair[:S0, 0] = head_pair[S0:, 1] = 1
    heads_mask = np.zeros((P, P), np.float32)
    for h in range(4):
        heads_mask[h * 32:(h + 1) * 32, h * 32:(h + 1) * 32] = 1
    ident = np.eye(P, dtype=np.float32)
    upper = np.triu(np.ones((P, P), np.float32), 1)
    L0, L1 = (lambda n: i["L0_" + n]), (lambda n: i["L1_" + n])
    return {
        "ident": ident, "exchange": ident[::-1], "upper": upper, "lower": upper.T, "ramp": np.arange(E_, dtype=np.float32),
        "head_mean": head_mean, "head_pair": head_pair, "heads_mask": heads_mask,
        "x": i["x"].reshape(T, D), "ctx_feat": by_feature(i["ctx_2048"]), "ctx_turned": by_feature(i["ctx_2048"])[:, ::-1],
        "norm_w": L0("attn_norm_w"), "w_in0": L0("attn_in_proj_w").T, "b_in0": L0("attn_in_proj_b"),
        "conv_w0": L0("attn_conv_w").reshape(DI0, 4), "conv_b0": L0("attn_conv_b"),
        "w_bc": np.concatenate([pairs(xp_w[:, 1:1 + S0]), pairs(xp_w[:, 1 + S0:])], -1),
        "b_bc": np.stack([xp_b[:, 1:1 + S0].reshape(H0 // 2, P), xp_b[:, 1 + S0:].reshape(H0 // 2, P)], -1),
        "w_dt0": xp_w[:, 0].T, "b_dt0": xp_b[:, 0], "a_log0": L0("attn_A_log"), "l2_alpha": L0("attn_log2_alpha_base"),
        "l2_beta": L0("attn_log2_beta"), "ema": L0("attn_surprise_ema"), "w_out0": L0("attn_out_proj_w").T, "b_out0": L0("attn_out_proj_b"),
        "gate": L0("attn_res_gate"), "taps": taps, "skip0": L0("xattn_D"), "router0": L0("ffn_router_w").T,
        "w_gu": np.concatenate([L0("ffn_w_gate"), L0("ffn_w_up")], -1).reshape(E_, KD, P, 2 * FF).transpose(0, 2, 1, 3), "w_down": L0("ffn_w_down"),
        "w_in1": L1("attn_W_in").T, "conv_w1": L1("attn_conv_w"), "conv_b1": L1("attn_conv_b"), "w_x1": L1("attn_W_x").T, "w_dt1": L1("attn_W_dt").T,
        "b_dt1": L1("attn_b_dt"), "a_log1": L1("attn_A_log"), "skip1": L1("attn_D"), "w_out1": L1("attn_W_out").T,
        "w_q": L1("xattn_Wq").T, "w_g": L1("xattn_Wg").T, "b_g": L1("xattn_bg"), "w_kv": L1("xattn_Wkv").T, "w_o": L1("xattn_Wo").T,
        "router1": L1("ffn_Wg"), "b_router1": L1("ffn_bg"), "w1": L1("ffn_W1"), "w2": L1("ffn_W2"),
    }


def kernel(**inputs):
    import numpy as np
    import concourse.bacc as bacc
    from concourse.bass_utils import run_bass_kernel_spmd

    nc = bacc.Bacc("TRN2", target_bir_lowering=False, num_devices=1)
    arrays = {n: np.ascontiguousarray(v) for n, v in laid_out({n: np.asarray(v) for n, v in inputs.items()}).items()}
    aps = {n: nc.dram_tensor(n, v.shape, mybir.dt.from_np(v.dtype), kind="ExternalInput").ap() for n, v in arrays.items()}
    out = nc.dram_tensor("out", (T, D), F32, kind="ExternalOutput").ap()
    decoder(nc, aps, out)
    result = run_bass_kernel_spmd(nc, [arrays], core_ids=[0])
    return result.results[0]["out"].reshape(NB, L, D)
```

```python
from contextlib import ExitStack

import concourse.bass as bass
from concourse import mybir
from concourse.alu_op_type import AluOpType as ALU

ACT = mybir.ActivationFunctionType
AX = mybir.AxisListType
F32 = mybir.dt.float32
F32R = mybir.dt.float32r
U32 = mybir.dt.uint32
P = 128
NB, L, D = 8, 256, 512
T = NB * L
KD = D // P
TILES = T // P
BANK = 512


class Space:

    def __init__(self, nc, name, phase):
        self.nc, self.name, self.phase, self.sems = nc, name, phase, []
        phase.callback(self.clear)

    def sb(self, name, shape, dt=F32):
        return self.phase.enter_context(self.nc.sbuf_tensor(f"{self.name}_{name}", shape, dt))

    def ps(self, name, shape=(P, BANK), dt=F32):
        return self.phase.enter_context(self.nc.psum_tensor(f"{self.name}_{name}", list(shape), dt))

    def sem(self, name):
        self.sems.append(self.nc.alloc_semaphore(name=f"{self.name}_{name}"))
        return self.sems[-1]

    def clear(self):
        self.nc.clear_and_free_semaphores(self.sems)
        self.nc.all_engine_barrier()


def alone(eng, tick):
    eng.sem_inc(tick, 1)


def linker(eng, sem, base=0):
    count = [0]

    def link(ins):
        count[0] += 1
        ins.then_inc(sem, 1)
        eng.wait_ge(sem, base + count[0])
    link.count = count
    return link


def ssm0_project(nc, x, ident, norm_w, w_in, b_in, conv_w, conv_b, w_dt, head_mean, u_feat, u_tok, z_tok, dt_mean, to_clear=()):
    DI = 1536
    F = DI // P
    EPS = 1.1920928955078125e-07
    CONSTS = 8
    LINKS_V, LINKS_A = 1 + 3 * F, 2
    WBUF = 6
    NORM_AT = 6
    with ExitStack() as phase:
        m = Space(nc, "a1", phase)
        w_raw = [m.sb(f"wraw{i}", [P, BANK]) for i in range(WBUF)]
        w_hi, w_lo = (m.sb("w" + n, [P, KD, 2 * DI], F32R) for n in ("hi", "lo"))
        H2 = 2 * w_dt.shape[1]
        wdt_sb = m.sb("wdt", [P, F, H2])
        dtm_sb = m.sb("dtm", [P, 2, H2])
        ident_sb = m.sb("ident", [P, P])
        nw_sb = m.sb("nw", [P, KD])
        bx_sb = m.sb("bx", [P, F])
        bz_sb = m.sb("bz", [P, DI])
        cw_sb = m.sb("cw", [P, F, 4])
        cb_sb = m.sb("cb", [P, F])
        eps_sb = m.sb("eps", [P, 1])
        x_sb = m.sb("x", [P, 2, D])
        sq_sb = m.sb("sq", [P, D])
        ss_sb = m.sb("ss", [P, 2])
        rt_sb = m.sb("rt", [P, 2])
        xn_sb = m.sb("xn", [P, 2, D])
        xnT_hi, xnT_lo = (m.sb("xnT" + n, [P, KD, L], F32R) for n in ("hi", "lo"))
        xpad = [m.sb(f"xpad{i}", [P, 3 + L]) for i in range(2)]
        acc = [m.sb(f"acc{i}", [P, L]) for i in range(2)]
        u_sb = m.sb("u", [P, F, L])
        ut_sb = m.sb("ut", [P, 2, DI])
        zb = [m.sb(f"zb{i}", [P, BANK]) for i in range(2)]
        z_sb = m.sb("z", [P, 2, DI])
        ZERO_ROWS = 2
        zeros = m.sb("zeros", [P, ZERO_ROWS, D])
        pT = m.ps("pT", (P, 2, BANK))
        px = [m.ps(f"px{i}") for i in range(2)]
        pz = [m.ps(f"pz{i}") for i in range(2)]
        pu = [m.ps(f"pu{i}") for i in range(2)]
        s_const, s_set, s_x = m.sem("const"), m.sem("set"), m.sem("x")
        s_w = [m.sem(f"w{i}") for i in range(WBUF)]
        s_wh, s_wl, s_xnTl = m.sem("wh"), m.sem("wl"), m.sem("xnTl")
        s_ss, s_root, s_xn, s_T, s_xnT = m.sem("ss"), m.sem("root"), m.sem("xn"), m.sem("T"), m.sem("xnT")
        s_px, s_xpad, s_conv, s_u = m.sem("px"), m.sem("xpad"), m.sem("conv"), m.sem("u")
        s_pz, s_zb, s_z = m.sem("pz"), m.sem("zb"), m.sem("z")
        s_pu, s_ut = m.sem("pu"), m.sem("ut")
        s_out_u, s_out_z, s_out_ut = m.sem("out_u"), m.sem("out_z"), m.sem("out_ut")
        s_lv, s_la, s_zero, s_clear = m.sem("lv"), m.sem("la"), m.sem("zero"), m.sem("clear")
        s_dt, s_dtm, s_out_dt = m.sem("dt"), m.sem("dtm"), m.sem("out_dt")
        tick_sp = m.sem("tick_sp")
        block = phase.enter_context(nc.Block())

        CHUNKS = [(k, slice(j * BANK, (j + 1) * BANK)) for j in range(2 * DI // BANK) for k in range(KD)]

        def batches(eng, norm, batch):
            norm(0)
            with eng.Fori(0, NB - 1) as b:
                batch(b, False)
            batch(NB - 1, True)

        @block.sync
        def _(sp):
            for dst, src in ((ident_sb[:, :], ident), (nw_sb[:, :], norm_w.rearrange("(k p) -> p k", p=P)),
                             (bx_sb[:, :], b_in[0:DI].rearrange("(k p) -> p k", p=P)),
                             (bz_sb[:, :], b_in[DI:2 * DI].partition_broadcast(P)),
                             (cw_sb[:, :, :], conv_w.rearrange("(k p) c -> p k c", p=P)),
                             (cb_sb[:, :], conv_b.rearrange("(k p) -> p k", p=P)),
                             (wdt_sb[:, :, 0:H2 // 2], w_dt.rearrange("(k p) h -> p k h", p=P)),
                             (wdt_sb[:, :, H2 // 2:H2], head_mean.rearrange("(k p) h -> p k h", p=P))):
                sp.dma_start(dst, src, allow_slow_non_contiguous=True).then_inc(s_const, 16)
            for n, (k, cols) in enumerate(CHUNKS):
                if n >= WBUF:
                    sp.wait_ge(s_wl, n - WBUF + 1)
                sp.dma_start(w_raw[n % WBUF][:, :], w_in[k * P:(k + 1) * P, cols]).then_inc(s_w[n % WBUF], 16)

            def load(b):
                sp.wait_ge(s_xn, b * 2)
                alone(sp, tick_sp)
                sp.dma_start(x_sb[:, :, :], x[bass.ds(b * L, L), :].rearrange("(c p) n -> p c n", p=P)).then_inc(s_x, 16)

            def batch(b, last):
                if not last:
                    load(b + 1)
                sp.wait_ge(s_u, b * F + F)
                alone(sp, tick_sp)
                sp.dma_start(u_feat[:, :, bass.ds(b * L, L)].rearrange("k p t -> p k t"), u_sb[:, :, :]).then_inc(s_out_u, 16)
                sp.wait_ge(s_dtm, b + 1)
                alone(sp, tick_sp)
                sp.dma_start(dt_mean[bass.ds(b * 2, 2), :, :].rearrange("c p h -> p c h"), dtm_sb[:, :, :]).then_inc(s_out_dt, 16)
                sp.wait_ge(s_z, b * 6 + 6)
                sp.dma_start(z_tok[bass.ds(b * L, L), :].rearrange("(c p) n -> p c n", p=P), z_sb[:, :, :]).then_inc(s_out_z, 16)
                sp.wait_ge(s_ut, b * 6 + 6)
                sp.dma_start(u_tok[bass.ds(b * L, L), :].rearrange("(c p) n -> p c n", p=P), ut_sb[:, :, :]).then_inc(s_out_ut, 16)
            batches(sp, load, batch)
            for s in (s_out_u, s_out_z, s_out_ut, s_out_dt):
                sp.wait_ge(s, NB * 16)

        @block.gpsimd
        def _(pool):
            pool.memset(zeros[:, :, :], 0.0).then_inc(s_zero, 1)
            pool.wait_ge(s_zero, 1)
            stores = 0
            for rows in to_clear:
                n = rows.shape[0] // (ZERO_ROWS * P)
                with pool.Fori(0, n) as r:
                    pool.dma_start(rows[bass.ds(r * ZERO_ROWS * P, ZERO_ROWS * P), :].rearrange("(p c) n -> p c n", p=P), zeros[:, :, :]).then_inc(s_clear, 16)
                stores += n
            if stores:
                pool.wait_ge(s_clear, stores * 16)

        @block.scalar
        def _(act):
            for n, (k, cols) in enumerate(CHUNKS):
                act.wait_ge(s_w[n % WBUF], 16 * (n // WBUF + 1))
                nc.scalar.copy(w_hi[:, k, cols], w_raw[n % WBUF][:, :]).then_inc(s_wh, 1)
            act.wait_ge(s_const, 16 * CONSTS)
            act.wait_ge(s_set, 3)

            def stats(b):
                link = linker(act, s_la, b * LINKS_A)
                act.wait_ge(s_x, b * 16 + 16)
                for c in range(2):
                    link(nc.scalar.activation(sq_sb[:, :], x_sb[:, c, :], ACT.Square, accum_out=ss_sb[:, c:c + 1]))
                nc.scalar.activation(rt_sb[:, :], ss_sb[:, :], ACT.Sqrt, bias=eps_sb[:, :], scale=1.0 / D).then_inc(s_root, 1)
                assert link.count[0] == LINKS_A

            def turned(b):
                act.wait_ge(s_T, b + 1)
                for k in range(KD):
                    nc.scalar.activation(xnT_hi[:, k, :], pT[:, k // 2, (k % 2) * L:(k % 2 + 1) * L], ACT.Copy,
                                         scale=nw_sb[:, k:k + 1]).then_inc(s_xnT, 1)

            def batch(b, last):
                for f in range(F + 1):
                    if f < F:
                        act.wait_ge(s_px, b * F + f + 1)
                        if f >= 2:
                            act.wait_ge(s_conv, b * F + f - 1)
                        nc.scalar.activation(xpad[f % 2][:, 3:3 + L], px[f % 2][:, 0:L], ACT.Identity,
                                             bias=bx_sb[:, f:f + 1]).then_inc(s_xpad, 1)
                    if f == NORM_AT and not last:
                        stats(b + 1)
                    if f >= 2 and f % 2 == 0:
                        n = f // 2 - 1
                        if n == 0:
                            act.wait_ge(s_out_z, b * 16)
                        act.wait_ge(s_zb, b * 6 + n + 1)
                        nc.scalar.activation(z_sb[:, n // 3, (n % 3) * BANK:(n % 3 + 1) * BANK], zb[n % 2][:, :], ACT.Silu).then_inc(s_z, 1)
                    if f >= 1:
                        g = f - 1
                        if g == 0:
                            act.wait_ge(s_out_u, b * 16)
                            act.wait_ge(s_pu, b * 6)
                        act.wait_ge(s_conv, b * F + g + 1)
                        nc.scalar.activation(u_sb[:, g, :], acc[g % 2][:, :], ACT.Silu, bias=cb_sb[:, g:g + 1]).then_inc(s_u, 1)
                if not last:
                    turned(b + 1)

            def norm(b):
                stats(b)
                turned(b)
            batches(act, norm, batch)

        @block.vector
        def _(dve):
            for i in range(2):
                nc.vector.memset(xpad[i][:, 0:3], 0.0).then_inc(s_set, 1)
            nc.vector.memset(eps_sb[:, :], EPS).then_inc(s_set, 1)
            for n, (k, cols) in enumerate(CHUNKS):
                dve.wait_ge(s_wh, n + 1)
                nc.vector.tensor_tensor(w_lo[:, k, cols], w_raw[n % WBUF][:, :], w_hi[:, k, cols].bitcast(F32), ALU.subtract).then_inc(s_wl, 1)
            dve.wait_ge(s_set, 3)
            dve.wait_ge(s_const, 16 * CONSTS)

            def norm(b, link=None):
                link = link or linker(dve, s_lv)
                dve.wait_ge(s_root, b + 1)
                link(nc.vector.reciprocal(ss_sb[:, :], rt_sb[:, :]))
                dve.wait_ge(s_x, b * 16 + 16)
                dve.wait_ge(s_T, b)
                for c in range(2):
                    nc.vector.tensor_scalar(xn_sb[:, c, :], x_sb[:, c, :], ss_sb[:, c:c + 1], None, ALU.mult).then_inc(s_xn, 1)

            def turned(b):
                for k in range(KD):
                    dve.wait_ge(s_xnT, b * KD + k // 2 * 2 + 2)
                    nc.vector.scalar_tensor_tensor(xnT_lo[:, k, :], pT[:, k // 2, (k % 2) * L:(k % 2 + 1) * L], nw_sb[:, k:k + 1],
                                                   xnT_hi[:, k, :].bitcast(F32), ALU.mult, ALU.subtract).then_inc(s_xnTl, 1)

            def batch(b, last):
                link = linker(dve, s_lv, 1 + b * LINKS_V)
                for f in range(F):
                    a, xp = acc[f % 2], xpad[f % 2]
                    dve.wait_ge(s_xpad, b * F + f + 1)
                    if f >= 2:
                        dve.wait_ge(s_u, b * F + f - 1)
                    else:
                        dve.wait_ge(s_u, b * F)
                    link(nc.vector.tensor_scalar(a[:, :], xp[:, 3:3 + L], cw_sb[:, f, 3:4], None, ALU.mult))
                    for j in (2, 1):
                        link(nc.vector.scalar_tensor_tensor(a[:, :], xp[:, j:j + L], cw_sb[:, f, j:j + 1], a[:, :], ALU.mult, ALU.add))
                    ins = nc.vector.scalar_tensor_tensor(a[:, :], xp[:, 0:L], cw_sb[:, f, 0:1], a[:, :], ALU.mult, ALU.add)
                    ins.then_inc(s_conv, 1)
                    if f == NORM_AT + 1 and not last:
                        norm(b + 1, link)
                    if f % 2:
                        n = f // 2
                        dve.wait_ge(s_pz, b * 6 + n + 1)
                        dve.wait_ge(s_z, b * 6 + max(n - 1, 0))
                        nc.vector.tensor_tensor(zb[n % 2][:, :], pz[n % 2][:, :], bz_sb[:, (n % 3) * BANK:(n % 3 + 1) * BANK], ALU.add).then_inc(s_zb, 1)
                assert last or link.count[0] == LINKS_V
                dve.wait_ge(s_dt, b + 1)
                dve.wait_ge(s_out_dt, b * 16)
                nc.vector.tensor_copy(dtm_sb[:, :, :], pT[:, :, 0:H2]).then_inc(s_dtm, 1)
                if not last:
                    turned(b + 1)
                dve.wait_ge(s_out_ut, b * 16)
                for n in range(6):
                    dve.wait_ge(s_pu, b * 6 + n + 1)
                    nc.vector.tensor_copy(ut_sb[:, n // 3, (n % 3) * BANK:(n % 3 + 1) * BANK], pu[n % 2][:, :]).then_inc(s_ut, 1)

            def first_norm(b):
                norm(b)
                turned(b)
            batches(dve, first_norm, batch)

        @block.tensor
        def _(pe):
            pe.wait_ge(s_const, 16 * CONSTS)
            pe.wait_ge(s_wl, len(CHUNKS))

            def parts(out, a, a_cols, b, b_cols, k):
                for n, (v, w) in enumerate(((a[0], b[0]), (a[0], b[1]), (a[1], b[0]))):
                    ins = nc.tensor.matmul(out, v[:, k, a_cols], w[:, k, b_cols], start=(k == 0 and n == 0), stop=(k == KD - 1 and n == 2))
                return ins

            def norm(b):
                pe.wait_ge(s_xn, b * 2 + 2)
                pe.wait_ge(s_xnTl, b * KD)
                for k in range(KD):
                    for c in range(2):
                        at = (k % 2) * L + c * P
                        ins = nc.tensor.transpose(pT[:, k // 2, at:at + P], xn_sb[:, c, k * P:(k + 1) * P], ident_sb[:, :])
                ins.then_inc(s_T, 1)

            def batch(b, last):
                pe.wait_ge(s_xnTl, b * KD + KD)

                def dt(k):
                    pe.wait_ge(s_u, b * F + k + 1)
                    for c in range(2):
                        ins = nc.tensor.matmul(pT[:, c, 0:H2], u_sb[:, k, c * P:(c + 1) * P], wdt_sb[:, k, :], start=(k == 0), stop=(k == F - 1))
                    if k == F - 1:
                        ins.then_inc(s_dt, 1)
                for f in range(F):
                    if f >= 3:
                        dt(f - 3)
                    pe.wait_ge(s_xpad, b * F + max(f - 1, 0))
                    for k in range(KD):
                        ins = parts(px[f % 2][:, 0:L], (w_hi, w_lo), slice(f * P, (f + 1) * P), (xnT_hi, xnT_lo), slice(0, L), k)
                    ins.then_inc(s_px, 1)
                    if f % 2:
                        n = f // 2
                        pe.wait_ge(s_zb, b * 6 + max(n - 1, 0))
                        c, j = n // 3, n % 3
                        for k in range(KD):
                            ins = parts(pz[n % 2][:, :], (xnT_hi, xnT_lo), slice(c * P, (c + 1) * P), (w_hi, w_lo), slice(DI + j * BANK, DI + (j + 1) * BANK), k)
                        ins.then_inc(s_pz, 1)
                for k in range(F - 3, F):
                    dt(k)
                if not last:
                    pe.wait_ge(s_dtm, b + 1)
                    norm(b + 1)
                for n in range(6):
                    pe.wait_ge(s_ut, b * 6 + max(n - 1, 0))
                    c, j = n // 3, n % 3
                    for q in range(4):
                        ins = nc.tensor.transpose(pu[n % 2][:, q * P:(q + 1) * P], u_sb[:, j * 4 + q, c * P:(c + 1) * P], ident_sb[:, :])
                    ins.then_inc(s_pu, 1)
            batches(pe, norm, batch)


def ssm0_scan(nc, u_feat, u_tok, dt_mean, y_tok, ident, w_bc, b_bc, head_pair, b_dt, a_log, l2_alpha, l2_beta, ema):
    H, S, F = 24, 64, 12
    PAIRS = H // 2
    LN2 = 0.6931471805599453
    HALVES = 2
    TH = T // HALVES
    NBH = NB // HALVES
    TT = TH // P
    NI = 2 * NBH
    BLK = TH // BANK
    NQ = 2 * BLK
    KC = 2
    UCH = BLK * F // KC
    UNITS = HALVES * PAIRS
    with ExitStack() as phase:
        m = Space(nc, "a2", phase)
        u_raw = [m.sb(f"uraw{i}", [P, KC, BANK]) for i in range(2)]
        u_hi, u_lo = (m.sb("u" + n, [P, F, TH], F32R) for n in ("hi", "lo"))
        w_raw = m.sb("wraw", [P, F, 2 * P])
        w_hi, w_lo = (m.sb("w" + n, [P, F, 2 * P], F32R) for n in ("hi", "lo"))
        bias_sb = [m.sb(f"bias{i}", [P, 2]) for i in range(2)]
        dtm_sb = m.sb("dtm", [P, TILES, 2 * H])
        pair_sb = m.sb("pair", [P, 2])
        idz = m.sb("idz", [P, 2 * P])
        BT, CT = ([m.sb(f"{n}{i}", [P, TH]) for i in range(2)] for n in ("BT", "CT"))
        sq = [m.sb(f"sq{i}", [P, BANK]) for i in range(2)]
        ut_sb = [m.sb(f"ut{i}", [P, TT, P]) for i in range(2)]
        y_sb = m.sb("y", [P, TT, P])
        hv = m.sb("hv", [P, 5, H])
        gain_sb = m.sb("gain", [P, H, TT])
        t0, t1, t2 = (m.sb(f"t{i}", [P, H, TT]) for i in range(3))
        base_w, rest_w = m.sb("basew", [P, H, TT]), m.sb("restw", [P, H, TT])
        nrm, inv = m.sb("nrm", [P, 2, 2, TT]), m.sb("inv", [P, 2, 2, TT])
        al, cB, q0 = (m.sb(n, [P, 2, TT]) for n in ("al", "cB", "q0"))
        M = [m.sb(f"M{i}", [P, 3 * P]) for i in range(2)]
        W = [m.sb(f"W{i}", [P, 3 * P]) for i in range(2)]
        one_sb = m.sb("one", [P, 1])
        pB = [m.ps(f"pB{i}") for i in range(2)]
        pn, py = m.ps("pn"), m.ps("py")
        pa = [m.ps(f"pa{i}") for i in range(2)]
        pG = [m.ps(f"pG{i}") for i in range(2)]
        s_const, s_w, s_ut, s_out = (m.sem(n) for n in "const w ut out".split())
        s_u = [m.sem(f"ld{n}") for n in ("u0", "u1")]
        s_uh, s_ul, s_wh, s_wl = (m.sem(n) for n in "uh ul wh wl".split())
        s_hv, s_ab, s_lv, s_la, s_va, s_av, s_set = (m.sem(n) for n in "hv ab lv la va av set".split())
        s_pB, s_bt, s_pn, s_root, s_arg, s_tanh, s_al = (m.sem(n) for n in "pB bt pn root arg tanh al".split())
        s_pa, s_M, s_G, s_W, s_y, s_ye = (m.sem(n) for n in "pa M G W y ye".split())
        tick_sp = m.sem("tick_sp")
        block = phase.enter_context(nc.Block())
        CONSTS = 8
        LV = 9
        LV_HALF, LV_ONCE = 8, 5
        LA_HALF = 3
        B_COLS, C_COLS = slice(0, P), slice(P, 2 * P)

        def schedule(eng, half_start, step):
            for half in range(HALVES):
                first = half * PAIRS
                step(half, first - 1 if half else None, first, first=True)
                half_start(half)
                with eng.Fori(0, (PAIRS - 2) // 2) as r:
                    for i in range(2):
                        step(half, first + 2 * r + i, first + 2 * r + i + 1, parity=(i + 1) % 2)
                step(half, first + PAIRS - 2, first + PAIRS - 1)
            step(half, UNITS - 1, None)

        def parities(nxt, cur, parity):
            if parity is None:
                parity = nxt % 2 if nxt is not None else (cur + 1) % 2
            return parity, 1 - parity

        @block.sync
        def _(sp):
            sp.dma_start(idz[:, 0:P], ident).then_inc(s_const, 16)
            sp.dma_start(pair_sb[:, :], head_pair).then_inc(s_const, 16)
            sp.dma_start(dtm_sb[:, :, :], dt_mean.rearrange("c p h -> p c h")).then_inc(s_const, 16)
            for n, v in enumerate((b_dt, a_log, l2_alpha, l2_beta, ema)):
                sp.dma_start(hv[:, n, :], v.partition_broadcast(P)).then_inc(s_const, 16)

            def weights(pair, nxt, parity):
                sp.dma_start(w_raw[:, :, :], w_bc[bass.ds(pair, 1), :, :, :].rearrange("a p k n -> (a p) k n")).then_inc(s_w, 16)
                sp.dma_start(bias_sb[parity][:, :], b_bc[bass.ds(pair, 1), :, :].rearrange("a p n -> (a p) n")).then_inc(s_w, 16)

            def step(half, cur, nxt, parity=None, first=False):
                into, at = parities(nxt, cur, parity)
                pair = None if nxt is None else nxt - half * PAIRS
                if nxt is not None:
                    if first and half == 0:
                        weights(0, nxt, into)
                    if cur is not None:
                        sp.wait_ge(s_y, cur * NI)
                        alone(sp, tick_sp)
                    sp.dma_start(ut_sb[into][:, :, :], u_tok[half * TH:(half + 1) * TH, bass.ds(pair * P, P)]
                                 .rearrange("(c p) n -> p c n", p=P)).then_inc(s_ut, 16)
                    sp.wait_ge(s_wl, nxt * 2 + 2)
                    alone(sp, tick_sp)
                    sp.wait_ge(s_bt, nxt * 2 * NQ)
                    if parity is not None or nxt < UNITS - 1:
                        alone(sp, tick_sp)
                        last = parity is None and not first
                        weights(0 if last else pair + 1, nxt + 1, 1 - into)
                if cur is not None:
                    before = half - 1 if first else half
                    sp.wait_ge(s_ye, cur * NBH + NBH)
                    alone(sp, tick_sp)
                    sp.dma_start(y_tok[before * TH:(before + 1) * TH, bass.ds((cur - before * PAIRS) * P, P)]
                                 .rearrange("(c p) n -> p c n", p=P), y_sb[:, :, :]).then_inc(s_out, 16)
            schedule(sp, lambda half: None, step)
            sp.wait_ge(s_out, UNITS * 16)

        @block.gpsimd
        def _(pool):
            for half in range(HALVES):
                for c in range(UCH):
                    j = half * UCH + c
                    n, k = c // (F // KC), c % (F // KC) * KC
                    if j >= 2:
                        pool.wait_ge(s_ul, j - 1)
                    pool.dma_start(u_raw[j % 2][:, :, :], u_feat[k:k + KC, :, half * TH + n * BANK:half * TH + (n + 1) * BANK]
                                   .rearrange("k p t -> p k t")).then_inc(s_u[j % 2], 16)

        def split_u(eng, half, split, chunks):
            for c in chunks:
                n, k = c // (F // KC), c % (F // KC) * KC
                if half and c % (F // KC) == 0:
                    eng.wait_ge(s_pB, (half * PAIRS - 1) * NQ + BLK + n + 1)
                split(half * UCH + c, slice(k, k + KC), slice(n * BANK, (n + 1) * BANK))

        @block.scalar
        def _(act):
            act.wait_ge(s_const, 16 * CONSTS)

            def split(j, ks, ts):
                act.wait_ge(s_u[j % 2], 16 * (j // 2 + 1))
                nc.scalar.copy(u_hi[:, ks, ts], u_raw[j % 2][:, :, :]).then_inc(s_uh, 1)

            def weights_hi(nxt, cols):
                act.wait_ge(s_w, nxt * 32 + 32)
                nc.scalar.copy(w_hi[:, :, cols], w_raw[:, :, cols]).then_inc(s_wh, 1)

            def half_start(half):
                link = linker(act, s_la, half * LA_HALF)
                act.wait_ge(s_va, 2 * half + 1)
                link(nc.scalar.activation(t1[:, :, :], t0[:, :, :], ACT.Abs))
                link(nc.scalar.activation(t1[:, :, :], t1[:, :, :], ACT.Exp, scale=-1.0))
                link(nc.scalar.activation(t1[:, :, :], t1[:, :, :], ACT.Ln, bias=one_sb[:, :], scale=1.0))
                nc.scalar.activation(t2[:, :, :], t0[:, :, :], ACT.Relu).then_inc(s_av, 1)
                act.wait_ge(s_va, 2 * half + 2)
                nc.scalar.activation(t1[:, :, :], t1[:, :, :], ACT.Exp).then_inc(s_av, 1)
                if half == 0:
                    act.wait_ge(s_hv, 1)
                    for n in (2, 3):
                        nc.scalar.activation(hv[:, n, :], hv[:, n, :], ACT.Exp, scale=LN2).then_inc(s_ab, 1)

            def step(half, cur, nxt, parity=None, first=False):
                into, at = parities(nxt, cur, parity)
                if cur is not None:
                    act.wait_ge(s_pn, cur * NQ + NQ)
                    nc.scalar.activation(nrm[:, :, :, :].rearrange("p a b c -> p (a b c)"), pn[:, 0:4 * TT], ACT.Sqrt).then_inc(s_root, 1)
                    act.wait_ge(s_arg, cur + 1)
                    nc.scalar.activation(q0[:, :, :], q0[:, :, :], ACT.Tanh).then_inc(s_tanh, 1)
                if nxt is None:
                    return
                if first and half == 0:
                    weights_hi(nxt, B_COLS)
                if cur is not None:
                    act.wait_ge(s_pB, nxt * NQ)
                weights_hi(nxt, C_COLS)
                if first:
                    split_u(act, half, split, range(UCH))
                if cur is not None:
                    act.wait_ge(s_G, cur * NI)
                for n in range(NQ):
                    dst = (BT, CT)[n // BLK][into]
                    act.wait_ge(s_pB, nxt * NQ + n + 1)
                    src, bias = pB[n % 2][:, :], bias_sb[into][:, n // BLK:n // BLK + 1]
                    nc.scalar.activation(dst[:, (n % BLK) * BANK:(n % BLK + 1) * BANK], src, ACT.Identity, bias=bias).then_inc(s_bt, 1)
                    if cur is not None or n >= 1:
                        act.wait_ge(s_pn, nxt * NQ + n - 1)
                    nc.scalar.activation(sq[n % 2][:, :], src, ACT.Square, bias=bias).then_inc(s_bt, 1)
                    if n == BLK - 1 and (parity is not None or nxt < UNITS - 1):
                        weights_hi(nxt + 1, B_COLS)
            schedule(act, half_start, step)

        @block.vector
        def _(dve):
            nc.vector.memset(idz[:, P:2 * P], 0.0).then_inc(s_set, 1)
            nc.vector.memset(one_sb[:, :], 1.0).then_inc(s_set, 1)
            dve.wait_ge(s_set, 2)
            dve.wait_ge(s_const, 16 * CONSTS)

            def split(j, ks, ts):
                dve.wait_ge(s_uh, j + 1)
                nc.vector.tensor_tensor(u_lo[:, ks, ts], u_raw[j % 2][:, :, :], u_hi[:, ks, ts].bitcast(F32), ALU.subtract).then_inc(s_ul, 1)

            def weights_lo(count, cols):
                dve.wait_ge(s_wh, count)
                nc.vector.tensor_tensor(w_lo[:, :, cols], w_raw[:, :, cols], w_hi[:, :, cols].bitcast(F32), ALU.subtract).then_inc(s_wl, 1)

            def wide(v, n=TT):
                return v.unsqueeze(2).to_broadcast([P, H, n])

            def half_start(half):
                link = linker(dve, s_lv, half * (LV_ONCE + LV_HALF + PAIRS * LV))
                if half == 0:
                    for n, (lo, hi) in ((1, (-2.3, -0.01)), (2, (-3.32, -0.015)), (3, (-2.0, 2.0))):
                        link(nc.vector.tensor_scalar(hv[:, n, :], hv[:, n, :], lo, hi, ALU.max, ALU.min))
                    link(nc.vector.tensor_scalar(hv[:, 4, :], hv[:, 4, :], 1e-6, None, ALU.add))
                    nc.vector.reciprocal(hv[:, 4, :], hv[:, 4, :]).then_inc(s_hv, 1)
                pd = dtm_sb[:, half * TT:(half + 1) * TT, :].rearrange("p c h -> p h c")
                nc.vector.tensor_tensor(t0[:, :, :], pd[:, 0:H, :], wide(hv[:, 0, :]), ALU.add).then_inc(s_va, 1)
                dve.wait_ge(s_av, 2 * half + 1)
                link(nc.vector.tensor_tensor(t1[:, :, :], t1[:, :, :], t2[:, :, :], ALU.add))
                nc.vector.tensor_tensor(t1[:, :, :], t1[:, :, :], wide(hv[:, 1, :]), ALU.mult).then_inc(s_va, 1)
                dve.wait_ge(s_av, 2 * half + 2)
                link(nc.vector.tensor_scalar(t1[:, :, :], t1[:, :, :], -1.0, 1.0, ALU.mult, ALU.add))
                link(nc.vector.tensor_tensor(t2[:, :, :], t1[:, :, :], pd[:, H:2 * H, :], ALU.mult))
                dve.wait_ge(s_ab, 2)
                if half == 0:
                    link(nc.vector.tensor_scalar(hv[:, 3, :], hv[:, 3, :], 1.0 / S, None, ALU.mult))
                link(nc.vector.tensor_tensor(t2[:, :, :], t2[:, :, :], t2[:, :, :], ALU.mult))
                link(nc.vector.tensor_tensor(t2[:, :, :], t2[:, :, :], wide(hv[:, 4, :]), ALU.mult))
                link(nc.vector.tensor_tensor(gain_sb[:, :, :], t2[:, :, :], wide(hv[:, 3, :]), ALU.mult))
                link(nc.vector.tensor_scalar(base_w[:, :, :], wide(hv[:, 2, :]), -1.0, 1.0, ALU.mult, ALU.add))
                link(nc.vector.tensor_scalar(rest_w[:, :, :], base_w[:, :, :], -1.0, 1.0, ALU.mult, ALU.add))
                assert link.count[0] == LV_HALF + (0 if half else LV_ONCE), link.count[0]

            def step(half, cur, nxt, parity=None, first=False):
                into, at = parities(nxt, cur, parity)
                if cur is None:
                    weights_lo(1, B_COLS)
                    weights_lo(2, C_COLS)
                    split_u(dve, half, split, range(UCH))
                    weights_lo(3, B_COLS)
                    return
                of = half - 1 if first else half
                pair = cur - of * PAIRS
                link = linker(dve, s_lv, LV_ONCE + LV_HALF * (of + 1) + cur * LV)
                dve.wait_ge(s_root, cur + 1)
                link(nc.vector.tensor_scalar(nrm[:, :, :, :], nrm[:, :, :, :], 1e-12, None, ALU.max))
                dve.wait_ge(s_ye, cur * NBH)
                link(nc.vector.reciprocal(inv[:, :, :, :], nrm[:, :, :, :]))
                rB = inv[:, 0, :, :]
                link(nc.vector.tensor_tensor(q0[:, :, :], pn[:, 0:2 * TT].rearrange("p (h c) -> p h c", h=2), rB, ALU.mult))
                link(nc.vector.tensor_tensor(q0[:, :, :], q0[:, :, :], rB, ALU.mult))
                nc.vector.tensor_tensor(q0[:, :, :], q0[:, :, :], gain_sb[:, bass.ds(2 * pair, 2), :], ALU.mult).then_inc(s_arg, 1)
                dve.wait_ge(s_tanh, cur + 1)
                link(nc.vector.tensor_scalar(q0[:, :, :], q0[:, :, :], 0.0, None, ALU.max))
                link(nc.vector.tensor_tensor(q0[:, :, :], q0[:, :, :], rest_w[:, bass.ds(2 * pair, 2), :], ALU.mult))
                link(nc.vector.tensor_tensor(q0[:, :, :], q0[:, :, :], base_w[:, bass.ds(2 * pair, 2), :], ALU.add))
                dve.wait_ge(s_pa, cur * NBH)
                nc.vector.tensor_scalar(al[:, :, :], q0[:, :, :], 0.01, 0.999, ALU.max, ALU.min).then_inc(s_al, 1)
                dve.wait_ge(s_al, cur + 1)
                link(nc.vector.tensor_scalar(cB[:, :, :], al[:, :, :], -1.0, 1.0, ALU.mult, ALU.add))
                link(nc.vector.tensor_tensor(cB[:, :, :], cB[:, :, :], rB, ALU.mult))
                assert link.count[0] == LV, link.count[0]
                if nxt is not None:
                    weights_lo(nxt * 2 + 2, C_COLS)
                for i in range(NI + 1):
                    if i < NI:
                        b, h = i // 2, i % 2
                        dve.wait_ge(s_pa, cur * NBH + b + 1)
                        nc.vector.tensor_tensor_scan(M[i % 2][:, 0:2 * P], pa[b % 2][:, h * L:(h + 1) * L], idz[:, :], 0.0, ALU.mult, ALU.add).then_inc(s_M, 1)
                        nc.vector.tensor_tensor_scan(M[i % 2][:, 2 * P:3 * P], pa[b % 2][:, h * L + P:(h + 1) * L], idz[:, 0:P], 0.0, ALU.mult, ALU.add).then_inc(s_M, 1)
                        dve.wait_ge(s_M, (cur * NI + i) * 2 + 2)
                        dve.wait_ge(s_G, cur * NI + i + 1)
                        dve.wait_ge(s_y, cur * NI + max(i - 1, 0))
                        for a, (lo, hi) in enumerate(((0, 2 * P), (2 * P, 3 * P))):
                            ins = nc.vector.scalar_tensor_tensor(W[i % 2][:, lo:hi], pG[i % 2][:, lo:hi], cB[:, h, 2 * b + a:2 * b + a + 1],
                                                                 M[i % 2][:, lo:hi], ALU.mult, ALU.mult)
                        ins.then_inc(s_W, 1)
                        if first:
                            split_u(dve, half, split, range(UCH * i // NI, UCH * (i + 1) // NI))
                    if i >= 2 and i % 2 == 0:
                        b = i // 2 - 1
                        if b == 0:
                            dve.wait_ge(s_out, cur * 16)
                        dve.wait_ge(s_y, cur * NI + i)
                        pyb = py[:, 0:L].rearrange("p (h c n) -> p h c n", h=2, c=2)
                        for h in range(2):
                            ins = nc.vector.tensor_tensor(y_sb[:, 2 * b:2 * b + 2, h * S:(h + 1) * S], pyb[:, h, :, :],
                                                          inv[:, 1, h, 2 * b:2 * b + 2].unsqueeze(2).to_broadcast([P, 2, S]), ALU.mult)
                        ins.then_inc(s_ye, 1)
                    if i == NI // 2 and nxt is not None and not first and (parity is not None or nxt < UNITS - 1):
                        weights_lo(nxt * 2 + 3, B_COLS)
                if first:
                    weights_lo(nxt * 2 + 3, B_COLS)
            schedule(dve, half_start, step)

        @block.tensor
        def _(pe):
            pe.wait_ge(s_set, 2)
            pe.wait_ge(s_const, 16 * CONSTS)

            def parts(out, w, u, cols, k, ts):
                for n, (a, b) in enumerate(((w[0], u[0]), (w[0], u[1]), (w[1], u[0]))):
                    ins = nc.tensor.matmul(out, a[:, k, cols], b[:, k, ts], start=(k == 0 and n == 0), stop=(k == F - 1 and n == 2))
                return ins

            def norms(unit, n):
                pe.wait_ge(s_bt, unit * 2 * NQ + 2 * n + 2)
                for q in range(4):
                    c = (n % BLK) * 4 + q
                    at = (n // BLK) * 2 * TT
                    ins = nc.tensor.matmul(pn[:, at:at + 2 * TT].rearrange("p (h c) -> p h c", h=2)[:, :, c],
                                           sq[n % 2][:, q * P:(q + 1) * P], pair_sb[:, :], start=True, stop=True)
                ins.then_inc(s_pn, 1)

            def step(half, cur, nxt, parity=None, first=False):
                into, at = parities(nxt, cur, parity)

                def decays(b):
                    pe.wait_ge(s_M, (cur * NI + 2 * max(b - 1, 0)) * 2)
                    for h in range(2):
                        for c in range(2):
                            ins = nc.tensor.matmul(pa[b % 2][:, h * L + c * P:h * L + (c + 1) * P],
                                                   al[:, h, 2 * b + c:2 * b + c + 1].to_broadcast([P, P]), idz[:, 0:P], start=True, stop=True)
                    ins.then_inc(s_pa, 1)

                def scores(i):
                    t, r = i // 2 * L, slice(i % 2 * S, (i % 2 + 1) * S)
                    B, C = BT[at], CT[at]
                    pe.wait_ge(s_W, cur * NI + max(i - 1, 0))
                    nc.tensor.matmul(pG[i % 2][:, 0:L], B[r, t:t + P], C[r, t:t + L], start=True, stop=True)
                    nc.tensor.matmul(pG[i % 2][:, L:L + P], B[r, t + P:t + L], C[r, t + P:t + L], start=True, stop=True).then_inc(s_G, 1)

                def output(i):
                    b, h = i // 2, i % 2
                    pe.wait_ge(s_W, cur * NI + i + 1)
                    if h == 0:
                        pe.wait_ge(s_ye, cur * NBH + b)
                    o = h * 2 * S
                    u0, u1 = ut_sb[at][:, 2 * b, h * S:(h + 1) * S], ut_sb[at][:, 2 * b + 1, h * S:(h + 1) * S]
                    nc.tensor.matmul(py[:, o:o + S], W[i % 2][:, 0:P], u0, start=True, stop=True)
                    nc.tensor.matmul(py[:, o + S:o + 2 * S], W[i % 2][:, P:2 * P], u0, start=True, stop=False)
                    nc.tensor.matmul(py[:, o + S:o + 2 * S], W[i % 2][:, 2 * P:3 * P], u1, start=False, stop=True).then_inc(s_y, 1)

                def project(j):
                    n, k = j // F, j % F
                    if k == 0:
                        if cur is not None or n >= 2:
                            pe.wait_ge(s_bt, nxt * 2 * NQ + 2 * (n - 1))
                        if n % BLK == 0:
                            pe.wait_ge(s_wl, nxt * 2 + n // BLK + 1)
                    if first and n < BLK and k % KC == 0:
                        pe.wait_ge(s_ul, half * UCH + n * (F // KC) + k // KC + 1)
                    cols = (B_COLS, C_COLS)[n // BLK]
                    ins = parts(pB[n % 2][:, :], (w_hi, w_lo), (u_hi, u_lo), cols, k, slice((n % BLK) * BANK, (n % BLK + 1) * BANK))
                    if k == F - 1:
                        ins.then_inc(s_pB, 1)
                    if k == 3 and n >= 1:
                        if n == 1 and cur is not None:
                            pe.wait_ge(s_arg, nxt)
                        norms(nxt, n - 1)
                if cur is not None:
                    norms(cur, NQ - 1)
                if cur is None:
                    for j in range(NQ * F):
                        project(j)
                    return
                slots = [[] for _ in range(NI + 1)]
                if nxt is not None and not first:
                    for j in range(F + 2):
                        project(j)
                    for j in range(F + 2, NQ * F):
                        slots[(j - F - 2) * (NI + 1) // (NQ * F - F - 2)].append(j)
                pe.wait_ge(s_al, cur + 1)
                pe.wait_ge(s_ut, cur * 16 + 16)
                decays(0)
                decays(1)
                scores(0)
                for i in range(NI + 1):
                    for j in slots[i]:
                        project(j)
                    if i < NI:
                        if i + 1 < NI:
                            scores(i + 1)
                        output(i)
                        if i % 2 == 1 and i // 2 + 2 < NBH:
                            decays(i // 2 + 2)
                if first:
                    for j in range(NQ * F):
                        project(j)
            schedule(pe, lambda half: None, step)


LN_EPS = 1e-5


def ssm0_out(nc, x, y_tok, z_tok, w_out, b_out, gate, ident, x1, x1_feat):
    DI = 1536
    F = DI // P
    with ExitStack() as phase:
        m = Space(nc, "a3", phase)
        w_sb = m.sb("w", [P, F, D])
        ident_sb = m.sb("ident", [P, P])
        b_sb, g_sb, eps_sb = m.sb("b", [P, D]), m.sb("g", [P, 1]), m.sb("eps", [P, 1])
        x_sb = [m.sb(f"x{i}", [P, 2, D]) for i in range(2)]
        y_sb = [m.sb(f"y{i}", [P, 2, DI]) for i in range(2)]
        z_sb = [m.sb(f"z{i}", [P, 2, DI]) for i in range(2)]
        yT = m.sb("yT", [P, 2, F, P])
        v_sb = m.sb("v", [P, 2, D])
        st, mv, sd = m.sb("st", [P, 2, 6]), m.sb("mv", [P, 2, 2]), m.sb("sd", [P, 2])
        o_sb = m.sb("o", [P, 2, D])
        oT = m.sb("oT", [P, 2, KD, P])
        pT = [m.ps(f"pT{i}") for i in range(2)]
        po = [m.ps(f"po{i}") for i in range(2)]
        px = [m.ps(f"px{i}") for i in range(2)]
        s_const, s_set, s_out, s_lv = (m.sem(n) for n in "const set out lv".split())
        s_in = [m.sem(f"in{i}") for i in range(2)]
        s_yz, s_T, s_yT, s_o, s_var, s_sd, s_ln, s_xT, s_oT = (m.sem(n) for n in "yz T yT o var sd ln xT oT".split())
        tick_dve, tick_sp = m.sem("tick_dve"), m.sem("tick_sp")
        block = phase.enter_context(nc.Block())
        LV = 9

        def pipelined(eng, products, norm):
            products(0, 0, 0)
            with eng.Fori(0, NB // 2 - 1) as r:
                for i in range(2):
                    products(2 * r + 1 + i, r + i, (1 + i) % 2)
                    norm(2 * r + i, i)
            products(NB - 1, NB // 2 - 1, 1)
            for i in range(2):
                norm(NB - 2 + i, i)

        def rows(a, b, n):
            return a[bass.ds(b * L, n), :].rearrange("(c p) n -> p c n", p=P)

        @block.sync
        def _(sp):
            for dst, src in ((ident_sb[:, :], ident), (b_sb[:, :], b_out.partition_broadcast(P)), (g_sb[:, :], gate.partition_broadcast(P)),
                             (w_sb[:, :, :], w_out.rearrange("(k p) n -> p k n", p=P))):
                sp.dma_start(dst, src).then_inc(s_const, 16)

            def load(b, i):
                for dst, src in ((x_sb, x), (y_sb, y_tok), (z_sb, z_tok)):
                    sp.dma_start(dst[i][:, :, :], rows(src, b, L)).then_inc(s_in[i], 16)

            def store(b):
                sp.wait_ge(s_oT, b * 2 + 2)
                alone(sp, tick_sp)
                sp.dma_start(rows(x1, b, L), o_sb[:, :, :]).then_inc(s_out, 16)
                for c in range(2):
                    sp.dma_start(x1_feat[:, :, bass.ds(b * L + c * P, P)].rearrange("k p t -> p k t"), oT[:, c, :, :]).then_inc(s_out, 16)
            for i in range(2):
                load(i, i)
            with sp.Fori(0, NB // 2 - 1) as r:
                for i in range(2):
                    b = 2 * r + i
                    sp.wait_ge(s_ln, b * 2 + 2)
                    alone(sp, tick_sp)
                    load(b + 2, i)
                    store(b)
            for i in range(2):
                store(NB - 2 + i)
            sp.wait_ge(s_out, NB * 48)

        @block.scalar
        def _(act):
            act.wait_ge(s_set, 1)

            def products(b, r, i):
                for n in range(6):
                    act.wait_ge(s_T, b * 6 + n + 1)
                    if n == 0:
                        act.wait_ge(s_o, b * 2)
                    nc.scalar.copy(yT[:, n // 3, (n % 3) * 4:(n % 3) * 4 + 4, :].rearrange("p k t -> p (k t)"), pT[n % 2][:, :]).then_inc(s_yT, 1)

            def norm(b, i):
                act.wait_ge(s_var, b * 2 + 2)
                nc.scalar.activation(sd[:, :], mv[:, :, 1], ACT.Sqrt, bias=eps_sb[:, :], scale=1.0).then_inc(s_sd, 1)
                act.wait_ge(s_out, b * 48)
                for c in range(2):
                    act.wait_ge(s_xT, b * 2 + c + 1)
                    nc.scalar.copy(oT[:, c, :, :].rearrange("p k t -> p (k t)"), px[c][:, :]).then_inc(s_oT, 1)
            pipelined(act, products, norm)

        @block.vector
        def _(dve):
            nc.vector.memset(eps_sb[:, :], LN_EPS).then_inc(s_set, 1)
            dve.wait_ge(s_const, 64)

            def products(b, r, i):
                dve.wait_ge(s_in[i], r * 48 + 48)
                for c in range(2):
                    nc.vector.tensor_tensor(y_sb[i][:, c, :], y_sb[i][:, c, :], z_sb[i][:, c, :], ALU.mult).then_inc(s_yz, 1)

            def norm(b, i):
                link = linker(dve, s_lv, b * LV)
                dve.wait_ge(s_ln, b * 2)
                for c in range(2):
                    dve.wait_ge(s_o, b * 2 + c + 1)
                    v = v_sb[:, c, :]
                    link(nc.vector.tensor_tensor(v, po[c][:, :], b_sb[:, :], ALU.add))
                    link(nc.vector.scalar_tensor_tensor(v, v, g_sb[:, 0:1], x_sb[i][:, c, :], ALU.mult, ALU.add))
                    link(nc.vector.tensor_tensor(v, v, x_sb[i][:, c, :], ALU.add))
                    link(nc.vector.bn_stats(st[:, c, :], v))
                    alone(dve, tick_dve)
                    nc.vector.bn_aggr(mv[:, c, :], st[:, c, :]).then_inc(s_var, 1)
                dve.wait_ge(s_sd, b + 1)
                link(nc.vector.reciprocal(sd[:, :], sd[:, :]))
                dve.wait_ge(s_out, b * 48)
                for c in range(2):
                    nc.vector.tensor_scalar(o_sb[:, c, :], v_sb[:, c, :], mv[:, c, 0:1], sd[:, c:c + 1], ALU.subtract, ALU.mult).then_inc(s_ln, 1)
                assert link.count[0] == LV
            pipelined(dve, products, norm)

        @block.tensor
        def _(pe):
            pe.wait_ge(s_const, 64)

            def products(b, r, i):
                for n in range(6):
                    c, j = n // 3, n % 3
                    pe.wait_ge(s_yz, b * 2 + c + 1)
                    pe.wait_ge(s_yT, b * 6 + max(n - 1, 0))
                    for q in range(4):
                        ins = nc.tensor.transpose(pT[n % 2][:, q * P:(q + 1) * P], y_sb[i][:, c, (j * 4 + q) * P:(j * 4 + q + 1) * P], ident_sb[:, :])
                    ins.then_inc(s_T, 1)
                for c in range(2):
                    pe.wait_ge(s_yT, b * 6 + 3 * c + 3)
                    pe.wait_ge(s_var, b * 2)
                    for k in range(F):
                        ins = nc.tensor.matmul(po[c][:, :], yT[:, c, k, :], w_sb[:, k, :], start=(k == 0), stop=(k == F - 1))
                    ins.then_inc(s_o, 1)

            def norm(b, i):
                for c in range(2):
                    pe.wait_ge(s_ln, b * 2 + c + 1)
                    pe.wait_ge(s_oT, b * 2)
                    for k in range(KD):
                        ins = nc.tensor.transpose(px[c][:, k * P:(k + 1) * P], o_sb[:, c, k * P:(k + 1) * P], ident_sb[:, :])
                    ins.then_inc(s_xT, 1)
            pipelined(pe, products, norm)


def long_conv(nc, x_feat, ctx_turned, taps, skip, exchange, r_feat):
    HEADS, R = 32, 8
    PAIRS = R * (R + 1) // 2
    OFF = [R * i - i * (i - 1) // 2 for i in range(R)]
    N = NB * PAIRS
    with ExitStack() as phase:
        m = Space(nc, "b1", phase)
        x_sb, c_sb = m.sb("x", [P, KD, T]), m.sb("c", [P, KD, T])
        x4 = x_sb[:, :, :].rearrange("p k (b t) -> p k b t", b=NB)
        c4 = c_sb[:, :, :].rearrange("p k (b t) -> p k b t", b=NB)
        exchange_sb, skip_sb = m.sb("exchange", [P, P]), m.sb("skip", [P, HEADS])
        toe = [m.sb(f"toe{i}", [P, D]) for i in range(2)]
        dg = [m.sb(f"dg{i}", [P, P]) for i in range(2)]
        kv = [m.sb(f"kv{i}", [P, KD, NB, PAIRS]) for i in range(2)]
        prod = [m.sb(f"prod{i}", [P, KD, NB, R, R]) for i in range(2)]
        red = [m.sb(f"red{i}", [P, KD, NB, R]) for i in range(2)]
        py = [m.ps(f"py{i}", (P, KD, BANK)) for i in range(2)]
        s_const, s_x, s_c, s_out, s_lv = (m.sem(n) for n in "const x c out lv".split())
        s_toe = [m.sem(f"toe{i}") for i in range(2)]
        s_kv, s_dg, s_y, s_prod, s_red, s_sum = (m.sem(n) for n in "kv dg y prod red sum".split())
        tick_sp = m.sem("tick_sp")
        block = phase.enter_context(nc.Block())
        PRODS = 2 * R - 1

        @block.sync
        def _(sp):
            sp.dma_start(exchange_sb[:, :], exchange).then_inc(s_const, 16)
            sp.dma_start(skip_sb[:, :], skip.partition_broadcast(P)).then_inc(s_const, 16)
            sp.dma_start(c_sb[:, :, :], ctx_turned.rearrange("k p t -> p k t")).then_inc(s_c, 16)
            sp.dma_start(x_sb[:, :, :], x_feat.rearrange("k p t -> p k t")).then_inc(s_x, 16)

            def filters(h, i):
                row = taps[bass.ds(h, 1), 0:D]
                sp.dma_start(toe[i][:, :], bass.AP(row.tensor, row.offset, [[1, P], [1, D]])).then_inc(s_toe[i], 16)
            for i in range(2):
                filters(i, i)
            with sp.Fori(0, HEADS // 2 - 1) as g:
                for i in range(2):
                    sp.wait_ge(s_y, 2 * g + i + 1)
                    alone(sp, tick_sp)
                    filters(2 * g + 2 + i, i)
            sp.wait_ge(s_sum, HEADS + 1)
            sp.dma_start(r_feat.rearrange("k p t -> p k t"), x_sb[:, :, :]).then_inc(s_out, 16)
            sp.wait_ge(s_out, 16)

        @block.gpsimd
        def _(pool):
            pool.sem_inc(s_sum, 1)
            pool.wait_ge(s_c, 16)
            pool.wait_ge(s_const, 32)

            def products(h, g, i):
                for r in range(R):
                    ins = pool.tensor_tensor(kv[i][:, :, :, OFF[r]:OFF[r] + R - r], c4[:, :, :, bass.ds(h * R + r, R - r)],
                                             c4[:, :, :, bass.ds(h * R + r, 1)].to_broadcast([P, KD, NB, R - r]), ALU.mult)
                    ins.then_inc(s_kv, 1)
                pool.tensor_tensor(dg[i][:, :], exchange_sb[:, :], skip_sb[:, bass.ds(h, 1)].to_broadcast([P, P]), ALU.mult).then_inc(s_dg, 1)
                pool.wait_ge(s_dg, 2 * h + 1)
                pool.wait_ge(s_toe[i], g * 16 + 16)
                pool.tensor_tensor(toe[i][:, 0:P], toe[i][:, 0:P], dg[i][:, :], ALU.add).then_inc(s_dg, 1)

            def add_back(h, i):
                pool.wait_ge(s_red, h + 1)
                at = x4[:, :, :, bass.ds(h * R, R)]
                pool.tensor_tensor(at, at, red[i][:, :, :, :], ALU.add).then_inc(s_sum, 1)
            for i in range(2):
                products(i, 0, i)
            with pool.Fori(0, HEADS // 2 - 1) as g:
                for i in range(2):
                    pool.wait_ge(s_y, 2 * g + i + 1)
                    products(2 * g + 2 + i, g + 1, i)
                    add_back(2 * g + i, i)
            for i in range(2):
                add_back(HEADS - 2 + i, i)

        @block.vector
        def _(dve):
            dve.sem_inc(s_prod, PRODS)
            dve.wait_ge(s_x, 16)
            with dve.Fori(0, HEADS // 2) as g:
                for i in range(2):
                    h = 2 * g + i
                    dve.wait_ge(s_y, h + 1)
                    dve.wait_ge(s_red, 2 * g)
                    for r in range(R):
                        n = R - r
                        src = py[i][:, :, 0:N].rearrange("p k (b n) -> p k b n", b=NB)
                        ins = nc.vector.tensor_tensor(prod[i][:, :, :, r:R, r], src[:, :, :, OFF[r]:OFF[r] + n],
                                                      x4[:, :, :, bass.ds(h * R + r, 1)].to_broadcast([P, KD, NB, n]), ALU.mult)
                        ins.then_inc(s_prod, 1)
                        if n > 1:
                            ins = nc.vector.tensor_tensor(prod[i][:, :, :, r, r + 1:R], src[:, :, :, OFF[r] + 1:OFF[r] + n],
                                                          x4[:, :, :, bass.ds(h * R + r + 1, n - 1)], ALU.mult)
                            ins.then_inc(s_prod, 1)
                    dve.wait_ge(s_prod, (h + 2) * PRODS)
                    dve.wait_ge(s_sum, h)
                    nc.vector.tensor_reduce(red[i][:, :, :, :].rearrange("p k b r -> p (k b r)"),
                                            prod[i][:, :, :, :, :].rearrange("p k b o r -> p (k b o) r"), AX.X, ALU.add).then_inc(s_red, 1)

        @block.tensor
        def _(pe):
            with pe.Fori(0, HEADS // 2) as g:
                for i in range(2):
                    h = 2 * g + i
                    pe.wait_ge(s_dg, 2 * h + 2)
                    pe.wait_ge(s_kv, h * R + R)
                    pe.wait_ge(s_prod, h * PRODS)
                    for o in range(KD):
                        for k in range(o + 1):
                            ins = nc.tensor.matmul(py[i][:, o, 0:N], toe[i][:, (o - k) * P:(o - k + 1) * P],
                                                   kv[i][:, k, :, :].rearrange("p b n -> p (b n)"), start=(k == 0), stop=(k == o))
                    ins.then_inc(s_y, 1)


def norm_from_feat(nc, name, v_feat, ident, o_tok, o_feat):
    LN_EPS = 1e-5
    BUF = 4
    with ExitStack() as phase:
        m = Space(nc, name, phase)
        ident_sb, eps_sb = m.sb("ident", [P, P]), m.sb("eps", [P, 1])
        v_sb = [m.sb(f"v{i}", [P, KD, P]) for i in range(BUF)]
        st = [m.sb(f"st{i}", [P, 6]) for i in range(BUF)]
        mv = [m.sb(f"mv{i}", [P, 2]) for i in range(BUF)]
        sd = [m.sb(f"sd{i}", [P, 1]) for i in range(BUF)]
        o_sb = [m.sb(f"o{i}", [P, D]) for i in range(BUF)]
        oT = [m.sb(f"oT{i}", [P, KD, P]) for i in range(BUF)]
        pv = [m.ps(f"pv{i}") for i in range(BUF)]
        po = [m.ps(f"po{i}") for i in range(BUF)]
        s_const, s_set, s_lv = m.sem("const"), m.sem("set"), m.sem("lv")
        s_in = [m.sem(f"in{i}") for i in range(BUF)]
        s_out = [m.sem(f"out{i}") for i in range(BUF)]
        s_T, s_var, s_sd, s_ln, s_oT, s_oc = (m.sem(n) for n in "T var sd ln oT oc".split())
        tick_dve, tick_sp, tick_pool = (m.sem("tick_" + n) for n in "dve sp pool".split())
        block = phase.enter_context(nc.Block())
        LV = 2

        @block.sync
        def _(sp):
            sp.dma_start(ident_sb[:, :], ident).then_inc(s_const, 16)
            with sp.Fori(0, TILES // BUF) as r:
                for i in range(BUF):
                    t = BUF * r + i
                    sp.wait_ge(s_T, t + 1)
                    alone(sp, tick_sp)
                    sp.dma_start(v_sb[i][:, :, :], v_feat[:, :, bass.ds(t * P, P)].rearrange("k p t -> p k t")).then_inc(s_in[i], 16)

        @block.gpsimd
        def _(pool):
            with pool.Fori(0, TILES // BUF) as r:
                for i in range(BUF):
                    t = BUF * r + i
                    pool.wait_ge(s_oc, t + 1)
                    alone(pool, tick_pool)
                    pool.dma_start(o_tok[bass.ds(t * P, P), :], o_sb[i][:, :]).then_inc(s_out[i], 16)
                    pool.dma_start(o_feat[:, :, bass.ds(t * P, P)].rearrange("k p t -> p k t"), oT[i][:, :, :]).then_inc(s_out[i], 16)
            for i in range(BUF):
                pool.wait_ge(s_out[i], TILES // BUF * 32)

        @block.scalar
        def _(act):
            act.wait_ge(s_set, 1)
            with act.Fori(0, TILES // BUF) as r:
                for i in range(BUF):
                    act.wait_ge(s_var, BUF * r + i + 1)
                    nc.scalar.activation(sd[i][:, :], mv[i][:, 1:2], ACT.Sqrt, bias=eps_sb[:, :], scale=1.0).then_inc(s_sd, 1)
                for i in range(BUF):
                    act.wait_ge(s_oT, BUF * r + i + 1)
                    act.wait_ge(s_out[i], r * 32)
                    nc.scalar.copy(oT[i][:, :, :].rearrange("p k t -> p (k t)"), po[i][:, :]).then_inc(s_oc, 1)

        @block.vector
        def _(dve):
            nc.vector.memset(eps_sb[:, :], LN_EPS).then_inc(s_set, 1)
            with dve.Fori(0, TILES // BUF) as r:
                for i in range(BUF):
                    link = linker(dve, s_lv, (BUF * r + i) * LV)
                    dve.wait_ge(s_T, BUF + BUF * r + i + 1)
                    link(nc.vector.bn_stats(st[i][:, :], pv[i][:, :]))
                    alone(dve, tick_dve)
                    nc.vector.bn_aggr(mv[i][:, :], st[i][:, :]).then_inc(s_var, 1)
                    dve.wait_ge(s_sd, BUF * r + i + 1)
                    link(nc.vector.reciprocal(sd[i][:, :], sd[i][:, :]))
                    dve.wait_ge(s_out[i], r * 32)
                    nc.vector.tensor_scalar(o_sb[i][:, :], pv[i][:, :], mv[i][:, 0:1], sd[i][:, :], ALU.subtract, ALU.mult).then_inc(s_ln, 1)

        @block.tensor
        def _(pe):
            nc.tensor.sem_inc(s_T, BUF)
            pe.wait_ge(s_const, 16)
            with pe.Fori(0, TILES // BUF) as r:
                for i in range(BUF):
                    pe.wait_ge(s_in[i], r * 16 + 16)
                    pe.wait_ge(s_ln, BUF * r)
                    for k in range(KD):
                        ins = nc.tensor.transpose(pv[i][:, k * P:(k + 1) * P], v_sb[i][:, k, :], ident_sb[:, :])
                    ins.then_inc(s_T, 1)
                for i in range(BUF):
                    pe.wait_ge(s_ln, BUF * r + i + 1)
                    pe.wait_ge(s_oc, BUF * r)
                    for k in range(KD):
                        ins = nc.tensor.transpose(po[i][:, k * P:(k + 1) * P], o_sb[i][:, k * P:(k + 1) * P], ident_sb[:, :])
                    ins.then_inc(s_oT, 1)


E_, K_, CAP, FF = 64, 8, 128, 192
SLOTS = E_ * CAP
FAR = 1 << 20


def moe0_route(nc, x_tok, x_feat, router, ident, before, ramp, x_slots, places, weights):
    with ExitStack() as phase:
        m = Space(nc, "c1", phase)
        rw = m.sb("rw", [P, KD, E_])
        before_sb = m.sb("before", [P, P])
        ones = m.sb("ones", [P, P])
        ramp_sb = m.sb("ramp", [P, E_])
        xf = [m.sb(f"xf{i}", [P, KD, P]) for i in range(2)]
        xt = [m.sb(f"xt{i}", [P, D]) for i in range(2)]
        mx, se, wn = m.sb("mx", [P, 1]), m.sb("se", [P, 1]), m.sb("wn", [P, 1])
        ex = m.sb("ex", [P, E_])
        top = m.sb("top", [P, K_])
        idx = m.sb("idx", [P, K_], U32)
        idf = m.sb("idf", [P, K_])
        hot = m.sb("hot", [P, K_, E_])
        tmp = m.sb("tmp", [P, K_, E_])
        A = m.sb("A", [P, E_])
        S = m.sb("S", [P, E_])
        pk, ok, pf = m.sb("pk", [P, K_]), m.sb("ok", [P, K_]), m.sb("pf", [P, K_])
        wk = [m.sb(f"wk{i}", [P, K_]) for i in range(2)]
        pl = [m.sb(f"pl{i}", [P, K_], U32) for i in range(2)]
        pL, pP = m.ps("pL"), m.ps("pP")
        s_const, s_set, s_lv = m.sem("const"), m.sem("set"), m.sem("lv")
        s_in = [m.sem(f"in{i}") for i in range(2)]
        s_log, s_neg, s_exp, s_A, s_pos, s_pl, s_used = (m.sem(n) for n in "log neg exp A pos pl used".split())
        s_out = [m.sem(f"out{i}") for i in range(2)]
        s_sc = [m.sem(f"sc{i}") for i in range(2)]
        tick_dve, tick_pool = m.sem("tick_dve"), m.sem("tick_pool")
        block = phase.enter_context(nc.Block())
        LV = 17

        @block.sync
        def _(sp):
            for dst, src in ((rw[:, :, :], router.rearrange("(k p) e -> p k e", p=P)), (before_sb[:, :], before), (ramp_sb[:, :], ramp.partition_broadcast(P))):
                sp.dma_start(dst, src).then_inc(s_const, 16)
            with sp.Fori(0, TILES // 2) as r:
                for i in range(2):
                    t = 2 * r + i
                    sp.wait_ge(s_log, 2 * r)
                    sp.wait_ge(s_sc[i], r * K_ * 16)
                    sp.dma_start(xf[i][:, :, :], x_feat[:, :, bass.ds(t * P, P)].rearrange("k p t -> p k t")).then_inc(s_in[i], 16)
                    sp.dma_start(xt[i][:, :], x_tok[bass.ds(t * P, P), :]).then_inc(s_in[i], 16)
                for i in range(2):
                    t = 2 * r + i
                    sp.wait_ge(s_pl, t + 1)
                    sp.dma_start(places[bass.ds(t * P, P), :], pl[i][:, :]).then_inc(s_out[i], 16)
                    sp.dma_start(weights[bass.ds(t * P, P), :], wk[i][:, :]).then_inc(s_out[i], 16)
            for i in range(2):
                sp.wait_ge(s_out[i], TILES // 2 * 32)

        @block.gpsimd
        def _(pool):
            with pool.Fori(0, TILES // 2) as r:
                for i in range(2):
                    t = 2 * r + i
                    pool.wait_ge(s_in[i], r * 32 + 32)
                    pool.wait_ge(s_pl, t + 1)
                    alone(pool, tick_pool)
                    for k in range(K_):
                        pool.indirect_dma_start(x_slots, bass.IndirectOffsetOnAxis(ap=pl[i][:, k:k + 1], axis=0), xt[i][:, :], None,
                                                bounds_check=SLOTS - 1, oob_is_err=False).then_inc(s_sc[i], 16)
            for i in range(2):
                pool.wait_ge(s_sc[i], TILES // 2 * K_ * 16)

        @block.scalar
        def _(act):
            with act.Fori(0, TILES) as t:
                act.wait_ge(s_neg, t + 1)
                nc.scalar.activation(ex[:, :], pL[:, 0:E_], ACT.Exp, bias=mx[:, :], scale=1.0, accum_out=se[:, :]).then_inc(s_exp, 1)

        @block.vector
        def _(dve):
            nc.vector.memset(ones[:, :], 1.0).then_inc(s_set, 1)
            nc.vector.memset(S[:, :], 0.0).then_inc(s_set, 1)
            dve.wait_ge(s_set, 2)
            dve.wait_ge(s_const, 48)
            with dve.Fori(0, TILES // 2) as r:
                for i in range(2):
                    t = 2 * r + i
                    link = linker(dve, s_lv, t * LV)
                    dve.wait_ge(s_log, t + 1)
                    link(nc.vector.tensor_reduce(mx[:, :], pL[:, 0:E_], AX.X, ALU.max))
                    nc.vector.tensor_scalar(mx[:, :], mx[:, :], -1.0, None, ALU.mult).then_inc(s_neg, 1)
                    dve.wait_ge(s_exp, t + 1)
                    link(nc.vector.reciprocal(se[:, :], se[:, :]))
                    link(nc.vector.tensor_scalar(ex[:, :], ex[:, :], se[:, :], None, ALU.mult))
                    alone(dve, tick_dve)
                    link(nc.vector.max(top[:, :], ex[:, :]))
                    alone(dve, tick_dve)
                    link(nc.vector.max_index(idx[:, :], top[:, :], ex[:, :]))
                    link(nc.vector.tensor_copy(idf[:, :], idx[:, :]))
                    link(nc.vector.tensor_tensor(hot[:, :, :], ramp_sb[:, :].unsqueeze(1).to_broadcast([P, K_, E_]),
                                                 idf[:, :].unsqueeze(2).to_broadcast([P, K_, E_]), ALU.is_equal))
                    dve.wait_ge(s_pos, t)
                    nc.vector.tensor_reduce(A[:, :], hot[:, :, :].rearrange("p k e -> p e k"), AX.X, ALU.add).then_inc(s_A, 1)
                    link(nc.vector.tensor_reduce(wn[:, :], top[:, :], AX.X, ALU.add))
                    link(nc.vector.tensor_scalar(wn[:, :], wn[:, :], 1e-20, None, ALU.add))
                    link(nc.vector.reciprocal(wn[:, :], wn[:, :]))
                    dve.wait_ge(s_pos, t + 1)
                    link(nc.vector.tensor_tensor(S[:, :], S[:, :], A[:, :], ALU.add))
                    link(nc.vector.tensor_tensor(tmp[:, :, :], hot[:, :, :], pP[:, 0:E_].unsqueeze(1).to_broadcast([P, K_, E_]), ALU.mult))
                    link(nc.vector.tensor_reduce(pk[:, :], tmp[:, :, :], AX.X, ALU.add))
                    link(nc.vector.tensor_scalar(ok[:, :], pk[:, :], float(CAP), None, ALU.is_lt))
                    link(nc.vector.scalar_tensor_tensor(pf[:, :], idf[:, :], float(CAP), pk[:, :], ALU.mult, ALU.add))
                    link(nc.vector.tensor_scalar(pk[:, :], ok[:, :], -float(FAR), float(FAR), ALU.mult, ALU.add))
                    dve.wait_ge(s_sc[i], r * K_ * 16)
                    dve.wait_ge(s_out[i], r * 32)
                    link(nc.vector.scalar_tensor_tensor(wk[i][:, :], top[:, :], wn[:, :], ok[:, :], ALU.mult, ALU.mult))
                    nc.vector.tensor_tensor(pl[i][:, :], pf[:, :], pk[:, :], ALU.add).then_inc(s_pl, 1)
                    assert link.count[0] == LV, link.count[0]

        @block.tensor
        def _(pe):
            pe.wait_ge(s_const, 48)
            pe.wait_ge(s_set, 2)
            with pe.Fori(0, TILES // 2) as r:
                for i in range(2):
                    t = 2 * r + i
                    pe.wait_ge(s_in[i], r * 32 + 32)
                    pe.wait_ge(s_exp, t)
                    for k in range(KD):
                        ins = nc.tensor.matmul(pL[:, 0:E_], xf[i][:, k, :], rw[:, k, :], start=(k == 0), stop=(k == KD - 1))
                    ins.then_inc(s_log, 1)
                    pe.wait_ge(s_A, t + 1)
                    pe.wait_ge(s_pl, t)
                    nc.tensor.matmul(pP[:, 0:E_], before_sb[:, :], A[:, :], start=True, stop=False)
                    nc.tensor.matmul(pP[:, 0:E_], ones[:, :], S[:, :], start=False, stop=True).then_inc(s_pos, 1)


def moe0_experts(nc, x_slots, w_gu, w_down, ident, y_slots):
    U, BUF = 8, 8
    F2 = FF - P
    with ExitStack() as phase:
        m = Space(nc, "c2", phase)
        ident_sb = m.sb("ident", [P, P])
        gu = [m.sb(f"gu{i}", [P, KD, 2 * FF]) for i in range(BUF)]
        wd = [m.sb(f"wd{i}", [P, 2, D]) for i in range(BUF)]
        xb = [m.sb(f"xb{i}", [P, D]) for i in range(BUF)]
        xT = [m.sb(f"xT{i}", [P, D]) for i in range(2)]
        g_sb = [m.sb(f"g{i}", [P, FF]) for i in range(2)]
        h_sb = [m.sb(f"h{i}", [P, FF]) for i in range(2)]
        hT = [m.sb(f"hT{i}", [P, 2, P]) for i in range(2)]
        y_sb = [m.sb(f"y{i}", [P, D]) for i in range(2)]
        pT = [m.ps(f"pT{i}") for i in range(2)]
        pG = [m.ps(f"pG{i}") for i in range(2)]
        pH = [m.ps(f"pH{i}") for i in range(2)]
        pY = [m.ps(f"pY{i}") for i in range(2)]
        s_const = m.sem("const")
        s_in = [m.sem(f"in{i}") for i in range(BUF)]
        s_T, s_xT, s_G, s_g, s_h, s_H, s_hT, s_Y, s_y = (m.sem(n) for n in "T xT G g h H hT Y y".split())
        s_out = [m.sem(f"out{i}") for i in range(2)]
        block = phase.enter_context(nc.Block())

        @block.sync
        def _(sp):
            sp.dma_start(ident_sb[:, :], ident).then_inc(s_const, 16)
            with sp.Fori(0, E_ // U) as r:
                for j in range(U):
                    e, q = r * U + j, j % BUF
                    sp.wait_ge(s_Y, e + 1)
                    sp.dma_start(gu[q][:, :, :], w_gu[bass.ds(e, 1), :, :, :].rearrange("e p k n -> (e p) k n")).then_inc(s_in[q], 16)
                    sp.dma_start(wd[q][:, 0, :], w_down[bass.ds(e, 1), 0:P, :].rearrange("e p n -> (e p) n")).then_inc(s_in[q], 16)
                    sp.dma_start(wd[q][0:F2, 1, :], w_down[bass.ds(e, 1), P:FF, :].rearrange("e p n -> (e p) n")).then_inc(s_in[q], 16)
                    sp.dma_start(xb[q][:, :], x_slots[bass.ds(e * CAP, CAP), :]).then_inc(s_in[q], 16)

        @block.gpsimd
        def _(pool):
            with pool.Fori(0, E_ // U) as r:
                for j in range(U):
                    e, q = r * U + j, j % 2
                    pool.wait_ge(s_y, e + 1)
                    pool.dma_start(y_slots[bass.ds(e * CAP, CAP), :], y_sb[q][:, :]).then_inc(s_out[q], 16)
            for q in range(2):
                pool.wait_ge(s_out[q], E_ // 2 * 16)

        def later(e, n, j):
            return e - n if j >= n else e - j

        @block.scalar
        def _(act):
            with act.Fori(0, E_ // U) as r:
                for s in range(U + 2):
                    if s < U:
                        e = r * U + s
                        act.wait_ge(s_T, e + 1)
                        act.wait_ge(s_G, later(e, 1, s))
                        nc.scalar.copy(xT[s % 2][:, :], pT[s % 2][:, :]).then_inc(s_xT, 1)
                    if 1 <= s <= U:
                        j = s - 1
                        e = r * U + j
                        act.wait_ge(s_G, e + 1)
                        act.wait_ge(s_h, later(e, 1, j))
                        nc.scalar.activation(g_sb[j % 2][:, :], pG[j % 2][:, 0:FF], ACT.Silu).then_inc(s_g, 1)

        @block.vector
        def _(dve):
            with dve.Fori(0, E_ // U) as r:
                for s in range(U + 2):
                    if s < U:
                        e = r * U + s
                        dve.wait_ge(s_g, e + 1)
                        dve.wait_ge(s_H, later(e, 1, s))
                        nc.vector.tensor_tensor(h_sb[s % 2][:, :], g_sb[s % 2][:, :], pG[s % 2][:, FF:2 * FF], ALU.mult).then_inc(s_h, 1)
                    if 1 <= s <= U:
                        j = s - 1
                        e = r * U + j
                        dve.wait_ge(s_H, e + 1)
                        dve.wait_ge(s_Y, BUF + later(e, 1, j))
                        nc.vector.tensor_copy(hT[j % 2][:, 0, :], pH[j % 2][:, 0:P]).then_inc(s_hT, 1)
                        nc.vector.tensor_copy(hT[j % 2][0:F2, 1, :], pH[j % 2][0:F2, P:2 * P]).then_inc(s_hT, 1)
                    if s >= 2:
                        j = s - 2
                        e = r * U + j
                        dve.wait_ge(s_Y, BUF + e + 1)
                        dve.wait_ge(s_out[j % 2], (r * (U // 2) + j // 2) * 16)
                        nc.vector.tensor_copy(y_sb[j % 2][:, :], pY[j % 2][:, :]).then_inc(s_y, 1)

        @block.tensor
        def _(pe):
            nc.tensor.sem_inc(s_Y, BUF)
            pe.wait_ge(s_const, 16)
            with pe.Fori(0, E_ // U) as r:
                for s in range(U + 3):
                    if s < U:
                        e, q = r * U + s, s % BUF
                        pe.wait_ge(s_in[q], (r * (U // BUF) + s // BUF + 1) * 64)
                        pe.wait_ge(s_xT, later(e, 1, s))
                        for k in range(KD):
                            ins = nc.tensor.transpose(pT[s % 2][:, k * P:(k + 1) * P], xb[q][:, k * P:(k + 1) * P], ident_sb[:, :])
                        ins.then_inc(s_T, 1)
                    if 1 <= s <= U:
                        j = s - 1
                        e = r * U + j
                        pe.wait_ge(s_xT, e + 1)
                        pe.wait_ge(s_h, later(e, 1, j))
                        for k in range(KD):
                            ins = nc.tensor.matmul(pG[j % 2][:, 0:2 * FF], xT[j % 2][:, k * P:(k + 1) * P], gu[j % BUF][:, k, :], start=(k == 0), stop=(k == KD - 1))
                        ins.then_inc(s_G, 1)
                    if 2 <= s <= U + 1:
                        j = s - 2
                        e = r * U + j
                        pe.wait_ge(s_h, e + 1)
                        pe.wait_ge(s_hT, 2 * later(e, 1, j))
                        nc.tensor.transpose(pH[j % 2][:, 0:P], h_sb[j % 2][:, 0:P], ident_sb[:, :])
                        nc.tensor.transpose(pH[j % 2][0:F2, P:2 * P], h_sb[j % 2][:, P:FF], ident_sb[:, :]).then_inc(s_H, 1)
                    if s >= 3:
                        j = s - 3
                        e = r * U + j
                        pe.wait_ge(s_hT, 2 * e + 2)
                        pe.wait_ge(s_y, later(e, 1, j))
                        nc.tensor.matmul(pY[j % 2][:, :], hT[j % 2][:, 0, :], wd[j % BUF][:, 0, :], start=True, stop=False)
                        nc.tensor.matmul(pY[j % 2][:, :], hT[j % 2][0:F2, 1, :], wd[j % BUF][0:F2, 1, :], start=False, stop=True).then_inc(s_Y, 1)


def gather_mix_norm(nc, name, K, y_slots, slots, x_tok, places, weights, ident, o_tok, o_feat):
    LN_EPS = 1e-5
    BUF = 4
    with ExitStack() as phase:
        m = Space(nc, name, phase)
        ident_sb, eps_sb = m.sb("ident", [P, P]), m.sb("eps", [P, 1])
        x_sb = [m.sb(f"x{i}", [P, D]) for i in range(BUF)]
        pl = [m.sb(f"pl{i}", [P, K], U32) for i in range(BUF)]
        wk = [m.sb(f"wk{i}", [P, K]) for i in range(BUF)]
        g = [m.sb(f"g{i}", [P, K, D]) for i in range(BUF)]
        st, mv, sd = m.sb("st", [P, 6]), m.sb("mv", [P, 2]), m.sb("sd", [P, 1])
        o_sb = [m.sb(f"o{i}", [P, D]) for i in range(BUF)]
        oT = [m.sb(f"oT{i}", [P, KD, P]) for i in range(BUF)]
        po = [m.ps(f"po{i}") for i in range(BUF)]
        s_const, s_set, s_lv = m.sem("const"), m.sem("set"), m.sem("lv")
        s_in = [m.sem(f"in{i}") for i in range(BUF)]
        s_g = [m.sem(f"g{i}") for i in range(BUF)]
        s_out = [m.sem(f"out{i}") for i in range(BUF)]
        s_var, s_sd, s_ln, s_oT, s_oc = (m.sem(n) for n in "var sd ln oT oc".split())
        tick_dve, tick_pool, tick_sp, tick_act = (m.sem("tick_" + n) for n in "dve pool sp act".split())
        block = phase.enter_context(nc.Block())
        LV = K + 2

        @block.sync
        def _(sp):
            sp.dma_start(ident_sb[:, :], ident).then_inc(s_const, 16)
            with sp.Fori(0, TILES // BUF) as r:
                for i in range(BUF):
                    t = BUF * r + i
                    sp.wait_ge(s_ln, t + 1)
                    alone(sp, tick_sp)
                    for dst, src in ((x_sb, x_tok), (pl, places), (wk, weights)):
                        sp.dma_start(dst[i][:, :], src[bass.ds(t * P, P), :]).then_inc(s_in[i], 16)
            for i in range(BUF):
                sp.wait_ge(s_out[i], TILES // BUF * (16 if o_feat is None else 32))
        stores = 16 if o_feat is None else 32

        @block.gpsimd
        def _(pool):
            pool.wait_ge(s_set, BUF + 1)
            with pool.Fori(0, TILES // BUF) as r:
                for i in range(BUF):
                    pool.wait_ge(s_in[i], r * 48 + 48)
                    pool.wait_ge(s_ln, BUF * r + i + 1)
                    alone(pool, tick_pool)
                    for k in range(K):
                        pool.indirect_dma_start(g[i][:, k, :], None, y_slots, bass.IndirectOffsetOnAxis(ap=pl[i][:, k:k + 1], axis=0),
                                                bounds_check=slots - 1, oob_is_err=False).then_inc(s_g[i], 16)

        @block.scalar
        def _(act):
            act.wait_ge(s_set, 1)
            with act.Fori(0, TILES // BUF) as r:
                for i in range(BUF):
                    t = BUF * r + i
                    act.wait_ge(s_var, t + 1)
                    nc.scalar.activation(sd[:, :], mv[:, 1:2], ACT.Sqrt, bias=eps_sb[:, :], scale=1.0).then_inc(s_sd, 1)
                    act.wait_ge(s_ln, BUF + t + 1)
                    alone(act, tick_act)
                    act.dma_start(o_tok[bass.ds(t * P, P), :], o_sb[i][:, :]).then_inc(s_out[i], 16)
                    if o_feat is not None:
                        act.wait_ge(s_oT, t + 1)
                        act.wait_ge(s_oc, t)
                        nc.scalar.copy(oT[i][:, :, :].rearrange("p k t -> p (k t)"), po[i][:, :]).then_inc(s_oc, 1)
                        act.wait_ge(s_oc, t + 1)
                        alone(act, tick_act)
                        act.dma_start(o_feat[:, :, bass.ds(t * P, P)].rearrange("k p t -> p k t"), oT[i][:, :, :]).then_inc(s_out[i], 16)

        @block.vector
        def _(dve):
            dve.sem_inc(s_ln, BUF)
            nc.vector.memset(eps_sb[:, :], LN_EPS).then_inc(s_set, 1)
            for i in range(BUF):
                nc.vector.memset(g[i][:, :, :], 0.0).then_inc(s_set, 1)
            dve.wait_ge(s_set, BUF + 1)
            with dve.Fori(0, TILES // BUF) as r:
                for i in range(BUF):
                    t = BUF * r + i
                    link = linker(dve, s_lv, t * LV)
                    dve.wait_ge(s_in[i], r * 48 + 48)
                    dve.wait_ge(s_g[i], (r + 1) * K * 16)
                    x = x_sb[i][:, :]
                    for k in range(K):
                        link(nc.vector.scalar_tensor_tensor(x, g[i][:, k, :], wk[i][:, k:k + 1], x, ALU.mult, ALU.add))
                    link(nc.vector.bn_stats(st[:, :], x))
                    alone(dve, tick_dve)
                    nc.vector.bn_aggr(mv[:, :], st[:, :]).then_inc(s_var, 1)
                    dve.wait_ge(s_sd, t + 1)
                    link(nc.vector.reciprocal(sd[:, :], sd[:, :]))
                    dve.wait_ge(s_out[i], r * stores)
                    nc.vector.tensor_scalar(o_sb[i][:, :], x, mv[:, 0:1], sd[:, :], ALU.subtract, ALU.mult).then_inc(s_ln, 1)

        if o_feat is not None:
            @block.tensor
            def _(pe):
                pe.wait_ge(s_const, 16)
                with pe.Fori(0, TILES // BUF) as r:
                    for i in range(BUF):
                        pe.wait_ge(s_ln, BUF + BUF * r + i + 1)
                        pe.wait_ge(s_oc, BUF * r)
                        for k in range(KD):
                            ins = nc.tensor.transpose(po[i][:, k * P:(k + 1) * P], o_sb[i][:, k * P:(k + 1) * P], ident_sb[:, :])
                        ins.then_inc(s_oT, 1)


DI1, N1 = 1024, 16
F1 = DI1 // P


def ssm1_project(nc, x_feat, w_in, conv_w, conv_b, w_x, w_dt, b_dt, u_feat, z_feat, dt_feat, bc_feat):
    WBUF = 6
    LAST = NB - 1
    with ExitStack() as phase:
        m = Space(nc, "d1", phase)
        w_raw = [m.sb(f"wraw{i}", [P, BANK]) for i in range(WBUF)]
        w_hi, w_lo = (m.sb("w" + n, [P, KD, 2 * DI1], F32R) for n in ("hi", "lo"))
        x_hi, x_lo = ([m.sb(f"x{n}{i}", [P, KD, L], F32R) for i in range(2)] for n in ("hi", "lo"))
        wx_sb = m.sb("wx", [P, F1, P + 2 * N1])
        wdt_sb = m.sb("wdt", [P, DI1])
        cw_sb, cb_sb, bdt_sb = m.sb("cw", [P, F1, 4]), m.sb("cb", [P, F1]), m.sb("bdt", [P, F1])
        one_sb = m.sb("one", [P, 1])
        xT = [m.sb(f"xT{i}", [P, KD, L]) for i in range(2)]
        xpad = [m.sb(f"xpad{i}", [P, 3 + L]) for i in range(2)]
        acc = [m.sb(f"acc{i}", [P, L]) for i in range(2)]
        u_sb, z_sb, dt_sb = m.sb("u", [P, F1, L]), m.sb("z", [P, F1, L]), m.sb("dt", [P, F1, L])
        v_sb, r_sb = m.sb("v", [P, F1, L]), m.sb("r", [P, F1, L])
        dr_sb, bc_sb = m.sb("dr", [P, L]), m.sb("bc", [2 * N1, L])
        px = [m.ps(f"px{i}") for i in range(2)]
        pz = [m.ps(f"pz{i}") for i in range(2)]
        pd = [m.ps(f"pd{i}") for i in range(2)]
        pr, pb = m.ps("pr"), m.ps("pb")
        s_const, s_set, s_lv = m.sem("const"), m.sem("set"), m.sem("lv")
        s_x = [m.sem(f"x{i}") for i in range(2)]
        s_px, s_xpad, s_conv, s_u, s_pz, s_z, s_pr, s_dr, s_pb, s_bc, s_pd, s_v, s_r, s_la, s_dt, s_out = (
            m.sem(n) for n in "px xpad conv u pz z pr dr pb bc pd v r la dt out".split())
        s_dts, tick_sp = m.sem("dts"), m.sem("tick_sp")
        block = phase.enter_context(nc.Block())
        s_w = [m.sem(f"w{i}") for i in range(WBUF)]
        s_wh, s_wl, s_xh, s_xl, s_out_u, s_out_z = (m.sem(n) for n in "wh wl xh xl out_u out_z".split())
        CONSTS = 5
        CHUNKS = [(k, slice(j * BANK, (j + 1) * BANK)) for j in range(2 * DI1 // BANK) for k in range(KD)]
        SPLIT_AT = 4

        def more(b):
            return not (isinstance(b, int) and b == LAST)

        def pipelined(eng, project, step_sizes):
            project(0, 0, 0, None)
            with eng.Fori(0, NB // 2 - 1) as r:
                for i in range(2):
                    b = 2 * r + 1 + i
                    project(b, r + i, 1 - i, lambda b=b: step_sizes(b - 1))
            project(LAST, NB // 2 - 1, 1, lambda: step_sizes(NB - 2))
            step_sizes(NB - 1)

        @block.sync
        def _(sp):
            for dst, src in ((cw_sb[:, :, :], conv_w.rearrange("(k p) c -> p k c", p=P)), (cb_sb[:, :], conv_b.rearrange("(k p) -> p k", p=P)),
                             (bdt_sb[:, :], b_dt.rearrange("(k p) -> p k", p=P)),
                             (wx_sb[:, :, :], w_x.rearrange("(k p) n -> p k n", p=P)), (wdt_sb[:, :], w_dt)):
                sp.dma_start(dst, src, allow_slow_non_contiguous=True).then_inc(s_const, 16)

            def load(b, i):
                sp.dma_start(xT[i][:, :, :], x_feat[:, :, bass.ds(b * L, L)].rearrange("k p t -> p k t")).then_inc(s_x[i], 16)

            def store(b, s, done, src, dst, stored):
                sp.wait_ge(s, done)
                alone(sp, tick_sp)
                sp.dma_start(dst[:, :, bass.ds(b * L, L)].rearrange("k p t -> p k t"), src[:, :, :]).then_inc(stored, 16)

            def project(b, r, i, step_sizes_before):
                store(b, s_u, b * F1 + F1, u_sb, u_feat, s_out_u)
                if step_sizes_before:
                    step_sizes_before()
                store(b, s_z, b * F1 + F1, z_sb, z_feat, s_out_z)
                sp.wait_ge(s_bc, b + 1)
                alone(sp, tick_sp)
                sp.dma_start(bc_feat[:, bass.ds(b * L, L)], bc_sb[:, :]).then_inc(s_out, 16)

            def step_sizes(b):
                store(b, s_dt, b + 1, dt_sb, dt_feat, s_dts)
            for i in range(2):
                load(i, i)
            for n, (k, cols) in enumerate(CHUNKS):
                if n >= WBUF:
                    sp.wait_ge(s_wl, n - WBUF + 1)
                sp.dma_start(w_raw[n % WBUF][:, :], w_in[k * P:(k + 1) * P, cols]).then_inc(s_w[n % WBUF], 16)
            project(0, 0, 0, None)
            with sp.Fori(0, NB // 2 - 1) as r:
                for i in range(2):
                    b = 2 * r + i
                    load(b + 2, i)
                    project(b + 1, None, None, lambda b=b: step_sizes(b))
            project(NB - 1, None, None, lambda: step_sizes(NB - 2))
            step_sizes(NB - 1)
            for s in (s_out, s_out_u, s_out_z, s_dts):
                sp.wait_ge(s, NB * 16)

        @block.scalar
        def _(act):
            act.wait_ge(s_const, 16 * CONSTS)
            act.wait_ge(s_set, 3)

            def split(count, i):
                act.wait_ge(s_x[i], count)
                nc.scalar.copy(x_hi[i][:, :, :], xT[i][:, :, :]).then_inc(s_xh, 1)
            split(16, 0)
            for n, (k, cols) in enumerate(CHUNKS):
                act.wait_ge(s_w[n % WBUF], 16 * (n // WBUF + 1))
                nc.scalar.copy(w_hi[:, k, cols], w_raw[n % WBUF][:, :]).then_inc(s_wh, 1)

            def biased(b):
                act.wait_ge(s_dt, b)
                for f in range(F1):
                    act.wait_ge(s_pd, b * F1 + f + 1)
                    nc.scalar.activation(v_sb[:, f, :], pd[f % 2][:, 0:L], ACT.Abs, bias=bdt_sb[:, f:f + 1], scale=1.0).then_inc(s_v, 1)
                    nc.scalar.activation(r_sb[:, f, :], pd[f % 2][:, 0:L], ACT.Relu, bias=bdt_sb[:, f:f + 1], scale=1.0).then_inc(s_v, 1)

            def project(b, r, i, step_sizes_before):
                if step_sizes_before:
                    step_sizes_before()
                for f in range(F1 + 1):
                    if f < F1:
                        act.wait_ge(s_px, b * F1 + f + 1)
                        act.wait_ge(s_conv, b * F1 + max(f - 1, 0))
                        nc.scalar.copy(xpad[f % 2][:, 3:3 + L], px[f % 2][:, 0:L]).then_inc(s_xpad, 1)
                    if f == SPLIT_AT and more(b):
                        act.wait_ge(s_pz, b * F1)
                        split((r + i) * 16 + 16, 1 - i)
                    if f >= 1:
                        g = f - 1
                        if g == 0:
                            act.wait_ge(s_out_u, b * 16)
                            act.wait_ge(s_out_z, b * 16)
                            act.wait_ge(s_pb, b)
                        act.wait_ge(s_pz, b * F1 + g + 1)
                        nc.scalar.activation(z_sb[:, g, :], pz[g % 2][:, 0:L], ACT.Silu).then_inc(s_z, 1)
                        act.wait_ge(s_conv, b * F1 + g + 1)
                        nc.scalar.activation(u_sb[:, g, :], acc[g % 2][:, :], ACT.Silu, bias=cb_sb[:, g:g + 1]).then_inc(s_u, 1)
                biased(b)

            def step_sizes(b):
                act.wait_ge(s_v, (b + 1) * 2 * F1)
                link = linker(act, s_la, b)
                link(nc.scalar.activation(v_sb[:, :, :], v_sb[:, :, :], ACT.Exp, scale=-1.0))
                nc.scalar.activation(v_sb[:, :, :], v_sb[:, :, :], ACT.Ln, bias=one_sb[:, :], scale=1.0).then_inc(s_r, 1)
            pipelined(act, project, step_sizes)

        @block.vector
        def _(dve):
            for i in range(2):
                nc.vector.memset(xpad[i][:, 0:3], 0.0).then_inc(s_set, 1)
            nc.vector.memset(one_sb[:, :], 1.0).then_inc(s_set, 1)
            dve.wait_ge(s_set, 3)
            dve.wait_ge(s_const, 16 * CONSTS)

            def split(turn, i):
                dve.wait_ge(s_xh, turn)
                nc.vector.tensor_tensor(x_lo[i][:, :, :], xT[i][:, :, :], x_hi[i][:, :, :].bitcast(F32), ALU.subtract).then_inc(s_xl, 1)
            split(1, 0)
            for n, (k, cols) in enumerate(CHUNKS):
                dve.wait_ge(s_wh, n + 1)
                nc.vector.tensor_tensor(w_lo[:, k, cols], w_raw[n % WBUF][:, :], w_hi[:, k, cols].bitcast(F32), ALU.subtract).then_inc(s_wl, 1)

            def project(b, r, i, step_sizes_before):
                link = linker(dve, s_lv, b * 3 * F1)
                for f in range(F1):
                    if f == 2 and step_sizes_before:
                        step_sizes_before()
                    if f == SPLIT_AT + 1 and more(b):
                        split(b + 2, 1 - i)
                    a, xp = acc[f % 2], xpad[f % 2]
                    dve.wait_ge(s_xpad, b * F1 + f + 1)
                    dve.wait_ge(s_u, b * F1 + max(f - 1, 0))
                    link(nc.vector.tensor_scalar(a[:, :], xp[:, 3:3 + L], cw_sb[:, f, 3:4], None, ALU.mult))
                    for j in (2, 1):
                        link(nc.vector.scalar_tensor_tensor(a[:, :], xp[:, j:j + L], cw_sb[:, f, j:j + 1], a[:, :], ALU.mult, ALU.add))
                    nc.vector.scalar_tensor_tensor(a[:, :], xp[:, 0:L], cw_sb[:, f, 0:1], a[:, :], ALU.mult, ALU.add).then_inc(s_conv, 1)
                dve.wait_ge(s_pr, b + 1)
                nc.vector.tensor_copy(dr_sb[:, :], pr[:, 0:L]).then_inc(s_dr, 1)
                dve.wait_ge(s_pb, b + 1)
                dve.wait_ge(s_out, b * 16)
                nc.vector.tensor_copy(bc_sb[:, :], pb[0:2 * N1, 0:L]).then_inc(s_bc, 1)

            def step_sizes(b):
                dve.wait_ge(s_r, b + 1)
                dve.wait_ge(s_dts, b * 16)
                nc.vector.tensor_tensor(dt_sb[:, :, :], v_sb[:, :, :], r_sb[:, :, :], ALU.add).then_inc(s_dt, 1)
            pipelined(dve, project, step_sizes)

        @block.tensor
        def _(pe):
            pe.wait_ge(s_const, 16 * CONSTS)
            pe.wait_ge(s_wl, len(CHUNKS))

            def parts(out, cols, i, k):
                for n, (w, x) in enumerate(((w_hi, x_hi), (w_hi, x_lo), (w_lo, x_hi))):
                    ins = nc.tensor.matmul(out, w[:, k, cols], x[i][:, k, :], start=(k == 0 and n == 0), stop=(k == KD - 1 and n == 2))
                return ins

            def project(b, r, i, step_sizes_before):
                pe.wait_ge(s_xl, b + 1)
                for f in range(F1):
                    pe.wait_ge(s_xpad, b * F1 + max(f - 1, 0))
                    for k in range(KD):
                        ins = parts(px[f % 2][:, 0:L], slice(f * P, (f + 1) * P), i, k)
                    ins.then_inc(s_px, 1)
                    pe.wait_ge(s_z, b * F1 + max(f - 1, 0))
                    for k in range(KD):
                        ins = parts(pz[f % 2][:, 0:L], slice(DI1 + f * P, DI1 + (f + 1) * P), i, k)
                    ins.then_inc(s_pz, 1)
                pe.wait_ge(s_u, b * F1 + F1)
                pe.wait_ge(s_dr, b)
                for k in range(F1):
                    ins = nc.tensor.matmul(pr[:, 0:L], wx_sb[:, k, 0:P], u_sb[:, k, :], start=(k == 0), stop=(k == F1 - 1))
                ins.then_inc(s_pr, 1)
                pe.wait_ge(s_bc, b)
                for k in range(F1):
                    ins = nc.tensor.matmul(pb[0:2 * N1, 0:L], wx_sb[:, k, P:P + 2 * N1], u_sb[:, k, :], start=(k == 0), stop=(k == F1 - 1))
                ins.then_inc(s_pb, 1)
                pe.wait_ge(s_dr, b + 1)
                for f in range(F1):
                    pe.wait_ge(s_v, (b * F1 + max(f - 1, 0)) * 2)
                    nc.tensor.matmul(pd[f % 2][:, 0:L], wdt_sb[:, f * P:(f + 1) * P], dr_sb[:, :], start=True, stop=True).then_inc(s_pd, 1)
            pipelined(pe, project, lambda b: None)


def ssm1_scan(nc, x_tok, u_feat, z_feat, dt_feat, bc_feat, a_log, skip, w_out, ident, o_tok, o_feat):
    LN_EPS = 1e-5
    G = 4
    Q = N1 // G
    C = F1 * Q
    RB, RH = 4, 4
    with ExitStack() as phase:
        m = Space(nc, "d2", phase)
        ident_sb, eps_sb, zero_sb = m.sb("ident", [P, P]), m.sb("eps", [P, 1]), m.sb("zero", [P, G])
        A_sb, D_sb = m.sb("A", [P, F1, N1]), m.sb("D", [P, F1])
        wo_sb = m.sb("wo", [P, F1, D])
        B_sb = [m.sb(f"B{i}", [P, N1, L]) for i in range(2)]
        C_sb = [m.sb(f"C{i}", [P, N1, L]) for i in range(2)]
        u_sb = [m.sb(f"u{i}", [P, F1, L]) for i in range(2)]
        z_sb = m.sb("z", [P, F1, L])
        dt_sb = [m.sb(f"dt{i}", [P, F1, L]) for i in range(2)]
        dtu = [m.sb(f"dtu{i}", [P, L]) for i in range(2)]
        dBu = [m.sb(f"dBu{i}", [P, G, L]) for i in range(RB)]
        hC = [m.sb(f"hC{i}", [P, G, L]) for i in range(RH)]
        t_sb = [m.sb(f"t{i}", [P, L]) for i in range(2)]
        yz = m.sb("yz", [P, F1, L])
        x_sb = m.sb("x", [P, 2, D])
        st, mv, sd = m.sb("st", [P, 2, 6]), m.sb("mv", [P, 2, 2]), m.sb("sd", [P, 2])
        oT = m.sb("oT", [P, 2, KD, P])
        ph = [m.ps(f"ph{i}", (P, G, L)) for i in range(2)]
        py = [m.ps(f"py{i}") for i in range(2)]
        po = [m.ps(f"po{i}") for i in range(2)]
        s_const, s_set, s_lv, s_A = m.sem("const"), m.sem("set"), m.sem("lv"), m.sem("A")
        s_B = [m.sem(f"ldB{i}") for i in range(2)]
        s_dt = [m.sem(f"lddt{i}") for i in range(2)]
        s_C, s_z, s_x, s_out = (m.sem("ld" + n) for n in "C z x out".split())
        s_dtu, s_dA, s_dBu, s_scan, s_hC, s_py, s_sum, s_yz, s_o, s_var, s_sd, s_ln, s_T, s_oc = (
            m.sem(n) for n in "dtu dA dBu scan hC py sum yz o var sd ln T oc".split())
        tick_dve, tick_sp = m.sem("tick_dve"), m.sem("tick_sp")
        block = phase.enter_context(nc.Block())
        CONSTS = 4

        def feat(a, b):
            return a[:, :, bass.ds(b * L, L)].rearrange("k p t -> p k t")

        def later(b, done, per, back):
            return b * per + max(done - back, 0)

        @block.sync
        def _(sp):
            for dst, src in ((ident_sb[:, :], ident), (A_sb[:, :, :], a_log.rearrange("(k p) n -> p k n", p=P)),
                             (D_sb[:, :], skip.rearrange("(k p) -> p k", p=P)), (wo_sb[:, :, :], w_out.rearrange("(k p) n -> p k n", p=P))):
                sp.dma_start(dst, src, allow_slow_non_contiguous=True).then_inc(s_const, 16)
            def inputs(b, i):
                sp.dma_start(dt_sb[i][:, :, :], feat(dt_feat, b)).then_inc(s_dt[i], 16)
                sp.dma_start(u_sb[i][:, :, :], feat(u_feat, b)).then_inc(s_dt[i], 16)
                sp.dma_start(B_sb[i][:, :, :], bc_feat[0:N1, bass.ds(b * L, L)].partition_broadcast(P)).then_inc(s_B[i], 16)
                sp.dma_start(C_sb[i][:, :, :], bc_feat[N1:2 * N1, bass.ds(b * L, L)].partition_broadcast(P)).then_inc(s_B[i], 16)

            def loads(b):
                sp.wait_ge(s_yz, b * F1)
                alone(sp, tick_sp)
                sp.dma_start(z_sb[:, :, :], feat(z_feat, b)).then_inc(s_z, 16)
                sp.wait_ge(s_T, b * 2)
                alone(sp, tick_sp)
                sp.wait_ge(s_out, b * 48)
                alone(sp, tick_sp)
                sp.dma_start(x_sb[:, :, :], x_tok[bass.ds(b * L, L), :].rearrange("(c p) n -> p c n", p=P)).then_inc(s_x, 16)

            def stores(b):
                sp.wait_ge(s_oc, b * 2 + 2)
                alone(sp, tick_sp)
                sp.dma_start(o_tok[bass.ds(b * L, L), :].rearrange("(c p) n -> p c n", p=P), x_sb[:, :, :]).then_inc(s_out, 16)
                for c in range(2):
                    sp.dma_start(o_feat[:, :, bass.ds(b * L + c * P, P)].rearrange("k p t -> p k t"), oT[:, c, :, :]).then_inc(s_out, 16)
            inputs(0, 0)
            loads(0)
            inputs(1, 1)
            with sp.Fori(0, NB // 2 - 1) as r:
                for i in range(2):
                    b = 2 * r + i
                    stores(b)
                    loads(b + 1)
                    sp.wait_ge(s_dA, b * C + C)
                    alone(sp, tick_sp)
                    sp.wait_ge(s_yz, b * F1 + F1)
                    alone(sp, tick_sp)
                    inputs(b + 2, i)
            stores(NB - 2)
            loads(NB - 1)
            stores(NB - 1)
            sp.wait_ge(s_out, NB * 48)

        @block.gpsimd
        def _(pool):
            with pool.Fori(0, NB // 2) as r:
                for i in range(2):
                    b = 2 * r + i
                    pool.wait_ge(s_B[i], r * 32 + 32)
                    for c in range(C):
                        f, q = c // Q, c % Q
                        pool.wait_ge(s_dtu, b * F1 + f + 1)
                        pool.wait_ge(s_scan, later(b, c, C, RB - 1))
                        pool.tensor_tensor(dBu[c % RB][:, :, :], B_sb[i][:, q * G:(q + 1) * G, :],
                                           dtu[f % 2][:, :].unsqueeze(1).to_broadcast([P, G, L]), ALU.mult).then_inc(s_dBu, 1)

        @block.scalar
        def _(act):
            act.wait_ge(s_const, 16 * CONSTS)
            act.wait_ge(s_set, 2)
            nc.scalar.activation(A_sb[:, :, :], A_sb[:, :, :], ACT.Exp).then_inc(s_A, 1)
            act.wait_ge(s_A, 2)
            with act.Fori(0, NB // 2) as r:
                for i in range(2):
                    b = 2 * r + i
                    act.wait_ge(s_dt[i], r * 32 + 32)
                    for c in range(C):
                        f, q = c // Q, c % Q
                        act.wait_ge(s_hC, later(b, c, C, 1))
                        nc.scalar.copy(ph[c % 2][:, :, 0:1], zero_sb[:, :].unsqueeze(2))
                        for n in range(G):
                            ins = nc.scalar.activation(ph[c % 2][:, n, 1:L], dt_sb[i][:, f, 1:L], ACT.Exp, scale=A_sb[:, f, q * G + n:q * G + n + 1])
                        ins.then_inc(s_dA, 1)
                    act.wait_ge(s_var, b * 2 + 2)
                    nc.scalar.activation(sd[:, :], mv[:, :, 1], ACT.Sqrt, bias=eps_sb[:, :], scale=1.0).then_inc(s_sd, 1)
                    act.wait_ge(s_out, b * 48)
                    for c in range(2):
                        act.wait_ge(s_T, b * 2 + c + 1)
                        nc.scalar.copy(oT[:, c, :, :].rearrange("p k t -> p (k t)"), py[c][:, :]).then_inc(s_oc, 1)

        @block.vector
        def _(dve):
            nc.vector.memset(eps_sb[:, :], LN_EPS).then_inc(s_set, 1)
            nc.vector.memset(zero_sb[:, :], 0.0).then_inc(s_set, 1)
            dve.wait_ge(s_set, 2)
            dve.wait_ge(s_A, 1)
            nc.vector.tensor_scalar(A_sb[:, :, :], A_sb[:, :, :], -1.0, None, ALU.mult).then_inc(s_A, 1)
            LV = 5
            with dve.Fori(0, NB // 2) as r:
                for i in range(2):
                    b = 2 * r + i
                    link = linker(dve, s_lv, b * LV)
                    dve.wait_ge(s_dt[i], r * 32 + 32)
                    dve.wait_ge(s_B[i], r * 32 + 32)

                    def step_sizes(f):
                        dve.wait_ge(s_dBu, later(b, f * Q, C, Q))
                        nc.vector.tensor_tensor(dtu[f % 2][:, :], dt_sb[i][:, f, :], u_sb[i][:, f, :], ALU.mult).then_inc(s_dtu, 1)

                    def channel_out(g):
                        dve.wait_ge(s_py, b * C + (g + 1) * Q)
                        dve.wait_ge(s_yz, later(b, g, F1, 1))
                        nc.vector.scalar_tensor_tensor(t_sb[g % 2][:, :], u_sb[i][:, g, :], D_sb[:, g:g + 1], py[g % 2][:, 0:L], ALU.mult, ALU.add).then_inc(s_sum, 1)
                        dve.wait_ge(s_sum, b * F1 + g + 1)
                        dve.wait_ge(s_o, b * 2)
                        nc.vector.tensor_tensor(yz[:, g, :], t_sb[g % 2][:, :], z_sb[:, g, :], ALU.mult).then_inc(s_yz, 1)
                    step_sizes(0)
                    for c in range(C):
                        f, q = c // Q, c % Q
                        if q == 0 and f + 1 < F1:
                            step_sizes(f + 1)
                        dve.wait_ge(s_dA, b * C + c + 1)
                        dve.wait_ge(s_dBu, b * C + c + 1)
                        h = ph[c % 2][:, :, :].rearrange("p n t -> p (n t)")
                        nc.vector.tensor_tensor_scan(h, h, dBu[c % RB][:, :, :].rearrange("p n t -> p (n t)"), 0.0, ALU.mult, ALU.add).then_inc(s_scan, 1)
                        dve.wait_ge(s_scan, b * C + c + 1)
                        dve.wait_ge(s_py, later(b, c, C, RH - 1))
                        nc.vector.tensor_tensor(hC[c % RH][:, :, :], ph[c % 2][:, :, :], C_sb[i][:, q * G:(q + 1) * G, :], ALU.mult).then_inc(s_hC, 1)
                        if q == 1 and f >= 1:
                            if f == 1:
                                dve.wait_ge(s_z, b * 16 + 16)
                            channel_out(f - 1)
                    channel_out(F1 - 1)
                    dve.wait_ge(s_x, b * 16 + 16)
                    for c in range(2):
                        dve.wait_ge(s_o, b * 2 + c + 1)
                        link(nc.vector.tensor_tensor(x_sb[:, c, :], x_sb[:, c, :], po[c][:, :], ALU.add))
                        link(nc.vector.bn_stats(st[:, c, :], x_sb[:, c, :]))
                        alone(dve, tick_dve)
                        nc.vector.bn_aggr(mv[:, c, :], st[:, c, :]).then_inc(s_var, 1)
                    dve.wait_ge(s_sd, b + 1)
                    link(nc.vector.reciprocal(sd[:, :], sd[:, :]))
                    for c in range(2):
                        nc.vector.tensor_scalar(x_sb[:, c, :], x_sb[:, c, :], mv[:, c, 0:1], sd[:, c:c + 1], ALU.subtract, ALU.mult).then_inc(s_ln, 1)
                    assert link.count[0] == LV

        @block.tensor
        def _(pe):
            pe.wait_ge(s_const, 16 * CONSTS)
            with pe.Fori(0, NB) as b:

                def project(g):
                    pe.wait_ge(s_yz, b * F1 + g + 1)
                    if g == 0:
                        pe.wait_ge(s_var, b * 2)
                    for c in range(2):
                        ins = nc.tensor.matmul(po[c][:, :], yz[:, g, c * P:(c + 1) * P], wo_sb[:, g, :], start=(g == 0), stop=(g == F1 - 1))
                        if g == F1 - 1:
                            ins.then_inc(s_o, 1)
                for c in range(C):
                    f, q = c // Q, c % Q
                    pe.wait_ge(s_hC, b * C + c + 1)
                    if q == 0:
                        pe.wait_ge(s_sum, later(b, f, F1, 1))
                        pe.wait_ge(s_oc, b * 2)
                    for n in range(G):
                        ins = nc.tensor.matmul(py[f % 2][:, 0:L], ident_sb[:, :], hC[c % RH][:, n, :], start=(q == 0 and n == 0), stop=(q == Q - 1 and n == G - 1))
                    ins.then_inc(s_py, 1)
                    if q == 2 and f >= 2:
                        project(f - 2)
                project(F1 - 2)
                project(F1 - 1)
                for c in range(2):
                    pe.wait_ge(s_ln, b * 2 + c + 1)
                    for k in range(KD):
                        ins = nc.tensor.transpose(py[c][:, k * P:(k + 1) * P], x_sb[:, c, k * P:(k + 1) * P], ident_sb[:, :])
                    ins.then_inc(s_T, 1)


def linear_attention(nc, x_tok, x_feat, ctx_feat, w_q, w_g, b_g, w_kv, w_o, ident, heads_mask, o_tok, o_feat):
    WBUF = 4
    LN_EPS, EPS = 1e-5, 1e-6
    with ExitStack() as phase:
        m = Space(nc, "e1", phase)
        ident_sb, eps_sb, mask_sb, ones = m.sb("ident", [P, P]), m.sb("eps", [P, 1]), m.sb("mask", [P, P]), m.sb("ones", [P, P])
        wo = m.sb("wo", [P, KD, D])
        w_raw = [m.sb(f"wraw{i}", [P, D]) for i in range(WBUF)]
        wq, wg = ([m.sb(n + part, [P, KD, D], F32R) for part in ("hi", "lo")] for n in ("wq", "wg"))
        wkv = [m.sb("wkv" + part, [P, KD, 2 * D], F32R) for part in ("hi", "lo")]
        x_parts, c_parts = ([[m.sb(f"{n}{part}{i}", [P, KD, L], F32R) for part in ("hi", "lo")] for i in range(2)] for n in "xc")
        bg_sb = m.sb("bg", [P, KD])
        xf = [m.sb(f"xf{i}", [P, KD, L]) for i in range(2)]
        cf = [m.sb(f"cf{i}", [P, KD, L]) for i in range(2)]
        xt = [m.sb(f"xt{i}", [P, 2, D]) for i in range(2)]
        k_sb, v_sb = m.sb("k", [P, 2, D]), m.sb("v", [P, 2, D])
        kneg = [m.sb(f"kneg{i}", [P, D]) for i in range(2)]
        q_sb, g_sb = m.sb("q", [P, KD, L]), m.sb("g", [P, KD, L])
        qneg = [m.sb(f"qneg{i}", [P, L]) for i in range(2)]
        kv_sb, ks_sb = m.sb("kv", [P, KD, P]), m.sb("ks", [P, KD, P])
        den = m.sb("den", [P, KD, L])
        ag = m.sb("ag", [P, KD, L])
        st, mv, sd = m.sb("st", [P, 2, 6]), m.sb("mv", [P, 2, 2]), m.sb("sd", [P, 2])
        o_sb, oT = m.sb("o", [P, 2, D]), m.sb("oT", [P, 2, KD, P])
        pa = [m.ps(f"pa{i}") for i in range(2)]
        pb = [m.ps(f"pb{i}") for i in range(2)]
        ps = [m.ps(f"ps{i}") for i in range(2)]
        po = [m.ps(f"po{i}") for i in range(2)]
        s_const, s_set, s_lv, s_out = m.sem("const"), m.sem("set"), m.sem("lv"), m.sem("out")
        s_in = [m.sem(f"in{i}") for i in range(2)]
        s_pk, s_kn, s_k, s_pv, s_v, s_pq, s_qn, s_q, s_pg, s_g, s_ps, s_kv, s_pa, s_ag, s_o, s_var, s_sd, s_ln, s_T, s_oc, s_ke, s_qe = (
            m.sem(n) for n in "pk kn k pv v pq qn q pg g ps kv pa ag o var sd ln T oc ke qe".split())
        s_lt, tick_dve, tick_sp = m.sem("lt"), m.sem("tick_dve"), m.sem("tick_sp")
        block = phase.enter_context(nc.Block())
        s_w = [m.sem(f"w{i}") for i in range(WBUF)]
        s_wh, s_wl, s_xh, s_xl = (m.sem(n) for n in "wh wl xh xl".split())
        CONSTS = 4
        HALF = (slice(0, D), slice(D, 2 * D))
        CHUNKS = [(src, dst, k, cols) for src, dst, parts in ((w_kv, wkv, HALF), (w_q, wq, HALF[:1]), (w_g, wg, HALF[:1]))
                  for cols in parts for k in range(KD)]

        def more(b):
            return not (isinstance(b, int) and b == NB - 1)

        def pipelined(eng, attend, norm):
            attend(0, 0, 0, None)
            with eng.Fori(0, NB // 2 - 1) as r:
                for i in range(2):
                    attend(2 * r + 1 + i, r + i, 1 - i, lambda b=2 * r + i, r=r, i=i: norm(b, r, i))
            attend(NB - 1, NB // 2 - 1, 1, lambda: norm(NB - 2, NB // 2 - 1, 0))
            norm(NB - 1, NB // 2 - 1, 1, last=True)

        @block.sync
        def _(sp):
            for dst, src in ((ident_sb[:, :], ident), (mask_sb[:, :], heads_mask), (bg_sb[:, :], b_g.rearrange("(k p) -> p k", p=P)),
                             (wo[:, :, :], w_o.rearrange("(k p) n -> p k n", p=P))):
                sp.dma_start(dst, src, allow_slow_non_contiguous=True).then_inc(s_const, 16)

            def load(b, i):
                sp.dma_start(cf[i][:, :, :], ctx_feat[:, :, bass.ds(b * L, L)].rearrange("k p t -> p k t")).then_inc(s_in[i], 16)
                sp.dma_start(xf[i][:, :, :], x_feat[:, :, bass.ds(b * L, L)].rearrange("k p t -> p k t")).then_inc(s_in[i], 16)
                sp.dma_start(xt[i][:, :, :], x_tok[bass.ds(b * L, L), :].rearrange("(c p) n -> p c n", p=P)).then_inc(s_in[i], 16)

            def store(b):
                sp.wait_ge(s_oc, b * 2 + 2)
                alone(sp, tick_sp)
                sp.dma_start(o_tok[bass.ds(b * L, L), :].rearrange("(c p) n -> p c n", p=P), o_sb[:, :, :]).then_inc(s_out, 16)
                for c in range(2):
                    sp.dma_start(o_feat[:, :, bass.ds(b * L + c * P, P)].rearrange("k p t -> p k t"), oT[:, c, :, :]).then_inc(s_out, 16)
            for i in range(2):
                load(i, i)
            for n, (src, dst, k, cols) in enumerate(CHUNKS):
                if n >= WBUF:
                    sp.wait_ge(s_wl, n - WBUF + 1)
                sp.dma_start(w_raw[n % WBUF][:, :], src[k * P:(k + 1) * P, cols]).then_inc(s_w[n % WBUF], 16)
            with sp.Fori(0, NB // 2 - 1) as r:
                for i in range(2):
                    b = 2 * r + i
                    sp.wait_ge(s_ln, b * 2 + 2)
                    alone(sp, tick_sp)
                    sp.wait_ge(s_xl, b * 2 + 2)
                    alone(sp, tick_sp)
                    load(b + 2, i)
                    store(b)
            for i in range(2):
                store(NB - 2 + i)
            sp.wait_ge(s_out, NB * 48)

        @block.scalar
        def _(act):
            act.wait_ge(s_const, 16 * CONSTS)
            act.wait_ge(s_set, 3)

            def split(count, i):
                act.wait_ge(s_in[i], count)
                for raw, parts in ((cf, c_parts), (xf, x_parts)):
                    nc.scalar.copy(parts[i][0][:, :, :], raw[i][:, :, :]).then_inc(s_xh, 1)
            split(48, 0)
            for n, (src, dst, k, cols) in enumerate(CHUNKS):
                act.wait_ge(s_w[n % WBUF], 16 * (n // WBUF + 1))
                nc.scalar.copy(dst[0][:, k, cols], w_raw[n % WBUF][:, :]).then_inc(s_wh, 1)

            def root(b):
                act.wait_ge(s_var, b * 2 + 2)
                nc.scalar.activation(sd[:, :], mv[:, :, 1], ACT.Sqrt, bias=eps_sb[:, :], scale=1.0).then_inc(s_sd, 1)

            def attend(b, r, i, norm_before):
                if norm_before:
                    root(b - 1)
                for c in range(2):
                    act.wait_ge(s_kn, b * 2 + c + 1)
                    nc.scalar.activation(kneg[c][:, :], kneg[c][:, :], ACT.Exp).then_inc(s_ke, 1)
                if norm_before:
                    norm_before()
                for c in range(2):
                    act.wait_ge(s_pv, b * 2 + c + 1)
                    nc.scalar.copy(v_sb[:, c, :], pa[c][:, :]).then_inc(s_v, 1)
                if more(b):
                    split((r + i) * 48 + 48, 1 - i)
                for k in range(KD):
                    act.wait_ge(s_pg, b * KD + k + 1)
                    act.wait_ge(s_ag, b * KD)
                    nc.scalar.activation(g_sb[:, k, :], pb[k % 2][:, 0:L], ACT.Exp, bias=bg_sb[:, k:k + 1], scale=-1.0).then_inc(s_g, 1)
                    act.wait_ge(s_qn, b * KD + k + 1)
                    nc.scalar.activation(qneg[k % 2][:, :], qneg[k % 2][:, :], ACT.Exp).then_inc(s_qe, 1)

            def norm(b, r, i, last=False):
                if last:
                    root(b)
                act.wait_ge(s_out, b * 48)
                for c in range(2):
                    act.wait_ge(s_T, b * 2 + c + 1)
                    nc.scalar.copy(oT[:, c, :, :].rearrange("p k t -> p (k t)"), ps[c][:, :]).then_inc(s_oc, 1)
            pipelined(act, attend, norm)

        @block.vector
        def _(dve):
            nc.vector.memset(eps_sb[:, :], LN_EPS).then_inc(s_set, 1)
            nc.vector.memset(ones[:, :], 1.0).then_inc(s_set, 1)
            dve.wait_ge(s_set, 2)
            dve.wait_ge(s_const, 16 * CONSTS)
            nc.vector.tensor_scalar(bg_sb[:, :], bg_sb[:, :], -1.0, None, ALU.mult).then_inc(s_set, 1)

            def split(batch, i):
                for n, (raw, parts) in enumerate(((cf, c_parts), (xf, x_parts))):
                    dve.wait_ge(s_xh, 2 * batch + n + 1)
                    nc.vector.tensor_tensor(parts[i][1][:, :, :], raw[i][:, :, :], parts[i][0][:, :, :].bitcast(F32), ALU.subtract).then_inc(s_xl, 1)
            split(0, 0)
            for n, (src, dst, k, cols) in enumerate(CHUNKS):
                dve.wait_ge(s_wh, n + 1)
                nc.vector.tensor_tensor(dst[1][:, k, cols], w_raw[n % WBUF][:, :], dst[0][:, k, cols].bitcast(F32), ALU.subtract).then_inc(s_wl, 1)
            LV, LN = 3 * KD, 5

            def attend(b, r, i, norm_before):
                if norm_before:
                    norm_before()
                link = linker(dve, s_lv, b * LV)
                for c in range(2):
                    dve.wait_ge(s_pk, b * 2 + c + 1)
                    nc.vector.tensor_scalar(kneg[c][:, :], pa[c][:, :], 0.0, None, ALU.min).then_inc(s_kn, 1)
                for c in range(2):
                    dve.wait_ge(s_ke, b * 2 + c + 1)
                    nc.vector.scalar_tensor_tensor(k_sb[:, c, :], pa[c][:, :], 0.0, kneg[c][:, :], ALU.max, ALU.add).then_inc(s_k, 1)

                def queries(k):
                    dve.wait_ge(s_pq, b * KD + k + 1)
                    dve.wait_ge(s_q, b * KD + max(k - 1, 0))
                    nc.vector.tensor_scalar(qneg[k % 2][:, :], pa[k % 2][:, 0:L], 0.0, None, ALU.min).then_inc(s_qn, 1)
                    dve.wait_ge(s_qe, b * KD + k + 1)
                    nc.vector.scalar_tensor_tensor(q_sb[:, k, :], pa[k % 2][:, 0:L], 0.0, qneg[k % 2][:, :], ALU.max, ALU.add).then_inc(s_q, 1)

                def gated(j):
                    dve.wait_ge(s_pa, b * KD + j + 1)
                    n = pb[j % 2]
                    link(nc.vector.tensor_scalar(den[:, j, :], n[:, L:2 * L], EPS, None, ALU.add))
                    dve.wait_ge(s_g, b * KD + j + 1)
                    link(nc.vector.scalar_tensor_tensor(den[:, j, :], g_sb[:, j, :], 1.0, den[:, j, :], ALU.add, ALU.mult))
                    link(nc.vector.reciprocal(den[:, j, :], den[:, j, :]))
                    nc.vector.tensor_tensor(ag[:, j, :], n[:, 0:L], den[:, j, :], ALU.mult).then_inc(s_ag, 1)
                queries(0)
                dve.wait_ge(s_ps, b + 1)
                for j in range(KD):
                    nc.vector.tensor_tensor(kv_sb[:, j, :], ps[0][:, j * P:(j + 1) * P], mask_sb[:, :], ALU.mult).then_inc(s_kv, 1)
                    nc.vector.tensor_tensor(ks_sb[:, j, :], ps[1][:, j * P:(j + 1) * P], mask_sb[:, :], ALU.mult).then_inc(s_kv, 1)
                for k in range(1, KD):
                    queries(k)
                    gated(k - 1)
                    if k == 1 and more(b):
                        split(b + 1, 1 - i)
                gated(KD - 1)
                assert link.count[0] == LV

            def norm(b, r, i, last=False):
                link = linker(dve, s_lt, b * LN)
                dve.wait_ge(s_in[i], r * 48 + 48)
                for c in range(2):
                    x = xt[i][:, c, :]
                    dve.wait_ge(s_o, b * 2 + c + 1)
                    link(nc.vector.tensor_tensor(x, x, po[c][:, :], ALU.add))
                    link(nc.vector.bn_stats(st[:, c, :], x))
                    alone(dve, tick_dve)
                    nc.vector.bn_aggr(mv[:, c, :], st[:, c, :]).then_inc(s_var, 1)
                dve.wait_ge(s_sd, b + 1)
                link(nc.vector.reciprocal(sd[:, :], sd[:, :]))
                dve.wait_ge(s_out, b * 48)
                for c in range(2):
                    nc.vector.tensor_scalar(o_sb[:, c, :], xt[i][:, c, :], mv[:, c, 0:1], sd[:, c:c + 1], ALU.subtract, ALU.mult).then_inc(s_ln, 1)
                assert link.count[0] == LN
            pipelined(dve, attend, norm)

        @block.tensor
        def _(pe):
            pe.wait_ge(s_const, 16 * CONSTS)
            pe.wait_ge(s_set, 2)
            pe.wait_ge(s_wl, len(CHUNKS))

            def parts(out, a, a_cols, b, b_cols, k):
                for n, (v, w) in enumerate(((a[0], b[0]), (a[0], b[1]), (a[1], b[0]))):
                    ins = nc.tensor.matmul(out, v[:, k, a_cols], w[:, k, b_cols], start=(k == 0 and n == 0), stop=(k == KD - 1 and n == 2))
                return ins

            def attend(b, r, i, norm_before):
                pe.wait_ge(s_xl, b * 2 + 2)
                pe.wait_ge(s_q, b * KD)
                for c in range(2):
                    for k in range(KD):
                        ins = parts(pa[c][:, :], c_parts[i], slice(c * P, (c + 1) * P), wkv, HALF[0], k)
                    ins.then_inc(s_pk, 1)
                if norm_before:
                    norm_before()
                pe.wait_ge(s_ag, b * KD)
                for c in range(2):
                    pe.wait_ge(s_k, b * 2 + c + 1)
                    for k in range(KD):
                        ins = parts(pa[c][:, :], c_parts[i], slice(c * P, (c + 1) * P), wkv, HALF[1], k)
                    ins.then_inc(s_pv, 1)

                def project(j):
                    if j < 2:
                        pe.wait_ge(s_v, b * 2 + j + 1)
                    else:
                        pe.wait_ge(s_q, b * KD + j - 1)
                    for k in range(KD):
                        ins = parts(pa[j % 2][:, 0:L], wq, slice(j * P, (j + 1) * P), x_parts[i], slice(0, L), k)
                    ins.then_inc(s_pq, 1)
                    pe.wait_ge(s_ag, b * KD + max(j - 1, 0))
                    for k in range(KD):
                        ins = parts(pb[j % 2][:, 0:L], wg, slice(j * P, (j + 1) * P), x_parts[i], slice(0, L), k)
                    ins.then_inc(s_pg, 1)

                def attended(j):
                    pe.wait_ge(s_g, b * KD + j + 1)
                    pe.wait_ge(s_q, b * KD + j + 1)
                    nc.tensor.matmul(pb[j % 2][:, 0:L], kv_sb[:, j, :], q_sb[:, j, :], start=True, stop=True)
                    nc.tensor.matmul(pb[j % 2][:, L:2 * L], ks_sb[:, j, :], q_sb[:, j, :], start=True, stop=True).then_inc(s_pa, 1)
                project(0)
                pe.wait_ge(s_oc, b * 2)
                pe.wait_ge(s_v, b * 2 + 2)
                for j in range(KD):
                    g = slice(j * P, (j + 1) * P)
                    for c in range(2):
                        nc.tensor.matmul(ps[0][:, g], k_sb[:, c, g], v_sb[:, c, g], start=(c == 0), stop=(c == 1))
                    for c in range(2):
                        ins = nc.tensor.matmul(ps[1][:, g], k_sb[:, c, g], ones[:, :], start=(c == 0), stop=(c == 1))
                ins.then_inc(s_ps, 1)
                for j in range(1, KD):
                    project(j)
                    if j == 1:
                        pe.wait_ge(s_kv, (b + 1) * 2 * KD)
                    attended(j - 1)
                attended(KD - 1)
                pe.wait_ge(s_ag, b * KD + KD)
                pe.wait_ge(s_var, 2 * b)
                for c in range(2):
                    for k in range(KD):
                        ins = nc.tensor.matmul(po[c][:, :], ag[:, k, c * P:(c + 1) * P], wo[:, k, :], start=(k == 0), stop=(k == KD - 1))
                    ins.then_inc(s_o, 1)

            def norm(b, r, i, last=False):
                for c in range(2):
                    pe.wait_ge(s_ln, b * 2 + c + 1)
                    for k in range(KD):
                        ins = nc.tensor.transpose(ps[c][:, k * P:(k + 1) * P], o_sb[:, c, k * P:(k + 1) * P], ident_sb[:, :])
                    ins.then_inc(s_T, 1)
            pipelined(pe, attend, norm)


EX, TOP, SEL, HID = 4, 2, 512, 2048
FAR = 1 << 20


def moe1_route(nc, x_tok, x_feat, w_router, b_router, before, ramp, x_rows, places, weights):
    BITS = 30
    with ExitStack() as phase:
        m = Space(nc, "f1", phase)
        before_sb, ones, ramp_sb = m.sb("before", [P, P]), m.sb("ones", [P, P]), m.sb("ramp", [P, EX])
        xf, xt = m.sb("xf", [P, KD, T]), m.sb("xt", [P, TILES, D])
        rw, rb = m.sb("rw", [P, KD, EX]), m.sb("rb", [P, EX])
        lg = m.sb("lg", [P, TILES, 8])
        top, idx, idf = m.sb("top", [P, TILES, 8]), m.sb("idx", [P, TILES, 8], U32), m.sb("idf", [P, TILES, TOP])
        pr = m.sb("pr", [P, TILES, TOP])
        e_sb, d_sb = m.sb("e", [P, TILES]), m.sb("d", [P, TILES])
        hot = m.sb("hot", [P, TILES, TOP, EX])
        wt = m.sb("wt", [P, TILES, TOP, EX])
        sc = m.sb("sc", [P, EX, TILES])
        bit, bit_int = m.sb("bit", [P, EX]), m.sb("bitint", [P, EX], U32)
        floor, trial, kept = (m.sb(n, [P, EX], U32) for n in ("floor", "trial", "kept"))
        over, equal, some = (m.sb(n, [P, EX, TILES]) for n in ("over", "equal", "some"))
        count, left = m.sb("count", [P, EX]), m.sb("left", [P, EX])
        sums, first = m.sb("sums", [P, EX, TILES]), m.sb("first", [P, EX, TILES])
        rank = m.sb("rank", [P, EX, TILES])
        rk, ok, far = m.sb("rk", [P, TILES, TOP]), m.sb("ok", [P, TILES, TOP]), m.sb("far", [P, TILES, TOP])
        pl = m.sb("pl", [P, TILES, TOP], U32)
        wk = m.sb("wk", [P, TILES, TOP])
        pL, pS, pT = m.ps("pL"), m.ps("pS"), m.ps("pT", (P, EX, 2, TILES))
        s_const, s_x, s_xt, s_lv, s_loop, s_log, s_d, s_e, s_count, s_total, s_taken, s_before, s_pl, s_scat, s_out = (
            m.sem(n) for n in "const x xt lv loop log d e count total taken before pl scat out".split())
        block = phase.enter_context(nc.Block())

        @block.sync
        def _(sp):
            for dst, src in ((before_sb[:, :], before), (ramp_sb[:, :], ramp[0:EX].partition_broadcast(P)),
                             (rw[:, :, :], w_router.rearrange("(k p) e -> p k e", p=P)), (rb[:, :], b_router.partition_broadcast(P))):
                sp.dma_start(dst, src).then_inc(s_const, 16)
            sp.dma_start(xf[:, :, :], x_feat.rearrange("k p t -> p k t")).then_inc(s_x, 16)
            sp.dma_start(xt[:, :, :], x_tok.rearrange("(c p) n -> p c n", p=P)).then_inc(s_xt, 16)
            sp.wait_ge(s_pl, 2)
            sp.dma_start(places.rearrange("(c p) k -> p c k", p=P), pl[:, :, :], allow_slow_non_contiguous=True).then_inc(s_out, 16)
            sp.dma_start(weights.rearrange("(c p) k -> p c k", p=P), wk[:, :, :], allow_slow_non_contiguous=True).then_inc(s_out, 16)
            sp.wait_ge(s_out, 32)

        @block.gpsimd
        def _(pool):
            pool.wait_ge(s_xt, 16)
            pool.wait_ge(s_pl, 2)
            for c in range(TILES):
                for k in range(TOP):
                    pool.indirect_dma_start(x_rows, bass.IndirectOffsetOnAxis(ap=pl[:, c, k:k + 1], axis=0), xt[:, c, :], None,
                                            bounds_check=EX * SEL - 1, oob_is_err=False).then_inc(s_scat, 16)
            pool.wait_ge(s_scat, TILES * TOP * 16)

        @block.scalar
        def _(act):
            act.wait_ge(s_d, 1)
            nc.scalar.activation(e_sb[:, :], d_sb[:, :], ACT.Exp).then_inc(s_e, 1)

        @block.vector
        def _(dve):
            link = linker(dve, s_lv)
            link(nc.vector.memset(lg[:, :, :], -3.0e38))
            link(nc.vector.memset(ones[:, :], 1.0))
            link(nc.vector.memset(first[:, :, :], 1.0))
            link(nc.vector.memset(first[:, :, 0:1], 0.0))
            link(nc.vector.memset(bit[:, :], float(1 << (BITS - 1))))
            link(nc.vector.memset(floor[:, :], 0))
            dve.wait_ge(s_const, 64)
            dve.wait_ge(s_log, 1)
            link(nc.vector.tensor_tensor(lg[:, :, 0:EX], pL[:, 0:TILES * EX].rearrange("p (c e) -> p c e", e=EX),
                                         rb[:, :].unsqueeze(1).to_broadcast([P, TILES, EX]), ALU.add))
            for c in range(TILES):
                ins = nc.vector.max(top[:, c, :], lg[:, c, :])
            link(ins)
            for c in range(TILES):
                ins = nc.vector.max_index(idx[:, c, :], top[:, c, :], lg[:, c, :])
            link(ins)
            nc.vector.tensor_tensor(d_sb[:, :], top[:, :, 1], top[:, :, 0], ALU.subtract).then_inc(s_d, 1)
            link(nc.vector.tensor_copy(idf[:, :, :], idx[:, :, 0:TOP]))
            link(nc.vector.tensor_tensor(hot[:, :, :, :].rearrange("p c k e -> p (c k) e"), ramp_sb[:, :].unsqueeze(1).to_broadcast([P, TILES * TOP, EX]),
                                         idf[:, :, :].rearrange("p c k -> p (c k)").unsqueeze(2).to_broadcast([P, TILES * TOP, EX]), ALU.is_equal))
            dve.wait_ge(s_e, 1)
            link(nc.vector.tensor_scalar(pr[:, :, 0], e_sb[:, :], 1.0, None, ALU.add))
            link(nc.vector.reciprocal(pr[:, :, 0], pr[:, :, 0]))
            link(nc.vector.tensor_tensor(pr[:, :, 1], pr[:, :, 0], e_sb[:, :], ALU.mult))
            link(nc.vector.tensor_tensor(wt[:, :, :, :].rearrange("p c k e -> p (c k) e"), hot[:, :, :, :].rearrange("p c k e -> p (c k) e"),
                                         pr[:, :, :].rearrange("p c k -> p (c k)").unsqueeze(2).to_broadcast([P, TILES * TOP, EX]), ALU.mult))
            link(nc.vector.tensor_tensor(sc[:, :, :], hot[:, :, 0, :].rearrange("p c e -> p e c"), hot[:, :, 1, :].rearrange("p c e -> p e c"), ALU.add))
            link(nc.vector.tensor_scalar(sc[:, :, :], sc[:, :, :], -1.0, None, ALU.add))
            link(nc.vector.tensor_tensor(sc[:, :, :], sc[:, :, :], wt[:, :, 0, :].rearrange("p c e -> p e c"), ALU.add))
            link(nc.vector.tensor_tensor(sc[:, :, :], sc[:, :, :], wt[:, :, 1, :].rearrange("p c e -> p e c"), ALU.add))
            LOOP = 6

            def wide(v):
                return v.unsqueeze(2).to_broadcast([P, EX, TILES])
            with dve.Fori(0, BITS) as n:
                step = linker(dve, s_loop, n * LOOP)
                step(nc.vector.tensor_copy(bit_int[:, :], bit[:, :]))
                step(nc.vector.tensor_tensor(trial[:, :], floor[:, :], bit_int[:, :], ALU.bitwise_or))
                step(nc.vector.tensor_tensor(some[:, :, :], sc[:, :, :], wide(trial[:, :].bitcast(F32)), ALU.is_ge))
                nc.vector.tensor_reduce(count[:, :], some[:, :, :], AX.X, ALU.add).then_inc(s_count, 1)
                dve.wait_ge(s_total, n + 1)
                step(nc.vector.scalar_tensor_tensor(kept[:, :], pS[:, 0:EX], float(SEL), bit[:, :], ALU.is_ge, ALU.mult))
                step(nc.vector.tensor_tensor(floor[:, :], floor[:, :], kept[:, :], ALU.bitwise_or))
                step(nc.vector.tensor_scalar(bit[:, :], bit[:, :], 0.5, None, ALU.mult))
                assert step.count[0] == LOOP
            lowest = floor[:, :].bitcast(F32)
            link(nc.vector.tensor_tensor(over[:, :, :], sc[:, :, :], wide(lowest), ALU.is_gt))
            link(nc.vector.tensor_tensor(equal[:, :, :], sc[:, :, :], wide(lowest), ALU.is_equal))
            nc.vector.tensor_reduce(count[:, :], over[:, :, :], AX.X, ALU.add).then_inc(s_count, 1)
            dve.wait_ge(s_total, BITS + 1)
            link(nc.vector.tensor_scalar(left[:, :], pS[:, 0:EX], -1.0, float(SEL), ALU.mult, ALU.add))

            def ahead(turn):
                dve.wait_ge(s_before, turn)
                link(nc.vector.tensor_copy(sums[:, :, :], pT[:, :, 1, :]))
                link(nc.vector.tensor_tensor_scan(rank[:, :, :].rearrange("p e c -> p (e c)"), first[:, :, :].rearrange("p e c -> p (e c)"),
                                                  sums[:, :, :].rearrange("p e c -> p (e c)"), 0.0, ALU.mult, ALU.add))
                link(nc.vector.tensor_tensor(rank[:, :, :], rank[:, :, :], sums[:, :, :], ALU.subtract))
                link(nc.vector.tensor_tensor(rank[:, :, :], rank[:, :, :], pT[:, :, 0, :], ALU.add))
            dve.sem_inc(s_taken, 1)
            ahead(1)
            link(nc.vector.tensor_tensor(some[:, :, :], rank[:, :, :], wide(left[:, :]), ALU.is_lt))
            link(nc.vector.tensor_tensor(equal[:, :, :], equal[:, :, :], some[:, :, :], ALU.mult))
            nc.vector.tensor_tensor(equal[:, :, :], equal[:, :, :], over[:, :, :], ALU.add).then_inc(s_taken, 1)
            ahead(2)
            link(nc.vector.tensor_scalar(over[:, :, :], equal[:, :, :], -2.0 * SEL, 2.0 * SEL, ALU.mult, ALU.add))
            link(nc.vector.tensor_tensor(rank[:, :, :], rank[:, :, :], over[:, :, :], ALU.add))
            for k in range(TOP):
                link(nc.vector.tensor_tensor(wt[:, :, k, :], hot[:, :, k, :], rank[:, :, :].rearrange("p e c -> p c e"), ALU.mult))
            link(nc.vector.tensor_reduce(rk[:, :, :].rearrange("p c k -> p (c k)"), wt[:, :, :, :].rearrange("p c k e -> p (c k) e"), AX.X, ALU.add))
            link(nc.vector.tensor_scalar(ok[:, :, :], rk[:, :, :], float(SEL), None, ALU.is_lt))
            link(nc.vector.tensor_scalar(far[:, :, :], ok[:, :, :], -float(FAR), float(FAR), ALU.mult, ALU.add))
            link(nc.vector.scalar_tensor_tensor(rk[:, :, :], idf[:, :, :], float(SEL), rk[:, :, :], ALU.mult, ALU.add))
            nc.vector.tensor_tensor(pl[:, :, :], rk[:, :, :], far[:, :, :], ALU.add).then_inc(s_pl, 1)
            nc.vector.tensor_tensor(wk[:, :, :], pr[:, :, :], ok[:, :, :], ALU.mult).then_inc(s_pl, 1)

        @block.tensor
        def _(pe):
            pe.wait_ge(s_const, 64)
            pe.wait_ge(s_x, 16)
            for c in range(TILES):
                for k in range(KD):
                    ins = nc.tensor.matmul(pL[:, c * EX:(c + 1) * EX], xf[:, k, c * P:(c + 1) * P], rw[:, k, :], start=(k == 0), stop=(k == KD - 1))
            ins.then_inc(s_log, 1)
            with pe.Fori(0, BITS) as n:
                pe.wait_ge(s_count, n + 1)
                nc.tensor.matmul(pS[:, 0:EX], ones[:, :], count[:, :], start=True, stop=True).then_inc(s_total, 1)
            pe.wait_ge(s_count, BITS + 1)
            nc.tensor.matmul(pS[:, 0:EX], ones[:, :], count[:, :], start=True, stop=True).then_inc(s_total, 1)
            for turn in range(2):
                pe.wait_ge(s_taken, turn + 1)
                for n, counts in enumerate((before_sb, ones)):
                    ins = nc.tensor.matmul(pT[:, :, n, :], counts[:, :], equal[:, :, :], start=True, stop=True)
                ins.then_inc(s_before, 1)


def moe1_experts(nc, x_rows, w1, w2, ident, y_rows):
    HB, RT = HID // P, SEL // P
    BUF = 4
    with ExitStack() as phase:
        m = Space(nc, "f2", phase)
        ident_sb = m.sb("ident", [P, P])
        w1_raw = [m.sb(f"w1r{i}", [P, KD, P]) for i in range(BUF)]
        w2_raw = [m.sb(f"w2r{i}", [P, D]) for i in range(BUF)]
        w1_hi, w1_lo = ([m.sb(f"w1{n}{i}", [P, KD, P], F32R) for i in range(2)] for n in ("hi", "lo"))
        w2_hi, w2_lo = ([m.sb(f"w2{n}{i}", [P, D], F32R) for i in range(2)] for n in ("hi", "lo"))
        x_sb = [m.sb(f"x{i}", [P, RT, D]) for i in range(2)]
        x_hi, x_lo = ([m.sb(f"x{n}{i}", [P, KD, SEL], F32R) for i in range(2)] for n in ("hi", "lo"))
        h_sb = [m.sb(f"h{i}", [P, SEL]) for i in range(2)]
        h_hi, h_lo = ([m.sb(f"h{n}{i}", [P, SEL], F32R) for i in range(2)] for n in ("hi", "lo"))
        y_sb = m.sb("y", [P, RT, D])
        pT = [m.ps(f"pT{i}") for i in range(2)]
        ph = [m.ps(f"ph{i}") for i in range(2)]
        py = [m.ps(f"py{c}") for c in range(RT)]
        s_w = [m.sem(f"w{i}") for i in range(BUF)]
        s_x = [m.sem(f"x{i}") for i in range(2)]
        s_const, s_wh, s_wl, s_T, s_xh, s_xl, s_h, s_g, s_hh, s_hl, s_y, s_ye, s_out = (
            m.sem(n) for n in "const wh wl T xh xl h g hh hl y ye out".split())
        tick_sp, tick_pool = m.sem("tick_sp"), m.sem("tick_pool")
        block = phase.enter_context(nc.Block())
        assert EX % 2 == 0 and HB % BUF == 0

        @block.sync
        def _(sp):
            sp.dma_start(ident_sb[:, :], ident).then_inc(s_const, 16)
            with sp.Fori(0, EX) as e:
                for n in range(HB):
                    q = n % BUF
                    sp.wait_ge(s_wl, e * 2 * HB + 2 * n + 2)
                    alone(sp, tick_sp)
                    sp.dma_start(w1_raw[q][:, :, :], w1[bass.ds(e, 1), :, n * P:(n + 1) * P].rearrange("e (k p) n -> p (e k) n", p=P)).then_inc(s_w[q], 16)
                    sp.dma_start(w2_raw[q][:, :], w2[bass.ds(e, 1), n * P:(n + 1) * P, :].rearrange("e p n -> (e p) n")).then_inc(s_w[q], 16)

        @block.gpsimd
        def _(pool):
            def rows(e, i):
                pool.dma_start(x_sb[i][:, :, :], x_rows[bass.ds(e * SEL, SEL), :].rearrange("(c p) n -> p c n", p=P)).then_inc(s_x[i], 16)
            for i in range(2):
                rows(i, i)

            def outputs(e):
                pool.wait_ge(s_ye, e * RT + RT)
                alone(pool, tick_pool)
                pool.dma_start(y_rows[bass.ds(e * SEL, SEL), :].rearrange("(c p) n -> p c n", p=P), y_sb[:, :, :]).then_inc(s_out, 16)
            with pool.Fori(0, EX // 2 - 1) as r:
                for i in range(2):
                    outputs(2 * r + i)
                    rows(2 * r + 2 + i, i)
            for i in range(2):
                outputs(EX - 2 + i)
            pool.wait_ge(s_out, EX * 16)

        @block.scalar
        def _(act):
            with act.Fori(0, EX // 2) as r:
                for i in range(2):
                    e = 2 * r + i
                    for c in range(RT):
                        act.wait_ge(s_T, e * RT + c + 1)
                        nc.scalar.copy(x_hi[i][:, :, c * P:(c + 1) * P], pT[c % 2][:, :].rearrange("p (k t) -> p k t", k=KD)).then_inc(s_xh, 1)

                    def weights(n):
                        q = n % BUF
                        act.wait_ge(s_w[q], e * (HB // BUF) * 32 + (n // BUF + 1) * 32)
                        if n >= 2:
                            act.wait_ge(s_h, e * HB + n - 1)
                        nc.scalar.copy(w1_hi[n % 2][:, :, :], w1_raw[q][:, :, :]).then_inc(s_wh, 1)
                        act.wait_ge(s_y, e * HB + max(n - 1, 0))
                        nc.scalar.copy(w2_hi[n % 2][:, :], w2_raw[q][:, :]).then_inc(s_wh, 1)
                    weights(0)
                    for n in range(HB):
                        if n + 1 < HB:
                            weights(n + 1)
                        act.wait_ge(s_h, e * HB + n + 1)
                        nc.scalar.activation(h_sb[n % 2][:, :], ph[n % 2][:, :], ACT.Gelu).then_inc(s_g, 1)
                        act.wait_ge(s_g, e * HB + n + 1)
                        nc.scalar.copy(h_hi[n % 2][:, :], h_sb[n % 2][:, :]).then_inc(s_hh, 1)

        @block.vector
        def _(dve):
            dve.sem_inc(s_wl, 2 * BUF)
            with dve.Fori(0, EX // 2) as r:
                for i in range(2):
                    e = 2 * r + i
                    for c in range(RT):
                        dve.wait_ge(s_xh, e * RT + c + 1)
                        at = slice(c * P, (c + 1) * P)
                        nc.vector.tensor_tensor(x_lo[i][:, :, at], pT[c % 2][:, :].rearrange("p (k t) -> p k t", k=KD),
                                                x_hi[i][:, :, at].bitcast(F32), ALU.subtract).then_inc(s_xl, 1)

                    def weights(n):
                        for j, (lo, hi, raw) in enumerate(((w1_lo, w1_hi, w1_raw), (w2_lo, w2_hi, w2_raw))):
                            dve.wait_ge(s_wh, (e * HB + n) * 2 + j + 1)
                            full = (slice(None),) * (3 - j)
                            nc.vector.tensor_tensor(lo[n % 2][full], raw[n % BUF][full], hi[n % 2][full].bitcast(F32), ALU.subtract).then_inc(s_wl, 1)
                    weights(0)
                    for n in range(HB):
                        if n + 1 < HB:
                            weights(n + 1)
                        dve.wait_ge(s_hh, e * HB + n + 1)
                        nc.vector.tensor_tensor(h_lo[n % 2][:, :], h_sb[n % 2][:, :], h_hi[n % 2][:, :].bitcast(F32), ALU.subtract).then_inc(s_hl, 1)
                    dve.wait_ge(s_y, e * HB + HB)
                    dve.wait_ge(s_out, e * 16)
                    for c in range(RT):
                        nc.vector.tensor_copy(y_sb[:, c, :], py[c][:, :]).then_inc(s_ye, 1)

        @block.tensor
        def _(pe):
            pe.wait_ge(s_const, 16)
            with pe.Fori(0, EX // 2) as r:
                for i in range(2):
                    e = 2 * r + i
                    pe.wait_ge(s_x[i], r * 16 + 16)
                    for c in range(RT):
                        pe.wait_ge(s_xl, e * RT + max(c - 1, 0))
                        for k in range(KD):
                            ins = nc.tensor.transpose(pT[c % 2][:, k * P:(k + 1) * P], x_sb[i][:, c, k * P:(k + 1) * P], ident_sb[:, :])
                        ins.then_inc(s_T, 1)
                    pe.wait_ge(s_xl, e * RT + RT)

                    def hidden(n):
                        pe.wait_ge(s_wl, 2 * BUF + (e * HB + n) * 2 + 1)
                        pe.wait_ge(s_g, e * HB + max(n - 1, 0))
                        for k in range(KD):
                            for j, (a, b) in enumerate(((w1_hi, x_hi), (w1_hi, x_lo), (w1_lo, x_hi))):
                                ins = nc.tensor.matmul(ph[n % 2][:, :], a[n % 2][:, k, :], b[i][:, k, :], start=(k == 0 and j == 0), stop=(k == KD - 1 and j == 2))
                        ins.then_inc(s_h, 1)

                    def output(n):
                        pe.wait_ge(s_hl, e * HB + n + 1)
                        pe.wait_ge(s_wl, 2 * BUF + (e * HB + n) * 2 + 2)
                        for c in range(RT):
                            at = slice(c * P, (c + 1) * P)
                            for j, (a, b) in enumerate(((h_hi, w2_hi), (h_hi, w2_lo), (h_lo, w2_hi))):
                                ins = nc.tensor.matmul(py[c][:, :], a[n % 2][:, at], b[n % 2][:, :], start=(n == 0 and j == 0), stop=(n == HB - 1 and j == 2))
                        ins.then_inc(s_y, 1)
                    hidden(0)
                    for n in range(HB):
                        if n + 1 < HB:
                            hidden(n + 1)
                        if n == 0:
                            pe.wait_ge(s_ye, e * RT)
                        output(n)


def decoder(nc, a, out):
    def scratch(name, *shape, dt=F32):
        return nc.dram_tensor(name, list(shape), dt).ap()

    def both(name):
        return scratch(name + "_tok", T, D), scratch(name + "_feat", KD, P, T)

    u_feat, u_tok, z_tok, y_tok = scratch("u0_feat", 12, P, T), scratch("u0_tok", T, 1536), scratch("z0_tok", T, 1536), scratch("y0_tok", T, 1536)
    slots, slots_y = scratch("slots", SLOTS, D), scratch("slots_y", SLOTS, D)
    rows, rows_y = scratch("rows", EX * SEL, D), scratch("rows_y", EX * SEL, D)
    dt_mean = scratch("dt_mean0", TILES, P, 48)
    x1_tok, x1_feat = both("x1")
    ssm0_project(nc, a["x"], a["ident"], a["norm_w"], a["w_in0"], a["b_in0"], a["conv_w0"], a["conv_b0"],
                 a["w_dt0"], a["head_mean"], u_feat, u_tok, z_tok, dt_mean, (slots, rows))
    ssm0_scan(nc, u_feat, u_tok, dt_mean, y_tok, a["ident"], a["w_bc"], a["b_bc"], a["head_pair"], a["b_dt0"],
              a["a_log0"], a["l2_alpha"], a["l2_beta"], a["ema"])
    ssm0_out(nc, a["x"], y_tok, z_tok, a["w_out0"], a["b_out0"], a["gate"], a["ident"], x1_tok, x1_feat)

    r_feat = scratch("r_feat", KD, P, T)
    x2_tok, x2_feat = both("x2")
    long_conv(nc, x1_feat, a["ctx_turned"], a["taps"], a["skip0"], a["exchange"], r_feat)
    norm_from_feat(nc, "b2", r_feat, a["ident"], x2_tok, x2_feat)

    places0, weights0 = scratch("places0", T, K_, dt=U32), scratch("weights0", T, K_)
    x3_tok, x3_feat = both("x3")
    moe0_route(nc, x2_tok, x2_feat, a["router0"], a["ident"], a["upper"], a["ramp"], slots, places0, weights0)
    moe0_experts(nc, slots, a["w_gu"], a["w_down"], a["ident"], slots_y)
    gather_mix_norm(nc, "c3", K_, slots_y, SLOTS, x2_tok, places0, weights0, a["ident"], x3_tok, x3_feat)

    u1, z1, dt1, bc1 = scratch("u1", F1, P, T), scratch("z1", F1, P, T), scratch("dt1", F1, P, T), scratch("bc1", 2 * N1, T)
    x4_tok, x4_feat = both("x4")
    ssm1_project(nc, x3_feat, a["w_in1"], a["conv_w1"], a["conv_b1"], a["w_x1"], a["w_dt1"], a["b_dt1"], u1, z1, dt1, bc1)
    ssm1_scan(nc, x3_tok, u1, z1, dt1, bc1, a["a_log1"], a["skip1"], a["w_out1"], a["ident"], x4_tok, x4_feat)

    x5_tok, x5_feat = both("x5")
    linear_attention(nc, x4_tok, x4_feat, a["ctx_feat"], a["w_q"], a["w_g"], a["b_g"], a["w_kv"], a["w_o"], a["ident"], a["heads_mask"], x5_tok, x5_feat)

    places1, weights1 = scratch("places1", T, TOP, dt=U32), scratch("weights1", T, TOP)
    moe1_route(nc, x5_tok, x5_feat, a["router1"], a["b_router1"], a["upper"], a["ramp"], rows, places1, weights1)
    moe1_experts(nc, rows, a["w1"], a["w2"], a["ident"], rows_y)
    gather_mix_norm(nc, "f3", TOP, rows_y, EX * SEL, x5_tok, places1, weights1, a["ident"], out, None)


def laid_out(i):
    import numpy as np
    H0, S0, DI0 = 24, 64, 1536
    by_feature = lambda v: v.reshape(T, D).T.reshape(KD, P, T)
    xp_w, xp_b = i["L0_attn_x_proj_w"].reshape(H0, 1 + 2 * S0, DI0), i["L0_attn_x_proj_b"].reshape(H0, 1 + 2 * S0)
    pairs = lambda w: w.reshape(H0 // 2, P, DI0 // P, P).transpose(0, 3, 2, 1)
    taps = np.zeros((32, P - 1 + D), np.float32)
    taps[:, P - 1:] = i["L0_xattn_ssm_kernel"]
    head_mean = np.zeros((DI0, H0), np.float32)
    for h in range(H0):
        head_mean[h * S0:(h + 1) * S0, h] = 1 / S0
    head_pair = np.zeros((P, 2), np.float32)
    head_pair[:S0, 0] = head_pair[S0:, 1] = 1
    heads_mask = np.zeros((P, P), np.float32)
    for h in range(4):
        heads_mask[h * 32:(h + 1) * 32, h * 32:(h + 1) * 32] = 1
    ident = np.eye(P, dtype=np.float32)
    upper = np.triu(np.ones((P, P), np.float32), 1)
    L0, L1 = (lambda n: i["L0_" + n]), (lambda n: i["L1_" + n])
    return {
        "ident": ident, "exchange": ident[::-1], "upper": upper, "ramp": np.arange(E_, dtype=np.float32),
        "head_mean": head_mean, "head_pair": head_pair, "heads_mask": heads_mask,
        "x": i["x"].reshape(T, D), "ctx_feat": by_feature(i["ctx_2048"]), "ctx_turned": by_feature(i["ctx_2048"])[:, ::-1],
        "norm_w": L0("attn_norm_w"), "w_in0": L0("attn_in_proj_w").T, "b_in0": L0("attn_in_proj_b"),
        "conv_w0": L0("attn_conv_w").reshape(DI0, 4), "conv_b0": L0("attn_conv_b"),
        "w_bc": np.concatenate([pairs(xp_w[:, 1:1 + S0]), pairs(xp_w[:, 1 + S0:])], -1),
        "b_bc": np.stack([xp_b[:, 1:1 + S0].reshape(H0 // 2, P), xp_b[:, 1 + S0:].reshape(H0 // 2, P)], -1),
        "w_dt0": xp_w[:, 0].T, "b_dt0": xp_b[:, 0], "a_log0": L0("attn_A_log"), "l2_alpha": L0("attn_log2_alpha_base"),
        "l2_beta": L0("attn_log2_beta"), "ema": L0("attn_surprise_ema"), "w_out0": L0("attn_out_proj_w").T, "b_out0": L0("attn_out_proj_b"),
        "gate": L0("attn_res_gate"), "taps": taps, "skip0": L0("xattn_D"), "router0": L0("ffn_router_w").T,
        "w_gu": np.concatenate([L0("ffn_w_gate"), L0("ffn_w_up")], -1).reshape(E_, KD, P, 2 * FF).transpose(0, 2, 1, 3), "w_down": L0("ffn_w_down"),
        "w_in1": L1("attn_W_in").T, "conv_w1": L1("attn_conv_w"), "conv_b1": L1("attn_conv_b"), "w_x1": L1("attn_W_x").T, "w_dt1": L1("attn_W_dt").T,
        "b_dt1": L1("attn_b_dt"), "a_log1": L1("attn_A_log"), "skip1": L1("attn_D"), "w_out1": L1("attn_W_out").T,
        "w_q": L1("xattn_Wq").T, "w_g": L1("xattn_Wg").T, "b_g": L1("xattn_bg"), "w_kv": L1("xattn_Wkv").T, "w_o": L1("xattn_Wo").T,
        "router1": L1("ffn_Wg"), "b_router1": L1("ffn_bg"), "w1": L1("ffn_W1"), "w2": L1("ffn_W2"),
    }


def kernel(**inputs):
    import numpy as np
    import concourse.bacc as bacc
    from concourse.bass_utils import run_bass_kernel_spmd

    nc = bacc.Bacc("TRN2", target_bir_lowering=False, num_devices=1)
    arrays = {n: np.ascontiguousarray(v) for n, v in laid_out({n: np.asarray(v) for n, v in inputs.items()}).items()}
    aps = {n: nc.dram_tensor(n, v.shape, mybir.dt.from_np(v.dtype), kind="ExternalInput").ap() for n, v in arrays.items()}
    out = nc.dram_tensor("out", (T, D), F32, kind="ExternalOutput").ap()
    decoder(nc, aps, out)
    result = run_bass_kernel_spmd(nc, [arrays], core_ids=[0])
    return result.results[0]["out"].reshape(NB, L, D)
```
